# Optimizing a Trainium2 kernel written in Bass

```python
import numpy as np
import jax
import jax.numpy as jnp

def _softmax(x, axis=-1):
    return jax.nn.softmax(x, axis=axis)

def _gelu(x):
    return jax.nn.gelu(x, approximate=True)

def _silu(x):
    return jax.nn.silu(x)

def _sigmoid(x):
    return jax.nn.sigmoid(x)

def _layernorm(x, axis=-1, eps=1e-05):
    m = jnp.mean(x, axis=axis, keepdims=True)
    v = jnp.var(x, axis=axis, keepdims=True)
    return (x - m) / jnp.sqrt(v + eps)

def _scatter_add(tgt, idx, src, axis=0):
    return tgt.at[idx].add(src)

def _segment_sum(src, seg, n):
    return jax.ops.segment_sum(src, seg, n)
kernel_name = 'mk_conv_attn_hybrid_d4_conv_nchw256_r4_b38b8c'

def setup_inputs(seed: int=0):
    np.random.seed(seed)
    _w = jnp.asarray

    def _rec_inputs():
        import jax
        import jax.numpy as jnp
        _gk = jax.random.key(seed)
        x = -0.0005207 + 1.001 * jax.random.normal(jax.random.fold_in(_gk, 1), (8, 64, 32, 32), jnp.float32)
        return x
    x = _rec_inputs()

    def _L0_conv_setup():
        import jax, jax.numpy as jnp
        import numpy as np
        DIM = 64
        DT_RANK = 32
        D_STATE = 16
        DEPTH = 12
        B, H, W = (8, 32, 32)
        LN_EPS = 1e-05

        def _ssm(x, dbc_w, dtp_w, dtp_b, A_log, Dp):
            A = -jnp.exp(A_log)
            dbc = jnp.einsum('bld,ed->ble', x, dbc_w)
            delta, Bm, Cm = jnp.split(dbc, [DT_RANK, DT_RANK + D_STATE], axis=-1)
            delta = jax.nn.softplus(jnp.einsum('blr,dr->bld', delta, dtp_w) + dtp_b)
            dA = jnp.exp(delta[..., None] * A)
            dBu = delta[..., None] * Bm[:, :, None, :] * x[..., None]

            def step(h, inputs):
                dA_t, dBu_t, C_t = inputs
                h = dA_t * h + dBu_t
                y = jnp.einsum('bdn,bn->bd', h, C_t)
                return (h, y)
            h0 = jnp.zeros((x.shape[0], x.shape[2], D_STATE), x.dtype)
            _, ys = jax.lax.scan(step, h0, (dA.transpose(1, 0, 2, 3), dBu.transpose(1, 0, 2, 3), Cm.transpose(1, 0, 2)))
            y = ys.transpose(1, 0, 2)
            return y + x * Dp

        def _block(x, p):
            ln_g, ln_b, pw, pb, cfw, cfb, cbw, cbb, dbcw, dtpw, dtpb, alog, dp = p
            skip = x
            mu = x.mean(-1, keepdims=True)
            var = ((x - mu) ** 2).mean(-1, keepdims=True)
            xn = (x - mu) / jnp.sqrt(var + LN_EPS) * ln_g + ln_b
            xp = jnp.einsum('bld,ed->ble', xn, pw) + pb
            z = jax.nn.silu(xp)
            xf = jax.nn.softplus(jnp.einsum('bld,ed->ble', xp, cfw) + cfb)
            x1 = _ssm(xf, dbcw, dtpw, dtpb, alog, dp)
            xr = xp[:, ::-1, :]
            xb = jax.nn.softplus(jnp.einsum('bld,ed->ble', xr, cbw) + cbb)
            x2 = _ssm(xb, dbcw, dtpw, dtpb, alog, dp)[:, ::-1, :]
            return x1 * z + x2 * z + skip
        key = jax.random.key(seed)
        ks = jax.random.split(key, 8)
        d, r, n, L = (DIM, DT_RANK, D_STATE, DEPTH)

        def nrm(k, shape, scale=0.02):
            return jax.random.normal(k, shape, dtype=jnp.float32) * scale
        A_log = jnp.tile(jnp.log(jnp.arange(1, n + 1, dtype=jnp.float32))[None, None, :], (L, d, 1))
        return {'x': jax.random.normal(ks[0], (B, d, H, W), dtype=jnp.float32), 'ln_g': jnp.ones((L, d), jnp.float32), 'ln_b': jnp.zeros((L, d), jnp.float32), 'proj_w': nrm(ks[1], (L, d, d)), 'proj_b': jnp.zeros((L, d), jnp.float32), 'convf_w': nrm(ks[2], (L, d, d)), 'convf_b': jnp.zeros((L, d), jnp.float32), 'convb_w': nrm(ks[3], (L, d, d)), 'convb_b': jnp.zeros((L, d), jnp.float32), 'dbc_w': nrm(ks[4], (L, r + 2 * n, d)), 'dtp_w': nrm(ks[5], (L, d, r)), 'dtp_b': jnp.zeros((L, d), jnp.float32), 'A_log': A_log, 'D_param': jnp.ones((L, d), jnp.float32)}
    _L0_conv_all = _L0_conv_setup()
    _L0_conv_in = {k: v for k, v in _L0_conv_all.items() if k in ('ln_g', 'ln_b', 'proj_w', 'proj_b', 'convf_w', 'convf_b', 'convb_w', 'convb_b', 'dbc_w', 'dtp_w', 'dtp_b', 'A_log', 'D_param')}
    del _L0_conv_all

    def _L1_conv_setup():
        import jax, jax.numpy as jnp
        import numpy as np
        from jax import lax
        DN = ('NCHW', 'OIHW', 'NCHW')

        def conv2d(x, w, b, pad):
            y = lax.conv_general_dilated(x, w, window_strides=(1, 1), padding=pad, dimension_numbers=DN)
            return y + b[None, :, None, None]
        key = jax.random.key(seed)
        ks = jax.random.split(key, 14)
        B, C, H, W = (4, 64, 16, 16)
        Cr = C // 4
        Hid = max(C // 16, 4)
        g = lambda k, shape, fan: jax.random.normal(k, shape, jnp.float32) * fan ** (-0.5)
        return {'x': jax.random.normal(ks[0], (B, C, H, W), jnp.float32), 'wq': g(ks[1], (Cr, C, 3, 3), C * 9), 'bq': jnp.zeros((Cr,), jnp.float32), 'wk': g(ks[2], (Cr, C, 3, 3), C * 9), 'bk': jnp.zeros((Cr,), jnp.float32), 'wv': g(ks[3], (C, C, 3, 3), C * 9), 'bv': jnp.zeros((C,), jnp.float32), 'fc1_w': g(ks[4], (Hid, C), C), 'fc1_b': jnp.zeros((Hid,), jnp.float32), 'fc2_w': g(ks[5], (C, Hid), Hid), 'fc2_b': jnp.zeros((C,), jnp.float32), 'fuse_w': g(ks[6], (C, 2 * C, 1, 1), 2 * C), 'fuse_b': jnp.zeros((C,), jnp.float32)}
    _L1_conv_all = _L1_conv_setup()
    _L1_conv_in = {k: v for k, v in _L1_conv_all.items() if k in ('wq', 'bq', 'wk', 'bk', 'wv', 'bv', 'fc1_w', 'fc1_b', 'fc2_w', 'fc2_b', 'fuse_w', 'fuse_b')}
    del _L1_conv_all

    def _L2_attn_setup():
        import jax, jax.numpy as jnp
        import numpy as np
        NUM_HEADS = 4
        HEAD_DIM = 16
        NEG_SLOPE = 0.2
        key = jax.random.key(seed)
        k1, k2 = jax.random.split(key)
        h = jax.random.normal(k1, (8, 512, 64), dtype=jnp.float32)
        W = jax.random.normal(k2, (64, 64), dtype=jnp.float32) * (1.0 / np.sqrt(256.0))
        return {'h': h, 'W': W}
    _L2_attn_all = _L2_attn_setup()
    _L2_attn_in = {k: v for k, v in _L2_attn_all.items() if k in ('W',)}
    del _L2_attn_all

    def _L2_ffn_setup():
        import jax, jax.numpy as jnp
        import numpy as np
        B, N, D = (16, 1024, 64)
        NUM_EXPERTS, TOP_K, HEADS = (4, 2, 4)
        N_EDGES = 262144
        LN_EPS = 1e-05

        def _layernorm(x, g, b):
            mu = x.mean(-1, keepdims=True)
            var = ((x - mu) ** 2).mean(-1, keepdims=True)
            return (x - mu) * jax.lax.rsqrt(var + LN_EPS) * g + b

        def _forward(x, edge_index, W_gat, att_src, att_dst, b_gat, ln_gamma, ln_beta, W1, b1, W2, b2):
            Bc, Nc, Dc = x.shape
            M = Bc * Nc
            x_flat = x.reshape(M, Dc)
            h = (x_flat @ W_gat).reshape(M, HEADS, NUM_EXPERTS)
            loops = jnp.arange(M, dtype=edge_index.dtype)
            src = jnp.concatenate([edge_index[0], loops])
            dst = jnp.concatenate([edge_index[1], loops])
            a_src = (h * att_src).sum(-1)
            a_dst = (h * att_dst).sum(-1)
            e = jax.nn.leaky_relu(a_src[src] + a_dst[dst], negative_slope=0.2)
            e_max = jax.ops.segment_max(e, dst, num_segments=M)
            ee = jnp.exp(e - e_max[dst])
            denom = jax.ops.segment_sum(ee, dst, num_segments=M)
            alpha = ee / (denom[dst] + 1e-16)
            msg = h[src] * alpha[:, :, None]
            agg = jax.ops.segment_sum(msg, dst, num_segments=M).reshape(M, HEADS * NUM_EXPERTS) + b_gat
            scores = _layernorm(agg, ln_gamma, ln_beta).reshape(M, HEADS, NUM_EXPERTS).mean(1)
            scores = scores.reshape(Bc, Nc, NUM_EXPERTS)
            topk_s, topk_i = jax.lax.top_k(scores, TOP_K)
            w = jax.nn.softmax(topk_s, axis=-1)
            out = jnp.zeros_like(x)
            for ei in range(NUM_EXPERTS):
                g = jnp.where(topk_i == ei, w, 0.0).sum(-1)
                hh = jax.nn.gelu(x @ W1[ei] + b1[ei], approximate=False)
                out = out + g[..., None] * (hh @ W2[ei] + b2[ei])
            return out
        key = jax.random.key(seed)
        ks = jax.random.split(key, 8)
        s = 0.05
        return {'x': jax.random.normal(ks[0], (B, N, D), jnp.float32), 'W_gat': jax.random.normal(ks[1], (D, HEADS * NUM_EXPERTS), jnp.float32) * s, 'att_src': jax.random.normal(ks[2], (HEADS, NUM_EXPERTS), jnp.float32) * s, 'att_dst': jax.random.normal(ks[3], (HEADS, NUM_EXPERTS), jnp.float32) * s, 'b_gat': jnp.zeros((HEADS * NUM_EXPERTS,), jnp.float32), 'ln_gamma': jnp.ones((HEADS * NUM_EXPERTS,), jnp.float32), 'ln_beta': jnp.zeros((HEADS * NUM_EXPERTS,), jnp.float32), 'W1': jax.random.normal(ks[4], (NUM_EXPERTS, D, 2 * D), jnp.float32) * s, 'b1': jnp.zeros((NUM_EXPERTS, 2 * D), jnp.float32), 'W2': jax.random.normal(ks[5], (NUM_EXPERTS, 2 * D, D), jnp.float32) * s, 'b2': jnp.zeros((NUM_EXPERTS, D), jnp.float32), 'edge_index': jax.random.randint(ks[6], (2, N_EDGES), 0, B * N, jnp.int32)}
    _L2_ffn_all = _L2_ffn_setup()
    _L2_ffn_in = {k: v for k, v in _L2_ffn_all.items() if k in ('W_gat', 'att_src', 'att_dst', 'b_gat', 'ln_gamma', 'ln_beta', 'W1', 'b1', 'W2', 'b2', 'edge_index')}
    del _L2_ffn_all

    def _L3_attn_setup():
        import jax, jax.numpy as jnp
        import numpy as np
        B, N, C = (4, 4096, 64)
        NC, S, H, D = (64, 16, 8, 32)
        key = jax.random.key(seed)
        ks = jax.random.split(key, 5)

        def dense_w(k, fan_in, fan_out):
            return jax.random.normal(k, (fan_in, fan_out), jnp.float32) * (1.0 / np.sqrt(fan_in))
        return {'x': jax.random.normal(ks[0], (B, N, C), jnp.float32), 'W0': dense_w(ks[1], C, NC), 'b0': jnp.zeros((NC,), jnp.float32), 'Ws': dense_w(ks[2], NC, S), 'bs': jnp.zeros((S,), jnp.float32), 'Wqkv': dense_w(ks[3], NC, 3 * H * D), 'bqkv': jnp.zeros((3 * H * D,), jnp.float32), 'Wout': dense_w(ks[4], H * D, C), 'bout': jnp.zeros((C,), jnp.float32)}
    _L3_attn_all = _L3_attn_setup()
    _L3_attn_in = {k: v for k, v in _L3_attn_all.items() if k in ('W0', 'b0', 'Ws', 'bs', 'Wqkv', 'bqkv', 'Wout', 'bout')}
    del _L3_attn_all

    def _L3_ffn_setup():
        import jax, jax.numpy as jnp
        import numpy as np
        D_MODEL = 64
        N_EXPERTS = 16
        HIDDEN = 128
        SCALE = 0.02
        key = jax.random.key(seed)
        ks = jax.random.split(key, 5)
        x = jax.random.normal(ks[0], (4, 2048, D_MODEL), dtype=jnp.float32)
        gate_w = jax.random.normal(ks[1], (D_MODEL, N_EXPERTS), dtype=jnp.float32) * SCALE
        gate_b = jnp.zeros((N_EXPERTS,), dtype=jnp.float32)
        w1 = jax.random.normal(ks[2], (N_EXPERTS, D_MODEL, HIDDEN), dtype=jnp.float32) * SCALE
        w2 = jax.random.normal(ks[3], (N_EXPERTS, D_MODEL, HIDDEN), dtype=jnp.float32) * SCALE
        w3 = jax.random.normal(ks[4], (N_EXPERTS, HIDDEN, D_MODEL), dtype=jnp.float32) * SCALE
        return {'x': x, 'gate_w': gate_w, 'gate_b': gate_b, 'w1': w1, 'w2': w2, 'w3': w3}
    _L3_ffn_all = _L3_ffn_setup()
    _L3_ffn_in = {k: v for k, v in _L3_ffn_all.items() if k in ('gate_w', 'gate_b', 'w1', 'w2', 'w3')}
    del _L3_ffn_all
    return {'x': x, 'L0_conv_ln_g': _L0_conv_in['ln_g'], 'L0_conv_ln_b': _L0_conv_in['ln_b'], 'L0_conv_proj_w': _L0_conv_in['proj_w'], 'L0_conv_proj_b': _L0_conv_in['proj_b'], 'L0_conv_convf_w': _L0_conv_in['convf_w'], 'L0_conv_convf_b': _L0_conv_in['convf_b'], 'L0_conv_convb_w': _L0_conv_in['convb_w'], 'L0_conv_convb_b': _L0_conv_in['convb_b'], 'L0_conv_dbc_w': _L0_conv_in['dbc_w'], 'L0_conv_dtp_w': _L0_conv_in['dtp_w'], 'L0_conv_dtp_b': _L0_conv_in['dtp_b'], 'L0_conv_A_log': _L0_conv_in['A_log'], 'L0_conv_D_param': _L0_conv_in['D_param'], 'L1_conv_wq': _L1_conv_in['wq'], 'L1_conv_bq': _L1_conv_in['bq'], 'L1_conv_wk': _L1_conv_in['wk'], 'L1_conv_bk': _L1_conv_in['bk'], 'L1_conv_wv': _L1_conv_in['wv'], 'L1_conv_bv': _L1_conv_in['bv'], 'L1_conv_fc1_w': _L1_conv_in['fc1_w'], 'L1_conv_fc1_b': _L1_conv_in['fc1_b'], 'L1_conv_fc2_w': _L1_conv_in['fc2_w'], 'L1_conv_fc2_b': _L1_conv_in['fc2_b'], 'L1_conv_fuse_w': _L1_conv_in['fuse_w'], 'L1_conv_fuse_b': _L1_conv_in['fuse_b'], 'L2_attn_W': _L2_attn_in['W'], 'L2_ffn_W_gat': _L2_ffn_in['W_gat'], 'L2_ffn_att_src': _L2_ffn_in['att_src'], 'L2_ffn_att_dst': _L2_ffn_in['att_dst'], 'L2_ffn_b_gat': _L2_ffn_in['b_gat'], 'L2_ffn_ln_gamma': _L2_ffn_in['ln_gamma'], 'L2_ffn_ln_beta': _L2_ffn_in['ln_beta'], 'L2_ffn_W1': _L2_ffn_in['W1'], 'L2_ffn_b1': _L2_ffn_in['b1'], 'L2_ffn_W2': _L2_ffn_in['W2'], 'L2_ffn_b2': _L2_ffn_in['b2'], 'L2_ffn_edge_index': _L2_ffn_in['edge_index'], 'L3_attn_W0': _L3_attn_in['W0'], 'L3_attn_b0': _L3_attn_in['b0'], 'L3_attn_Ws': _L3_attn_in['Ws'], 'L3_attn_bs': _L3_attn_in['bs'], 'L3_attn_Wqkv': _L3_attn_in['Wqkv'], 'L3_attn_bqkv': _L3_attn_in['bqkv'], 'L3_attn_Wout': _L3_attn_in['Wout'], 'L3_attn_bout': _L3_attn_in['bout'], 'L3_ffn_gate_w': _L3_ffn_in['gate_w'], 'L3_ffn_gate_b': _L3_ffn_in['gate_b'], 'L3_ffn_w1': _L3_ffn_in['w1'], 'L3_ffn_w2': _L3_ffn_in['w2'], 'L3_ffn_w3': _L3_ffn_in['w3']}

def reference(x, L0_conv_ln_g, L0_conv_ln_b, L0_conv_proj_w, L0_conv_proj_b, L0_conv_convf_w, L0_conv_convf_b, L0_conv_convb_w, L0_conv_convb_b, L0_conv_dbc_w, L0_conv_dtp_w, L0_conv_dtp_b, L0_conv_A_log, L0_conv_D_param, L1_conv_wq, L1_conv_bq, L1_conv_wk, L1_conv_bk, L1_conv_wv, L1_conv_bv, L1_conv_fc1_w, L1_conv_fc1_b, L1_conv_fc2_w, L1_conv_fc2_b, L1_conv_fuse_w, L1_conv_fuse_b, L2_attn_W, L2_ffn_W_gat, L2_ffn_att_src, L2_ffn_att_dst, L2_ffn_b_gat, L2_ffn_ln_gamma, L2_ffn_ln_beta, L2_ffn_W1, L2_ffn_b1, L2_ffn_W2, L2_ffn_b2, L2_ffn_edge_index, L3_attn_W0, L3_attn_b0, L3_attn_Ws, L3_attn_bs, L3_attn_Wqkv, L3_attn_bqkv, L3_attn_Wout, L3_attn_bout, L3_ffn_gate_w, L3_ffn_gate_b, L3_ffn_w1, L3_ffn_w2, L3_ffn_w3):
    import jax
    import jax.numpy as jnp

    def _L0_conv_ref(x, ln_g, ln_b, proj_w, proj_b, convf_w, convf_b, convb_w, convb_b, dbc_w, dtp_w, dtp_b, A_log, D_param):
        import jax, jax.numpy as jnp
        import numpy as np
        DIM = 64
        DT_RANK = 32
        D_STATE = 16
        DEPTH = 12
        B, H, W = (8, 32, 32)
        LN_EPS = 1e-05

        def _ssm(x, dbc_w, dtp_w, dtp_b, A_log, Dp):
            A = -jnp.exp(A_log)
            dbc = jnp.einsum('bld,ed->ble', x, dbc_w)
            delta, Bm, Cm = jnp.split(dbc, [DT_RANK, DT_RANK + D_STATE], axis=-1)
            delta = jax.nn.softplus(jnp.einsum('blr,dr->bld', delta, dtp_w) + dtp_b)
            dA = jnp.exp(delta[..., None] * A)
            dBu = delta[..., None] * Bm[:, :, None, :] * x[..., None]

            def step(h, inputs):
                dA_t, dBu_t, C_t = inputs
                h = dA_t * h + dBu_t
                y = jnp.einsum('bdn,bn->bd', h, C_t)
                return (h, y)
            h0 = jnp.zeros((x.shape[0], x.shape[2], D_STATE), x.dtype)
            _, ys = jax.lax.scan(step, h0, (dA.transpose(1, 0, 2, 3), dBu.transpose(1, 0, 2, 3), Cm.transpose(1, 0, 2)))
            y = ys.transpose(1, 0, 2)
            return y + x * Dp

        def _block(x, p):
            ln_g, ln_b, pw, pb, cfw, cfb, cbw, cbb, dbcw, dtpw, dtpb, alog, dp = p
            skip = x
            mu = x.mean(-1, keepdims=True)
            var = ((x - mu) ** 2).mean(-1, keepdims=True)
            xn = (x - mu) / jnp.sqrt(var + LN_EPS) * ln_g + ln_b
            xp = jnp.einsum('bld,ed->ble', xn, pw) + pb
            z = jax.nn.silu(xp)
            xf = jax.nn.softplus(jnp.einsum('bld,ed->ble', xp, cfw) + cfb)
            x1 = _ssm(xf, dbcw, dtpw, dtpb, alog, dp)
            xr = xp[:, ::-1, :]
            xb = jax.nn.softplus(jnp.einsum('bld,ed->ble', xr, cbw) + cbb)
            x2 = _ssm(xb, dbcw, dtpw, dtpb, alog, dp)[:, ::-1, :]
            return x1 * z + x2 * z + skip
        b, c, h, w = x.shape
        seq = x.reshape(b, c, h * w).transpose(0, 2, 1)
        params = (ln_g, ln_b, proj_w, proj_b, convf_w, convf_b, convb_w, convb_b, dbc_w, dtp_w, dtp_b, A_log, D_param)

        def layer_step(s, p):
            return (_block(s, p), None)
        seq, _ = jax.lax.scan(layer_step, seq, params)
        return seq.transpose(0, 2, 1).reshape(b, c, h, w)

    def _L1_conv_ref(x, wq, bq, wk, bk, wv, bv, fc1_w, fc1_b, fc2_w, fc2_b, fuse_w, fuse_b):
        import jax, jax.numpy as jnp
        import numpy as np
        from jax import lax
        DN = ('NCHW', 'OIHW', 'NCHW')

        def conv2d(x, w, b, pad):
            y = lax.conv_general_dilated(x, w, window_strides=(1, 1), padding=pad, dimension_numbers=DN)
            return y + b[None, :, None, None]
        b, c, h, w = x.shape
        hw = h * w
        q = conv2d(x, wq, bq, 'SAME').reshape(b, -1, hw)
        k = conv2d(x, wk, bk, 'SAME').reshape(b, -1, hw)
        v = conv2d(x, wv, bv, 'SAME').reshape(b, c, hw)
        scale = q.shape[1] ** (-0.5)
        attn = jnp.einsum('bci,bcj->bij', q, k) * scale
        attn = jax.nn.softmax(attn, axis=-1)
        local = jnp.einsum('bcj,bij->bci', v, attn).reshape(b, c, h, w)
        y = jnp.mean(x, axis=(2, 3))
        y = jax.nn.relu(y @ fc1_w.T + fc1_b)
        y = jax.nn.sigmoid(y @ fc2_w.T + fc2_b)
        glob = x * y[:, :, None, None]
        cat = jnp.concatenate([local, glob], axis=1)
        return conv2d(cat, fuse_w, fuse_b, 'VALID')

    def _L2_attn_ref(h, W):
        import jax, jax.numpy as jnp
        import numpy as np
        NUM_HEADS = 4
        HEAD_DIM = 16
        NEG_SLOPE = 0.2
        B, T, _ = h.shape
        Wh = (h @ W).reshape(B, T, NUM_HEADS, HEAD_DIM).transpose(0, 2, 1, 3)
        scale = 1.0 / HEAD_DIM ** 0.5
        scores = jnp.einsum('bhtd,bhsd->bhts', Wh, Wh) * scale
        attention = jax.nn.softmax(jax.nn.leaky_relu(scores, negative_slope=NEG_SLOPE), axis=-1)
        h_prime = jnp.einsum('bhts,bhsd->bhtd', attention, Wh)
        return h_prime.transpose(0, 2, 1, 3).reshape(B, T, NUM_HEADS * HEAD_DIM)

    def _L2_ffn_ref(x, W_gat, att_src, att_dst, b_gat, ln_gamma, ln_beta, W1, b1, W2, b2, edge_index):
        import jax, jax.numpy as jnp
        import numpy as np
        B, N, D = (16, 1024, 64)
        NUM_EXPERTS, TOP_K, HEADS = (4, 2, 4)
        N_EDGES = 262144
        LN_EPS = 1e-05

        def _layernorm(x, g, b):
            mu = x.mean(-1, keepdims=True)
            var = ((x - mu) ** 2).mean(-1, keepdims=True)
            return (x - mu) * jax.lax.rsqrt(var + LN_EPS) * g + b

        def _forward(x, edge_index, W_gat, att_src, att_dst, b_gat, ln_gamma, ln_beta, W1, b1, W2, b2):
            Bc, Nc, Dc = x.shape
            M = Bc * Nc
            x_flat = x.reshape(M, Dc)
            h = (x_flat @ W_gat).reshape(M, HEADS, NUM_EXPERTS)
            loops = jnp.arange(M, dtype=edge_index.dtype)
            src = jnp.concatenate([edge_index[0], loops])
            dst = jnp.concatenate([edge_index[1], loops])
            a_src = (h * att_src).sum(-1)
            a_dst = (h * att_dst).sum(-1)
            e = jax.nn.leaky_relu(a_src[src] + a_dst[dst], negative_slope=0.2)
            e_max = jax.ops.segment_max(e, dst, num_segments=M)
            ee = jnp.exp(e - e_max[dst])
            denom = jax.ops.segment_sum(ee, dst, num_segments=M)
            alpha = ee / (denom[dst] + 1e-16)
            msg = h[src] * alpha[:, :, None]
            agg = jax.ops.segment_sum(msg, dst, num_segments=M).reshape(M, HEADS * NUM_EXPERTS) + b_gat
            scores = _layernorm(agg, ln_gamma, ln_beta).reshape(M, HEADS, NUM_EXPERTS).mean(1)
            scores = scores.reshape(Bc, Nc, NUM_EXPERTS)
            topk_s, topk_i = jax.lax.top_k(scores, TOP_K)
            w = jax.nn.softmax(topk_s, axis=-1)
            out = jnp.zeros_like(x)
            for ei in range(NUM_EXPERTS):
                g = jnp.where(topk_i == ei, w, 0.0).sum(-1)
                hh = jax.nn.gelu(x @ W1[ei] + b1[ei], approximate=False)
                out = out + g[..., None] * (hh @ W2[ei] + b2[ei])
            return out
        return _forward(x, edge_index, W_gat, att_src, att_dst, b_gat, ln_gamma, ln_beta, W1, b1, W2, b2)

    def _L3_attn_ref(x, W0, b0, Ws, bs, Wqkv, bqkv, Wout, bout):
        import jax, jax.numpy as jnp
        import numpy as np
        B, N, C = (4, 4096, 64)
        NC, S, H, D = (64, 16, 8, 32)
        b, n, c = x.shape
        h = x @ W0 + b0
        sw = jax.nn.softmax(h @ Ws + bs, axis=-1)
        qkv = (h @ Wqkv + bqkv).reshape(b, n, 3, H, D)
        qkv = jnp.transpose(qkv, (2, 0, 3, 1, 4))
        q, k, v = (qkv[0], qkv[1], qkv[2])
        denom = jnp.sum(sw, axis=1)[:, None, :, None] + 1e-09
        qs = jnp.einsum('bhnd,bns->bhsd', q, sw) / denom
        ks = jnp.einsum('bhnd,bns->bhsd', k, sw) / denom
        vs = jnp.einsum('bhnd,bns->bhsd', v, sw) / denom
        scale = jnp.float32(D) ** 0.5
        attn = jax.nn.softmax(jnp.einsum('bhsd,bhtd->bhst', qs, ks) / scale, axis=-1)
        tok = jnp.einsum('bhst,bhtd->bhsd', attn, vs)
        out = jnp.einsum('bhsd,bns->bnhd', tok, sw).reshape(b, n, H * D)
        return out @ Wout + bout

    def _L3_ffn_ref(x, gate_w, gate_b, w1, w2, w3):
        import jax, jax.numpy as jnp
        import numpy as np
        D_MODEL = 64
        N_EXPERTS = 16
        HIDDEN = 128
        SCALE = 0.02
        n_experts = w1.shape[0]
        logits = jnp.einsum('bsd,de->bse', x, gate_w) + gate_b
        probs = jax.nn.softmax(logits, axis=-1)
        top_probs, top_idx = jax.lax.top_k(probs, 2)
        top_probs = top_probs / jnp.sum(top_probs, axis=-1, keepdims=True)
        dispatch = jnp.sum(jax.nn.one_hot(top_idx, n_experts, dtype=x.dtype) * top_probs[..., None], axis=-2)
        h1 = jnp.einsum('bsd,edh->bseh', x, w1)
        h2 = jnp.einsum('bsd,edh->bseh', x, w2)
        hidden = jax.nn.silu(h1) * h2
        expert_out = jnp.einsum('bseh,eho->bseo', hidden, w3)
        return jnp.einsum('bseo,bse->bso', expert_out, dispatch)

    def _gn(v, G=32, eps=1e-05):
        B_, C_, H_, W_ = v.shape
        g = v.reshape(B_, G, C_ // G, H_, W_)
        m = jnp.mean(g, axis=(2, 3, 4), keepdims=True)
        s = jnp.var(g, axis=(2, 3, 4), keepdims=True)
        return ((g - m) / jnp.sqrt(s + eps)).reshape(v.shape)

    def _ln_c(v, eps=1e-06):
        m = jnp.mean(v, axis=1, keepdims=True)
        s = jnp.var(v, axis=1, keepdims=True)
        return (v - m) / jnp.sqrt(s + eps)

    def _ln_t(v, eps=1e-05):
        m = jnp.mean(v, axis=-1, keepdims=True)
        s = jnp.var(v, axis=-1, keepdims=True)
        return (v - m) / jnp.sqrt(s + eps)

    def _to_tokens(v):
        B_, C_, H_, W_ = v.shape
        return v.reshape(B_, C_, H_ * W_).transpose(0, 2, 1)

    def _from_tokens(t, like):
        B_, C_, H_, W_ = like.shape
        return t.transpose(0, 2, 1).reshape(B_, C_, H_, W_)
    x = _L0_conv_ref(x, L0_conv_ln_g, L0_conv_ln_b, L0_conv_proj_w, L0_conv_proj_b, L0_conv_convf_w, L0_conv_convf_b, L0_conv_convb_w, L0_conv_convb_b, L0_conv_dbc_w, L0_conv_dtp_w, L0_conv_dtp_b, L0_conv_A_log, L0_conv_D_param)
    x = x + _L1_conv_ref(_gn(x), L1_conv_wq, L1_conv_bq, L1_conv_wk, L1_conv_bk, L1_conv_wv, L1_conv_bv, L1_conv_fc1_w, L1_conv_fc1_b, L1_conv_fc2_w, L1_conv_fc2_b, L1_conv_fuse_w, L1_conv_fuse_b)
    t = _to_tokens(x)
    t = t + _L2_attn_ref(_ln_t(t), L2_attn_W)
    t = t + _L2_ffn_ref(_ln_t(t), L2_ffn_W_gat, L2_ffn_att_src, L2_ffn_att_dst, L2_ffn_b_gat, L2_ffn_ln_gamma, L2_ffn_ln_beta, L2_ffn_W1, L2_ffn_b1, L2_ffn_W2, L2_ffn_b2, L2_ffn_edge_index)
    t = t + _L3_attn_ref(_ln_t(t), L3_attn_W0, L3_attn_b0, L3_attn_Ws, L3_attn_bs, L3_attn_Wqkv, L3_attn_bqkv, L3_attn_Wout, L3_attn_bout)
    t = t + _L3_ffn_ref(_ln_t(t), L3_ffn_gate_w, L3_ffn_gate_b, L3_ffn_w1, L3_ffn_w2, L3_ffn_w3)
    x = _from_tokens(t, x)
    return x

_drawn_inputs = setup_inputs


def setup_inputs(seed=0):
    import zlib

    import numpy as np

    out = dict(_drawn_inputs(seed))
    spreads = {'L0_conv_ln_g': (1.0, 0.2),
     'L0_conv_ln_b': (0.0, 0.1),
     'L0_conv_proj_b': (0.0, 0.1),
     'L0_conv_convf_b': (0.0, 0.365),
     'L0_conv_convb_b': (0.0, 0.1),
     'L0_conv_dtp_b': (0.0, 0.8),
     'L0_conv_D_param': (1.0, 0.2),
     'L1_conv_bq': (0.0, 0.8),
     'L1_conv_bk': (0.0, 0.8),
     'L1_conv_bv': (0.0, 0.1),
     'L1_conv_fc1_b': (0.0, 0.579),
     'L1_conv_fc2_b': (0.0, 0.476),
     'L1_conv_fuse_b': (0.0, 0.1),
     'L2_ffn_b_gat': (0.0, 0.1),
     'L2_ffn_ln_gamma': (1.0, 0.2),
     'L2_ffn_ln_beta': (0.0, 0.369),
     'L2_ffn_b1': (0.0, 0.309),
     'L2_ffn_b2': (0.0, 0.1),
     'L3_attn_b0': (0.0, 0.1),
     'L3_attn_bs': (0.0, 0.8),
     'L3_attn_bqkv': (0.0, 0.1),
     'L3_attn_bout': (0.0, 0.1),
     'L3_ffn_gate_b': (0.0, 0.8)}
    factors = {'L0_conv_convf_w': 7.055,
     'L0_conv_convb_w': 5.96,
     'L0_conv_dtp_w': 8.0,
     'L0_conv_A_log': 5.363,
     'L1_conv_fc1_w': 4.087,
     'L1_conv_fc2_w': 2.991,
     'L2_ffn_att_src': 5.617,
     'L2_ffn_att_dst': 6.605,
     'L3_attn_Ws': 4.335,
     'L3_ffn_gate_w': 8.0,
     'L3_ffn_w1': 8.0,
     'L3_ffn_w2': 8.0,
     'L3_ffn_w3': 8.0}
    for name, (base, spread) in spreads.items():
        noise = np.random.default_rng([zlib.crc32(name.encode()), seed]).standard_normal(out[name].shape)
        drawn = base * np.exp(spread * noise) if base else spread * noise
        out[name] = jnp.asarray(drawn.astype(out[name].dtype))
    for name, factor in factors.items():
        out[name] = (out[name] * factor).astype(out[name].dtype)
    return out
```

```python
P = 128
B, C, H, W = 8, 64, 32, 32
L = H * W
PAIRS = B // 2
LAYERS = 12
NST = 16
RANK = 32
HALF = 512
TOK = B * L
TILES = TOK // P
PER = L // P

W_PROJ, W_CF, W_CB = 0, 128, 256
W_DL = 384
W_B = W_DL + 2 * RANK
W_C = W_B + 96
W_DT = W_C + 96
W_D = W_DT + 128
V_G, V_LB, V_PB, V_CFB, V_CBB, V_DTB = range(W_D + 128, W_D + 134)
V_ALOG = W_D + 134
W_COLS = V_ALOG + NST

K_MEAN, K_ID, K_PAIR, K_ONE = 0, 128, 256, 384
K_SPLIT = 512
K_MASK = 520
K_SIGN = K_MASK + 64
K_COLS = K_SIGN + 9


class Steps:

    def __init__(self, names):
        self.names = names.split()
        assert len(set(self.names)) == len(self.names)

    def after(self, name, turn=0):
        return turn * len(self.names) + (self.names.index(name) + 2)

    def all(self, turn):
        return turn * len(self.names) + 1


def ssm_stage(nc, x_in, params, consts, selectors, x_sb, tables):
    import concourse.bass as bass
    from concourse import mybir
    from contextlib import ExitStack

    fp32, bf16 = mybir.dt.float32, mybir.dt.bfloat16
    ALU, ACT = mybir.AluOpType, mybir.ActivationFunctionType

    pe_s = Steps("mean var xp cf cb dl0 dt0 B0 C0 dl1 dt1 B1 C1")
    act_s = Steps("sq lnv rstd xps ez cf_v cf_abs cf_exp cf_ln cb_v cb_abs cb_exp cb_ln "
                  "dl_copy0 dt_v0 dt_abs0 dt_exp0 dt_ln0 B_hi0 B_mid0 C_hi0 C_mid0 "
                  "dl_copy1 dt_v1 dt_abs1 dt_exp1 dt_ln1 B_hi1 B_mid1 C_hi1 C_mid1")
    dve_s = Steps("xc xhat xn ez1 rz z xf xb "
                  "delta0 dx0 B_r0 B_split0 C_r0 C_split0 "
                  "delta1 dx1 B_r1 B_split1 C_r1 C_split1 gated xnew")
    UNROLL = 4

    with ExitStack() as ctx:
        def sb(name, shape, dt=fp32):
            return ctx.enter_context(nc.sbuf_tensor(name, shape, dt))

        def sem(name):
            return ctx.enter_context(nc.semaphore(name))

        par = sb("par", [P, W_COLS])
        con = sb("con", [P, K_COLS])
        sel = sb("sel", [96, NST, P], bf16)
        negA = sb("negA", [P, NST])
        xc, sq, rstd, xn, xp, z, t1, t2 = (sb(n, [P, L]) for n in
                                           ("xc", "sq", "rstd", "xn", "xp", "z", "t1", "t2"))
        u = [sb("u_fwd", [P, L]), sb("u_bwd", [P, L])]
        low = sb("low", [2 * RANK, L])
        delta = [sb("delta0", [P, L]), sb("delta1", [P, L])]
        dx = [sb("dx0", [P, L]), sb("dx1", [P, L])]
        bhi = sb("bhi", [96, L], bf16)
        br = sb("br", [96, L])
        B3 = [sb("B3_0", [96, L], bf16), sb("B3_1", [96, L], bf16)]
        C3 = [sb("C3_0", [96, L], bf16), sb("C3_1", [96, L], bf16)]
        dA = [sb("dA0", [P, L]), sb("dA1", [P, L])]
        dBu = [sb("dBu0", [P, L]), sb("dBu1", [P, L])]
        hst = [sb("h0", [P, L]), sb("h1", [P, L])]
        hC = [sb("hC0", [P, L]), sb("hC1", [P, L])]
        pp = ctx.enter_context(nc.psum_tensor("pp", [P, L], fp32))
        y_ps = ctx.enter_context(nc.psum_tensor("y_ps", [P, L], fp32))
        B_ps = ctx.enter_context(nc.psum_tensor("B_ps", [P, L], fp32))
        C_ps = ctx.enter_context(nc.psum_tensor("C_ps", [P, L], fp32))

        loaded, par_loaded = sem("loaded"), sem("par_loaded")
        pe_done, act_done, dve_done = sem("pe_done"), sem("act_done"), sem("dve_done")
        a_exp, sel_ready = sem("a_exp"), sem("sel_ready")
        b_ready, c_ready = sem("b_ready"), sem("c_ready")
        decay_ready, dbu_ready, scanned = sem("decay_ready"), sem("dbu_ready"), sem("scanned")
        prod_ready, y_added, y_ready = sem("prod_ready"), sem("y_added"), sem("y_ready")

        notes = EndsNotes(nc, ctx, tables["ends_i"], tables["place_i"], tables["ends"])
        halves = [slice(0, HALF), slice(HALF, L)]

        def vec(v):
            return par[:, v:v + 1]

        with nc.Block() as block:
            @block.sync
            def _(sp):
                sp.dma_start(x_sb[:, :, :], x_in).then_inc(loaded, 16)
                sp.dma_start(con[:, :], consts).then_inc(loaded, 16)
                for half, part in enumerate((t1, t2)):
                    sp.dma_start(part[0:96, :], selectors[:, half * L:(half + 1) * L]).then_inc(loaded, 16)
                sp.dma_start(par[:, :], params[0, :, :]).then_inc(par_loaded, 16)
                with sp.Fori(1, LAYERS) as layer:
                    sp.wait_ge(y_ready, layer * PAIRS)
                    sp.wait_ge(act_done, act_s.all(layer * PAIRS))
                    sp.wait_ge(dve_done, dve_s.all(layer * PAIRS))
                    sp.dma_start(par[:, :], params[bass.ds(layer, 1), :, :].rearrange("o p w -> (o p) w")
                                 ).then_inc(par_loaded, 16)

            @block.gpsimd
            def _(pool):
                notes.program(pool)

            @block.tensor
            def _(pe):
                def product(lhsT, rhs, out=pp):
                    for hs in halves:
                        last = nc.tensor.matmul(out[0:lhsT.shape[1], hs], lhsT, rhs(hs), start=True, stop=True)
                    return last

                pe.wait_ge(loaded, 64)
                pe.wait_ge(sel_ready, 2)
                with pe.Fori(0, LAYERS) as layer:
                    with pe.Fori(0, PAIRS) as pair:
                        pe.wait_ge(par_loaded, layer * 16 + 16)
                        it = layer * PAIRS + pair
                        pe.wait_ge(dve_done, dve_s.all(it))
                        product(con[:, K_MEAN:K_MEAN + P],
                                lambda hs: x_sb[:, bass.ds(pair, 1), hs].rearrange("p o t -> p (o t)")
                                ).then_inc(pe_done, 1)
                        pe.wait_ge(act_done, act_s.after("sq", it))
                        product(con[:, K_MEAN:K_MEAN + P], lambda hs: sq[:, hs]).then_inc(pe_done, 1)
                        pe.wait_ge(dve_done, dve_s.after("xn", it))
                        product(par[:, W_PROJ:W_PROJ + P], lambda hs: xn[:, hs]).then_inc(pe_done, 1)
                        pe.wait_ge(act_done, act_s.after("xps", it))
                        product(par[:, W_CF:W_CF + P], lambda hs: xp[:, hs]).then_inc(pe_done, 1)
                        pe.wait_ge(act_done, act_s.after("cf_v", it))
                        product(par[:, W_CB:W_CB + P], lambda hs: xp[:, hs]).then_inc(pe_done, 1)
                        pe.wait_ge(act_done, act_s.after("cb_v", it))
                        pe.wait_ge(dve_done, dve_s.after("xb", it))
                        for d in range(2):
                            if d:
                                pe.wait_ge(dve_done, dve_s.after("C_r0", it))
                            product(par[:, W_DL:W_DL + 2 * RANK], lambda hs: u[d][:, hs]).then_inc(pe_done, 1)
                            pe.wait_ge(act_done, act_s.after(f"dl_copy{d}", it))
                            product(par[0:2 * RANK, W_DT:W_DT + P], lambda hs: low[:, hs]).then_inc(pe_done, 1)
                            pe.wait_ge(act_done, act_s.after(f"dt_v{d}", it))
                            product(par[:, W_B:W_B + 96], lambda hs: u[d][:, hs]).then_inc(pe_done, 1)
                            pe.wait_ge(dve_done, dve_s.after(f"B_r{d}", it))
                            product(par[:, W_C:W_C + 96], lambda hs: u[d][:, hs]).then_inc(pe_done, 1)
                        for hs in halves:
                            nc.tensor.matmul(y_ps[:, hs], par[:, W_D:W_D + P], u[0][:, hs], start=True, stop=False)

                        def add_y(s, j):
                            for h, hs in enumerate(halves):
                                pe.wait_ge(prod_ready, s * 2 + 3 + h)
                                nc.tensor.matmul(y_ps[:, hs], con[:, K_ID:K_ID + P], hC[j % 2][:, hs],
                                                 start=False, stop=False).then_inc(y_added, 1)

                        for d in range(2):
                            with pe.Fori(0, NST // UNROLL) as m:
                                pe.wait_ge(dve_done, dve_s.after(f"C_split{d}", it))
                                for j in range(UNROLL):
                                    n = m * UNROLL + j
                                    s = it * (2 * NST) + d * NST + n
                                    for h, hs in enumerate(halves):
                                        pe.wait_ge(dbu_ready, s * 2 + 1 + h)
                                        nc.tensor.matmul(B_ps[:, hs],
                                                         sel[:, bass.ds(n, 1), :].rearrange("k o m -> k (o m)"),
                                                         B3[d][:, hs], start=True, stop=True).then_inc(b_ready, 1)
                                    for h, hs in enumerate(halves):
                                        pe.wait_ge(prod_ready, s * 2 + 1 + h)
                                        nc.tensor.matmul(C_ps[:, hs],
                                                         sel[:, bass.ds(n, 1), :].rearrange("k o m -> k (o m)"),
                                                         C3[d][:, hs], start=True, stop=True).then_inc(c_ready, 1)
                                    if j:
                                        add_y(s - 1, j - 1)
                                add_y(s, UNROLL - 1)
                        for hs in halves:
                            last = nc.tensor.matmul(y_ps[:, hs], par[:, W_D:W_D + P], u[1][:, hs],
                                                    start=False, stop=True)
                        last.then_inc(y_ready, 1)

            @block.scalar
            def _(act):
                nc.scalar.preload_act_table_set("natural_log_exp_and_others")
                act.wait_ge(loaded, 64)
                for half, part in enumerate((t1, t2)):
                    nc.scalar.activation(sel[:, half * (NST // 2):(half + 1) * (NST // 2), :],
                                         part[0:96, :].rearrange("k (n m) -> k n m", n=NST // 2), ACT.Copy).then_inc(sel_ready, 1)
                act.wait_ge(sel_ready, 2)
                nc.scalar.activation(negA[:, :], con[:, 0:NST], ACT.Copy).then_inc(act_done, 1)
                with act.Fori(0, LAYERS) as layer:
                    with act.Fori(0, PAIRS) as pair:
                        act.wait_ge(par_loaded, layer * 16 + 16)
                        it = layer * PAIRS + pair

                        def after_pe(name):
                            act.wait_ge(pe_done, pe_s.after(name, it) - 1)

                        def after_own(name):
                            act.wait_ge(act_done, act_s.after(name, it))

                        def after_dve(name):
                            act.wait_ge(dve_done, dve_s.after(name, it))

                        after_dve("xc")
                        nc.scalar.activation(sq[:, :], xc[:, :], ACT.Square).then_inc(act_done, 1)
                        after_pe("var")
                        nc.scalar.activation(rstd[:, :], pp[:, :], ACT.Ln,
                                             bias=con[:, K_SPLIT + 2:K_SPLIT + 3]).then_inc(act_done, 1)
                        after_own("lnv")
                        nc.scalar.activation(rstd[:, :], rstd[:, :], ACT.Exp, scale=-0.5).then_inc(act_done, 1)
                        after_pe("xp")
                        nc.scalar.activation(xp[:, :], pp[:, :], ACT.Identity, bias=vec(V_PB)).then_inc(act_done, 1)
                        after_own("xps")
                        nc.scalar.activation(z[:, :], xp[:, :], ACT.Exp, scale=-1.0).then_inc(act_done, 1)

                        def log_part(pe_step, prefix, bias):
                            after_pe(pe_step)
                            nc.scalar.activation(t2[:, :], pp[:, :], ACT.Identity, bias=vec(bias)).then_inc(act_done, 1)
                            after_own(prefix.format("v"))
                            nc.scalar.activation(t1[:, :], t2[:, :], ACT.Abs).then_inc(act_done, 1)
                            after_own(prefix.format("abs"))
                            nc.scalar.activation(t1[:, :], t1[:, :], ACT.Exp, scale=-1.0).then_inc(act_done, 1)
                            after_own(prefix.format("exp"))
                            nc.scalar.activation(t1[:, :], t1[:, :], ACT.Ln, bias=con[:, K_ONE:K_ONE + 1]).then_inc(act_done, 1)

                        log_part("cf", "cf_{}", V_CFB)
                        after_dve("xf")
                        log_part("cb", "cb_{}", V_CBB)
                        for d in range(2):
                            after_pe(f"dl{d}")
                            nc.scalar.activation(low[:, :], pp[0:2 * RANK, :], ACT.Copy).then_inc(act_done, 1)
                            after_dve(("xb", "delta0")[d])
                            log_part(f"dt{d}", "dt_{}" + str(d), V_DTB)
                            for name in ("B", "C"):
                                after_pe(f"{name}{d}")
                                if name == "C" or d:
                                    after_dve(f"B_split{d}" if name == "C" else "C_split0")
                                nc.scalar.activation(bhi[:, :], pp[0:96, :], ACT.Copy).then_inc(act_done, 1)
                                after_dve(f"{name}_r{d}")
                                nc.scalar.activation(bhi[:, :], br[:, :], ACT.Copy).then_inc(act_done, 1)
                        nc.scalar.activation(negA[:, :], par[:, V_ALOG:V_ALOG + NST], ACT.Exp).then_inc(a_exp, 1)
                        act.wait_ge(a_exp, it * 2 + 1)
                        nc.scalar.activation(negA[:, :], negA[:, :], ACT.Copy, scale=-1.0).then_inc(a_exp, 1)
                        act.wait_ge(a_exp, it * 2 + 2)
                        for d in range(2):
                            after_dve(f"delta{d}")
                            with act.Fori(0, NST // UNROLL) as m:
                                for j in range(UNROLL):
                                    n = m * UNROLL + j
                                    s = it * (2 * NST) + d * NST + n
                                    act.wait_ge(scanned, s + 1)
                                    nc.scalar.activation(dA[j % 2][:, :], delta[d][:, :], ACT.Exp,
                                                         scale=negA[:, bass.ds(n, 1)]).then_inc(decay_ready, 1)

            @block.vector
            def _(dve):
                V = nc.vector
                dve.wait_ge(loaded, 64)
                dve.wait_ge(sel_ready, 2)
                V.memset(t2[:, 0:1], 0.0).then_inc(dve_done, 1)
                V.memset(t2[:, 1:2], 0.0).then_inc(dbu_ready, 2)
                V.memset(t2[:, 2:3], 0.0).then_inc(prod_ready, 2)
                V.memset(t2[:, 3:4], 0.0).then_inc(scanned, 2)
                V.memset(t2[:, 4:5], 0.0).then_inc(y_added, 3)
                with dve.Fori(0, LAYERS) as layer:
                    with dve.Fori(0, PAIRS) as pair:
                        dve.wait_ge(par_loaded, layer * 16 + 16)
                        it = layer * PAIRS + pair
                        x_pair = x_sb[:, bass.ds(pair, 1), :].rearrange("p o t -> p (o t)")

                        def after_pe(name):
                            dve.wait_ge(pe_done, pe_s.after(name, it) - 1)

                        def after_act(name):
                            dve.wait_ge(act_done, act_s.after(name, it))

                        def after_own(name):
                            dve.wait_ge(dve_done, dve_s.after(name, it))

                        after_pe("mean")
                        V.tensor_tensor(xc[:, :], x_pair, pp[:, :], ALU.subtract).then_inc(dve_done, 1)
                        after_act("rstd")
                        V.tensor_tensor(xn[:, :], xc[:, :], rstd[:, :], ALU.mult).then_inc(dve_done, 1)
                        after_own("xhat")
                        V.tensor_scalar(xn[:, :], xn[:, :], vec(V_G), vec(V_LB), ALU.mult, ALU.add).then_inc(dve_done, 1)
                        after_act("ez")
                        V.tensor_scalar_add(z[:, :], z[:, :], 1.0).then_inc(dve_done, 1)
                        after_own("ez1")
                        V.reciprocal(z[:, :], z[:, :]).then_inc(dve_done, 1)
                        after_own("rz")
                        V.tensor_tensor(z[:, :], z[:, :], xp[:, :], ALU.mult).then_inc(dve_done, 1)

                        def softplus(out, act_ln):
                            after_act(act_ln)
                            V.scalar_tensor_tensor(out, t2[:, :], 0.0, t1[:, :], ALU.max, ALU.add).then_inc(dve_done, 1)

                        softplus(u[0][:, :], "cf_ln")
                        softplus(u[1][:, :], "cb_ln")
                        for d in range(2):
                            softplus(delta[d][:, :], f"dt_ln{d}")
                            after_own(f"delta{d}")
                            V.tensor_tensor(dx[d][:, :], delta[d][:, :], u[d][:, :], ALU.mult).then_inc(dve_done, 1)
                            for name, parts in (("B", B3), ("C", C3)):
                                after_act(f"{name}_hi{d}")
                                V.scalar_tensor_tensor(br[:, :], bhi[:, :], con[0:96, K_SPLIT:K_SPLIT + 1], pp[0:96, :],
                                                       ALU.mult, ALU.add).then_inc(dve_done, 1)
                                after_act(f"{name}_mid{d}")
                                V.scalar_tensor_tensor(parts[d][:, :], bhi[:, :], con[0:96, K_SPLIT + 1:K_SPLIT + 2], br[:, :],
                                                       ALU.mult, ALU.add).then_inc(dve_done, 1)

                        for d in range(2):
                            with dve.Fori(0, NST // UNROLL) as m:
                                def input_part(s, j):
                                    for h, hs in enumerate(halves):
                                        dve.wait_ge(b_ready, s * 2 + 1 + h)
                                        V.tensor_tensor(dBu[j % 2][:, hs], dx[d][:, hs], B_ps[:, hs],
                                                        ALU.mult).then_inc(dbu_ready, 1)

                                s0 = it * (2 * NST) + d * NST + m * UNROLL
                                dve.wait_ge(scanned, s0 + 1)
                                dve.wait_ge(dve_done, dve_s.after("C_split1", it))
                                input_part(s0, 0)
                                for j in range(UNROLL):
                                    s = s0 + j
                                    dve.wait_ge(dbu_ready, s * 2 + 4)
                                    dve.wait_ge(decay_ready, s + 1)
                                    step = 1 if d == 0 else -1
                                    V.tensor_tensor_scan(hst[j % 2][:, ::step], dA[j % 2][:, ::step], dBu[j % 2][:, ::step],
                                                         0.0, ALU.mult, ALU.add).then_inc(scanned, 1)
                                    if j + 1 < UNROLL:
                                        input_part(s + 1, j + 1)
                                    dve.wait_ge(scanned, s + 3)
                                    dve.wait_ge(y_added, s * 2 + 1)
                                    for h, hs in enumerate(halves):
                                        dve.wait_ge(c_ready, s * 2 + 1 + h)
                                        V.tensor_tensor(hC[j % 2][:, hs], hst[j % 2][:, hs], C_ps[:, hs],
                                                        ALU.mult).then_inc(prod_ready, 1)
                        dve.wait_ge(y_ready, it + 1)
                        V.tensor_tensor(t2[:, :], z[:, :], y_ps[:, :], ALU.mult).then_inc(dve_done, 1)
                        after_own("gated")
                        V.tensor_tensor(x_pair, x_pair, t2[:, :], ALU.add).then_inc(dve_done, 1)
Q_COLS = 64
CW_Q, CW_K, CW_V = 0, 9 * Q_COLS, 18 * Q_COLS
CW_FC1 = CW_V + 9 * P
CW_FC2 = CW_FC1 + 8
CW_FL = CW_FC2 + P
CW_FG = CW_FL + C
CV_BQ, CV_BK, CV_B1, CV_B2, CV_BV = range(CW_FG + C, CW_FG + C + 5)
CR_FB = CV_BV + 1
CW_COLS = CR_FB + C


def conv_stage(nc, weights, consts, x_sb, t_sb):
    import concourse.bass as bass
    from concourse import mybir
    from contextlib import ExitStack

    fp32 = mybir.dt.float32
    ALU, ACT, AX = mybir.AluOpType, mybir.ActivationFunctionType, mybir.AxisListType.X
    IMAGES = range(2)
    BLK = range(PER)
    SCALE = (C // 4) ** -0.5
    PW = W + 2
    ROWS = HALF // W

    pe_s = Steps("gm gv fc1 fc2 q k v vt " + " ".join(
        " ".join(f"S{b}_{i}" for i in BLK) + f" mrep{b} " + " ".join(f"T{b}_{i}" for i in BLK)
        + f" loc{b} den{b} res{b} out{b}" for b in IMAGES))
    act_s = Steps("sq lnv rstd relu esig qs ks vb " + " ".join(
        f"mrepc{b} " + " ".join(f"E{b}_{i}" for i in BLK) + f" locc{b}" for b in IMAGES))
    dve_s = Steps("s1 gmean xc s2 v2 xhat ysum h1 h2 y xg vs " + " ".join(
        " ".join(f"max{b}_{i}" for i in BLK) + f" diag{b} " + " ".join(f"sub{b}_{i}" for i in BLK)
        + f" rden{b} scaled{b} summed{b} t{b}" for b in IMAGES))

    with ExitStack() as ctx:
        def sb(name, shape, dt=fp32):
            return ctx.enter_context(nc.sbuf_tensor(name, shape, dt))

        def ps(name, cols):
            return ctx.enter_context(nc.psum_tensor(name, [P, cols], fp32))

        def sem(name):
            return ctx.enter_context(nc.semaphore(name))

        cw = sb("cw", [P, CW_COLS])
        con = sb("con_c", [P, K_COLS])
        xc, sq, xg = (sb(n, [P, L]) for n in ("cxc", "csq", "cxg"))
        xw = sb("xw", [P, L])
        xpad = sb("xpad", [P, PW, PW])
        st = sb("st", [P, 16])
        S1, GM, S2, GV, YS, HID, Y = (st[:, i:i + 1] for i in range(7))
        q_sb, k_sb = sb("q_sb", [Q_COLS, L]), sb("k_sb", [Q_COLS, L])
        v_sb = sb("v_sb", [P, L])
        vT = sb("vT", [P, PER, P])
        mrow = sb("mrow", [P, 2, PER])
        diag = sb("diag", [P, PER, P])
        mrep = sb("mrep", [P, L])
        E = [sb("E0", [P, PER, L]), sb("E1", [P, PER, L])]
        loc = sb("loc", [C, L])
        rden = sb("rden", [P, 2, PER])
        tmp = sb("tmp", [P, PER, C])
        psA, psB, psM = ps("psA", L), ps("psB", L), ps("psM", L)
        psO, psT = ps("psO", HALF), ps("psT", HALF)
        psS = [psA, psB]

        loaded, zeroed = sem("c_loaded"), sem("c_zeroed")
        xw_ready = sem("xw_ready")
        pe_done, act_done, dve_done = sem("c_pe"), sem("c_act"), sem("c_dve")
        halves = [slice(0, HALF), slice(HALF, L)]
        inner = xpad[:, 1:H + 1, 1:W + 1]
        EPS = con[:, K_SPLIT + 2:K_SPLIT + 3]

        def window(tap, row, rows):
            dy, dx = divmod(tap, 3)
            return xpad[:, row + dy:row + dy + rows, dx:dx + W]

        with nc.Block() as block:
            @block.sync
            def _(sp):
                sp.dma_start(cw[:, :], weights).then_inc(loaded, 16)
                sp.dma_start(con[:, :], consts).then_inc(loaded, 16)

            @block.gpsimd
            def _(pool):
                nc.gpsimd.memset(xpad[:, :, :], 0.0).then_inc(zeroed, 1)

            @block.tensor
            def _(pe):
                M = nc.tensor.matmul
                pe.wait_ge(loaded, 32)
                with pe.Fori(0, PAIRS) as pair:
                    def act(name):
                        pe.wait_ge(act_done, act_s.after(name, pair))

                    def dve(name):
                        pe.wait_ge(dve_done, dve_s.after(name, pair))

                    dve("s1")
                    M(psT[:, 0:1], con[:, K_PAIR:K_PAIR + P], S1, start=True, stop=True).then_inc(pe_done, 1)
                    dve("s2")
                    M(psT[:, 1:2], con[:, K_PAIR:K_PAIR + P], S2, start=True, stop=True).then_inc(pe_done, 1)
                    dve("ysum")
                    M(psT[0:8, 2:3], cw[:, CW_FC1:CW_FC1 + 8], YS, start=True, stop=True).then_inc(pe_done, 1)
                    act("relu")
                    M(psT[:, 3:4], cw[0:8, CW_FC2:CW_FC2 + P], HID[0:8, :], start=True, stop=True).then_inc(pe_done, 1)
                    for cols, width, before in ((CW_Q, Q_COLS, None), (CW_K, Q_COLS, "qs"), (CW_V, P, "ks")):
                        if before:
                            act(before)
                        for h, hs in enumerate(halves):
                            for tap in range(9):
                                last = M(psM[0:width, hs], cw[:, cols + tap * width:cols + (tap + 1) * width],
                                         window(tap, h * ROWS, ROWS), start=tap == 0, stop=tap == 8)
                        last.then_inc(pe_done, 1)
                    act("vb")
                    for i in BLK:
                        last = M(psM[:, i * P:(i + 1) * P], v_sb[:, i * P:(i + 1) * P], con[:, K_ID:K_ID + P],
                                 start=True, stop=True)
                    last.then_inc(pe_done, 1)
                    for b in IMAGES:
                        qb, kb = q_sb[32 * b:32 * b + 32, :], k_sb[32 * b:32 * b + 32, :]
                        for i in BLK:
                            if i >= 2:
                                dve(f"max{b}_{i - 2}")
                            elif b:
                                dve(f"sub0_{PER - 2 + i}")
                            for hs in halves:
                                last = M(psS[i % 2][:, hs], qb[:, i * P:(i + 1) * P], kb[:, hs], start=True, stop=True)
                            last.then_inc(pe_done, 1)
                        dve(f"diag{b}")
                        if b:
                            act("locc0")
                        else:
                            dve("vs")
                        for i in BLK:
                            last = M(psM[:, i * P:(i + 1) * P], con[:, K_ONE:K_ONE + P], diag[:, i, :], start=True, stop=True)
                        last.then_inc(pe_done, 1)
                        for i in BLK:
                            dve(f"sub{b}_{i - 2}" if i >= 2 else f"max{b}_{PER - 2 + i}")
                            for hs in halves:
                                last = M(psS[i % 2][:, hs], kb[:, i * P:(i + 1) * P], qb[:, hs], start=True, stop=True)
                            last.then_inc(pe_done, 1)
                        act(f"E{b}_{PER - 1}")
                        for hs in halves:
                            for i in BLK:
                                last = M(psM[0:C, hs], vT[:, i, b * C:(b + 1) * C], E[b][:, i, hs],
                                         start=i == 0, stop=i == PER - 1)
                        last.then_inc(pe_done, 1)
                        if b:
                            dve("summed0")
                        for i in BLK:
                            for j in BLK:
                                last = M(psT[:, 8 + i:9 + i], E[b][:, j, i * P:(i + 1) * P], con[:, K_ONE:K_ONE + 1],
                                         start=j == 0, stop=j == PER - 1)
                        last.then_inc(pe_done, 1)
                        dve(f"rden{b}")
                        rows = slice(b * C, (b + 1) * C)
                        for i in BLK:
                            M(psT[:, i * C:(i + 1) * C], xw[rows, i * P:(i + 1) * P], con[rows, K_ID + b * C:K_ID + (b + 1) * C],
                              start=True, stop=False)
                            last = M(psT[:, i * C:(i + 1) * C], xg[rows, i * P:(i + 1) * P], cw[rows, CW_FG:CW_FG + C],
                                     start=False, stop=True)
                        last.then_inc(pe_done, 1)
                        act(f"locc{b}")
                        for i in BLK:
                            last = M(psO[:, i * C:(i + 1) * C], loc[:, i * P:(i + 1) * P], cw[0:C, CW_FL:CW_FL + C],
                                     start=True, stop=True)
                        last.then_inc(pe_done, 1)

            @block.scalar
            def _(act):
                A = nc.scalar.activation
                nc.scalar.preload_act_table_set("natural_log_exp_and_others")
                act.wait_ge(loaded, 32)
                A(st[:, 8:9], con[:, 0:1], ACT.Copy).then_inc(act_done, 1)
                with act.Fori(0, PAIRS) as pair:
                    def pe(name):
                        act.wait_ge(pe_done, pe_s.after(name, pair) - 1)

                    def dve(name):
                        act.wait_ge(dve_done, dve_s.after(name, pair))

                    def own(name):
                        act.wait_ge(act_done, act_s.after(name, pair))

                    dve("xc")
                    A(sq[:, :], xc[:, :], ACT.Square).then_inc(act_done, 1)
                    dve("v2")
                    A(GV, GV, ACT.Ln, bias=EPS).then_inc(act_done, 1)
                    own("lnv")
                    A(GV, GV, ACT.Exp, scale=-0.5).then_inc(act_done, 1)
                    pe("fc1")
                    A(HID[0:8, :], psT[0:8, 2:3], ACT.Relu, bias=cw[0:8, CV_B1:CV_B1 + 1],
                      scale=1.0 / L).then_inc(act_done, 1)
                    dve("h1")
                    A(Y, Y, ACT.Exp, scale=-1.0).then_inc(act_done, 1)
                    pe("q")
                    A(q_sb[:, :], psM[0:Q_COLS, :], ACT.Identity, bias=cw[0:Q_COLS, CV_BQ:CV_BQ + 1]).then_inc(act_done, 1)
                    pe("k")
                    A(k_sb[:, :], psM[0:Q_COLS, :], ACT.Identity, bias=cw[0:Q_COLS, CV_BK:CV_BK + 1]).then_inc(act_done, 1)
                    pe("v")
                    A(v_sb[:, :], psM[:, :], ACT.Identity, bias=cw[:, CV_BV:CV_BV + 1]).then_inc(act_done, 1)
                    for b in IMAGES:
                        pe(f"mrep{b}")
                        if b:
                            dve(f"sub0_{PER - 1}")
                        A(mrep[:, :], psM[:, :], ACT.Copy).then_inc(act_done, 1)
                        for i in BLK:
                            dve(f"sub{b}_{i}")
                            A(E[b][:, i, :], E[b][:, i, :], ACT.Exp, scale=SCALE).then_inc(act_done, 1)
                        pe(f"loc{b}")
                        if b:
                            pe("out0")
                        A(loc[:, :], psM[0:C, :], ACT.Copy).then_inc(act_done, 1)

            @block.vector
            def _(dve):
                V = nc.vector
                dve.wait_ge(loaded, 32)
                dve.wait_ge(zeroed, 1)
                V.memset(st[:, 9:10], 0.0).then_inc(dve_done, 1)
                with dve.Fori(0, PAIRS) as pair:
                    def pe(name):
                        dve.wait_ge(pe_done, pe_s.after(name, pair) - 1)

                    def act(name):
                        dve.wait_ge(act_done, act_s.after(name, pair))

                    def own(name):
                        dve.wait_ge(dve_done, dve_s.after(name, pair))

                    def done(ins):
                        ins.then_inc(dve_done, 1)

                    x_pair = x_sb[:, bass.ds(pair, 1), :].rearrange("p o t -> p (o t)")
                    dve.wait_ge(dve_done, dve_s.all(pair))
                    V.tensor_copy(xw[:, :], x_pair).then_inc(xw_ready, 1)
                    dve.wait_ge(xw_ready, pair + 1)
                    V.reduce_sum(S1, xw[:, :], AX).then_inc(dve_done, 1)
                    pe("gm")
                    V.tensor_scalar(GM, psT[:, 0:1], 1.0 / L, None, ALU.mult).then_inc(dve_done, 1)
                    own("gmean")
                    V.tensor_scalar(xc[:, :], xw[:, :], GM, None, ALU.subtract).then_inc(dve_done, 1)
                    act("sq")
                    V.reduce_sum(S2, sq[:, :], AX).then_inc(dve_done, 1)
                    pe("gv")
                    V.tensor_scalar(GV, psT[:, 1:2], 1.0 / L, None, ALU.mult).then_inc(dve_done, 1)
                    act("rstd")
                    V.tensor_scalar(inner, xc[:, :].rearrange("p (h w) -> p h w", h=H), GV, None,
                                    ALU.mult).then_inc(dve_done, 1)
                    own("xhat")
                    V.tensor_reduce(YS, inner, mybir.AxisListType.XY, ALU.add).then_inc(dve_done, 1)
                    pe("fc2")
                    V.tensor_scalar(Y, psT[:, 3:4], cw[:, CV_B2:CV_B2 + 1], None, ALU.add).then_inc(dve_done, 1)
                    act("esig")
                    V.tensor_scalar_add(Y, Y, 1.0).then_inc(dve_done, 1)
                    own("h2")
                    V.reciprocal(Y, Y).then_inc(dve_done, 1)
                    own("y")
                    V.tensor_scalar(xg[:, :].rearrange("p (h w) -> p h w", h=H), inner, Y, None,
                                    ALU.mult).then_inc(dve_done, 1)
                    pe("vt")
                    V.tensor_copy(vT[:, :, :], psM[:, :].rearrange("p (i c) -> p i c", i=PER)).then_inc(dve_done, 1)
                    for b in IMAGES:
                        for i in BLK:
                            pe(f"S{b}_{i}")
                            V.reduce_max(mrow[:, b, i:i + 1], psS[i % 2][:, :], AX).then_inc(dve_done, 1)
                        own(f"max{b}_{PER - 1}")
                        V.tensor_tensor(diag[:, :, :], con[:, K_ID:K_ID + P].unsqueeze(1).broadcast_to([P, PER, P]),
                                        mrow[:, b, :].unsqueeze(2).broadcast_to([P, PER, P]),
                                        ALU.mult).then_inc(dve_done, 1)
                        act(f"mrepc{b}")
                        for i in BLK:
                            pe(f"T{b}_{i}")
                            V.tensor_tensor(E[b][:, i, :], psS[i % 2][:, :], mrep[:, :], ALU.subtract).then_inc(dve_done, 1)
                        pe(f"den{b}")
                        V.reciprocal(rden[:, b, :], psT[:, 8:8 + PER]).then_inc(dve_done, 1)
                        pe(f"out{b}")
                        own(f"rden{b}")
                        V.tensor_tensor(tmp[:, :, :], psO[:, :].rearrange("p (i c) -> p i c", i=PER),
                                        rden[:, b, :].unsqueeze(2).broadcast_to([P, PER, C]), ALU.mult).then_inc(dve_done, 1)
                        own(f"scaled{b}")
                        V.tensor_tensor(tmp[:, :, :], tmp[:, :, :], psT[:, :].rearrange("p (i c) -> p i c", i=PER),
                                        ALU.add).then_inc(dve_done, 1)
                        own(f"summed{b}")
                        V.tensor_tensor(t_sb[:, bass.ds(pair * 2 * PER + b * PER, PER), :], tmp[:, :, :],
                                        cw[:, CR_FB:CR_FB + C].unsqueeze(1).broadcast_to([P, PER, C]),
                                        ALU.add).then_inc(dve_done, 1)
def norm_stage(nc, consts, t_sb, tn_sb, tag):
    from concourse import mybir
    from contextlib import ExitStack

    fp32 = mybir.dt.float32
    ALU, ACT, AX = mybir.AluOpType, mybir.ActivationFunctionType, mybir.AxisListType.X
    act_s = Steps("sq lnv rstd")
    dve_s = Steps("sum mean centred sum2 normed")
    with ExitStack() as ctx:
        sq = ctx.enter_context(nc.sbuf_tensor(tag + "_sq", [P, TILES, C], fp32))
        mean = ctx.enter_context(nc.sbuf_tensor(tag + "_mean", [P, TILES], fp32))
        rstd = ctx.enter_context(nc.sbuf_tensor(tag + "_rstd", [P, TILES], fp32))
        eps = ctx.enter_context(nc.sbuf_tensor(tag + "_eps", [P, 1], fp32))
        act_done, dve_done, eps_set = (ctx.enter_context(nc.semaphore(tag + n)) for n in ("_act", "_dve", "_eps_set"))

        with nc.Block() as block:
            @block.gpsimd
            def _(pool):
                nc.gpsimd.memset(eps[:, :], 1e-5).then_inc(eps_set, 1)

            @block.scalar
            def _(act):
                nc.scalar.preload_act_table_set("natural_log_exp_and_others")
                act.wait_ge(dve_done, dve_s.after("centred") - 1)
                nc.scalar.activation(sq[:, :, :], tn_sb[:, :, :], ACT.Square).then_inc(act_done, 1)
                act.wait_ge(dve_done, dve_s.after("sum2") - 1)
                act.wait_ge(eps_set, 1)
                nc.scalar.activation(rstd[:, :], rstd[:, :], ACT.Ln, bias=eps[:, :], scale=1.0 / C).then_inc(act_done, 1)
                act.wait_ge(act_done, act_s.after("lnv") - 1)
                nc.scalar.activation(rstd[:, :], rstd[:, :], ACT.Exp, scale=-0.5).then_inc(act_done, 1)

            @block.vector
            def _(dve):
                V = nc.vector
                V.reduce_sum(mean[:, :], t_sb[:, :, :], AX).then_inc(dve_done, 1)
                dve.wait_ge(dve_done, dve_s.after("sum") - 1)
                V.tensor_scalar(mean[:, :], mean[:, :], 1.0 / C, None, ALU.mult).then_inc(dve_done, 1)
                dve.wait_ge(dve_done, dve_s.after("mean") - 1)
                V.tensor_tensor(tn_sb[:, :, :], t_sb[:, :, :], mean[:, :].unsqueeze(2).broadcast_to([P, TILES, C]),
                                ALU.subtract).then_inc(dve_done, 1)
                dve.wait_ge(act_done, act_s.after("sq") - 1)
                V.reduce_sum(rstd[:, :], sq[:, :, :], AX).then_inc(dve_done, 1)
                dve.wait_ge(act_done, act_s.after("rstd") - 1)
                V.tensor_tensor(tn_sb[:, :, :], tn_sb[:, :, :], rstd[:, :].unsqueeze(2).broadcast_to([P, TILES, C]),
                                ALU.mult).then_inc(dve_done, 1)


HEADS2, HDIM2 = 4, 16


def graph_attn_stage(nc, w_padded, w_plain, consts, tn_sb, t_sb):
    import concourse.bass as bass
    from concourse import mybir
    from contextlib import ExitStack

    fp32 = mybir.dt.float32
    ALU, ACT, AX = mybir.AluOpType, mybir.ActivationFunctionType, mybir.AxisListType.X
    BLK, HEADS = range(PER), range(HEADS2)
    SCALE, SLOPE = HDIM2 ** -0.5, 0.2
    D1 = HDIM2 + 1

    def order(per_head, at):
        return " ".join(at(h) for h in HEADS)

    def scores(h, *kinds):
        return " ".join(f"{k}{h}_{i}" for i in BLK for k in kinds)

    pe_s = Steps("turn WhT Wh " + scores(0, "S") + " " + " ".join(
        f"mrep{h} " + (scores(h + 1, "S") if h + 1 < HEADS2 else "") + f" out{h}" for h in HEADS))
    act_s = Steps("copy tnT WhTc " + " ".join(scores(h, "relu") + " " + scores(h, "E") for h in HEADS))
    dve_s = Steps("V " + scores(0, "leaky", "max") + " " + " ".join(
        f"diag{h} " + scores(h, "sub") + " " + (scores(h + 1, "leaky", "max") if h + 1 < HEADS2 else "")
        + f" rden{h} scaled{h} t{h}" for h in HEADS))

    with ExitStack() as ctx:
        def sb(name, shape, dt=fp32):
            return ctx.enter_context(nc.sbuf_tensor(name, shape, dt))

        def ps(name, cols):
            return ctx.enter_context(nc.psum_tensor(name, [P, cols], fp32))

        def sem(name):
            return ctx.enter_context(nc.semaphore(name))

        wp, wq = sb("g_wp", [C, P]), sb("g_w", [C, C])
        con = sb("g_con", [P, K_COLS])
        tw = sb("g_tw", [P, PER, C])
        tnT, whT = sb("g_tnT", [C, L]), sb("g_whT", [P, L])
        val = sb("g_val", [P, PER, HEADS2, D1])
        S = [sb("g_S0", [P, PER, L]), sb("g_S1", [P, PER, L])]
        mrow = sb("g_mrow", [P, HEADS2, PER])
        diag = sb("g_diag", [P, PER, P])
        rden = sb("g_rden", [P, HEADS2, PER])
        tmp = sb("g_tmp", [P, PER, HDIM2])
        psS = [ps("g_psA", L), ps("g_psB", L)]
        psM, psV, psO = ps("g_psM", L), ps("g_psV", HALF), ps("g_psO", HALF)
        loaded, ones_set = sem("g_loaded"), sem("g_ones")
        pe_done, act_done, dve_done = sem("g_pe"), sem("g_act"), sem("g_dve")
        halves = [slice(0, HALF), slice(HALF, L)]

        with nc.Block() as block:
            @block.sync
            def _(sp):
                sp.dma_start(wp[:, :], w_padded).then_inc(loaded, 16)
                sp.dma_start(wq[:, :], w_plain).then_inc(loaded, 16)
                sp.dma_start(con[:, :], consts).then_inc(loaded, 16)

            @block.gpsimd
            def _(pool):
                nc.gpsimd.memset(val[:, :, :, :], 1.0).then_inc(ones_set, 1)

            @block.tensor
            def _(pe):
                M = nc.tensor.matmul
                pe.wait_ge(loaded, 48)
                with pe.Fori(0, B) as img:
                    def act(name):
                        pe.wait_ge(act_done, act_s.after(name, img))

                    def dve(name):
                        pe.wait_ge(dve_done, dve_s.after(name, img))

                    act("copy")
                    for i in BLK:
                        last = M(psM[0:C, i * P:(i + 1) * P], tw[:, i, :], con[:, K_ID:K_ID + P], start=True, stop=True)
                    last.then_inc(pe_done, 1)
                    act("tnT")
                    for hs in halves:
                        last = M(psM[:, hs], wp[:, :], tnT[:, hs], start=True, stop=True)
                    last.then_inc(pe_done, 1)
                    for i in BLK:
                        last = M(psV[:, i * C:(i + 1) * C], tnT[:, i * P:(i + 1) * P], wq[:, :], start=True, stop=True)
                    last.then_inc(pe_done, 1)
                    act("WhTc")

                    def score_tiles(h):
                        rows = slice(32 * h, 32 * h + 32)
                        for i in BLK:
                            if i >= 2:
                                dve(f"leaky{h}_{i - 2}")
                            elif h:
                                dve(f"leaky{h - 1}_{PER - 2 + i}")
                            for hs in halves:
                                last = M(psS[i % 2][:, hs], whT[rows, i * P:(i + 1) * P], whT[rows, hs], start=True, stop=True)
                            last.then_inc(pe_done, 1)

                    score_tiles(0)
                    for h in HEADS:
                        dve(f"diag{h}")
                        if h:
                            dve(f"sub{h - 1}_{PER - 1}")
                        for i in BLK:
                            last = M(psM[:, i * P:(i + 1) * P], con[:, K_ONE:K_ONE + P], diag[:, i, :], start=True, stop=True)
                        last.then_inc(pe_done, 1)
                        if h + 1 < HEADS2:
                            score_tiles(h + 1)
                        act(f"E{h}_{PER - 1}")
                        if h:
                            dve(f"scaled{h - 1}")
                        for i in BLK:
                            for j in BLK:
                                last = M(psO[:, i * D1:(i + 1) * D1], S[h % 2][:, j, i * P:(i + 1) * P], val[:, j, h, :],
                                         start=j == 0, stop=j == PER - 1)
                        last.then_inc(pe_done, 1)

            @block.scalar
            def _(act):
                A = nc.scalar.activation
                nc.scalar.preload_act_table_set("natural_log_exp_and_others")
                act.wait_ge(loaded, 48)
                A(mrow[:, 0, 0:1], con[:, 0:1], ACT.Copy).then_inc(act_done, 1)
                with act.Fori(0, B) as img:
                    def pe(name):
                        act.wait_ge(pe_done, pe_s.after(name, img) - 1)

                    def dve(name):
                        act.wait_ge(dve_done, dve_s.after(name, img))

                    act.wait_ge(dve_done, dve_s.all(img))
                    A(tw[:, :, :], tn_sb[:, bass.ds(img * PER, PER), :], ACT.Copy).then_inc(act_done, 1)
                    pe("turn")
                    A(tnT[:, :], psM[0:C, :], ACT.Copy).then_inc(act_done, 1)
                    pe("WhT")
                    A(whT[:, :], psM[:, :], ACT.Copy).then_inc(act_done, 1)
                    for h in HEADS:
                        for i in BLK:
                            pe(f"S{h}_{i}")
                            if h >= 2 and i == 0:
                                pe(f"out{h - 2}")
                            A(S[h % 2][:, i, :], psS[i % 2][:, :], ACT.Relu, scale=SCALE * (1 - SLOPE)).then_inc(act_done, 1)
                        for i in BLK:
                            dve(f"sub{h}_{i}")
                            A(S[h % 2][:, i, :], S[h % 2][:, i, :], ACT.Exp).then_inc(act_done, 1)

            @block.vector
            def _(dve):
                V = nc.vector
                dve.wait_ge(loaded, 48)
                dve.wait_ge(ones_set, 1)
                V.memset(tmp[:, 0, 0:1], 0.0).then_inc(dve_done, 1)
                with dve.Fori(0, B) as img:
                    def pe(name):
                        dve.wait_ge(pe_done, pe_s.after(name, img) - 1)

                    def act(name):
                        dve.wait_ge(act_done, act_s.after(name, img))

                    def own(name):
                        dve.wait_ge(dve_done, dve_s.after(name, img))

                    pe("Wh")
                    V.tensor_copy(val[:, :, :, 0:HDIM2],
                                  psV[:, :].rearrange("p (i h d) -> p i h d", i=PER, h=HEADS2)).then_inc(dve_done, 1)

                    def leaky_tiles(h):
                        for i in BLK:
                            act(f"relu{h}_{i}")
                            V.scalar_tensor_tensor(S[h % 2][:, i, :], psS[i % 2][:, :], SCALE * SLOPE, S[h % 2][:, i, :],
                                                   ALU.mult, ALU.add).then_inc(dve_done, 1)
                            own(f"leaky{h}_{i}")
                            V.reduce_max(mrow[:, h, i:i + 1], S[h % 2][:, i, :], AX).then_inc(dve_done, 1)

                    leaky_tiles(0)
                    for h in HEADS:
                        own(f"max{h}_{PER - 1}")
                        V.tensor_tensor(diag[:, :, :], con[:, K_ID:K_ID + P].unsqueeze(1).broadcast_to([P, PER, P]),
                                        mrow[:, h, :].unsqueeze(2).broadcast_to([P, PER, P]), ALU.mult).then_inc(dve_done, 1)
                        pe(f"mrep{h}")
                        for i in BLK:
                            V.tensor_tensor(S[h % 2][:, i, :], S[h % 2][:, i, :], psM[:, :], ALU.subtract).then_inc(dve_done, 1)
                        if h + 1 < HEADS2:
                            leaky_tiles(h + 1)
                        pe(f"out{h}")
                        out = psO[:, 0:PER * D1].rearrange("p (i d) -> p i d", i=PER)
                        V.reciprocal(rden[:, h, :], out[:, :, HDIM2]).then_inc(dve_done, 1)
                        own(f"rden{h}")
                        V.tensor_tensor(tmp[:, :, :], out[:, :, 0:HDIM2], rden[:, h, :].unsqueeze(2).broadcast_to([P, PER, HDIM2]),
                                        ALU.mult).then_inc(dve_done, 1)
                        own(f"scaled{h}")
                        t_head = t_sb[:, bass.ds(img * PER, PER), h * HDIM2:(h + 1) * HDIM2]
                        V.tensor_tensor(t_head, t_head, tmp[:, :, :], ALU.add).then_inc(dve_done, 1)
GROUP = 4
EXPERTS = 16


def project_stage(nc, weight, bias_rows, consts, tn_sb, tnT_sb, out_sb, tag):
    import concourse.bass as bass
    from concourse import mybir
    from contextlib import ExitStack

    fp32 = mybir.dt.float32
    ALU, ACT = mybir.AluOpType, mybir.ActivationFunctionType
    E = out_sb.shape[2]
    with ExitStack() as ctx:
        w = ctx.enter_context(nc.sbuf_tensor(tag + "_w", [C, E], fp32))
        brow = ctx.enter_context(nc.sbuf_tensor(tag + "_b", [P, E], fp32))
        con = ctx.enter_context(nc.sbuf_tensor(tag + "_con", [P, K_COLS], fp32))
        tw = [ctx.enter_context(nc.sbuf_tensor(f"{tag}_tw{k}", [P, GROUP, C], fp32)) for k in range(2)]
        wT = [ctx.enter_context(nc.sbuf_tensor(f"{tag}_wT{k}", [C, HALF], fp32)) for k in range(2)]
        psT = [ctx.enter_context(nc.psum_tensor(f"{tag}_psT{k}", [P, HALF], fp32)) for k in range(2)]
        psL = [ctx.enter_context(nc.psum_tensor(f"{tag}_psL{k}", [P, HALF], fp32)) for k in range(2)]
        loaded, copied, turned, kept, kept_all, projected, stored = (
            ctx.enter_context(nc.semaphore(tag + n)) for n in
            ("_loaded", "_copied", "_turned", "_kept", "_kept_all", "_projected", "_stored"))
        TURNS = TILES // GROUP

        with nc.Block() as block:
            @block.sync
            def _(sp):
                sp.dma_start(w[:, :], weight).then_inc(loaded, 16)
                sp.dma_start(brow[:, :], bias_rows).then_inc(loaded, 16)
                sp.dma_start(con[:, :], consts).then_inc(loaded, 16)

            @block.tensor
            def _(pe):
                pe.wait_ge(loaded, 48)
                with pe.Fori(0, TURNS // 2) as pair:
                    for k in range(2):
                        turn = pair * 2 + k
                        pe.wait_ge(copied, turn + 1)
                        for g in range(GROUP):
                            last = nc.tensor.matmul(psT[k][0:C, g * P:(g + 1) * P], tw[k][:, g, :], con[:, K_ID:K_ID + P],
                                                    start=True, stop=True)
                        last.then_inc(turned, 1)
                        pe.wait_ge(kept, turn + 1)
                        for g in range(GROUP):
                            last = nc.tensor.matmul(psL[k][:, g * E:(g + 1) * E], wT[k][:, g * P:(g + 1) * P], w[:, :],
                                                    start=True, stop=True)
                        last.then_inc(projected, 1)

            @block.scalar
            def _(act):
                act.wait_ge(loaded, 48)
                with act.Fori(0, TURNS // 2) as pair:
                    for k in range(2):
                        turn = pair * 2 + k
                        act.wait_ge(turned, turn + 1)
                        nc.scalar.activation(wT[k][:, :], psT[k][0:C, :], ACT.Copy).then_inc(kept, 1)
                        act.wait_ge(kept, turn + 1)
                        nc.scalar.activation(tnT_sb[:, bass.ds(turn * HALF, HALF)], wT[k][:, :], ACT.Copy).then_inc(kept_all, 1)

            @block.vector
            def _(dve):
                V = nc.vector
                dve.wait_ge(loaded, 48)
                V.memset(tw[0][:, 0, 0:1], 0.0).then_inc(stored, 2)
                with dve.Fori(0, TURNS // 2) as pair:
                    for k in range(2):
                        turn = pair * 2 + k
                        dve.wait_ge(stored, turn + 1)
                        V.tensor_copy(tw[k][:, :, :], tn_sb[:, bass.ds(turn * GROUP, GROUP), :]).then_inc(copied, 1)
                    for k in range(2):
                        turn = pair * 2 + k
                        dve.wait_ge(projected, turn + 1)
                        dve.wait_ge(kept_all, turn + 1)
                        V.tensor_tensor(out_sb[:, bass.ds(turn * GROUP, GROUP), :],
                                        psL[k][:, 0:GROUP * E].rearrange("p (g e) -> p g e", g=GROUP),
                                        brow[:, :].unsqueeze(1).broadcast_to([P, GROUP, E]), ALU.add).then_inc(stored, 1)


def top2_stage(nc, logits, tag):
    from concourse import mybir
    from contextlib import ExitStack

    fp32 = mybir.dt.float32
    ALU, ACT, AX = mybir.AluOpType, mybir.ActivationFunctionType, mybir.AxisListType.X
    E = logits.shape[2]
    FAR = 1e30
    with ExitStack() as ctx:
        rank, hit, first = (ctx.enter_context(nc.sbuf_tensor(tag + n, [P, TILES, E], fp32)) for n in ("_rank", "_hit", "_first"))
        top, pos, g1, g2 = (ctx.enter_context(nc.sbuf_tensor(tag + n, [P, 2, TILES], fp32)) for n in ("_top", "_pos", "_g1", "_g2"))
        ranked, exp_done, link = (ctx.enter_context(nc.semaphore(tag + n)) for n in ("_ranked", "_exp_done", "_link"))

        def wide(a):
            return a.unsqueeze(2).broadcast_to([P, TILES, E])

        with nc.Block() as block:
            @block.gpsimd
            def _(pool):
                for e in range(E):
                    nc.gpsimd.memset(rank[:, :, e:e + 1], float(E - e)).then_inc(ranked, 1)

            @block.scalar
            def _(act):
                act.wait_ge(link, 8)
                nc.scalar.activation(g2[:, 0, :], g2[:, 0, :], ACT.Exp).then_inc(exp_done, 1)

            @block.vector
            def _(dve):
                V = nc.vector
                dve.wait_ge(ranked, E)
                V.reduce_max(top[:, 0, :], logits[:, :, :], AX).then_inc(link, 1)
                dve.wait_ge(link, 1)
                V.tensor_tensor(hit[:, :, :], logits[:, :, :], wide(top[:, 0, :]), ALU.is_equal).then_inc(link, 1)
                dve.wait_ge(link, 2)
                V.tensor_tensor(hit[:, :, :], hit[:, :, :], rank[:, :, :], ALU.mult).then_inc(link, 1)
                dve.wait_ge(link, 3)
                V.reduce_max(pos[:, 0, :], hit[:, :, :], AX).then_inc(link, 1)
                dve.wait_ge(link, 4)
                V.tensor_tensor(first[:, :, :], rank[:, :, :], wide(pos[:, 0, :]), ALU.is_equal).then_inc(link, 1)
                dve.wait_ge(link, 5)
                V.scalar_tensor_tensor(logits[:, :, :], first[:, :, :], -FAR, logits[:, :, :], ALU.mult, ALU.add).then_inc(link, 1)
                dve.wait_ge(link, 6)
                V.reduce_max(top[:, 1, :], logits[:, :, :], AX).then_inc(link, 1)
                dve.wait_ge(link, 7)
                V.tensor_tensor(g2[:, 0, :], top[:, 1, :], top[:, 0, :], ALU.subtract).then_inc(link, 1)
                V.tensor_tensor(hit[:, :, :], logits[:, :, :], wide(top[:, 1, :]), ALU.is_equal).then_inc(link, 1)
                dve.wait_ge(link, 9)
                V.tensor_tensor(hit[:, :, :], hit[:, :, :], rank[:, :, :], ALU.mult).then_inc(link, 1)
                dve.wait_ge(link, 10)
                V.reduce_max(pos[:, 1, :], hit[:, :, :], AX).then_inc(link, 1)
                dve.wait_ge(link, 11)
                V.tensor_tensor(hit[:, :, :], rank[:, :, :], wide(pos[:, 1, :]), ALU.is_equal).then_inc(link, 1)
                dve.wait_ge(exp_done, 1)
                V.tensor_scalar_add(g1[:, 0, :], g2[:, 0, :], 1.0).then_inc(link, 1)
                dve.wait_ge(link, 13)
                V.reciprocal(g1[:, 0, :], g1[:, 0, :]).then_inc(link, 1)
                dve.wait_ge(link, 14)
                V.tensor_tensor(g2[:, 0, :], g2[:, 0, :], g1[:, 0, :], ALU.mult).then_inc(link, 1)
                V.tensor_tensor(first[:, :, :], first[:, :, :], wide(g1[:, 0, :]), ALU.mult).then_inc(link, 1)
                dve.wait_ge(link, 16)
                V.tensor_tensor(hit[:, :, :], hit[:, :, :], wide(g2[:, 0, :]), ALU.mult).then_inc(link, 1)
                dve.wait_ge(link, 17)
                V.tensor_tensor(logits[:, :, :], first[:, :, :], hit[:, :, :], ALU.add).then_inc(link, 1)
                dve.wait_ge(link, 18)


def expert_stage(nc, w_in, w_gate, w_out, bias_in, bias_out, gates, tnT_sb, t_sb, tag):
    import concourse.bass as bass
    from concourse import mybir
    from contextlib import ExitStack

    fp32 = mybir.dt.float32
    ALU, ACT = mybir.AluOpType, mybir.ActivationFunctionType
    E = gates.shape[2]
    FOUR = 4
    QUADS = E // FOUR
    TURNS = TILES // GROUP
    with ExitStack() as ctx:
        def sb(name, shape):
            return ctx.enter_context(nc.sbuf_tensor(tag + name, shape, fp32))

        def sem(name):
            return ctx.enter_context(nc.semaphore(tag + name))

        win, wout = sb("_win", [C, E, P]), sb("_wout", [P, E, C])
        wg = sb("_wg", [C, E, P]) if w_gate is not None else None
        bin_, bout = (sb("_bin", [P, E]), sb("_bout", [P, E, C])) if w_gate is None else (None, None)
        hid = [sb(f"_hid{k}", [P, HALF]) for k in range(2)]
        act_out = [sb(f"_act{k}", [P, HALF]) for k in range(2)]
        tmp = sb("_tmp", [P, GROUP, FOUR, C])
        red = sb("_red", [P, GROUP, C])
        ps1 = [ctx.enter_context(nc.psum_tensor(f"{tag}_ps1{k}", [P, HALF], fp32)) for k in range(2)]
        ps2 = [ctx.enter_context(nc.psum_tensor(f"{tag}_ps2{k}", [P, HALF], fp32)) for k in range(2)]
        psY = [ctx.enter_context(nc.psum_tensor(f"{tag}_psY{k}", [P, GROUP * FOUR * C], fp32)) for k in range(2)]
        loaded, h_ready, activated, hid_ready, y_ready, gated, link = (
            sem(n) for n in ("_loaded", "_h_ready", "_activated", "_hid_ready", "_y_ready", "_gated", "_link"))
        reduced, added, fetched = sem("_reduced"), sem("_added"), sem("_fetched")
        turns_done = sem("_turns_done")
        tokens = [sb(f"_tok{k}", [C, HALF]) for k in range(2)]
        loads = [(win, w_in), (wout, w_out)] + ([(wg, w_gate)] if wg is not None else [(bin_, bias_in), (bout, bias_out)])
        LOADED = 16 * len(loads)
        hid_of = hid if wg is not None else act_out
        hid_sem = hid_ready if wg is not None else activated

        with nc.Block() as block:
            @block.sync
            def _(sp):
                for dst, src in loads:
                    sp.dma_start(dst[tuple([slice(None)] * len(dst.shape))], src).then_inc(loaded, 16)

            @block.tensor
            def _(pe):
                M = nc.tensor.matmul
                pe.wait_ge(loaded, LOADED)
                with pe.Fori(0, TURNS // 2) as pair:
                    def into(turn, e):
                        s = turn * E + e
                        rhs = tokens[k][:, :]
                        if e == 0:
                            pe.wait_ge(fetched, turn + 1)
                        pe.wait_ge(hid_sem, s + 1)
                        M(ps1[e % 2][:, :], win[:, e, :], rhs, start=True, stop=True).then_inc(h_ready, 1)
                        if wg is not None:
                            M(ps2[e % 2][:, :], wg[:, e, :], rhs, start=True, stop=True).then_inc(h_ready, 1)

                    def out_of(turn, e):
                        s = turn * E + e
                        quad, q = divmod(e, FOUR)
                        if q == 0:
                            pe.wait_ge(gated, turn * QUADS + quad + 1)
                        pe.wait_ge(hid_sem, s + 3)
                        for g in range(GROUP):
                            last = M(psY[(quad if QUADS > 1 else 0) % 2][:, (g * FOUR + q) * C:(g * FOUR + q + 1) * C],
                                     hid_of[e % 2][:, g * P:(g + 1) * P], wout[:, e, :], start=True, stop=True)
                            if e == E - 1 and g == 0:
                                last.then_inc(turns_done, 1)
                        last.then_inc(y_ready, 1)

                    for k in range(2):
                        turn = pair * 2 + k
                        into(turn, 0)
                        for e in range(E):
                            if e + 1 < E:
                                into(turn, e + 1)
                            out_of(turn, e)

            @block.gpsimd
            def _(pool):
                with pool.Fori(0, TURNS // 2) as pair:
                    for k in range(2):
                        turn = pair * 2 + k
                        pool.wait_ge(turns_done, turn + 1)
                        nc.gpsimd.tensor_copy(tokens[k][:, :], tnT_sb[:, bass.ds(turn * HALF, HALF)]).then_inc(fetched, 1)

            @block.scalar
            def _(act):
                act.wait_ge(loaded, LOADED)
                if wg is None:
                    nc.scalar.activation(act_out[0][:, 0:1], bin_[:, 0:1], ACT.Copy).then_inc(activated, 2)
                with act.Fori(0, TURNS // 2) as pair:
                    for k, e in [(k, e) for k in range(2) for e in range(E)]:
                        s = (pair * 2 + k) * E + e
                        if wg is not None:
                            act.wait_ge(h_ready, s * 2 + 1)
                            act.wait_ge(hid_ready, s + 1)
                            nc.scalar.activation(act_out[e % 2][:, :], ps1[e % 2][:, :], ACT.Silu).then_inc(activated, 1)
                        else:
                            act.wait_ge(h_ready, s + 1)
                            act.wait_ge(y_ready, s + 1)
                            nc.scalar.activation(act_out[e % 2][:, :], ps1[e % 2][:, :], ACT.Gelu,
                                                 bias=bin_[:, e:e + 1]).then_inc(activated, 1)

            @block.vector
            def _(dve):
                V = nc.vector
                dve.wait_ge(loaded, LOADED)
                V.memset(red[:, 0, 0:1], 0.0).then_inc(y_ready, 2)
                V.memset(red[:, 0, 1:2], 0.0).then_inc(gated, 2 if QUADS > 1 else 1)
                V.memset(red[:, 0, 2:3], 0.0).then_inc(hid_ready, 2)
                V.memset(red[:, 0, 3:4], 0.0).then_inc(turns_done, 2)
                GOT = 2 if QUADS > 1 else 1
                with dve.Fori(0, TURNS // 2) as pair:
                    def gate(turn, quad):
                        k = (quad if QUADS > 1 else 0) % 2
                        s = turn * QUADS + quad
                        y = psY[k][:, :].rearrange("p (g e c) -> p g e c", g=GROUP, e=FOUR)
                        dve.wait_ge(y_ready, s * FOUR + FOUR + 2)
                        if wg is None:
                            for g in range(GROUP):
                                last = V.tensor_tensor(tmp[:, g, :, :], y[:, g, :, :], bout[:, :, :], ALU.add)
                            last.then_inc(link, 1)
                            dve.wait_ge(link, s + 1)
                            y = tmp[:, :, :, :]
                        g4 = gates[:, bass.ds(turn * GROUP, GROUP), quad * FOUR:(quad + 1) * FOUR]
                        V.tensor_tensor(tmp[:, :, :, :], y, g4.unsqueeze(3).broadcast_to([P, GROUP, FOUR, C]),
                                        ALU.mult).then_inc(gated, 1)
                        dve.wait_ge(gated, s + 1 + GOT)
                        V.tensor_reduce(red[:, :, :], tmp[:, :, :, :].rearrange("p g e c -> p g c e"),
                                        mybir.AxisListType.X, ALU.add).then_inc(reduced, 1)
                        dve.wait_ge(reduced, s + 1)
                        t_now = t_sb[:, bass.ds(turn * GROUP, GROUP), :]
                        V.tensor_tensor(t_now, t_now, red[:, :, :], ALU.add).then_inc(added, 1)
                        dve.wait_ge(added, s + 1)

                    for k2, e in [(k2, e) for k2 in range(2) for e in range(E)]:
                        turn = pair * 2 + k2
                        s = turn * E + e
                        if wg is not None:
                            dve.wait_ge(activated, s + 1)
                            dve.wait_ge(h_ready, s * 2 + 2)
                            dve.wait_ge(y_ready, s + 1)
                            V.tensor_tensor(hid[e % 2][:, :], act_out[e % 2][:, :], ps2[e % 2][:, :], ALU.mult).then_inc(hid_ready, 1)
                        if e % FOUR == 1 and e > FOUR:
                            gate(turn, e // FOUR - 1)
                        if e == E - 1:
                            gate(turn, QUADS - 1)
SLICES, HEADS3, HDIM3 = 16, 8, 32
HD3 = HEADS3 * HDIM3
SW_0 = 0
SW_S = SW_0 + P
SW_QKV = SW_S + SLICES
SW_OUT = SW_QKV + 3 * HD3
SV_B0 = SW_OUT + 2 * C
SR_B0 = SV_B0 + 1
SR_BS = SR_B0 + C
SR_BO = SR_BS + SLICES
SW_COLS = SR_BO + C


def slice_attn_stage(nc, weights, consts, tn_sb, t_sb):
    import concourse.bass as bass
    from concourse import mybir
    from contextlib import ExitStack

    fp32 = mybir.dt.float32
    ALU, ACT, AX = mybir.AluOpType, mybir.ActivationFunctionType, mybir.AxisListType.X
    BLK = range(PER)
    HG = 4
    pe_s = Steps("turn hT h logits swT pool poolT qk v scores attnT tokT fold out")
    act_s = Steps("copy tnT hTc esw swTc poolTc qkc eat attnTc foldc")
    dve_s = Steps("hx lg max sub sum rsum sw dn rdn pooled vc qdiag smax ssub ssum srec attn tokm tok outb t")

    with ExitStack() as ctx:
        def sb(name, shape):
            return ctx.enter_context(nc.sbuf_tensor("s_" + name, shape, fp32))

        def ps(name, cols=HALF):
            return ctx.enter_context(nc.psum_tensor("s_" + name, [P, cols], fp32))

        def sem(name):
            return ctx.enter_context(nc.semaphore("s_" + name))

        w, con = sb("w", [P, SW_COLS]), sb("con", [P, K_COLS])
        tw = sb("tw", [P, PER, C])
        tnT, hT = sb("tnT", [C, L]), sb("hT", [C, L])
        hx = sb("hx", [P, PER, C + 1])
        sw = sb("sw", [P, PER, SLICES])
        r8 = sb("r8", [P, 2, PER])
        swT = sb("swT", [SLICES, L])
        pooled, dn = sb("pooled", [SLICES, C + 1]), sb("dn", [SLICES, 1])
        poolT = sb("poolT", [C + 1, SLICES])
        qk = sb("qk", [P, 4, SLICES])
        v = sb("v", [SLICES, HD3])
        qd = sb("qd", [P, 2, HG, SLICES])
        at = sb("at", [P, 2, SLICES])
        rs = sb("rs", [HG * SLICES, 2, 2])
        atT = sb("atT", [SLICES, 2 * HG * SLICES])
        tokm, tok = sb("tokm", [P, 2, HG, SLICES]), sb("tok", [P, 2, SLICES])
        fold = sb("fold", [SLICES, C])
        tmp = sb("tmp", [P, PER, C])
        psM = ps("psM", L)
        psH, psL, psG, psQ, psS, psO = (ps(n) for n in ("psH", "psL", "psG", "psQ", "psS", "psO"))
        loaded, ones_set = sem("loaded"), sem("ones")
        pe_done, act_done, dve_done = sem("pe"), sem("act"), sem("dve")
        halves = [slice(0, HALF), slice(HALF, L)]
        at4 = at[0:HG * SLICES, :, :]
        ID = con[:, K_ID:K_ID + P]

        with nc.Block() as block:
            @block.sync
            def _(sp):
                sp.dma_start(w[:, :], weights).then_inc(loaded, 16)
                sp.dma_start(con[:, :], consts).then_inc(loaded, 16)

            @block.gpsimd
            def _(pool):
                nc.gpsimd.memset(hx[:, :, :], 1.0).then_inc(ones_set, 1)
                nc.gpsimd.memset(at[:, :, :], 0.0).then_inc(ones_set, 1)

            @block.tensor
            def _(pe):
                M = nc.tensor.matmul
                pe.wait_ge(loaded, 32)
                with pe.Fori(0, B) as img:
                    def act(name):
                        pe.wait_ge(act_done, act_s.after(name, img))

                    def dve(name):
                        pe.wait_ge(dve_done, dve_s.after(name, img))

                    def done(ins):
                        ins.then_inc(pe_done, 1)

                    act("copy")
                    for i in BLK:
                        last = M(psM[0:C, i * P:(i + 1) * P], tw[:, i, :], ID, start=True, stop=True)
                    done(last)
                    act("tnT")
                    for hs in halves:
                        last = M(psM[:, hs], w[0:C, SW_0:SW_0 + P], tnT[:, hs], start=True, stop=True)
                    done(last)
                    for i in BLK:
                        last = M(psH[:, i * C:(i + 1) * C], tnT[:, i * P:(i + 1) * P], w[0:C, SW_0:SW_0 + C],
                                 start=True, stop=True)
                    done(last)
                    act("hTc")
                    for i in BLK:
                        last = M(psL[:, i * SLICES:(i + 1) * SLICES], hT[:, i * P:(i + 1) * P], w[0:C, SW_S:SW_S + SLICES],
                                 start=True, stop=True)
                    done(last)
                    dve("sw")
                    for i in BLK:
                        last = M(psM[0:SLICES, i * P:(i + 1) * P], sw[:, i, :], ID, start=True, stop=True)
                    done(last)
                    for i in BLK:
                        last = M(psG[0:SLICES, 0:C + 1], sw[:, i, :], hx[:, i, :], start=i == 0, stop=i == PER - 1)
                    done(last)
                    dve("pooled")
                    done(M(psS[0:C + 1, 0:SLICES], pooled[:, :], con[0:SLICES, K_ID:K_ID + SLICES], start=True, stop=True))
                    act("poolTc")
                    for j in range(4):
                        last = M(psQ[:, j * SLICES:(j + 1) * SLICES], w[0:C + 1, SW_QKV + j * P:SW_QKV + (j + 1) * P], poolT[:, :],
                                 start=True, stop=True)
                    done(last)
                    done(M(psG[0:SLICES, 0:HD3], poolT[:, :], w[0:C + 1, SW_QKV + 2 * HD3:SW_QKV + 3 * HD3],
                           start=True, stop=True))
                    dve("qdiag")
                    for g in range(2):
                        last = M(psS[0:HG * SLICES, g * SLICES:(g + 1) * SLICES], qd[:, g, :, :].rearrange("p h s -> p (h s)"),
                                 qk[:, 2 + g, :], start=True, stop=True)
                    done(last)
                    dve("attn")
                    for g in range(2):
                        last = M(psL[0:SLICES, g * HG * SLICES:(g + 1) * HG * SLICES], at[:, g, :],
                                 con[:, K_ID:K_ID + HG * SLICES], start=True, stop=True)
                    done(last)
                    act("attnTc")
                    for g in range(2):
                        last = M(psQ[:, g * HG * SLICES:(g + 1) * HG * SLICES], v[:, g * P:(g + 1) * P],
                                 atT[:, g * HG * SLICES:(g + 1) * HG * SLICES], start=True, stop=True)
                    done(last)
                    dve("tok")
                    for g in range(2):
                        last = M(psG[0:SLICES, 0:C], tok[:, g, :], w[:, SW_OUT + g * C:SW_OUT + (g + 1) * C],
                                 start=g == 0, stop=g == 1)
                    done(last)
                    act("foldc")
                    for i in BLK:
                        last = M(psO[:, i * C:(i + 1) * C], swT[:, i * P:(i + 1) * P], fold[:, :], start=True, stop=True)
                    done(last)

            @block.scalar
            def _(act):
                A = nc.scalar.activation
                act.wait_ge(loaded, 32)
                A(rs[:, 0, 0:1], con[0:HG * SLICES, 0:1], ACT.Copy).then_inc(act_done, 1)
                with act.Fori(0, B) as img:
                    def pe(name):
                        act.wait_ge(pe_done, pe_s.after(name, img) - 1)

                    def dve(name):
                        act.wait_ge(dve_done, dve_s.after(name, img))

                    act.wait_ge(dve_done, dve_s.all(img))
                    A(tw[:, :, :], tn_sb[:, bass.ds(img * PER, PER), :], ACT.Copy).then_inc(act_done, 1)
                    pe("turn")
                    A(tnT[:, :], psM[0:C, :], ACT.Copy).then_inc(act_done, 1)
                    pe("hT")
                    A(hT[:, :], psM[0:C, :], ACT.Identity, bias=w[0:C, SV_B0:SV_B0 + 1]).then_inc(act_done, 1)
                    dve("sub")
                    A(sw[:, :, :], sw[:, :, :], ACT.Exp).then_inc(act_done, 1)
                    pe("swT")
                    A(swT[:, :], psM[0:SLICES, :], ACT.Copy).then_inc(act_done, 1)
                    pe("poolT")
                    A(poolT[:, :], psS[0:C + 1, 0:SLICES], ACT.Copy).then_inc(act_done, 1)
                    pe("qk")
                    A(qk[:, :, :], psQ[:, 0:4 * SLICES].rearrange("p (j s) -> p j s", j=4), ACT.Copy).then_inc(act_done, 1)
                    dve("ssub")
                    A(at4, at4, ACT.Exp, scale=HDIM3 ** -0.5).then_inc(act_done, 1)
                    pe("attnT")
                    A(atT[:, :], psL[0:SLICES, 0:2 * HG * SLICES], ACT.Copy).then_inc(act_done, 1)
                    pe("fold")
                    A(fold[:, :], psG[0:SLICES, 0:C], ACT.Copy).then_inc(act_done, 1)

            @block.vector
            def _(dve):
                V = nc.vector
                dve.wait_ge(loaded, 32)
                dve.wait_ge(ones_set, 2)
                V.memset(tmp[:, 0, 0:1], 0.0).then_inc(dve_done, 1)
                with dve.Fori(0, B) as img:
                    def pe(name):
                        dve.wait_ge(pe_done, pe_s.after(name, img) - 1)

                    def act(name):
                        dve.wait_ge(act_done, act_s.after(name, img))

                    def own(name):
                        dve.wait_ge(dve_done, dve_s.after(name, img))

                    def done(ins):
                        ins.then_inc(dve_done, 1)

                    def row(v_, shape):
                        return v_.unsqueeze(1).broadcast_to(shape)

                    pe("h")
                    done(V.tensor_tensor(hx[:, :, 0:C], psH[:, :].rearrange("p (i c) -> p i c", i=PER),
                                         row(w[:, SR_B0:SR_B0 + C], [P, PER, C]), ALU.add))
                    pe("logits")
                    done(V.tensor_tensor(sw[:, :, :], psL[:, 0:PER * SLICES].rearrange("p (i s) -> p i s", i=PER),
                                         row(w[:, SR_BS:SR_BS + SLICES], [P, PER, SLICES]), ALU.add))
                    own("lg")
                    done(V.reduce_max(r8[:, 0, :], sw[:, :, :], AX))
                    own("max")
                    wide = [P, PER, SLICES]
                    done(V.tensor_tensor(sw[:, :, :], sw[:, :, :], r8[:, 0, :].unsqueeze(2).broadcast_to(wide), ALU.subtract))
                    act("esw")
                    done(V.reduce_sum(r8[:, 1, :], sw[:, :, :], AX))
                    own("sum")
                    done(V.reciprocal(r8[:, 1, :], r8[:, 1, :]))
                    own("rsum")
                    done(V.tensor_tensor(sw[:, :, :], sw[:, :, :], r8[:, 1, :].unsqueeze(2).broadcast_to(wide), ALU.mult))
                    pe("pool")
                    done(V.tensor_scalar_add(dn[:, :], psG[0:SLICES, C:C + 1], 1e-9))
                    own("dn")
                    done(V.reciprocal(dn[:, :], dn[:, :]))
                    own("rdn")
                    done(V.tensor_scalar(pooled[:, :], psG[0:SLICES, 0:C + 1], dn[:, :], None, ALU.mult))
                    pe("v")
                    done(V.tensor_copy(v[:, :], psG[0:SLICES, 0:HD3]))
                    act("qkc")
                    done(V.tensor_tensor(qd[:, :, :, :], qk[:, 0:2, :].unsqueeze(2).broadcast_to([P, 2, HG, SLICES]),
                                         con[:, K_MASK:K_MASK + 64].rearrange("p (h s) -> p h s", h=HG).unsqueeze(1).broadcast_to(
                                             [P, 2, HG, SLICES]), ALU.mult))
                    pe("scores")
                    sc = psS[0:HG * SLICES, 0:2 * SLICES].rearrange("p (g s) -> p g s", g=2)
                    done(V.reduce_max(rs[:, 0, :], sc, AX))
                    own("smax")
                    wide2 = [HG * SLICES, 2, SLICES]
                    done(V.tensor_tensor(at4, sc, rs[:, 0, :].unsqueeze(2).broadcast_to(wide2), ALU.subtract))
                    act("eat")
                    done(V.reduce_sum(rs[:, 1, :], at4, AX))
                    own("ssum")
                    done(V.reciprocal(rs[:, 1, :], rs[:, 1, :]))
                    own("srec")
                    done(V.tensor_tensor(at4, at4, rs[:, 1, :].unsqueeze(2).broadcast_to(wide2), ALU.mult))
                    pe("tokT")
                    done(V.tensor_tensor(tokm[:, :, :, :], psQ[:, 0:2 * HG * SLICES].rearrange("p (g h s) -> p g h s", g=2, h=HG),
                                         con[:, K_MASK:K_MASK + 64].rearrange("p (h s) -> p h s", h=HG).unsqueeze(1).broadcast_to(
                                             [P, 2, HG, SLICES]), ALU.mult))
                    own("tokm")
                    done(V.tensor_reduce(tok[:, :, :], tokm[:, :, :, :].rearrange("p g h s -> p g s h"), AX, ALU.add))
                    pe("out")
                    done(V.tensor_tensor(tmp[:, :, :], psO[:, :].rearrange("p (i c) -> p i c", i=PER),
                                         row(w[:, SR_BO:SR_BO + C], [P, PER, C]), ALU.add))
                    own("outb")
                    t_now = t_sb[:, bass.ds(img * PER, PER), :]
                    done(V.tensor_tensor(t_now, t_now, tmp[:, :, :], ALU.add))
EDGES = 262144
ECOLS = EDGES // P
COL_BITS, PART_BITS = 11, 7
NODES = TOK
SRC_BITS = 13
KEY_BASE = 0x20000000
OUTSIDE = 1 << 20
BIG = 1e30


def sort_stage(nc, edges, consts, src_d, keep_d, pen_d, first_d, ends_d, place_d, target0_d):
    import concourse.bass as bass
    from concourse import mybir
    from contextlib import ExitStack

    fp32, i32 = mybir.dt.float32, mybir.dt.int32
    ALU, ACT = mybir.AluOpType, mybir.ActivationFunctionType

    with ExitStack() as ctx:
        def sb(name, shape, dt=fp32):
            return ctx.enter_context(nc.sbuf_tensor("o_" + name, shape, dt))

        def sem(name):
            return ctx.enter_context(nc.semaphore("o_" + name))

        con = sb("con", [P, K_COLS])
        es, ed = sb("es", [P, ECOLS], i32), sb("ed", [P, ECOLS], i32)
        f1, f2 = sb("f1", [P, ECOLS]), sb("f2", [P, ECOLS])
        key = [sb("key0", [P, ECOLS]), sb("key1", [P, ECOLS])]
        edge_col = sb("edge_col", [P, 2], i32)
        es2 = sb("es2", [P, ECOLS], i32)
        place = sb("place", [P, ECOLS], i32)
        ps = ctx.enter_context(nc.psum_tensor("o_ps", [P, ECOLS], fp32))
        loaded, link, turned, copied, shifted, placed, stored = (
            sem(n) for n in ("loaded", "link", "turned", "copied", "shifted", "placed", "stored"))
        apart = sem("apart")
        BLOCKS = ECOLS // P

        steps = []
        for k in range(1, COL_BITS + PART_BITS + 1):
            steps.append(("flip", k))
            if k > COL_BITS:
                steps.append(("turn", None))
                steps += [("across", j - COL_BITS) for j in range(k - 1, COL_BITS - 1, -1)]
                steps.append(("turn", None))
            steps += [("along", j) for j in range(min(k, COL_BITS) - 1, -1, -1)]
        link_at, buf_at, made, buf = {}, {}, 9, 0
        for n, (kind, at) in enumerate(steps):
            link_at[n], buf_at[n] = made, buf
            if kind == "flip":
                made += 2 if at == COL_BITS else 1
            elif kind != "turn":
                made, buf = made + 2, 1 - buf
        TURNS = [n for n, (kind, _) in enumerate(steps) if kind == "turn"]

        with nc.Block() as block:
            @block.sync
            def _(sp):
                sp.dma_start(con[:, :], consts).then_inc(loaded, 16)
                sp.dma_start(es[:, :], edges[0, :, :]).then_inc(loaded, 16)
                sp.dma_start(ed[:, :], edges[1, :, :]).then_inc(loaded, 16)
                sp.wait_ge(shifted, 2)
                sp.wait_ge(apart, 1)
                sp.dma_start(edge_col[1:P, 0:1], ed[0:P - 1, ECOLS - 1:ECOLS]).then_inc(placed, 16)
                sp.dma_start(edge_col[0:P - 1, 1:2], ed[1:P, 0:1]).then_inc(placed, 16)
                sp.dma_start(src_d, es[:, :]).then_inc(stored, 16)
                sp.dma_start(target0_d, ed[:, 0:1]).then_inc(stored, 16)
                sp.wait_ge(copied, len(TURNS) + 1)
                sp.dma_start(keep_d, f1[:, :]).then_inc(stored, 16)
                sp.dma_start(pen_d, f2[:, :]).then_inc(stored, 16)
                sp.wait_ge(copied, len(TURNS) + 2)
                sp.dma_start(first_d, key[0][:, :]).then_inc(stored, 16)
                sp.wait_ge(copied, len(TURNS) + 3)
                sp.dma_start(ends_d, key[1][:, :].bitcast(i32)).then_inc(stored, 16)
                sp.dma_start(place_d, place[:, :]).then_inc(stored, 16)
                sp.wait_ge(stored, 16 * 7)

            @block.gpsimd
            def _(pool):
                nc.gpsimd.iota(place[:, :], pattern=[[2, ECOLS]], base=0, channel_multiplier=2 * ECOLS).then_inc(shifted, 1)
                nc.gpsimd.memset(edge_col[:, :], -1).then_inc(shifted, 1)

            @block.tensor
            def _(pe):
                pe.wait_ge(loaded, 48)
                for turn, n in enumerate(TURNS):
                    pe.wait_ge(link, link_at[n])
                    for r in range(BLOCKS):
                        last = nc.tensor.transpose(ps[:, r * P:(r + 1) * P], key[buf_at[n]][:, r * P:(r + 1) * P],
                                                   con[:, K_ID:K_ID + P])
                    last.then_inc(turned, 1)

            @block.scalar
            def _(act):
                for turn, n in enumerate(TURNS):
                    act.wait_ge(turned, turn + 1)
                    nc.scalar.activation(key[buf_at[n]][:, :], ps[:, :], ACT.Copy).then_inc(copied, 1)

            @block.vector
            def _(dve):
                V = nc.vector
                count = [0]

                def after(ins):
                    ins.then_inc(link, 1)
                    count[0] += 1

                def ready():
                    dve.wait_ge(link, count[0])

                dve.wait_ge(loaded, 48)
                after(V.tensor_scalar(f1[:, :], es[:, :], 0.0, float(NODES), ALU.is_lt, ALU.mult)); ready()
                after(V.tensor_tensor(f1[:, :], f1[:, :], es[:, :], ALU.add)); ready()
                after(V.tensor_scalar(es[:, :], f1[:, :], 0.0, float(NODES - 1), ALU.max, ALU.min)); ready()
                after(V.tensor_scalar(f1[:, :], ed[:, :], 0.0, float(NODES), ALU.is_lt, ALU.mult)); ready()
                after(V.tensor_scalar(f2[:, :], ed[:, :], 0.0, float(NODES), ALU.max, ALU.min)); ready()
                after(V.tensor_tensor(f1[:, :], f1[:, :], f2[:, :], ALU.add)); ready()
                after(V.tensor_scalar(ed[:, :], f1[:, :], float(NODES), None, ALU.min)); ready()
                after(V.tensor_scalar(ed[:, :], ed[:, :], SRC_BITS, KEY_BASE, ALU.logical_shift_left, ALU.bitwise_or)); ready()
                after(V.tensor_tensor(key[0][:, :].bitcast(i32), ed[:, :], es[:, :], ALU.bitwise_or)); ready()

                cur, turns = 0, 0
                for n, (kind, at) in enumerate(steps):
                    K = key[cur]
                    if kind == "flip" and at < COL_BITS:
                        w = 1 << (at - 1)
                        four = K[:, :].rearrange("p (b w) -> p b w", w=4 * w)
                        part = four[:, :, w:3 * w] if at > 1 else four[:, :, 2:4]
                        after(V.tensor_scalar(part, part, -1.0, None, ALU.mult)); ready()
                    elif kind == "flip" and at == COL_BITS:
                        half = ECOLS // 2
                        for h in range(2):
                            part = K[:, h * half:(h + 1) * half]
                            after(V.tensor_scalar(part, part, con[:, K_SIGN + h:K_SIGN + h + 1], None, ALU.mult))
                        ready()
                    elif kind == "flip":
                        c = K_SIGN + 1 + at - COL_BITS
                        after(V.tensor_scalar(K[:, :], K[:, :], con[:, c:c + 1], None, ALU.mult)); ready()
                    elif kind == "turn":
                        assert (link_at[n], buf_at[n]) == (count[0], cur)
                        turns += 1
                        dve.wait_ge(copied, turns)
                    else:
                        w = 1 << at
                        a = K[:, :].rearrange("p (b two w) -> p b two w", two=2, w=w)
                        o = key[1 - cur][:, :].rearrange("p (b two w) -> p b two w", two=2, w=w)
                        after(V.tensor_tensor(o[:, :, 0, :], a[:, :, 0, :], a[:, :, 1, :], ALU.min))
                        after(V.tensor_tensor(o[:, :, 1, :], a[:, :, 0, :], a[:, :, 1, :], ALU.max))
                        ready()
                        cur = 1 - cur

                S = key[cur][:, :].bitcast(i32)
                after(V.tensor_scalar(es[:, :], S, NODES - 1, None, ALU.bitwise_and)); ready()
                V.tensor_scalar(ed[:, :], S, SRC_BITS, 2 * NODES - 1, ALU.logical_shift_right, ALU.bitwise_and).then_inc(apart, 1)
                dve.wait_ge(apart, 1)
                dve.wait_ge(placed, 32)
                after(V.tensor_tensor(f1[:, 1:ECOLS], ed[:, 1:ECOLS], ed[:, 0:ECOLS - 1], ALU.is_equal))
                after(V.tensor_tensor(f1[:, 0:1], ed[:, 0:1], edge_col[:, 0:1], ALU.is_equal)); ready()
                V.tensor_scalar(f2[:, :], f1[:, :], 1.0, BIG, ALU.subtract, ALU.mult).then_inc(copied, 1)
                dve.wait_ge(copied, len(TURNS) + 1)
                V.tensor_tensor_scan(key[0][:, :], f1[:, :], f1[:, :], 1.0, ALU.mult, ALU.mult).then_inc(copied, 1)
                dve.wait_ge(copied, len(TURNS) + 2)
                after(V.tensor_copy(es2[:, :], key[0][:, :])); ready()
                after(V.tensor_tensor(place[:, :], place[:, :], es2[:, :], ALU.bitwise_or)); ready()
                E1 = key[1][:, :].bitcast(i32)
                after(V.tensor_tensor(E1[:, 0:ECOLS - 1], ed[:, 0:ECOLS - 1], ed[:, 1:ECOLS], ALU.is_equal))
                after(V.tensor_tensor(E1[:, ECOLS - 1:ECOLS], ed[:, ECOLS - 1:ECOLS], edge_col[:, 1:2], ALU.is_equal)); ready()
                after(V.tensor_scalar(E1, E1, float(OUTSIDE), None, ALU.mult)); ready()
                V.tensor_tensor(E1, E1, ed[:, :], ALU.bitwise_or).then_inc(copied, 1)
                dve.wait_ge(copied, len(TURNS) + 3)


def graph_tables(nc):
    from concourse import mybir
    fp32, i32 = mybir.dt.float32, mybir.dt.int32

    def dram(name, shape, dt):
        return nc.dram_tensor("scratch_" + name, shape, dt, kind="Internal").ap()

    return {
        "src": dram("src", (P, ECOLS), i32), "keep": dram("keep", (P, ECOLS), fp32), "pen": dram("pen", (P, ECOLS), fp32),
        "first": dram("first", (P, ECOLS), fp32), "ends_i": dram("ends_i", (P, ECOLS), i32),
        "place_i": dram("place_i", (P, ECOLS), i32), "target0": dram("target0", (P, 1), i32),
        "ends": dram("ends", (NODES, 1), i32), "start": dram("start", (NODES, 1), i32),
        "node": dram("node", (NODES, 20), fp32), "target": dram("target", (NODES, 4), fp32),
        "place": dram("place", (EDGES, 4), fp32), "edge": dram("edge", (EDGES, 24), fp32),
        "carry": dram("carry", (P, 24), fp32),
    }
GATES = 4
HEADS_G = 4
HE = HEADS_G * GATES
ROW_T = HE + HEADS_G
ROW_O = 2 * HEADS_G + HE
CHUNK = 32
CHUNKS = ECOLS // CHUNK


class EndsNotes:

    def __init__(self, nc, ctx, ends_d, place_d, ends_tbl):
        from concourse import mybir
        i32 = mybir.dt.int32
        self.nc, self.ends_d, self.place_d, self.ends_tbl = nc, ends_d, place_d, ends_tbl
        self.ends, self.place = (ctx.enter_context(nc.sbuf_tensor("e_" + n, [P, ECOLS], i32)) for n in ("ends", "place"))
        self.ends_w, self.place_w = (ctx.enter_context(nc.sbuf_tensor("e_" + n, [P, CHUNK], i32)) for n in ("ends_w", "place_w"))
        self.none, self.gate = (ctx.enter_context(nc.sbuf_tensor("e_" + n, [P, TILES], i32)) for n in ("none", "gate"))
        self.loaded, self.copied, self.scattered, self.set_ = (
            ctx.enter_context(nc.semaphore("e_" + n)) for n in ("loaded", "copied", "scattered", "set"))

    def program(self, pool):
        import concourse.bass as bass
        from concourse import mybir
        nc = self.nc
        pool.dma_start(self.ends[:, :], self.ends_d).then_inc(self.loaded, 16)
        pool.dma_start(self.place[:, :], self.place_d).then_inc(self.loaded, 16)
        nc.gpsimd.memset(self.none[:, :], -1).then_inc(self.set_, 1)
        nc.gpsimd.memset(self.gate[:, :], 0).then_inc(self.set_, 1)
        pool.wait_ge(self.set_, 2)
        pool.dma_start(self.ends_tbl.rearrange("(p i) o -> p (i o)", p=P), self.none[:, :]).then_inc(self.scattered, 16)
        pool.wait_ge(self.loaded, 32)
        with pool.Fori(0, CHUNKS) as c:
            pool.wait_ge(self.scattered, c * (16 * CHUNK) + 16)
            nc.gpsimd.tensor_copy(self.ends_w[:, :], self.ends[:, bass.ds(c * CHUNK, CHUNK)]).then_inc(self.copied, 1)
            nc.gpsimd.tensor_copy(self.place_w[:, :], self.place[:, bass.ds(c * CHUNK, CHUNK)]).then_inc(self.copied, 1)
            pool.wait_ge(self.copied, c * 2 + 2)
            nc.gpsimd.tensor_tensor(self.gate[:, 0:1], self.gate[:, 1:2], self.gate[:, 2:3], mybir.AluOpType.add)
            for j in range(CHUNK):
                nc.gpsimd.indirect_dma_start(
                    out=self.ends_tbl, out_offset=bass.IndirectOffsetOnAxis(ap=self.ends_w[:, j:j + 1], axis=0),
                    in_=self.place_w[:, j:j + 1], in_offset=None, bounds_check=NODES - 1, oob_is_err=False,
                ).then_inc(self.scattered, 16)
        pool.wait_ge(self.scattered, 16 * CHUNK * CHUNKS + 16)


def graph_stage(nc, att_rows, feat, tables, x):
    import concourse.bass as bass
    from concourse import mybir
    from contextlib import ExitStack

    fp32, i32 = mybir.dt.float32, mybir.dt.int32
    ALU, ACT, AX = mybir.AluOpType, mybir.ActivationFunctionType, mybir.AxisListType.X
    Off = bass.IndirectOffsetOnAxis
    node_tbl, target_tbl, place_tbl, edge_tbl, carry_tbl, start_tbl, ends_tbl = (
        tables[n] for n in ("node", "target", "place", "edge", "carry", "start", "ends"))
    scores = x["scores"]

    def whole(t):
        return t[tuple([slice(None)] * len(t.shape))]

    with ExitStack() as outer:
        def keep_sb(name, shape, dt=fp32):
            return outer.enter_context(nc.sbuf_tensor("r_" + name, shape, dt))

        row = keep_sb("row", [P, TILES, ROW_T])
        adst = keep_sb("adst", [P, TILES, HEADS_G])
        att = keep_sb("att", [P, 5 * HE])
        end_i, end_f = keep_sb("end_i", [P, TILES], i32), keep_sb("end_f", [P, TILES])
        end_idx, start_idx, carry_idx = (keep_sb(n, [P, TILES], i32) for n in ("end_idx", "start_idx", "carry_idx"))
        state = keep_sb("state", [P, ROW_O])
        ad0 = keep_sb("ad0", [P, HEADS_G])

        with ExitStack() as ctx:
            def sb(name, shape, dt=fp32):
                return ctx.enter_context(nc.sbuf_tensor("n_" + name, shape, dt))

            def sem(name):
                return ctx.enter_context(nc.semaphore("n_" + name))

            prod = sb("prod", [P, TILES, HE])
            zero = sb("zero", [P, ECOLS])
            line = sb("line", [1, NODES], i32)
            top = sb("top", [1, NODES + 1])
            t0 = sb("t0", [P, 1], i32)
            part = sb("part", [P, TILES], i32)
            lf, lg = sb("lf", [P, TILES]), sb("lg", [P, TILES])
            loaded, zeroed, link, rows_out, starts_out, starts_in, filled, spread = (
                sem(n) for n in ("loaded", "zeroed", "link", "rows_out", "starts_out", "starts_in", "filled", "spread"))

            with nc.Block() as block:
                NODE_ROWS, START_ROW = 5, 11

                @block.sync
                def _(sp):
                    sp.dma_start(whole(att), att_rows).then_inc(loaded, 16)
                    sp.dma_start(line[:, :], ends_tbl.rearrange("n o -> o n")).then_inc(loaded, 16)
                    sp.dma_start(end_i[:, :], ends_tbl.rearrange("(i p) o -> p (i o)", p=P),
                                 allow_slow_non_contiguous=True).then_inc(loaded, 16)
                    sp.dma_start(t0[:, :], x["target0"]).then_inc(loaded, 16)
                    sp.wait_ge(zeroed, 1)
                    place_v = place_tbl.rearrange("(q p c) h -> q p (c h)", q=4, p=P)
                    for q in range(4):
                        sp.dma_start(place_v[q, :, :], zero[:, :]).then_inc(filled, 16)
                    sp.wait_ge(link, NODE_ROWS)
                    sp.dma_start(node_tbl.rearrange("(i p) f -> p i f", p=P), whole(row)).then_inc(rows_out, 16)
                    sp.dma_start(target_tbl.rearrange("(i p) f -> p i f", p=P), whole(adst)).then_inc(rows_out, 16)
                    sp.wait_ge(link, START_ROW)
                    sp.dma_start(start_tbl.rearrange("n o -> o n"), line[:, :]).then_inc(starts_out, 16)
                    sp.wait_ge(starts_out, 16)
                    sp.dma_start(start_idx[:, :], start_tbl.rearrange("(i p) o -> p (i o)", p=P),
                                 allow_slow_non_contiguous=True).then_inc(starts_in, 16)
                    sp.wait_ge(starts_in, 16)

                @block.gpsimd
                def _(pool):
                    nc.gpsimd.memset(zero[:, :], 0.0).then_inc(zeroed, 1)
                    nc.gpsimd.memset(ad0[:, :], 0.0).then_inc(zeroed, 1)
                    pool.wait_ge(zeroed, 2)
                    pool.wait_ge(loaded, 64)
                    pool.wait_ge(rows_out, 32)
                    nc.gpsimd.indirect_dma_start(out=ad0[:, :], out_offset=None, in_=target_tbl,
                                                 in_offset=Off(ap=t0[:, 0:1], axis=0),
                                                 bounds_check=NODES - 1, oob_is_err=False).then_inc(spread, 16)
                    pool.wait_ge(filled, 64)
                    pool.wait_ge(starts_in, 16)
                    for i in range(TILES):
                        nc.gpsimd.indirect_dma_start(out=place_tbl, out_offset=Off(ap=start_idx[:, i:i + 1], axis=0),
                                                     in_=adst[:, i, :], in_offset=None,
                                                     bounds_check=EDGES - 1, oob_is_err=False).then_inc(spread, 16)
                    pool.wait_ge(spread, 16 * (TILES + 1))

                @block.vector
                def _(dve):
                    V = nc.vector
                    count = [0]

                    def link_(ins):
                        ins.then_inc(link, 1)
                        count[0] += 1
                        dve.wait_ge(link, count[0])

                    dve.wait_ge(loaded, 64)

                    def att_sum(out, at):
                        link_(V.tensor_tensor(whole(prod), whole(feat), att[:, at * HE:(at + 1) * HE].unsqueeze(1).broadcast_to([P, TILES, HE]), ALU.mult))
                        link_(V.tensor_reduce(out, prod[:, :, :].rearrange("p i (h e) -> p i h e", h=HEADS_G), AX, ALU.add))

                    att_sum(adst[:, :, :], 1)
                    att_sum(row[:, :, HE:ROW_T], 0)
                    link_(V.tensor_copy(row[:, :, 0:HE], whole(feat)))
                    assert count[0] == NODE_ROWS
                    link_(V.tensor_scalar(line[:, :], line[:, :], 1, None, ALU.arith_shift_right))
                    link_(V.memset(top[:, 0:1], -1.0))
                    link_(V.tensor_tensor_scan(top[:, 1:NODES + 1], line[:, :], line[:, :], -1.0, ALU.max, ALU.max))
                    link_(V.tensor_scalar(line[:, :], line[:, :], 0.0, float(OUTSIDE), ALU.is_lt, ALU.mult))
                    link_(V.scalar_tensor_tensor(line[:, :], top[:, 0:NODES], 1.0, line[:, :], ALU.add, ALU.add))
                    link_(V.tensor_copy(part[:, :], end_i[:, :]))
                    assert count[0] == START_ROW
                    link_(V.tensor_scalar(end_idx[:, :], end_i[:, :], 1, None, ALU.arith_shift_right))
                    link_(V.tensor_copy(end_f[:, :], end_idx[:, :]))
                    link_(V.tensor_scalar(lg[:, :], end_f[:, :], 0.0, 2.0 * OUTSIDE, ALU.is_lt, ALU.mult))
                    link_(V.tensor_tensor(end_f[:, :], end_f[:, :], lg[:, :], ALU.add))
                    link_(V.tensor_scalar(part[:, :], part[:, :], 1, None, ALU.bitwise_and))
                    link_(V.tensor_copy(lf[:, :], part[:, :]))
                    link_(V.tensor_scalar(lf[:, :], lf[:, :], -float(OUTSIDE), float(OUTSIDE), ALU.mult, ALU.add))
                    link_(V.tensor_tensor(lf[:, :], lf[:, :], lg[:, :], ALU.add))
                    link_(V.tensor_scalar(part[:, :], end_idx[:, :], COL_BITS, None, ALU.arith_shift_right))
                    link_(V.tensor_copy(lg[:, :], part[:, :]))
                    link_(V.tensor_tensor(carry_idx[:, :], lf[:, :], lg[:, :], ALU.add))
                    link_(V.tensor_copy(end_idx[:, :], end_f[:, :]))

        with ExitStack() as ctx:
            def sb(name, shape, dt=fp32):
                return ctx.enter_context(nc.sbuf_tensor("g2_" + name, shape, dt))

            def sem(name):
                return ctx.enter_context(nc.semaphore("g2_" + name))

            src = sb("src", [P, ECOLS], i32)
            keep, pen = sb("keep", [P, ECOLS]), sb("pen", [P, ECOLS])
            tgt = sb("tgt", [P, ECOLS, HEADS_G])
            gate, spare, done = sb("gate", [P, 4]), sb("spare", [P, 4]), sb("done", [P, 1])
            idx = [sb(f"idx{k}", [P, CHUNK], i32) for k in range(2)]
            got = [sb(f"got{k}", [P, CHUNK, ROW_T]) for k in range(2)]
            out = [sb(f"out{k}", [P, CHUNK, ROW_O]) for k in range(2)]
            ad, e, w, r = (sb(n, [P, HEADS_G, CHUNK]) for n in ("ad", "e", "w", "r"))
            m = sb("m", [P, HEADS_G, CHUNK + 1])
            msg = sb("msg", [P, HE, CHUNK])
            loaded, copied, set_, link = sem("loaded"), sem("copied"), sem("set"), sem("link")
            gathered = [sem("gathered0"), sem("gathered1")]
            consumed, exps, written = sem("consumed"), sem("exps"), [sem("written0"), sem("written1")]
            DVE_STEPS = Steps("t1 t2 t3 t4 adkeep e leaky m1 m2 m3 m4 w0 r0 r1 s1 s2 s3 s4 msg "
                              + " ".join(f"f{k}" for k in range(HE)) + " mcopy mkeep skeep")
            edge_v = edge_tbl.rearrange("(p c) f -> p (c f)", p=P)

            with nc.Block() as block:
                @block.sync
                def _(sp):
                    sp.dma_start(src[:, :], x["src"]).then_inc(loaded, 16)
                    sp.dma_start(keep[:, :], x["keep"]).then_inc(loaded, 16)
                    sp.dma_start(pen[:, :], x["pen"]).then_inc(loaded, 16)
                    sp.dma_start(whole(tgt), place_tbl.rearrange("(p c) h -> p c h", p=P)).then_inc(loaded, 16)
                    for k in range(2):
                        sp.dma_start(spare[:, 2 * k:2 * k + 2], x["first"][:, 0:2]).then_inc(written[k], 16)
                    with sp.Fori(0, CHUNKS // 2) as pair:
                        for k in range(2):
                            c = pair * 2 + k
                            sp.wait_ge(link, DVE_STEPS.after("skeep", c))
                            sp.dma_start(edge_v[:, bass.ds(c * (CHUNK * ROW_O), CHUNK * ROW_O)],
                                         out[k][:, :, :].rearrange("p c f -> p (c f)")).then_inc(written[k], 16)
                    for k in range(2):
                        sp.wait_ge(written[k], 16 * (CHUNKS // 2) + 16)

                @block.gpsimd
                def _(pool):
                    nc.gpsimd.memset(gate[:, :], 0.0).then_inc(set_, 1)
                    pool.wait_ge(loaded, 64)
                    pool.wait_ge(set_, 1)
                    with pool.Fori(0, CHUNKS // 2) as pair:
                        for k in range(2):
                            c = pair * 2 + k
                            pool.wait_ge(consumed, c + 1)
                            nc.gpsimd.tensor_copy(idx[k][:, :], src[:, bass.ds(c * CHUNK, CHUNK)]).then_inc(copied, 1)
                            pool.wait_ge(copied, c + 1)
                            nc.gpsimd.tensor_tensor(gate[:, 0:1], gate[:, 1:2], gate[:, 2:3], ALU.add)
                            for j in range(CHUNK):
                                nc.gpsimd.indirect_dma_start(out=got[k][:, j, :], out_offset=None, in_=node_tbl,
                                                             in_offset=Off(ap=idx[k][:, j:j + 1], axis=0),
                                                             bounds_check=NODES - 1, oob_is_err=False).then_inc(gathered[k], 16)

                @block.scalar
                def _(act):
                    nc.scalar.preload_act_table_set("natural_log_exp_and_others")
                    with act.Fori(0, CHUNKS) as c:
                        act.wait_ge(link, DVE_STEPS.after("w0", c))
                        nc.scalar.activation(w[:, :, :], w[:, :, :], ACT.Exp).then_inc(exps, 1)
                        act.wait_ge(link, DVE_STEPS.after("r1", c))
                        nc.scalar.activation(r[:, :, :], r[:, :, :], ACT.Exp).then_inc(exps, 1)

                @block.vector
                def _(dve):
                    V = nc.vector
                    dve.wait_ge(loaded, 64)
                    V.memset(m[:, :, 0:1], -BIG).then_inc(link, 1)
                    V.memset(state[:, :], 0.0).then_inc(consumed, 2)
                    dve.wait_ge(link, 1)
                    dve.wait_ge(consumed, 2)
                    with dve.Fori(0, CHUNKS // 2) as pair:
                        for k in range(2):
                            c = pair * 2 + k
                            cols = bass.ds(c * CHUNK, CHUNK)

                            def own(name):
                                dve.wait_ge(link, DVE_STEPS.after(name, c))

                            for h in range(HEADS_G):
                                V.tensor_tensor_scan(ad[:, h, :], keep[:, cols], tgt[:, cols, h:h + 1].rearrange("p c o -> p (c o)"),
                                                     ad0[:, h:h + 1], ALU.mult, ALU.add).then_inc(link, 1)
                            own("t4")
                            V.tensor_copy(ad0[:, :], ad[:, :, CHUNK - 1]).then_inc(link, 1)
                            dve.wait_ge(gathered[k], pair * (16 * CHUNK) + 16 * CHUNK)
                            V.tensor_tensor(e[:, :, :], ad[:, :, :], got[k][:, :, HE:ROW_T].rearrange("p c h -> p h c"),
                                            ALU.add).then_inc(link, 1)
                            own("e")
                            V.scalar_tensor_tensor(e[:, :, :], e[:, :, :], 0.2, e[:, :, :], ALU.mult, ALU.max).then_inc(link, 1)
                            own("leaky")
                            for h in range(HEADS_G):
                                V.tensor_tensor_scan(m[:, h, 1:CHUNK + 1], pen[:, cols], e[:, h, :],
                                                     m[:, h, 0:1], ALU.add, ALU.max).then_inc(link, 1)
                            own("m4")
                            V.tensor_tensor(w[:, :, :], e[:, :, :], m[:, :, 1:CHUNK + 1], ALU.subtract).then_inc(link, 1)
                            V.tensor_tensor(r[:, :, :], m[:, :, 0:CHUNK],
                                            pen[:, cols].unsqueeze(1).broadcast_to([P, HEADS_G, CHUNK]), ALU.add).then_inc(link, 1)
                            own("r0")
                            V.tensor_tensor(r[:, :, :], r[:, :, :], m[:, :, 1:CHUNK + 1], ALU.subtract).then_inc(link, 1)
                            dve.wait_ge(exps, c * 2 + 2)
                            dve.wait_ge(written[k], pair * 16 + 16)
                            for h in range(HEADS_G):
                                V.tensor_tensor_scan(out[k][:, :, HEADS_G + h], r[:, h, :], w[:, h, :],
                                                     state[:, HEADS_G + h:HEADS_G + h + 1], ALU.mult, ALU.add).then_inc(link, 1)
                            V.tensor_tensor(msg[:, :, :].rearrange("p (h e) c -> p h e c", h=HEADS_G),
                                            got[k][:, :, 0:HE].rearrange("p c (h e) -> p h e c", h=HEADS_G),
                                            w[:, :, :].unsqueeze(2).broadcast_to([P, HEADS_G, GATES, CHUNK]), ALU.mult).then_inc(link, 1)
                            own("msg")
                            for f in range(HE):
                                V.tensor_tensor_scan(out[k][:, :, 2 * HEADS_G + f], r[:, f // GATES, :], msg[:, f, :],
                                                     state[:, 2 * HEADS_G + f:2 * HEADS_G + f + 1],
                                                     ALU.mult, ALU.add).then_inc(link, 1)
                            V.tensor_copy(out[k][:, :, 0:HEADS_G].rearrange("p c h -> p h c"), m[:, :, 1:CHUNK + 1]).then_inc(link, 1)
                            own("mcopy")
                            V.tensor_copy(m[:, :, 0:1], m[:, :, CHUNK:CHUNK + 1]).then_inc(link, 1)
                            V.tensor_copy(state[:, :], out[k][:, CHUNK - 1, :]).then_inc(link, 1)
                            own("skeep")
                            V.tensor_copy(done[:, 0:1], state[:, 0:1]).then_inc(consumed, 1)
                            dve.wait_ge(consumed, c + 3)

        with ExitStack() as ctx:
            def sb(name, shape, dt=fp32):
                return ctx.enter_context(nc.sbuf_tensor("k_" + name, shape, dt))

            def sem(name):
                return ctx.enter_context(nc.semaphore("k_" + name))

            con = sb("con", [P, K_COLS])
            whole_run = sb("whole_run", [P, 2])
            wide = sb("wide", [P, 4, HE])
            line, prev = sb("line", [HE, 4, P]), sb("prev", [HE, P])
            grow, wt = sb("grow", [HE, P]), sb("wt", [HE, P])
            shifted = sb("shifted", [HE, 3, P])
            back = sb("back", [P, ROW_O])
            ps = ctx.enter_context(nc.psum_tensor("k_ps", [P, HALF], fp32))
            ps2 = ctx.enter_context(nc.psum_tensor("k_ps2", [P, HALF], fp32))
            loaded, link, pe_done, exp_done, out_done = sem("loaded"), sem("link"), sem("pe"), sem("exp"), sem("out")
            exp_in = sem("exp_in")

            with nc.Block() as block:
                WIDE, EXPS, SHIFTED, LAST = 4, 11, 18, 21

                @block.sync
                def _(sp):
                    sp.dma_start(con[:, :], x["consts"]).then_inc(loaded, 16)
                    sp.dma_start(whole_run[:, :], x["first"][:, ECOLS - 2:ECOLS]).then_inc(loaded, 16)
                    sp.wait_ge(link, LAST)
                    sp.dma_start(carry_tbl, back[:, :]).then_inc(out_done, 16)
                    sp.wait_ge(out_done, 16)

                @block.tensor
                def _(pe):
                    pe.wait_ge(loaded, 32)
                    pe.wait_ge(link, WIDE)
                    for q in range(4):
                        last = nc.tensor.transpose(ps[0:HE, q * P:(q + 1) * P], wide[:, q, :], con[:, K_ID:K_ID + P])
                    last.then_inc(pe_done, 1)
                    pe.wait_ge(link, SHIFTED)
                    for q in range(3):
                        last = nc.tensor.transpose(ps2[:, q * HE:(q + 1) * HE], shifted[:, q, :], con[0:HE, K_ID:K_ID + HE])
                    last.then_inc(pe_done, 1)

                @block.scalar
                def _(act):
                    act.wait_ge(link, EXPS)
                    nc.scalar.activation(grow[:, :], grow[:, :], ACT.Exp).then_inc(exp_done, 1)
                    nc.scalar.activation(wt[:, :], wt[:, :], ACT.Exp).then_inc(exp_done, 1)

                @block.vector
                def _(dve):
                    V = nc.vector
                    count = [0]

                    def link_(ins):
                        ins.then_inc(link, 1)
                        count[0] += 1
                        dve.wait_ge(link, count[0])

                    def spread(a):
                        return a.unsqueeze(2).broadcast_to([P, HEADS_G, GATES])

                    def q4(q):
                        return wide[:, q, :].rearrange("p (h e) -> p h e", h=HEADS_G)

                    dve.wait_ge(loaded, 32)
                    link_(V.tensor_copy(wide[:, 0, :], whole_run[:, 1:2].broadcast_to([P, HE])))
                    link_(V.tensor_copy(q4(1), spread(state[:, 0:HEADS_G])))
                    link_(V.tensor_copy(q4(2), spread(state[:, HEADS_G:2 * HEADS_G])))
                    link_(V.tensor_copy(wide[:, 3, :], state[:, 2 * HEADS_G:ROW_O]))
                    assert count[0] == WIDE
                    dve.wait_ge(pe_done, 1)
                    link_(V.tensor_copy(line[:, :, :], ps[0:HE, :].rearrange("p (q c) -> p q c", q=4)))
                    link_(V.tensor_scalar(line[:, 0, :], line[:, 0, :], 1.0, BIG, ALU.subtract, ALU.mult))
                    link_(V.tensor_tensor_scan(shifted[:, 0, :], line[:, 0, :], line[:, 1, :], -BIG, ALU.add, ALU.max))
                    link_(V.memset(prev[:, 0:1], -BIG))
                    link_(V.tensor_copy(prev[:, 1:P], shifted[:, 0, 0:P - 1]))
                    link_(V.tensor_tensor(grow[:, :], prev[:, :], line[:, 0, :], ALU.add))
                    V.tensor_tensor(wt[:, :], line[:, 1, :], shifted[:, 0, :], ALU.subtract).then_inc(exp_in, 1)
                    dve.wait_ge(exp_in, 1)
                    link_(V.tensor_tensor(grow[:, :], grow[:, :], shifted[:, 0, :], ALU.subtract))
                    assert count[0] == EXPS
                    dve.wait_ge(exp_done, 2)
                    link_(V.tensor_tensor(line[:, 2, :], line[:, 2, :], wt[:, :], ALU.mult))
                    link_(V.tensor_tensor(line[:, 3, :], line[:, 3, :], wt[:, :], ALU.mult))
                    link_(V.memset(shifted[:, 1:3, 0:1], 0.0))
                    link_(V.tensor_tensor_scan(shifted[:, 1, 1:P], grow[:, 0:P - 1], line[:, 2, 0:P - 1], 0.0, ALU.mult, ALU.add))
                    link_(V.tensor_tensor_scan(shifted[:, 2, 1:P], grow[:, 0:P - 1], line[:, 3, 0:P - 1], 0.0, ALU.mult, ALU.add))
                    link_(V.tensor_copy(shifted[:, 0, :], prev[:, :]))
                    link_(V.memset(line[:, 0, 0:1], 0.0))
                    assert count[0] == SHIFTED
                    dve.wait_ge(pe_done, 2)

                    def head(q):
                        return ps2[:, q * HE:(q + 1) * HE].rearrange("p (h e) -> p h e", h=HEADS_G)[:, :, 0]

                    link_(V.tensor_copy(back[:, 0:HEADS_G], head(0)))
                    link_(V.tensor_copy(back[:, HEADS_G:2 * HEADS_G], head(1)))
                    link_(V.tensor_copy(back[:, 2 * HEADS_G:ROW_O], ps2[:, 2 * HE:3 * HE]))
                    assert count[0] == LAST

        with ExitStack() as ctx:
            def sb(name, shape, dt=fp32):
                return ctx.enter_context(nc.sbuf_tensor("j_" + name, shape, dt))

            def sem(name):
                return ctx.enter_context(nc.semaphore("j_" + name))

            near, far = sb("near", [P, TILES, ROW_O]), sb("far", [P, TILES, ROW_O])
            H4, H16 = [P, TILES, HEADS_G], [P, TILES, HE]
            es, top = sb("es", H4), sb("top", H4)
            wts = sb("wts", [P, 3, TILES, HEADS_G])
            den, tmp4 = sb("den", H4), sb("tmp4", H4)
            agg, tmp = sb("agg", H16), sb("tmp", H16)
            mean, rstd = sb("mean", [P, TILES]), sb("rstd", [P, TILES])
            eps = sb("eps", [P, 1])
            set_, link, taken, exps = sem("set"), sem("link"), sem("taken"), sem("exps")

            with nc.Block() as block:
                VAR = 25

                @block.gpsimd
                def _(pool):
                    G = nc.gpsimd
                    for t in (near, far):
                        G.memset(t[:, :, 0:HEADS_G], -BIG).then_inc(set_, 1)
                        G.memset(t[:, :, HEADS_G:ROW_O], 0.0).then_inc(set_, 1)
                    G.memset(eps[:, :], 1e-5).then_inc(set_, 1)
                    pool.wait_ge(set_, 5)
                    for i in range(TILES):
                        G.indirect_dma_start(out=near[:, i, :], out_offset=None, in_=edge_tbl,
                                             in_offset=Off(ap=end_idx[:, i:i + 1], axis=0),
                                             bounds_check=EDGES - 1, oob_is_err=False).then_inc(taken, 16)
                        G.indirect_dma_start(out=far[:, i, :], out_offset=None, in_=carry_tbl,
                                             in_offset=Off(ap=carry_idx[:, i:i + 1], axis=0),
                                             bounds_check=P - 1, oob_is_err=False).then_inc(taken, 16)

                @block.scalar
                def _(act):
                    nc.scalar.preload_act_table_set("natural_log_exp_and_others")
                    act.wait_ge(link, 7)
                    nc.scalar.activation(whole(wts), whole(wts), ACT.Exp).then_inc(exps, 1)
                    act.wait_ge(link, VAR)
                    nc.scalar.activation(rstd[:, :], rstd[:, :], ACT.Ln, bias=eps[:, :], scale=1.0 / HE).then_inc(exps, 1)
                    act.wait_ge(exps, 2)
                    nc.scalar.activation(rstd[:, :], rstd[:, :], ACT.Exp, scale=-0.5).then_inc(exps, 1)

                @block.vector
                def _(dve):
                    V = nc.vector
                    TT = V.tensor_tensor
                    count = [0]

                    def link_(ins):
                        ins.then_inc(link, 1)
                        count[0] += 1
                        dve.wait_ge(link, count[0])

                    def spread(a):
                        return a.unsqueeze(3).broadcast_to([P, TILES, HEADS_G, GATES])

                    def heads(a):
                        return a.rearrange("p i (h e) -> p i h e", h=HEADS_G)

                    def vec(at):
                        return att[:, at * HE:(at + 1) * HE].unsqueeze(1).broadcast_to(H16)

                    NM, NS, NF = slice(0, HEADS_G), slice(HEADS_G, 2 * HEADS_G), slice(2 * HEADS_G, ROW_O)
                    dve.wait_ge(set_, 5)
                    link_(TT(whole(es), row[:, :, HE:ROW_T], whole(adst), ALU.add))
                    link_(V.scalar_tensor_tensor(whole(es), whole(es), 0.2, whole(es), ALU.mult, ALU.max))
                    dve.wait_ge(taken, 16 * 2 * TILES)
                    link_(TT(whole(top), near[:, :, NM], far[:, :, NM], ALU.max))
                    link_(TT(whole(top), whole(top), whole(es), ALU.max))
                    link_(TT(wts[:, 0, :, :], near[:, :, NM], whole(top), ALU.subtract))
                    link_(TT(wts[:, 1, :, :], far[:, :, NM], whole(top), ALU.subtract))
                    link_(TT(wts[:, 2, :, :], whole(es), whole(top), ALU.subtract))
                    dve.wait_ge(exps, 1)
                    link_(TT(whole(den), near[:, :, NS], wts[:, 0, :, :], ALU.mult))
                    link_(TT(whole(tmp4), far[:, :, NS], wts[:, 1, :, :], ALU.mult))
                    link_(TT(whole(den), whole(den), whole(tmp4), ALU.add))
                    link_(TT(whole(den), whole(den), wts[:, 2, :, :], ALU.add))
                    link_(V.tensor_scalar_add(whole(den), whole(den), 1e-16))
                    link_(V.reciprocal(whole(den), whole(den)))
                    link_(TT(heads(whole(agg)), heads(near[:, :, NF]), spread(wts[:, 0, :, :]), ALU.mult))
                    link_(TT(heads(whole(tmp)), heads(far[:, :, NF]), spread(wts[:, 1, :, :]), ALU.mult))
                    link_(TT(whole(agg), whole(agg), whole(tmp), ALU.add))
                    link_(TT(heads(whole(tmp)), heads(row[:, :, 0:HE]), spread(wts[:, 2, :, :]), ALU.mult))
                    link_(TT(whole(agg), whole(agg), whole(tmp), ALU.add))
                    link_(TT(heads(whole(agg)), heads(whole(agg)), spread(whole(den)), ALU.mult))
                    link_(TT(whole(agg), whole(agg), vec(2), ALU.add))
                    link_(V.reduce_sum(mean[:, :], whole(agg), AX))
                    link_(V.tensor_scalar(mean[:, :], mean[:, :], 1.0 / HE, None, ALU.mult))
                    link_(TT(whole(agg), whole(agg), mean[:, :].unsqueeze(2).broadcast_to(H16), ALU.subtract))
                    link_(TT(whole(tmp), whole(agg), whole(agg), ALU.mult))
                    link_(V.reduce_sum(rstd[:, :], whole(tmp), AX))
                    assert count[0] == VAR
                    dve.wait_ge(exps, 3)
                    link_(TT(whole(agg), whole(agg), rstd[:, :].unsqueeze(2).broadcast_to(H16), ALU.mult))
                    link_(TT(whole(agg), whole(agg), vec(3), ALU.mult))
                    link_(TT(whole(agg), whole(agg), vec(4), ALU.add))
                    link_(V.tensor_reduce(whole(scores), agg[:, :, :].rearrange("p i (h e) -> p i e h", h=HEADS_G), AX, ALU.add))
                    link_(V.tensor_scalar(whole(scores), whole(scores), 1.0 / HEADS_G, None, ALU.mult))
def _blocks(w):
    import numpy as np
    out = np.zeros(w.shape[:-2] + (2 * w.shape[-2], 2 * w.shape[-1]), w.dtype)
    out[..., :w.shape[-2], :w.shape[-1]] = w
    out[..., w.shape[-2]:, w.shape[-1]:] = w
    return out


def _ssm_parameters(inp):
    import numpy as np
    T = lambda a: np.swapaxes(a, -1, -2)
    out = np.zeros((LAYERS, P, W_COLS), np.float32)
    out[:, :, W_PROJ:W_PROJ + P] = _blocks(T(inp["L0_conv_proj_w"]))
    out[:, :, W_CF:W_CF + P] = _blocks(T(inp["L0_conv_convf_w"]))
    out[:, :, W_CB:W_CB + P] = _blocks(T(inp["L0_conv_convb_w"]))
    dbc = inp["L0_conv_dbc_w"]
    out[:, :, W_DL:W_DL + 2 * RANK] = _blocks(T(dbc[:, :RANK]))
    for part in range(3):
        out[:, :, W_B + 32 * part:W_B + 32 * part + 32] = _blocks(T(dbc[:, RANK:RANK + NST]))
        out[:, :, W_C + 32 * part:W_C + 32 * part + 32] = _blocks(T(dbc[:, RANK + NST:]))
    out[:, :2 * RANK, W_DT:W_DT + P] = _blocks(T(inp["L0_conv_dtp_w"]))
    d2 = np.concatenate([inp["L0_conv_D_param"]] * 2, 1)
    out[:, np.arange(P), W_D + np.arange(P)] = d2
    for col, name in ((V_G, "ln_g"), (V_LB, "ln_b"), (V_PB, "proj_b"), (V_CFB, "convf_b"), (V_CBB, "convb_b"), (V_DTB, "dtp_b")):
        out[:, :, col] = np.concatenate([inp["L0_conv_" + name]] * 2, 1)
    out[:, :, V_ALOG:V_ALOG + NST] = np.concatenate([inp["L0_conv_A_log"]] * 2, 1)
    return out


def _constants():
    import numpy as np
    k = np.zeros((P, K_COLS), np.float32)
    row = np.arange(P)
    k[:, K_MEAN:K_MEAN + P] = (row[:, None] // C == row[None, :] // C) / np.float32(C)
    k[:, K_ID:K_ID + P] = np.eye(P)
    k[:, K_PAIR:K_PAIR + P] = (row[:, None] // 2 == row[None, :] // 2) / np.float32(2)
    k[:, K_ONE:K_ONE + P] = 1
    k[:, K_SPLIT] = np.where(row >= 32, -1, 0)
    k[:, K_SPLIT + 1] = np.where(row >= 64, -1, 0)
    k[:, K_SPLIT + 2] = 1e-5
    sign = lambda bit: 1 - 2 * ((row >> bit) & 1)
    k[:, K_SIGN], k[:, K_SIGN + 1] = sign(0), -sign(0)
    for b in range(1, 7):
        k[:, K_SIGN + 1 + b] = sign(b) * sign(b - 1)
    k[:, K_SIGN + 8] = sign(6)
    k[:, K_MASK:K_MASK + 64] = row[:, None] // 32 == np.arange(64)[None, :] // 16
    return k


def _selectors():
    import numpy as np
    k = np.arange(96)[:, None, None] % 32
    n = np.arange(NST)[None, :, None]
    m = np.arange(P)[None, None, :]
    return (k == (m // C) * NST + n).astype(np.float32).reshape(96, NST * P)


def _conv_weights(inp):
    import numpy as np
    out = np.zeros((P, CW_COLS), np.float32)
    tap = lambda w: w.transpose(2, 3, 1, 0).reshape(9, C, w.shape[0])
    for col, w in ((CW_Q, inp["L1_conv_wq"]), (CW_K, inp["L1_conv_wk"])):
        padded = np.zeros((9, C, 32), np.float32)
        padded[:, :, :C // 4] = tap(w)
        out[:, col:col + 9 * Q_COLS] = _blocks(padded).transpose(1, 0, 2).reshape(P, -1)
    out[:, CW_V:CW_V + 9 * P] = _blocks(tap(inp["L1_conv_wv"])).transpose(1, 0, 2).reshape(P, -1)
    out[:, CW_FC1:CW_FC1 + 8] = _blocks(inp["L1_conv_fc1_w"].T)
    out[:8, CW_FC2:CW_FC2 + P] = _blocks(inp["L1_conv_fc2_w"].T)
    fuse = inp["L1_conv_fuse_w"][:, :, 0, 0].T
    out[:C, CW_FL:CW_FL + C] = fuse[:C]
    out[:C, CW_FG:CW_FG + C] = out[C:, CW_FG:CW_FG + C] = fuse[C:]
    for b in range(2):
        out[32 * b:32 * b + 16, CV_BQ] = inp["L1_conv_bq"]
        out[32 * b:32 * b + 16, CV_BK] = inp["L1_conv_bk"]
        out[4 * b:4 * b + 4, CV_B1] = inp["L1_conv_fc1_b"]
        out[C * b:C * (b + 1), CV_B2] = inp["L1_conv_fc2_b"]
    out[:, CV_BV] = np.concatenate([inp["L1_conv_bv"]] * 2)
    out[:, CR_FB:CR_FB + C] = inp["L1_conv_fuse_b"][None]
    return out


def _padded_heads(w):
    import numpy as np
    out = np.zeros((C, HEADS2, 32), np.float32)
    out[:, :, :HDIM2] = w.reshape(C, HEADS2, HDIM2)
    return out.reshape(C, P)


def _slice_weights(inp):
    import numpy as np
    out = np.zeros((P, SW_COLS), np.float32)
    out[:C, SW_0:SW_0 + C] = inp["L3_attn_W0"]
    out[:C, SW_S:SW_S + SLICES] = inp["L3_attn_Ws"]
    out[:C, SW_QKV:SW_QKV + 3 * HD3] = inp["L3_attn_Wqkv"]
    out[C, SW_QKV:SW_QKV + 3 * HD3] = inp["L3_attn_bqkv"]
    out[:, SW_OUT:SW_OUT + 2 * C] = inp["L3_attn_Wout"].reshape(2, P, C).transpose(1, 0, 2).reshape(P, 2 * C)
    out[:C, SV_B0] = inp["L3_attn_b0"]
    out[:, SR_B0:SR_B0 + C] = inp["L3_attn_b0"][None]
    out[:, SR_BS:SR_BS + SLICES] = inp["L3_attn_bs"][None]
    out[:, SR_BO:SR_BO + C] = inp["L3_attn_bout"][None]
    return out


def _graph_vectors(inp):
    import numpy as np
    row = np.concatenate([inp["L2_ffn_" + n].reshape(-1) for n in ("att_src", "att_dst", "b_gat", "ln_gamma", "ln_beta")])
    return np.ascontiguousarray(np.broadcast_to(row[None], (P, row.size)))
def build(nc, a, out):
    from concourse import mybir
    fp32 = mybir.dt.float32
    con = a["consts"]
    tables = graph_tables(nc)
    sort_stage(nc, a["edges"], con, *[tables[n] for n in ("src", "keep", "pen", "first", "ends_i", "place_i", "target0")])
    with nc.sbuf_tensor("t_sb", [P, TILES, C], fp32) as t_sb:
        with nc.sbuf_tensor("x_sb", [P, PAIRS, L], fp32) as x_sb:
            ssm_stage(nc, a["x"], a["ssm"], con, a["selectors"], x_sb, tables)
            conv_stage(nc, a["conv"], con, x_sb, t_sb)
        with nc.sbuf_tensor("tn_sb", [P, TILES, C], fp32) as tn_sb:
            norm_stage(nc, con, t_sb, tn_sb, "n1")
            graph_attn_stage(nc, a["attn_padded"], a["attn"], con, tn_sb, t_sb)
            norm_stage(nc, con, t_sb, tn_sb, "n2")
            with (nc.sbuf_tensor("tnT_a", [C, TOK], fp32) as tnT_sb,
                  nc.sbuf_tensor("gates_a", [P, TILES, GATES], fp32) as gates,
                  nc.sbuf_tensor("feat", [P, TILES, HE], fp32) as feat):
                project_stage(nc, a["gat"], a["gat_bias"], con, tn_sb, tnT_sb, feat, "pa")
                graph_stage(nc, a["gat_vectors"], feat, tables, dict(tables, scores=gates, consts=con))
                top2_stage(nc, gates, "ta")
                expert_stage(nc, a["moe2_in"], None, a["moe2_out"], a["moe2_b1"], a["moe2_b2"], gates, tnT_sb, t_sb, "ea")
            norm_stage(nc, con, t_sb, tn_sb, "n3")
            slice_attn_stage(nc, a["slice"], con, tn_sb, t_sb)
            norm_stage(nc, con, t_sb, tn_sb, "n4")
            with (nc.sbuf_tensor("tnT_b", [C, TOK], fp32) as tnT_sb,
                  nc.sbuf_tensor("gates_b", [P, TILES, EXPERTS], fp32) as gates):
                project_stage(nc, a["gate_w"], a["gate_b"], con, tn_sb, tnT_sb, gates, "pb")
                top2_stage(nc, gates, "tb")
                expert_stage(nc, a["moe3_in"], a["moe3_gate"], a["moe3_out"], None, None, gates, tnT_sb, t_sb, "eb")
        with nc.semaphore("written_out") as written_out, nc.Block() as block:
            @block.sync
            def _(sp):
                sp.dma_start(out, t_sb[:, :, :]).then_inc(written_out, 16)
                sp.wait_ge(written_out, 16)


def kernel(**inputs):
    import numpy as np
    import concourse.bacc as bacc
    from concourse import mybir
    from concourse.bass_utils import run_bass_kernel_spmd

    inp = {k: np.asarray(v) for k, v in inputs.items()}
    flat = np.ascontiguousarray

    def rows(v):
        return flat(np.broadcast_to(v[None], (P,) + v.shape))

    arrays = {
        "x": flat(inp["x"].reshape(PAIRS, P, L).transpose(1, 0, 2)),
        "edges": flat(inp["L2_ffn_edge_index"].reshape(2, P, ECOLS)),
        "consts": _constants(), "selectors": _selectors(),
        "ssm": _ssm_parameters(inp), "conv": _conv_weights(inp),
        "attn_padded": _padded_heads(inp["L2_attn_W"]), "attn": flat(inp["L2_attn_W"]),
        "gat": flat(inp["L2_ffn_W_gat"]), "gat_bias": np.zeros((P, HE), np.float32), "gat_vectors": _graph_vectors(inp),
        "moe2_in": flat(inp["L2_ffn_W1"].transpose(1, 0, 2)), "moe2_out": flat(inp["L2_ffn_W2"].transpose(1, 0, 2)),
        "moe2_b1": flat(inp["L2_ffn_b1"].T), "moe2_b2": rows(inp["L2_ffn_b2"]),
        "slice": _slice_weights(inp),
        "gate_w": flat(inp["L3_ffn_gate_w"]), "gate_b": rows(inp["L3_ffn_gate_b"]),
        "moe3_in": flat(inp["L3_ffn_w1"].transpose(1, 0, 2)), "moe3_gate": flat(inp["L3_ffn_w2"].transpose(1, 0, 2)),
        "moe3_out": flat(inp["L3_ffn_w3"].transpose(1, 0, 2)),
    }
    nc = bacc.Bacc("TRN2", target_bir_lowering=False, num_devices=1)
    aps = {n: nc.dram_tensor("in_" + n, a.shape, mybir.dt.from_np(a.dtype), kind="ExternalInput").ap()
           for n, a in arrays.items()}
    out = nc.dram_tensor("out", (P, TILES, C), mybir.dt.float32, kind="ExternalOutput").ap()
    build(nc, aps, out)
    result = run_bass_kernel_spmd(nc, [{"in_" + n: a for n, a in arrays.items()}], core_ids=[0])
    tokens = result.results[0]["out"].transpose(1, 0, 2).reshape(B, L, C)
    return flat(tokens.transpose(0, 2, 1)).reshape(B, C, H, W)
```

```python
P = 128
B, C, H, W = 8, 64, 32, 32
L = H * W
PAIRS = B // 2
LAYERS = 12
NST = 16
RANK = 32
HALF = 512
TOK = B * L
TILES = TOK // P
PER = L // P

W_PROJ, W_CF, W_CB = 0, 128, 256
W_B = 384
W_C = W_B + 96
W_DL = W_C + 96
W_DT = W_DL + P
V_G, V_LB, V_PB, V_CFB, V_CBB, V_DTB, V_D = range(W_DT + P, W_DT + P + 7)
V_ALOG = V_D + 1
W_COLS = V_ALOG + NST

K_MEAN, K_ID, K_PAIR, K_ONE = 0, 128, 256, 384
K_SPLIT = 512
K_MASK = 520
K_SIGN = K_MASK + 64
K_CEN = K_SIGN + 9
K_COLS = K_CEN + P


class Steps:

    def __init__(self, names):
        self.names = names.split()
        assert len(set(self.names)) == len(self.names)

    def after(self, name, turn=0):
        return turn * len(self.names) + (self.names.index(name) + 2)

    def all(self, turn):
        return turn * len(self.names) + 1


def ssm_stage(nc, x_in, params, consts, selectors, x_sb):
    import concourse.bass as bass
    from concourse import mybir
    from contextlib import ExitStack

    fp32, bf16 = mybir.dt.float32, mybir.dt.bfloat16
    ALU, ACT = mybir.AluOpType, mybir.ActivationFunctionType
    TURNS = LAYERS * PAIRS
    STEPS = 2 * NST

    pe_s = Steps("xc var fold xp cf cb dt0 B0 C0 dt1 B1 C1")
    act_s = Steps("xc sq lnv rstd xn fold A_exp A_neg xp z_abs z_relu cf_abs cf_relu cf_exp cf_ln cb_abs cb_relu cb_exp cb_ln "
                  "dt_abs0 dt_relu0 dt_exp0 dt_ln0 B_copy0 B_hi0 C_copy0 C_hi0 B_mid0 C_mid0 z_exp z_ln sig "
                  "dt_abs1 dt_relu1 dt_exp1 dt_ln1 B_copy1 B_hi1 D_us B_mid1 C_copy1 C_hi1 C_mid1")
    pool_s = Steps("xhat xf xb delta0 dx0 B_r0 C_r0 B_split0 C_split0 z_soft "
                   "z us delta1 dx1 B_r1 dz B_split1 C_r1 C_split1 xd")

    with ExitStack() as ctx:
        def sb(name, shape, dt=fp32):
            return ctx.enter_context(nc.sbuf_tensor(name, shape, dt))

        def sem(name):
            return ctx.enter_context(nc.semaphore(name))

        def two(name, shape, dt=fp32):
            return [sb(name + "_0", shape, dt), sb(name + "_1", shape, dt)]

        par = sb("par", [P, W_COLS])
        con = sb("con", [P, K_COLS])
        sel = sb("sel", [96, NST, P], bf16)
        negA, next_negA = sb("negA", [P, NST]), sb("next_negA", [P, NST])
        w_dt = sb("w_dt", [P, P])
        xc, sq, rstd, xn, xp, sig, neg, z, us, gz = (sb(n, [P, L]) for n in
                                                     ("xc", "sq", "rstd", "xn", "xp", "sig", "neg", "z", "us", "gz"))
        relu, soft = two("relu", [P, L]), two("soft", [P, L])
        start = sb("start", [P, 8])
        u, delta, dx = two("u", [P, L]), two("delta", [P, L]), two("dx", [P, L])
        B3, C3 = two("B3", [96, L], bf16), two("C3", [96, L], bf16)
        raw, hi, rest = (dict(zip("BC", two(n, [96, L], dt))) for n, dt in (("raw", fp32), ("hi", bf16), ("rest", fp32)))
        dA, dBu, hst, hC = (two(n, [P, L]) for n in ("dA", "dBu", "h", "hC"))
        pp = ctx.enter_context(nc.psum_tensor("pp", [P, L], fp32))
        y_ps = ctx.enter_context(nc.psum_tensor("y_ps", [P, L], fp32))
        B_ps = ctx.enter_context(nc.psum_tensor("B_ps", [P, L], fp32))
        C_ps = ctx.enter_context(nc.psum_tensor("C_ps", [P, L], fp32))

        loaded, par_loaded, sel_ready, started, a_ready = (
            sem(n) for n in ("loaded", "par_loaded", "sel_ready", "started", "a_ready"))
        pe_done, act_done, pool_done = sem("pe_done"), sem("act_done"), sem("pool_done")
        b_ready, c_ready, decay_ready, dbu_ready, scanned, prod_ready, y_added = (
            sem(n) for n in ("b_ready", "c_ready", "decay_ready", "dbu_ready", "scanned", "prod_ready", "y_added"))
        gated, updated, carried = sem("gated"), sem("updated"), sem("carried")

        halves = [slice(0, HALF), slice(HALF, L)]

        def vec(col):
            return par[:, col:col + 1]

        def x_of(turn):
            if isinstance(turn, int):
                return x_sb[:, turn % PAIRS, :]
            return x_sb[:, bass.ds(turn % PAIRS, 1), :].rearrange("p o t -> p (o t)")

        def par_of(turn):
            return (turn // PAIRS) * 16 + 16

        def dir_of(k):
            return (k % STEPS) // NST, k % NST

        with nc.Block() as block:
            @block.sync
            def _(sp):
                sp.dma_start(x_sb[:, :, :], x_in).then_inc(loaded, 16)
                sp.dma_start(con[:, :], consts).then_inc(loaded, 16)
                for half in range(2):
                    sp.dma_start(soft[half][0:96, :], selectors[:, half * L:(half + 1) * L]).then_inc(loaded, 16)
                sp.dma_start(par[:, :], params[0, :, :]).then_inc(par_loaded, 16)
                with sp.Fori(1, LAYERS) as layer:
                    sp.wait_ge(pe_done, pe_s.after("C1", layer * PAIRS - 1) - 1)
                    sp.wait_ge(act_done, act_s.after("D_us", layer * PAIRS - 1))
                    sp.dma_start(par[:, :], params[bass.ds(layer, 1), :, :].rearrange("o p w -> (o p) w")
                                 ).then_inc(par_loaded, 16)

            @block.tensor
            def _(pe):
                def product(lhsT, rhs):
                    for hs in halves:
                        last = nc.tensor.matmul(pp[0:lhsT.shape[1], hs], lhsT, rhs[:, hs], start=True, stop=True)
                    last.then_inc(pe_done, 1)

                def after_act(name, turn):
                    pe.wait_ge(act_done, act_s.after(name, turn))

                def after_pool(name, turn):
                    pe.wait_ge(pool_done, pool_s.after(name, turn))

                def prepare_backward(t, k):
                    if k == 1:
                        after_act("C_hi0", t)
                        after_pool("xb", t)
                        product(w_dt[:, :], u[1])
                    elif k == 3:
                        after_act("dt_relu1", t)
                        product(par[:, W_B:W_B + 96], u[1])
                    elif k == 5:
                        after_act("B_hi1", t)
                        product(par[:, W_C:W_C + 96], u[1])
                    elif k == 7:
                        after_act("C_hi1", t)

                def prepare_next(t, k):
                    if k == 7:
                        product_x(t)
                    elif k == 9:
                        after_act("sq", t)
                        product(con[:, K_MEAN:K_MEAN + P], sq)
                    elif k == 11:
                        after_act("lnv", t)
                        pe.wait_ge(par_loaded, par_of(t))
                        nc.tensor.matmul(pp[:, 0:P], par[0:2 * RANK, W_DL:W_DL + P], par[0:2 * RANK, W_DT:W_DT + P],
                                         start=True, stop=True).then_inc(pe_done, 1)
                    elif k == 14:
                        after_act("fold", t)
                        product(par[:, W_PROJ:W_PROJ + P], xn)
                    elif k == 16:
                        after_act("xp", t)
                        product(par[:, W_CF:W_CF + P], xp)
                    elif k == 18:
                        after_act("cf_relu", t)
                        product(par[:, W_CB:W_CB + P], xp)
                    elif k == 20:
                        after_act("cb_relu", t)
                        after_pool("xf", t)
                        product(w_dt[:, :], u[0])
                    elif k == 22:
                        after_act("dt_relu0", t)
                        product(par[:, W_B:W_B + 96], u[0])
                    elif k == 24:
                        after_act("B_hi0", t)
                        product(par[:, W_C:W_C + 96], u[0])

                def product_x(t):
                    for hs in halves:
                        xs = x_sb[:, t % PAIRS, hs] if isinstance(t, int) else \
                            x_sb[:, bass.ds(t % PAIRS, 1), hs].rearrange("p o t -> p (o t)")
                        last = nc.tensor.matmul(pp[:, hs], con[:, K_CEN:K_CEN + P], xs, start=True, stop=True)
                    last.then_inc(pe_done, 1)

                def copies(out, parts, k, ready):
                    d, n = dir_of(k)
                    for hs in halves:
                        last = nc.tensor.matmul(out[:, hs], sel[:, n, :], parts[d][:, hs], start=True, stop=True)
                    last.then_inc(ready, 1)

                def add_y(k):
                    for hs in halves:
                        last = nc.tensor.matmul(y_ps[:, hs], con[:, K_ID:K_ID + P], hC[k % 2][:, hs],
                                                start=(k == 0), stop=(k == STEPS - 1))
                    last.then_inc(y_added, 1)
                    return last

                def turn(it, last_turn):
                    for k in range(1, STEPS + 1):
                        s = it * STEPS + k
                        if last_turn and k == STEPS:
                            break
                        if not (last_turn and k == STEPS - 1):
                            if k == NST - 1:
                                after_pool("B_split1", it)
                            elif k == STEPS - 1:
                                after_pool("B_split0", it + 1)
                            pe.wait_ge(dbu_ready, s + 1)
                            copies(B_ps, B3, k + 1, b_ready)
                        if k == NST:
                            after_pool("C_split1", it)
                        elif k == STEPS:
                            after_pool("C_split0", it + 1)
                        pe.wait_ge(prod_ready, s)
                        copies(C_ps, C3, k, c_ready)
                        if k == 1:
                            pe.wait_ge(gated, it + 1)
                        add_y(k - 1)
                        prepare_backward(it, k)
                        if not last_turn:
                            prepare_next(it + 1, k)
                    if last_turn:
                        pe.wait_ge(prod_ready, TURNS * STEPS)
                        add_y(STEPS - 1)

                pe.wait_ge(loaded, 64)
                pe.wait_ge(sel_ready, 2)
                for k in range(1, STEPS):
                    prepare_next(0, k)
                after_pool("B_split0", 0)
                copies(B_ps, B3, 0, b_ready)
                pe.wait_ge(dbu_ready, 1)
                copies(B_ps, B3, 1, b_ready)
                after_pool("C_split0", 0)
                copies(C_ps, C3, 0, c_ready)
                with pe.Fori(0, TURNS - 1) as it:
                    turn(it, False)
                turn(TURNS - 1, True)

            @block.scalar
            def _(act):
                A = nc.scalar.activation

                def own(name, turn):
                    act.wait_ge(act_done, act_s.after(name, turn))

                def after_pe(name, turn):
                    act.wait_ge(pe_done, pe_s.after(name, turn) - 1)

                def after_pool(name, turn):
                    act.wait_ge(pool_done, pool_s.after(name, turn))

                def argument(t, name, pe_step, k, bias):
                    after_pe(pe_step, t)
                    A(soft[k][:, :], pp[:, :], ACT.Abs, bias=vec(bias)).then_inc(act_done, 1)
                    A(relu[k][:, :], pp[:, :], ACT.Relu, bias=vec(bias)).then_inc(act_done, 1)

                def logarithm(t, name, k):
                    own(name.format("abs"), t)
                    A(soft[k][:, :], soft[k][:, :], ACT.Exp, scale=-1.0).then_inc(act_done, 1)
                    own(name.format("exp"), t)
                    A(soft[k][:, :], soft[k][:, :], ACT.Ln, bias=con[:, K_ONE:K_ONE + 1]).then_inc(act_done, 1)

                def first_part(t, name, d):
                    after_pe(f"{name}{d}", t)
                    A(raw[name][:, :], pp[0:96, :], ACT.Copy).then_inc(act_done, 1)
                    A(hi[name][:, :], pp[0:96, :], ACT.Identity, scale=con[0:96, K_SPLIT:K_SPLIT + 1]).then_inc(act_done, 1)

                def second_part(t, name, d):
                    after_pool(f"{name}_r{d}", t)
                    A(hi[name][:, :], rest[name][:, :], ACT.Identity, scale=con[0:96, K_SPLIT + 1:K_SPLIT + 2]).then_inc(act_done, 1)

                def prepare_backward(t, k):
                    if k == 2:
                        argument(t, "dt_{}1", "dt1", 1, V_DTB)
                    elif k == 3:
                        logarithm(t, "dt_{}1", 1)
                    elif k == 4:
                        first_part(t, "B", 1)
                        after_pool("us", t)
                        A(us[:, :], us[:, :], ACT.Identity, scale=vec(V_D)).then_inc(act_done, 1)
                    elif k == 6:
                        second_part(t, "B", 1)
                        first_part(t, "C", 1)
                    elif k == 8:
                        second_part(t, "C", 1)

                def prepare_next(t, k):
                    if k == 8:
                        after_pe("xc", t)
                        A(xc[:, :], pp[:, :], ACT.Copy).then_inc(act_done, 1)
                        A(sq[:, :], pp[:, :], ACT.Square).then_inc(act_done, 1)
                    elif k == 10:
                        after_pe("var", t)
                        A(rstd[:, :], pp[:, :], ACT.Ln, bias=con[:, K_SPLIT + 2:K_SPLIT + 3]).then_inc(act_done, 1)
                        own("lnv", t)
                        A(rstd[:, :], rstd[:, :], ACT.Exp, scale=-0.5).then_inc(act_done, 1)
                    elif k == 13:
                        after_pool("xhat", t)
                        act.wait_ge(par_loaded, par_of(t))
                        A(xn[:, :], xn[:, :], ACT.Identity, bias=vec(V_LB), scale=vec(V_G)).then_inc(act_done, 1)
                        after_pe("fold", t)
                        A(w_dt[:, :], pp[:, 0:P], ACT.Copy).then_inc(act_done, 1)
                        A(next_negA[:, :], par[:, V_ALOG:V_ALOG + NST], ACT.Exp).then_inc(act_done, 1)
                    elif k == 14:
                        own("A_exp", t)
                        A(next_negA[:, :], next_negA[:, :], ACT.Copy, scale=-1.0).then_inc(act_done, 1)
                    elif k == 15:
                        after_pe("xp", t)
                        A(xp[:, :], pp[:, :], ACT.Identity, bias=vec(V_PB)).then_inc(act_done, 1)
                        own("xp", t)
                        A(sig[:, :], xp[:, :], ACT.Abs).then_inc(act_done, 1)
                        A(neg[:, :], xp[:, :], ACT.Relu, scale=-1.0).then_inc(act_done, 1)
                    elif k == 17:
                        argument(t, "cf_{}", "cf", 0, V_CFB)
                    elif k == 18:
                        logarithm(t, "cf_{}", 0)
                    elif k == 19:
                        argument(t, "cb_{}", "cb", 1, V_CBB)
                    elif k == 20:
                        logarithm(t, "cb_{}", 1)
                    elif k == 21:
                        after_pool("xf", t)
                        argument(t, "dt_{}0", "dt0", 0, V_DTB)
                    elif k == 22:
                        logarithm(t, "dt_{}0", 0)
                    elif k == 23:
                        first_part(t, "B", 0)
                    elif k == 25:
                        first_part(t, "C", 0)
                    elif k == 26:
                        second_part(t, "B", 0)
                    elif k == 27:
                        second_part(t, "C", 0)
                    elif k == 28:
                        A(sig[:, :], sig[:, :], ACT.Exp, scale=-1.0).then_inc(act_done, 1)
                        own("z_exp", t)
                        A(sig[:, :], sig[:, :], ACT.Ln, bias=con[:, K_ONE:K_ONE + 1]).then_inc(act_done, 1)
                    elif k == 30:
                        after_pool("z_soft", t)
                        A(sig[:, :], sig[:, :], ACT.Exp, scale=-1.0).then_inc(act_done, 1)

                def decay(k):
                    d, n = dir_of(k)
                    A(dA[k % 2][:, :], delta[d][:, :], ACT.Exp, scale=negA[:, n:n + 1]).then_inc(decay_ready, 1)

                def turn(it, last_turn):
                    for k in range(1, STEPS + 1):
                        s = it * STEPS + k
                        if last_turn and k >= STEPS - 1:
                            break
                        if k == NST - 1:
                            after_pool("delta1", it)
                        elif k == STEPS - 1:
                            act.wait_ge(decay_ready, s + 1)
                            A(negA[:, :], next_negA[:, :], ACT.Copy).then_inc(a_ready, 1)
                            act.wait_ge(a_ready, it + 2)
                            after_pool("delta0", it + 1)
                        act.wait_ge(scanned, s)
                        decay(k + 1)
                        prepare_backward(it, k)
                        if not last_turn:
                            prepare_next(it + 1, k)

                nc.scalar.preload_act_table_set("natural_log_exp_and_others")
                act.wait_ge(loaded, 64)
                for half in range(2):
                    A(sel[:, half * (NST // 2):(half + 1) * (NST // 2), :],
                      soft[half][0:96, :].rearrange("k (n m) -> k n m", n=NST // 2), ACT.Copy).then_inc(sel_ready, 1)
                act.wait_ge(sel_ready, 2)
                A(start[:, 0:1], con[:, 0:1], ACT.Copy).then_inc(act_done, 1)
                for k in range(1, STEPS):
                    prepare_next(0, k)
                own("A_neg", 0)
                A(negA[:, :], next_negA[:, :], ACT.Copy).then_inc(a_ready, 1)
                act.wait_ge(a_ready, 1)
                after_pool("delta0", 0)
                decay(0)
                decay(1)
                with act.Fori(0, TURNS - 1) as it:
                    turn(it, False)
                turn(TURNS - 1, True)

            @block.gpsimd
            def _(pool):
                G = nc.gpsimd

                def after_act(name, turn):
                    pool.wait_ge(act_done, act_s.after(name, turn))

                def own(name, turn):
                    pool.wait_ge(pool_done, pool_s.after(name, turn))

                def done(ins):
                    ins.then_inc(pool_done, 1)

                def carry_waits():
                    G.tensor_tensor(start[:, 5:6], start[:, 6:7], start[:, 7:8], ALU.add)

                def softplus(out, t, act_step, k):
                    after_act(act_step, t)
                    done(G.tensor_tensor(out[:, :], relu[k][:, :], soft[k][:, :], ALU.add))

                def remainder(t, name, d):
                    after_act(f"{name}_hi{d}", t)
                    done(G.tensor_tensor(rest[name][:, :], raw[name][:, :], hi[name][:, :], ALU.add))

                def split(t, name, d):
                    after_act(f"{name}_mid{d}", t)
                    done(G.tensor_tensor({"B": B3, "C": C3}[name][d][:, :], rest[name][:, :], hi[name][:, :], ALU.add))

                def prepare_backward(t, k):
                    if k == 2:
                        pool.wait_ge(gated, t + 1)
                        after_act("sig", t)
                        done(G.tensor_tensor(z[:, :], xp[:, :], sig[:, :], ALU.mult))
                    elif k == 3:
                        done(G.tensor_tensor(us[:, :], u[0][:, :], u[1][:, :], ALU.add))
                    elif k == 4:
                        pool.wait_ge(decay_ready, t * STEPS + 1)
                        softplus(delta[1], t, "dt_ln1", 1)
                    elif k == 5:
                        own("delta1", t)
                        pool.wait_ge(dbu_ready, t * STEPS + 1)
                        done(G.tensor_tensor(dx[1][:, :], delta[1][:, :], u[1][:, :], ALU.mult))
                        remainder(t, "B", 1)
                        after_act("D_us", t)
                        done(G.tensor_tensor(us[:, :], us[:, :], z[:, :], ALU.mult))
                    elif k == 7:
                        pool.wait_ge(b_ready, t * STEPS + 1)
                        split(t, "B", 1)
                        remainder(t, "C", 1)
                    elif k == 9:
                        pool.wait_ge(c_ready, t * STEPS + 1)
                        split(t, "C", 1)
                    elif k == 10:
                        own("dz", t)
                        carry_waits()
                        done(G.tensor_tensor(x_of(t), x_of(t), us[:, :], ALU.add))

                def prepare_next(t, k, running=True):
                    def read_by_forward(sem_):
                        if running:
                            pool.wait_ge(sem_, (t - 1) * STEPS + NST)

                    if k == 12:
                        after_act("rstd", t)
                        done(G.tensor_tensor(xn[:, :], xc[:, :], rstd[:, :], ALU.mult))
                    elif k == 19:
                        softplus(u[0], t, "cf_ln", 0)
                    elif k == 21:
                        softplus(u[1], t, "cb_ln", 1)
                    elif k == 23:
                        read_by_forward(decay_ready)
                        softplus(delta[0], t, "dt_ln0", 0)
                    elif k == 24:
                        own("delta0", t)
                        read_by_forward(dbu_ready)
                        done(G.tensor_tensor(dx[0][:, :], delta[0][:, :], u[0][:, :], ALU.mult))
                    elif k == 25:
                        remainder(t, "B", 0)
                    elif k == 26:
                        remainder(t, "C", 0)
                    elif k == 27:
                        read_by_forward(b_ready)
                        split(t, "B", 0)
                    elif k == 28:
                        read_by_forward(c_ready)
                        split(t, "C", 0)
                    elif k == 29:
                        after_act("z_ln", t)
                        done(G.tensor_tensor(sig[:, :], sig[:, :], neg[:, :], ALU.add))

                def update(it):
                    pool.wait_ge(gated, it + 2)
                    carry_waits()
                    G.tensor_tensor(x_of(it), x_of(it), gz[:, :], ALU.add).then_inc(updated, 1)

                def turn(it, last_turn):
                    for k in range(1, STEPS):
                        prepare_backward(it, k)
                        if not last_turn:
                            prepare_next(it + 1, k)
                    own("xd", it)
                    update(it)

                pool.wait_ge(loaded, 64)
                G.memset(start[:, 1:2], 0.0).then_inc(pool_done, 1)
                G.memset(start[:, 2:3], 0.0).then_inc(updated, 1)
                G.memset(start[:, 5:8], 0.0).then_inc(carried, 1)
                pool.wait_ge(carried, 1)
                for k in range(1, STEPS):
                    prepare_next(0, k, running=False)
                with pool.Fori(0, TURNS - 1) as it:
                    turn(it, False)
                turn(TURNS - 1, True)

            @block.vector
            def _(dve):
                V = nc.vector

                def input_part(k, s):
                    dve.wait_ge(b_ready, s + 1)
                    V.tensor_tensor(dBu[k % 2][:, :], dx[dir_of(k)[0]][:, :], B_ps[:, :], ALU.mult).then_inc(dbu_ready, 1)

                def scan(k, s):
                    step = (1, -1)[dir_of(k)[0]]
                    dve.wait_ge(dbu_ready, s + 1)
                    dve.wait_ge(decay_ready, s + 1)
                    V.tensor_tensor_scan(hst[k % 2][:, ::step], dA[k % 2][:, ::step], dBu[k % 2][:, ::step],
                                         0.0, ALU.mult, ALU.add).then_inc(scanned, 1)

                def output_part(k, s):
                    dve.wait_ge(scanned, s + 1)
                    dve.wait_ge(c_ready, s + 1)
                    dve.wait_ge(y_added, s + 1)
                    V.tensor_tensor(hC[k % 2][:, :], hst[k % 2][:, :], C_ps[:, :], ALU.mult).then_inc(prod_ready, 1)

                def gate(it):
                    dve.wait_ge(y_added, (it + 1) * STEPS + 2)
                    dve.wait_ge(updated, it + 1)
                    V.tensor_tensor(gz[:, :], z[:, :], y_ps[:, :], ALU.mult).then_inc(gated, 1)

                def turn(it, last_turn):
                    for k in range(1, STEPS + 1):
                        s = it * STEPS + k
                        if last_turn and k == STEPS:
                            break
                        scan(k, s)
                        if not (last_turn and k == STEPS - 1):
                            if k == NST - 1:
                                dve.wait_ge(pool_done, pool_s.after("dx1", it))
                            elif k == STEPS - 1:
                                dve.wait_ge(pool_done, pool_s.after("dx0", it + 1))
                            dve.wait_ge(scanned, s)
                            input_part(k + 1, s + 1)
                        if k == STEPS:
                            gate(it)
                        output_part(k, s)
                    if last_turn:
                        gate(it)

                dve.wait_ge(loaded, 64)
                V.memset(start[:, 3:4], 0.0).then_inc(gated, 1)
                V.memset(start[:, 4:5], 0.0).then_inc(y_added, 2)
                dve.wait_ge(pool_done, pool_s.after("dx0", 0))
                input_part(0, 0)
                scan(0, 0)
                input_part(1, 1)
                output_part(0, 0)
                with dve.Fori(0, TURNS - 1) as it:
                    turn(it, False)
                turn(TURNS - 1, True)


Q_COLS = 64
CW_Q, CW_K, CW_V = 0, 9 * Q_COLS, 18 * Q_COLS
CW_FC1 = CW_V + 9 * P
CW_FC2 = CW_FC1 + 8
CW_FL = CW_FC2 + P
CW_FG = CW_FL + C
CV_BQ, CV_BK, CV_B1, CV_B2, CV_BV = range(CW_FG + C, CW_FG + C + 5)
CR_FB = CV_BV + 1
CW_COLS = CR_FB + C


def conv_stage(nc, weights, consts, x_sb, t_sb, notes):
    import concourse.bass as bass
    from concourse import mybir
    from contextlib import ExitStack

    fp32 = mybir.dt.float32
    ALU, ACT, AX = mybir.AluOpType, mybir.ActivationFunctionType, mybir.AxisListType.X
    IMAGES = range(2)
    BLK = range(PER)
    SCALE = (C // 4) ** -0.5
    PW = W + 2
    ROWS = HALF // W

    pe_s = Steps("gm gv fc1 fc2 q k v vt " + " ".join(
        " ".join(f"S{b}_{i}" for i in BLK) + f" mrep{b} " + " ".join(f"T{b}_{i}" for i in BLK)
        + f" loc{b} den{b} res{b} out{b}" for b in IMAGES))
    act_s = Steps("sq lnv rstd relu esig qs ks vb " + " ".join(
        f"mrepc{b} " + " ".join(f"E{b}_{i}" for i in BLK) + f" locc{b}" for b in IMAGES))
    dve_s = Steps("s1 gmean xc s2 v2 xhat ysum h1 h2 y xg vs " + " ".join(
        " ".join(f"max{b}_{i}" for i in BLK) + f" diag{b} " + " ".join(f"sub{b}_{i}" for i in BLK)
        + f" rden{b} scaled{b} summed{b} t{b}" for b in IMAGES))

    with ExitStack() as ctx:
        def sb(name, shape, dt=fp32):
            return ctx.enter_context(nc.sbuf_tensor(name, shape, dt))

        def ps(name, cols):
            return ctx.enter_context(nc.psum_tensor(name, [P, cols], fp32))

        def sem(name):
            return ctx.enter_context(nc.semaphore(name))

        cw = sb("cw", [P, CW_COLS])
        con = sb("con_c", [P, K_COLS])
        xc, sq, xg = (sb(n, [P, L]) for n in ("cxc", "csq", "cxg"))
        xw = sb("xw", [P, L])
        xpad = sb("xpad", [P, PW, PW])
        st = sb("st", [P, 16])
        S1, GM, S2, GV, YS, HID, Y = (st[:, i:i + 1] for i in range(7))
        q_sb, k_sb = sb("q_sb", [Q_COLS, L]), sb("k_sb", [Q_COLS, L])
        v_sb = sb("v_sb", [P, L])
        vT = sb("vT", [P, PER, P])
        mrow = sb("mrow", [P, 2, PER])
        diag = sb("diag", [P, PER, P])
        mrep = sb("mrep", [P, L])
        E = [sb("E0", [P, PER, L]), sb("E1", [P, PER, L])]
        loc = sb("loc", [C, L])
        rden = sb("rden", [P, 2, PER])
        tmp = sb("tmp", [P, PER, C])
        psA, psB, psM = ps("psA", L), ps("psB", L), ps("psM", L)
        psO, psT = ps("psO", HALF), ps("psT", HALF)
        psS = [psA, psB]

        loaded, zeroed = sem("c_loaded"), sem("c_zeroed")
        xw_ready = sem("xw_ready")
        pe_done, act_done, dve_done = sem("c_pe"), sem("c_act"), sem("c_dve")
        halves = [slice(0, HALF), slice(HALF, L)]
        inner = xpad[:, 1:H + 1, 1:W + 1]
        EPS = con[:, K_SPLIT + 2:K_SPLIT + 3]

        def window(tap, row, rows):
            dy, dx = divmod(tap, 3)
            return xpad[:, row + dy:row + dy + rows, dx:dx + W]

        with nc.Block() as block:
            @block.sync
            def _(sp):
                sp.dma_start(cw[:, :], weights).then_inc(loaded, 16)
                sp.dma_start(con[:, :], consts).then_inc(loaded, 16)

            @block.gpsimd
            def _(pool):
                nc.gpsimd.memset(xpad[:, :, :], 0.0).then_inc(zeroed, 1)
                notes.scatter(pool, 0, CHUNKS // 4)

            @block.tensor
            def _(pe):
                M = nc.tensor.matmul
                pe.wait_ge(loaded, 32)
                with pe.Fori(0, PAIRS) as pair:
                    def act(name):
                        pe.wait_ge(act_done, act_s.after(name, pair))

                    def dve(name):
                        pe.wait_ge(dve_done, dve_s.after(name, pair))

                    dve("s1")
                    M(psT[:, 0:1], con[:, K_PAIR:K_PAIR + P], S1, start=True, stop=True).then_inc(pe_done, 1)
                    dve("s2")
                    M(psT[:, 1:2], con[:, K_PAIR:K_PAIR + P], S2, start=True, stop=True).then_inc(pe_done, 1)
                    dve("ysum")
                    M(psT[0:8, 2:3], cw[:, CW_FC1:CW_FC1 + 8], YS, start=True, stop=True).then_inc(pe_done, 1)
                    act("relu")
                    M(psT[:, 3:4], cw[0:8, CW_FC2:CW_FC2 + P], HID[0:8, :], start=True, stop=True).then_inc(pe_done, 1)
                    for cols, width, before in ((CW_Q, Q_COLS, None), (CW_K, Q_COLS, "qs"), (CW_V, P, "ks")):
                        if before:
                            act(before)
                        for h, hs in enumerate(halves):
                            for tap in range(9):
                                last = M(psM[0:width, hs], cw[:, cols + tap * width:cols + (tap + 1) * width],
                                         window(tap, h * ROWS, ROWS), start=tap == 0, stop=tap == 8)
                        last.then_inc(pe_done, 1)
                    act("vb")
                    for i in BLK:
                        last = M(psM[:, i * P:(i + 1) * P], v_sb[:, i * P:(i + 1) * P], con[:, K_ID:K_ID + P],
                                 start=True, stop=True)
                    last.then_inc(pe_done, 1)
                    for b in IMAGES:
                        qb, kb = q_sb[32 * b:32 * b + 32, :], k_sb[32 * b:32 * b + 32, :]
                        for i in BLK:
                            if i >= 2:
                                dve(f"max{b}_{i - 2}")
                            elif b:
                                dve(f"sub0_{PER - 2 + i}")
                            for hs in halves:
                                last = M(psS[i % 2][:, hs], qb[:, i * P:(i + 1) * P], kb[:, hs], start=True, stop=True)
                            last.then_inc(pe_done, 1)
                        dve(f"diag{b}")
                        if b:
                            act("locc0")
                        else:
                            dve("vs")
                        for i in BLK:
                            last = M(psM[:, i * P:(i + 1) * P], con[:, K_ONE:K_ONE + P], diag[:, i, :], start=True, stop=True)
                        last.then_inc(pe_done, 1)
                        for i in BLK:
                            dve(f"sub{b}_{i - 2}" if i >= 2 else f"max{b}_{PER - 2 + i}")
                            for hs in halves:
                                last = M(psS[i % 2][:, hs], kb[:, i * P:(i + 1) * P], qb[:, hs], start=True, stop=True)
                            last.then_inc(pe_done, 1)
                        act(f"E{b}_{PER - 1}")
                        for hs in halves:
                            for i in BLK:
                                last = M(psM[0:C, hs], vT[:, i, b * C:(b + 1) * C], E[b][:, i, hs],
                                         start=i == 0, stop=i == PER - 1)
                        last.then_inc(pe_done, 1)
                        if b:
                            dve("summed0")
                        for i in BLK:
                            for j in BLK:
                                last = M(psT[:, 8 + i:9 + i], E[b][:, j, i * P:(i + 1) * P], con[:, K_ONE:K_ONE + 1],
                                         start=j == 0, stop=j == PER - 1)
                        last.then_inc(pe_done, 1)
                        dve(f"rden{b}")
                        rows = slice(b * C, (b + 1) * C)
                        for i in BLK:
                            M(psT[:, i * C:(i + 1) * C], xw[rows, i * P:(i + 1) * P], con[rows, K_ID + b * C:K_ID + (b + 1) * C],
                              start=True, stop=False)
                            last = M(psT[:, i * C:(i + 1) * C], xg[rows, i * P:(i + 1) * P], cw[rows, CW_FG:CW_FG + C],
                                     start=False, stop=True)
                        last.then_inc(pe_done, 1)
                        act(f"locc{b}")
                        for i in BLK:
                            last = M(psO[:, i * C:(i + 1) * C], loc[:, i * P:(i + 1) * P], cw[0:C, CW_FL:CW_FL + C],
                                     start=True, stop=True)
                        last.then_inc(pe_done, 1)

            @block.scalar
            def _(act):
                A = nc.scalar.activation
                nc.scalar.preload_act_table_set("natural_log_exp_and_others")
                act.wait_ge(loaded, 32)
                A(st[:, 8:9], con[:, 0:1], ACT.Copy).then_inc(act_done, 1)
                with act.Fori(0, PAIRS) as pair:
                    def pe(name):
                        act.wait_ge(pe_done, pe_s.after(name, pair) - 1)

                    def dve(name):
                        act.wait_ge(dve_done, dve_s.after(name, pair))

                    def own(name):
                        act.wait_ge(act_done, act_s.after(name, pair))

                    dve("xc")
                    A(sq[:, :], xc[:, :], ACT.Square).then_inc(act_done, 1)
                    dve("v2")
                    A(GV, GV, ACT.Ln, bias=EPS).then_inc(act_done, 1)
                    own("lnv")
                    A(GV, GV, ACT.Exp, scale=-0.5).then_inc(act_done, 1)
                    pe("fc1")
                    A(HID[0:8, :], psT[0:8, 2:3], ACT.Relu, bias=cw[0:8, CV_B1:CV_B1 + 1],
                      scale=1.0 / L).then_inc(act_done, 1)
                    dve("h1")
                    A(Y, Y, ACT.Exp, scale=-1.0).then_inc(act_done, 1)
                    pe("q")
                    A(q_sb[:, :], psM[0:Q_COLS, :], ACT.Identity, bias=cw[0:Q_COLS, CV_BQ:CV_BQ + 1]).then_inc(act_done, 1)
                    pe("k")
                    A(k_sb[:, :], psM[0:Q_COLS, :], ACT.Identity, bias=cw[0:Q_COLS, CV_BK:CV_BK + 1]).then_inc(act_done, 1)
                    pe("v")
                    A(v_sb[:, :], psM[:, :], ACT.Identity, bias=cw[:, CV_BV:CV_BV + 1]).then_inc(act_done, 1)
                    for b in IMAGES:
                        pe(f"mrep{b}")
                        if b:
                            dve(f"sub0_{PER - 1}")
                        A(mrep[:, :], psM[:, :], ACT.Copy).then_inc(act_done, 1)
                        for i in BLK:
                            dve(f"sub{b}_{i}")
                            A(E[b][:, i, :], E[b][:, i, :], ACT.Exp, scale=SCALE).then_inc(act_done, 1)
                        pe(f"loc{b}")
                        if b:
                            pe("out0")
                        A(loc[:, :], psM[0:C, :], ACT.Copy).then_inc(act_done, 1)

            @block.vector
            def _(dve):
                V = nc.vector
                dve.wait_ge(loaded, 32)
                dve.wait_ge(zeroed, 1)
                V.memset(st[:, 9:10], 0.0).then_inc(dve_done, 1)
                with dve.Fori(0, PAIRS) as pair:
                    def pe(name):
                        dve.wait_ge(pe_done, pe_s.after(name, pair) - 1)

                    def act(name):
                        dve.wait_ge(act_done, act_s.after(name, pair))

                    def own(name):
                        dve.wait_ge(dve_done, dve_s.after(name, pair))

                    def done(ins):
                        ins.then_inc(dve_done, 1)

                    x_pair = x_sb[:, bass.ds(pair, 1), :].rearrange("p o t -> p (o t)")
                    dve.wait_ge(dve_done, dve_s.all(pair))
                    V.tensor_copy(xw[:, :], x_pair).then_inc(xw_ready, 1)
                    dve.wait_ge(xw_ready, pair + 1)
                    V.reduce_sum(S1, xw[:, :], AX).then_inc(dve_done, 1)
                    pe("gm")
                    V.tensor_scalar(GM, psT[:, 0:1], 1.0 / L, None, ALU.mult).then_inc(dve_done, 1)
                    own("gmean")
                    V.tensor_scalar(xc[:, :], xw[:, :], GM, None, ALU.subtract).then_inc(dve_done, 1)
                    act("sq")
                    V.reduce_sum(S2, sq[:, :], AX).then_inc(dve_done, 1)
                    pe("gv")
                    V.tensor_scalar(GV, psT[:, 1:2], 1.0 / L, None, ALU.mult).then_inc(dve_done, 1)
                    act("rstd")
                    V.tensor_scalar(inner, xc[:, :].rearrange("p (h w) -> p h w", h=H), GV, None,
                                    ALU.mult).then_inc(dve_done, 1)
                    own("xhat")
                    V.tensor_reduce(YS, inner, mybir.AxisListType.XY, ALU.add).then_inc(dve_done, 1)
                    pe("fc2")
                    V.tensor_scalar(Y, psT[:, 3:4], cw[:, CV_B2:CV_B2 + 1], None, ALU.add).then_inc(dve_done, 1)
                    act("esig")
                    V.tensor_scalar_add(Y, Y, 1.0).then_inc(dve_done, 1)
                    own("h2")
                    V.reciprocal(Y, Y).then_inc(dve_done, 1)
                    own("y")
                    V.tensor_scalar(xg[:, :].rearrange("p (h w) -> p h w", h=H), inner, Y, None,
                                    ALU.mult).then_inc(dve_done, 1)
                    pe("vt")
                    V.tensor_copy(vT[:, :, :], psM[:, :].rearrange("p (i c) -> p i c", i=PER)).then_inc(dve_done, 1)
                    for b in IMAGES:
                        for i in BLK:
                            pe(f"S{b}_{i}")
                            V.reduce_max(mrow[:, b, i:i + 1], psS[i % 2][:, :], AX).then_inc(dve_done, 1)
                        own(f"max{b}_{PER - 1}")
                        V.tensor_tensor(diag[:, :, :], con[:, K_ID:K_ID + P].unsqueeze(1).broadcast_to([P, PER, P]),
                                        mrow[:, b, :].unsqueeze(2).broadcast_to([P, PER, P]),
                                        ALU.mult).then_inc(dve_done, 1)
                        act(f"mrepc{b}")
                        for i in BLK:
                            pe(f"T{b}_{i}")
                            V.tensor_tensor(E[b][:, i, :], psS[i % 2][:, :], mrep[:, :], ALU.subtract).then_inc(dve_done, 1)
                        pe(f"den{b}")
                        V.reciprocal(rden[:, b, :], psT[:, 8:8 + PER]).then_inc(dve_done, 1)
                        pe(f"out{b}")
                        own(f"rden{b}")
                        V.tensor_tensor(tmp[:, :, :], psO[:, :].rearrange("p (i c) -> p i c", i=PER),
                                        rden[:, b, :].unsqueeze(2).broadcast_to([P, PER, C]), ALU.mult).then_inc(dve_done, 1)
                        own(f"scaled{b}")
                        V.tensor_tensor(tmp[:, :, :], tmp[:, :, :], psT[:, :].rearrange("p (i c) -> p i c", i=PER),
                                        ALU.add).then_inc(dve_done, 1)
                        own(f"summed{b}")
                        V.tensor_tensor(t_sb[:, bass.ds(pair * 2 * PER + b * PER, PER), :], tmp[:, :, :],
                                        cw[:, CR_FB:CR_FB + C].unsqueeze(1).broadcast_to([P, PER, C]),
                                        ALU.add).then_inc(dve_done, 1)
def norm_stage(nc, consts, t_sb, tn_sb, tag):
    from concourse import mybir
    from contextlib import ExitStack

    fp32 = mybir.dt.float32
    ALU, ACT, AX = mybir.AluOpType, mybir.ActivationFunctionType, mybir.AxisListType.X
    act_s = Steps("sq lnv rstd")
    dve_s = Steps("sum mean centred sum2 normed")
    with ExitStack() as ctx:
        sq = ctx.enter_context(nc.sbuf_tensor(tag + "_sq", [P, TILES, C], fp32))
        mean = ctx.enter_context(nc.sbuf_tensor(tag + "_mean", [P, TILES], fp32))
        rstd = ctx.enter_context(nc.sbuf_tensor(tag + "_rstd", [P, TILES], fp32))
        eps = ctx.enter_context(nc.sbuf_tensor(tag + "_eps", [P, 1], fp32))
        act_done, dve_done, eps_set = (ctx.enter_context(nc.semaphore(tag + n)) for n in ("_act", "_dve", "_eps_set"))

        with nc.Block() as block:
            @block.gpsimd
            def _(pool):
                nc.gpsimd.memset(eps[:, :], 1e-5).then_inc(eps_set, 1)

            @block.scalar
            def _(act):
                nc.scalar.preload_act_table_set("natural_log_exp_and_others")
                act.wait_ge(dve_done, dve_s.after("centred") - 1)
                nc.scalar.activation(sq[:, :, :], tn_sb[:, :, :], ACT.Square).then_inc(act_done, 1)
                act.wait_ge(dve_done, dve_s.after("sum2") - 1)
                act.wait_ge(eps_set, 1)
                nc.scalar.activation(rstd[:, :], rstd[:, :], ACT.Ln, bias=eps[:, :], scale=1.0 / C).then_inc(act_done, 1)
                act.wait_ge(act_done, act_s.after("lnv") - 1)
                nc.scalar.activation(rstd[:, :], rstd[:, :], ACT.Exp, scale=-0.5).then_inc(act_done, 1)

            @block.vector
            def _(dve):
                V = nc.vector
                V.reduce_sum(mean[:, :], t_sb[:, :, :], AX).then_inc(dve_done, 1)
                dve.wait_ge(dve_done, dve_s.after("sum") - 1)
                V.tensor_scalar(mean[:, :], mean[:, :], 1.0 / C, None, ALU.mult).then_inc(dve_done, 1)
                dve.wait_ge(dve_done, dve_s.after("mean") - 1)
                V.tensor_tensor(tn_sb[:, :, :], t_sb[:, :, :], mean[:, :].unsqueeze(2).broadcast_to([P, TILES, C]),
                                ALU.subtract).then_inc(dve_done, 1)
                dve.wait_ge(act_done, act_s.after("sq") - 1)
                V.reduce_sum(rstd[:, :], sq[:, :, :], AX).then_inc(dve_done, 1)
                dve.wait_ge(act_done, act_s.after("rstd") - 1)
                V.tensor_tensor(tn_sb[:, :, :], tn_sb[:, :, :], rstd[:, :].unsqueeze(2).broadcast_to([P, TILES, C]),
                                ALU.mult).then_inc(dve_done, 1)


HEADS2, HDIM2 = 4, 16


def graph_attn_stage(nc, w_padded, w_plain, consts, tn_sb, t_sb, notes):
    import concourse.bass as bass
    from concourse import mybir
    from contextlib import ExitStack

    fp32 = mybir.dt.float32
    ALU, ACT, AX = mybir.AluOpType, mybir.ActivationFunctionType, mybir.AxisListType.X
    BLK, HEADS = range(PER), range(HEADS2)
    SCALE, SLOPE = HDIM2 ** -0.5, 0.2
    D1 = HDIM2 + 1

    def scores(h, *kinds):
        return " ".join(f"{k}{h}_{i}" for i in BLK for k in kinds)

    pe_s = Steps("turn WhT Wh " + scores(0, "S") + " " + " ".join(
        f"mrep{h} " + (scores(h + 1, "S") if h + 1 < HEADS2 else "") + f" out{h}" for h in HEADS))
    act_s = Steps("copy tnT WhTc " + " ".join(scores(h, "relu") + " " + scores(h, "E") for h in HEADS))
    dve_s = Steps("V " + scores(0, "leaky", "max") + " " + " ".join(
        f"diag{h} " + scores(h, "sub") + " " + (scores(h + 1, "leaky", "max") if h + 1 < HEADS2 else "")
        + f" rden{h} scaled{h} t{h}" for h in HEADS))

    with ExitStack() as ctx:
        def sb(name, shape, dt=fp32):
            return ctx.enter_context(nc.sbuf_tensor(name, shape, dt))

        def ps(name, cols):
            return ctx.enter_context(nc.psum_tensor(name, [P, cols], fp32))

        def sem(name):
            return ctx.enter_context(nc.semaphore(name))

        wp, wq = sb("g_wp", [C, P]), sb("g_w", [C, C])
        con = sb("g_con", [P, K_COLS])
        tw = sb("g_tw", [P, PER, C])
        tnT, whT = sb("g_tnT", [C, L]), sb("g_whT", [P, L])
        val = sb("g_val", [P, PER, HEADS2, D1])
        S = [sb("g_S0", [P, PER, L]), sb("g_S1", [P, PER, L])]
        mrow = sb("g_mrow", [P, HEADS2, PER])
        diag = sb("g_diag", [P, PER, P])
        rden = sb("g_rden", [P, HEADS2, PER])
        tmp = sb("g_tmp", [P, PER, HDIM2])
        psS = [ps("g_psA", L), ps("g_psB", L)]
        psM, psV, psO = ps("g_psM", L), ps("g_psV", HALF), ps("g_psO", HALF)
        loaded, ones_set = sem("g_loaded"), sem("g_ones")
        pe_done, act_done, dve_done = sem("g_pe"), sem("g_act"), sem("g_dve")
        halves = [slice(0, HALF), slice(HALF, L)]

        with nc.Block() as block:
            @block.sync
            def _(sp):
                sp.dma_start(wp[:, :], w_padded).then_inc(loaded, 16)
                sp.dma_start(wq[:, :], w_plain).then_inc(loaded, 16)
                sp.dma_start(con[:, :], consts).then_inc(loaded, 16)

            @block.gpsimd
            def _(pool):
                nc.gpsimd.memset(val[:, :, :, :], 1.0).then_inc(ones_set, 1)
                notes.scatter(pool, CHUNKS // 4, CHUNKS)

            @block.tensor
            def _(pe):
                M = nc.tensor.matmul
                pe.wait_ge(loaded, 48)
                with pe.Fori(0, B) as img:
                    def act(name):
                        pe.wait_ge(act_done, act_s.after(name, img))

                    def dve(name):
                        pe.wait_ge(dve_done, dve_s.after(name, img))

                    act("copy")
                    for i in BLK:
                        last = M(psM[0:C, i * P:(i + 1) * P], tw[:, i, :], con[:, K_ID:K_ID + P], start=True, stop=True)
                    last.then_inc(pe_done, 1)
                    act("tnT")
                    for hs in halves:
                        last = M(psM[:, hs], wp[:, :], tnT[:, hs], start=True, stop=True)
                    last.then_inc(pe_done, 1)
                    for i in BLK:
                        last = M(psV[:, i * C:(i + 1) * C], tnT[:, i * P:(i + 1) * P], wq[:, :], start=True, stop=True)
                    last.then_inc(pe_done, 1)
                    act("WhTc")

                    def score_tiles(h):
                        rows = slice(32 * h, 32 * h + 32)
                        for i in BLK:
                            if i >= 2:
                                dve(f"leaky{h}_{i - 2}")
                            elif h:
                                dve(f"leaky{h - 1}_{PER - 2 + i}")
                            for hs in halves:
                                last = M(psS[i % 2][:, hs], whT[rows, i * P:(i + 1) * P], whT[rows, hs], start=True, stop=True)
                            last.then_inc(pe_done, 1)

                    score_tiles(0)
                    for h in HEADS:
                        dve(f"diag{h}")
                        if h:
                            dve(f"sub{h - 1}_{PER - 1}")
                        for i in BLK:
                            last = M(psM[:, i * P:(i + 1) * P], con[:, K_ONE:K_ONE + P], diag[:, i, :], start=True, stop=True)
                        last.then_inc(pe_done, 1)
                        if h + 1 < HEADS2:
                            score_tiles(h + 1)
                        act(f"E{h}_{PER - 1}")
                        if h:
                            dve(f"scaled{h - 1}")
                        for i in BLK:
                            for j in BLK:
                                last = M(psO[:, i * D1:(i + 1) * D1], S[h % 2][:, j, i * P:(i + 1) * P], val[:, j, h, :],
                                         start=j == 0, stop=j == PER - 1)
                        last.then_inc(pe_done, 1)

            @block.scalar
            def _(act):
                A = nc.scalar.activation
                nc.scalar.preload_act_table_set("natural_log_exp_and_others")
                act.wait_ge(loaded, 48)
                A(mrow[:, 0, 0:1], con[:, 0:1], ACT.Copy).then_inc(act_done, 1)
                with act.Fori(0, B) as img:
                    def pe(name):
                        act.wait_ge(pe_done, pe_s.after(name, img) - 1)

                    def dve(name):
                        act.wait_ge(dve_done, dve_s.after(name, img))

                    act.wait_ge(dve_done, dve_s.all(img))
                    A(tw[:, :, :], tn_sb[:, bass.ds(img * PER, PER), :], ACT.Copy).then_inc(act_done, 1)
                    pe("turn")
                    A(tnT[:, :], psM[0:C, :], ACT.Copy).then_inc(act_done, 1)
                    pe("WhT")
                    A(whT[:, :], psM[:, :], ACT.Copy).then_inc(act_done, 1)
                    for h in HEADS:
                        for i in BLK:
                            pe(f"S{h}_{i}")
                            if h >= 2 and i == 0:
                                pe(f"out{h - 2}")
                            A(S[h % 2][:, i, :], psS[i % 2][:, :], ACT.Relu, scale=SCALE * (1 - SLOPE)).then_inc(act_done, 1)
                        for i in BLK:
                            dve(f"sub{h}_{i}")
                            A(S[h % 2][:, i, :], S[h % 2][:, i, :], ACT.Exp).then_inc(act_done, 1)

            @block.vector
            def _(dve):
                V = nc.vector
                dve.wait_ge(loaded, 48)
                dve.wait_ge(ones_set, 1)
                V.memset(tmp[:, 0, 0:1], 0.0).then_inc(dve_done, 1)
                with dve.Fori(0, B) as img:
                    def pe(name):
                        dve.wait_ge(pe_done, pe_s.after(name, img) - 1)

                    def act(name):
                        dve.wait_ge(act_done, act_s.after(name, img))

                    def own(name):
                        dve.wait_ge(dve_done, dve_s.after(name, img))

                    pe("Wh")
                    V.tensor_copy(val[:, :, :, 0:HDIM2],
                                  psV[:, :].rearrange("p (i h d) -> p i h d", i=PER, h=HEADS2)).then_inc(dve_done, 1)

                    def leaky_tiles(h):
                        for i in BLK:
                            act(f"relu{h}_{i}")
                            V.scalar_tensor_tensor(S[h % 2][:, i, :], psS[i % 2][:, :], SCALE * SLOPE, S[h % 2][:, i, :],
                                                   ALU.mult, ALU.add).then_inc(dve_done, 1)
                            own(f"leaky{h}_{i}")
                            V.reduce_max(mrow[:, h, i:i + 1], S[h % 2][:, i, :], AX).then_inc(dve_done, 1)

                    leaky_tiles(0)
                    for h in HEADS:
                        own(f"max{h}_{PER - 1}")
                        V.tensor_tensor(diag[:, :, :], con[:, K_ID:K_ID + P].unsqueeze(1).broadcast_to([P, PER, P]),
                                        mrow[:, h, :].unsqueeze(2).broadcast_to([P, PER, P]), ALU.mult).then_inc(dve_done, 1)
                        pe(f"mrep{h}")
                        for i in BLK:
                            V.tensor_tensor(S[h % 2][:, i, :], S[h % 2][:, i, :], psM[:, :], ALU.subtract).then_inc(dve_done, 1)
                        if h + 1 < HEADS2:
                            leaky_tiles(h + 1)
                        pe(f"out{h}")
                        out = psO[:, 0:PER * D1].rearrange("p (i d) -> p i d", i=PER)
                        V.reciprocal(rden[:, h, :], out[:, :, HDIM2]).then_inc(dve_done, 1)
                        own(f"rden{h}")
                        V.tensor_tensor(tmp[:, :, :], out[:, :, 0:HDIM2], rden[:, h, :].unsqueeze(2).broadcast_to([P, PER, HDIM2]),
                                        ALU.mult).then_inc(dve_done, 1)
                        own(f"scaled{h}")
                        t_head = t_sb[:, bass.ds(img * PER, PER), h * HDIM2:(h + 1) * HDIM2]
                        V.tensor_tensor(t_head, t_head, tmp[:, :, :], ALU.add).then_inc(dve_done, 1)
GROUP = 4
EXPERTS = 16


def project_stage(nc, weight, bias_rows, consts, tn_sb, tnT_sb, out_sb, tag):
    import concourse.bass as bass
    from concourse import mybir
    from contextlib import ExitStack

    fp32 = mybir.dt.float32
    ALU, ACT = mybir.AluOpType, mybir.ActivationFunctionType
    E = out_sb.shape[2]
    with ExitStack() as ctx:
        w = ctx.enter_context(nc.sbuf_tensor(tag + "_w", [C, E], fp32))
        brow = ctx.enter_context(nc.sbuf_tensor(tag + "_b", [P, E], fp32))
        con = ctx.enter_context(nc.sbuf_tensor(tag + "_con", [P, K_COLS], fp32))
        tw = [ctx.enter_context(nc.sbuf_tensor(f"{tag}_tw{k}", [P, GROUP, C], fp32)) for k in range(2)]
        wT = [ctx.enter_context(nc.sbuf_tensor(f"{tag}_wT{k}", [C, HALF], fp32)) for k in range(2)]
        psT = [ctx.enter_context(nc.psum_tensor(f"{tag}_psT{k}", [P, HALF], fp32)) for k in range(2)]
        psL = [ctx.enter_context(nc.psum_tensor(f"{tag}_psL{k}", [P, HALF], fp32)) for k in range(2)]
        loaded, copied, turned, kept, kept_all, projected, stored = (
            ctx.enter_context(nc.semaphore(tag + n)) for n in
            ("_loaded", "_copied", "_turned", "_kept", "_kept_all", "_projected", "_stored"))
        TURNS = TILES // GROUP

        with nc.Block() as block:
            @block.sync
            def _(sp):
                sp.dma_start(w[:, :], weight).then_inc(loaded, 16)
                sp.dma_start(brow[:, :], bias_rows).then_inc(loaded, 16)
                sp.dma_start(con[:, :], consts).then_inc(loaded, 16)

            @block.tensor
            def _(pe):
                pe.wait_ge(loaded, 48)
                with pe.Fori(0, TURNS // 2) as pair:
                    for k in range(2):
                        turn = pair * 2 + k
                        pe.wait_ge(copied, turn + 1)
                        for g in range(GROUP):
                            last = nc.tensor.matmul(psT[k][0:C, g * P:(g + 1) * P], tw[k][:, g, :], con[:, K_ID:K_ID + P],
                                                    start=True, stop=True)
                        last.then_inc(turned, 1)
                        pe.wait_ge(kept, turn + 1)
                        for g in range(GROUP):
                            last = nc.tensor.matmul(psL[k][:, g * E:(g + 1) * E], wT[k][:, g * P:(g + 1) * P], w[:, :],
                                                    start=True, stop=True)
                        last.then_inc(projected, 1)

            @block.scalar
            def _(act):
                act.wait_ge(loaded, 48)
                with act.Fori(0, TURNS // 2) as pair:
                    for k in range(2):
                        turn = pair * 2 + k
                        act.wait_ge(turned, turn + 1)
                        nc.scalar.activation(wT[k][:, :], psT[k][0:C, :], ACT.Copy).then_inc(kept, 1)
                        act.wait_ge(kept, turn + 1)
                        nc.scalar.activation(tnT_sb[:, bass.ds(turn * HALF, HALF)], wT[k][:, :], ACT.Copy).then_inc(kept_all, 1)

            @block.vector
            def _(dve):
                V = nc.vector
                dve.wait_ge(loaded, 48)
                V.memset(tw[0][:, 0, 0:1], 0.0).then_inc(stored, 2)
                with dve.Fori(0, TURNS // 2) as pair:
                    for k in range(2):
                        turn = pair * 2 + k
                        dve.wait_ge(stored, turn + 1)
                        V.tensor_copy(tw[k][:, :, :], tn_sb[:, bass.ds(turn * GROUP, GROUP), :]).then_inc(copied, 1)
                    for k in range(2):
                        turn = pair * 2 + k
                        dve.wait_ge(projected, turn + 1)
                        dve.wait_ge(kept_all, turn + 1)
                        V.tensor_tensor(out_sb[:, bass.ds(turn * GROUP, GROUP), :],
                                        psL[k][:, 0:GROUP * E].rearrange("p (g e) -> p g e", g=GROUP),
                                        brow[:, :].unsqueeze(1).broadcast_to([P, GROUP, E]), ALU.add).then_inc(stored, 1)


def top2_stage(nc, logits, tag):
    from concourse import mybir
    from contextlib import ExitStack

    fp32 = mybir.dt.float32
    ALU, ACT, AX = mybir.AluOpType, mybir.ActivationFunctionType, mybir.AxisListType.X
    E = logits.shape[2]
    FAR = 1e30
    with ExitStack() as ctx:
        rank, hit, first = (ctx.enter_context(nc.sbuf_tensor(tag + n, [P, TILES, E], fp32)) for n in ("_rank", "_hit", "_first"))
        top, pos, g1, g2 = (ctx.enter_context(nc.sbuf_tensor(tag + n, [P, 2, TILES], fp32)) for n in ("_top", "_pos", "_g1", "_g2"))
        ranked, exp_done, link = (ctx.enter_context(nc.semaphore(tag + n)) for n in ("_ranked", "_exp_done", "_link"))

        def wide(a):
            return a.unsqueeze(2).broadcast_to([P, TILES, E])

        with nc.Block() as block:
            @block.gpsimd
            def _(pool):
                for e in range(E):
                    nc.gpsimd.memset(rank[:, :, e:e + 1], float(E - e)).then_inc(ranked, 1)

            @block.scalar
            def _(act):
                act.wait_ge(link, 8)
                nc.scalar.activation(g2[:, 0, :], g2[:, 0, :], ACT.Exp).then_inc(exp_done, 1)

            @block.vector
            def _(dve):
                V = nc.vector
                dve.wait_ge(ranked, E)
                V.reduce_max(top[:, 0, :], logits[:, :, :], AX).then_inc(link, 1)
                dve.wait_ge(link, 1)
                V.tensor_tensor(hit[:, :, :], logits[:, :, :], wide(top[:, 0, :]), ALU.is_equal).then_inc(link, 1)
                dve.wait_ge(link, 2)
                V.tensor_tensor(hit[:, :, :], hit[:, :, :], rank[:, :, :], ALU.mult).then_inc(link, 1)
                dve.wait_ge(link, 3)
                V.reduce_max(pos[:, 0, :], hit[:, :, :], AX).then_inc(link, 1)
                dve.wait_ge(link, 4)
                V.tensor_tensor(first[:, :, :], rank[:, :, :], wide(pos[:, 0, :]), ALU.is_equal).then_inc(link, 1)
                dve.wait_ge(link, 5)
                V.scalar_tensor_tensor(logits[:, :, :], first[:, :, :], -FAR, logits[:, :, :], ALU.mult, ALU.add).then_inc(link, 1)
                dve.wait_ge(link, 6)
                V.reduce_max(top[:, 1, :], logits[:, :, :], AX).then_inc(link, 1)
                dve.wait_ge(link, 7)
                V.tensor_tensor(g2[:, 0, :], top[:, 1, :], top[:, 0, :], ALU.subtract).then_inc(link, 1)
                V.tensor_tensor(hit[:, :, :], logits[:, :, :], wide(top[:, 1, :]), ALU.is_equal).then_inc(link, 1)
                dve.wait_ge(link, 9)
                V.tensor_tensor(hit[:, :, :], hit[:, :, :], rank[:, :, :], ALU.mult).then_inc(link, 1)
                dve.wait_ge(link, 10)
                V.reduce_max(pos[:, 1, :], hit[:, :, :], AX).then_inc(link, 1)
                dve.wait_ge(link, 11)
                V.tensor_tensor(hit[:, :, :], rank[:, :, :], wide(pos[:, 1, :]), ALU.is_equal).then_inc(link, 1)
                dve.wait_ge(exp_done, 1)
                V.tensor_scalar_add(g1[:, 0, :], g2[:, 0, :], 1.0).then_inc(link, 1)
                dve.wait_ge(link, 13)
                V.reciprocal(g1[:, 0, :], g1[:, 0, :]).then_inc(link, 1)
                dve.wait_ge(link, 14)
                V.tensor_tensor(g2[:, 0, :], g2[:, 0, :], g1[:, 0, :], ALU.mult).then_inc(link, 1)
                V.tensor_tensor(first[:, :, :], first[:, :, :], wide(g1[:, 0, :]), ALU.mult).then_inc(link, 1)
                dve.wait_ge(link, 16)
                V.tensor_tensor(hit[:, :, :], hit[:, :, :], wide(g2[:, 0, :]), ALU.mult).then_inc(link, 1)
                dve.wait_ge(link, 17)
                V.tensor_tensor(logits[:, :, :], first[:, :, :], hit[:, :, :], ALU.add).then_inc(link, 1)
                dve.wait_ge(link, 18)


def expert_stage(nc, w_in, w_gate, w_out, bias_in, bias_out, gates, tnT_sb, t_sb, tag):
    import concourse.bass as bass
    from concourse import mybir
    from contextlib import ExitStack

    fp32 = mybir.dt.float32
    ALU, ACT = mybir.AluOpType, mybir.ActivationFunctionType
    E = gates.shape[2]
    FOUR = 4
    QUADS = E // FOUR
    TURNS = TILES // GROUP
    with ExitStack() as ctx:
        def sb(name, shape):
            return ctx.enter_context(nc.sbuf_tensor(tag + name, shape, fp32))

        def sem(name):
            return ctx.enter_context(nc.semaphore(tag + name))

        win, wout = sb("_win", [C, E, P]), sb("_wout", [P, E, C])
        wg = sb("_wg", [C, E, P]) if w_gate is not None else None
        bin_, bout = (sb("_bin", [P, E]), sb("_bout", [P, E, C])) if w_gate is None else (None, None)
        hid = [sb(f"_hid{k}", [P, HALF]) for k in range(2)]
        act_out = [sb(f"_act{k}", [P, HALF]) for k in range(2)]
        tmp = sb("_tmp", [P, GROUP, FOUR, C])
        red = sb("_red", [P, GROUP, C])
        ps1 = [ctx.enter_context(nc.psum_tensor(f"{tag}_ps1{k}", [P, HALF], fp32)) for k in range(2)]
        ps2 = [ctx.enter_context(nc.psum_tensor(f"{tag}_ps2{k}", [P, HALF], fp32)) for k in range(2)]
        psY = [ctx.enter_context(nc.psum_tensor(f"{tag}_psY{k}", [P, GROUP * FOUR * C], fp32)) for k in range(2)]
        loaded, h_ready, activated, hid_ready, y_ready, gated, link = (
            sem(n) for n in ("_loaded", "_h_ready", "_activated", "_hid_ready", "_y_ready", "_gated", "_link"))
        reduced, added, fetched = sem("_reduced"), sem("_added"), sem("_fetched")
        turns_done = sem("_turns_done")
        tokens = [sb(f"_tok{k}", [C, HALF]) for k in range(2)]
        loads = [(win, w_in), (wout, w_out)] + ([(wg, w_gate)] if wg is not None else [(bin_, bias_in), (bout, bias_out)])
        LOADED = 16 * len(loads)
        hid_of = hid if wg is not None else act_out
        hid_sem = hid_ready if wg is not None else activated

        with nc.Block() as block:
            @block.sync
            def _(sp):
                for dst, src in loads:
                    sp.dma_start(dst[tuple([slice(None)] * len(dst.shape))], src).then_inc(loaded, 16)

            @block.tensor
            def _(pe):
                M = nc.tensor.matmul
                pe.wait_ge(loaded, LOADED)
                with pe.Fori(0, TURNS // 2) as pair:
                    def into(turn, e):
                        s = turn * E + e
                        rhs = tokens[k][:, :]
                        if e == 0:
                            pe.wait_ge(fetched, turn + 1)
                        pe.wait_ge(hid_sem, s + 1)
                        M(ps1[e % 2][:, :], win[:, e, :], rhs, start=True, stop=True).then_inc(h_ready, 1)
                        if wg is not None:
                            M(ps2[e % 2][:, :], wg[:, e, :], rhs, start=True, stop=True).then_inc(h_ready, 1)

                    def out_of(turn, e):
                        s = turn * E + e
                        quad, q = divmod(e, FOUR)
                        if q == 0:
                            pe.wait_ge(gated, turn * QUADS + quad + 1)
                        pe.wait_ge(hid_sem, s + 3)
                        for g in range(GROUP):
                            last = M(psY[(quad if QUADS > 1 else 0) % 2][:, (g * FOUR + q) * C:(g * FOUR + q + 1) * C],
                                     hid_of[e % 2][:, g * P:(g + 1) * P], wout[:, e, :], start=True, stop=True)
                            if e == E - 1 and g == 0:
                                last.then_inc(turns_done, 1)
                        last.then_inc(y_ready, 1)

                    for k in range(2):
                        turn = pair * 2 + k
                        into(turn, 0)
                        for e in range(E):
                            if e + 1 < E:
                                into(turn, e + 1)
                            out_of(turn, e)

            @block.gpsimd
            def _(pool):
                with pool.Fori(0, TURNS // 2) as pair:
                    for k in range(2):
                        turn = pair * 2 + k
                        pool.wait_ge(turns_done, turn + 1)
                        nc.gpsimd.tensor_copy(tokens[k][:, :], tnT_sb[:, bass.ds(turn * HALF, HALF)]).then_inc(fetched, 1)

            @block.scalar
            def _(act):
                act.wait_ge(loaded, LOADED)
                if wg is None:
                    nc.scalar.activation(act_out[0][:, 0:1], bin_[:, 0:1], ACT.Copy).then_inc(activated, 2)
                with act.Fori(0, TURNS // 2) as pair:
                    for k, e in [(k, e) for k in range(2) for e in range(E)]:
                        s = (pair * 2 + k) * E + e
                        if wg is not None:
                            act.wait_ge(h_ready, s * 2 + 1)
                            act.wait_ge(hid_ready, s + 1)
                            nc.scalar.activation(act_out[e % 2][:, :], ps1[e % 2][:, :], ACT.Silu).then_inc(activated, 1)
                        else:
                            act.wait_ge(h_ready, s + 1)
                            act.wait_ge(y_ready, s + 1)
                            nc.scalar.activation(act_out[e % 2][:, :], ps1[e % 2][:, :], ACT.Gelu,
                                                 bias=bin_[:, e:e + 1]).then_inc(activated, 1)

            @block.vector
            def _(dve):
                V = nc.vector
                dve.wait_ge(loaded, LOADED)
                V.memset(red[:, 0, 0:1], 0.0).then_inc(y_ready, 2)
                V.memset(red[:, 0, 1:2], 0.0).then_inc(gated, 2 if QUADS > 1 else 1)
                V.memset(red[:, 0, 2:3], 0.0).then_inc(hid_ready, 2)
                V.memset(red[:, 0, 3:4], 0.0).then_inc(turns_done, 2)
                GOT = 2 if QUADS > 1 else 1
                with dve.Fori(0, TURNS // 2) as pair:
                    def gate(turn, quad):
                        k = (quad if QUADS > 1 else 0) % 2
                        s = turn * QUADS + quad
                        y = psY[k][:, :].rearrange("p (g e c) -> p g e c", g=GROUP, e=FOUR)
                        dve.wait_ge(y_ready, s * FOUR + FOUR + 2)
                        if wg is None:
                            for g in range(GROUP):
                                last = V.tensor_tensor(tmp[:, g, :, :], y[:, g, :, :], bout[:, :, :], ALU.add)
                            last.then_inc(link, 1)
                            dve.wait_ge(link, s + 1)
                            y = tmp[:, :, :, :]
                        g4 = gates[:, bass.ds(turn * GROUP, GROUP), quad * FOUR:(quad + 1) * FOUR]
                        V.tensor_tensor(tmp[:, :, :, :], y, g4.unsqueeze(3).broadcast_to([P, GROUP, FOUR, C]),
                                        ALU.mult).then_inc(gated, 1)
                        dve.wait_ge(gated, s + 1 + GOT)
                        V.tensor_reduce(red[:, :, :], tmp[:, :, :, :].rearrange("p g e c -> p g c e"),
                                        mybir.AxisListType.X, ALU.add).then_inc(reduced, 1)
                        dve.wait_ge(reduced, s + 1)
                        t_now = t_sb[:, bass.ds(turn * GROUP, GROUP), :]
                        V.tensor_tensor(t_now, t_now, red[:, :, :], ALU.add).then_inc(added, 1)
                        dve.wait_ge(added, s + 1)

                    for k2, e in [(k2, e) for k2 in range(2) for e in range(E)]:
                        turn = pair * 2 + k2
                        s = turn * E + e
                        if wg is not None:
                            dve.wait_ge(activated, s + 1)
                            dve.wait_ge(h_ready, s * 2 + 2)
                            dve.wait_ge(y_ready, s + 1)
                            V.tensor_tensor(hid[e % 2][:, :], act_out[e % 2][:, :], ps2[e % 2][:, :], ALU.mult).then_inc(hid_ready, 1)
                        if e % FOUR == 1 and e > FOUR:
                            gate(turn, e // FOUR - 1)
                        if e == E - 1:
                            gate(turn, QUADS - 1)
SLICES, HEADS3, HDIM3 = 16, 8, 32
HD3 = HEADS3 * HDIM3
SW_0 = 0
SW_S = SW_0 + P
SW_QKV = SW_S + SLICES
SW_OUT = SW_QKV + 3 * HD3
SV_B0 = SW_OUT + 2 * C
SR_B0 = SV_B0 + 1
SR_BS = SR_B0 + C
SR_BO = SR_BS + SLICES
SW_COLS = SR_BO + C


def slice_attn_stage(nc, weights, consts, tn_sb, t_sb):
    import concourse.bass as bass
    from concourse import mybir
    from contextlib import ExitStack

    fp32 = mybir.dt.float32
    ALU, ACT, AX = mybir.AluOpType, mybir.ActivationFunctionType, mybir.AxisListType.X
    BLK = range(PER)
    HG = 4
    pe_s = Steps("turn hT h logits swT pool poolT qk v scores attnT tokT fold out")
    act_s = Steps("copy tnT hTc esw swTc poolTc qkc eat attnTc foldc")
    dve_s = Steps("hx lg max sub sum rsum sw dn rdn pooled vc qdiag smax ssub ssum srec attn tokm tok outb t")

    with ExitStack() as ctx:
        def sb(name, shape):
            return ctx.enter_context(nc.sbuf_tensor("s_" + name, shape, fp32))

        def ps(name, cols=HALF):
            return ctx.enter_context(nc.psum_tensor("s_" + name, [P, cols], fp32))

        def sem(name):
            return ctx.enter_context(nc.semaphore("s_" + name))

        w, con = sb("w", [P, SW_COLS]), sb("con", [P, K_COLS])
        tw = sb("tw", [P, PER, C])
        tnT, hT = sb("tnT", [C, L]), sb("hT", [C, L])
        hx = sb("hx", [P, PER, C + 1])
        sw = sb("sw", [P, PER, SLICES])
        r8 = sb("r8", [P, 2, PER])
        swT = sb("swT", [SLICES, L])
        pooled, dn = sb("pooled", [SLICES, C + 1]), sb("dn", [SLICES, 1])
        poolT = sb("poolT", [C + 1, SLICES])
        qk = sb("qk", [P, 4, SLICES])
        v = sb("v", [SLICES, HD3])
        qd = sb("qd", [P, 2, HG, SLICES])
        at = sb("at", [P, 2, SLICES])
        rs = sb("rs", [HG * SLICES, 2, 2])
        atT = sb("atT", [SLICES, 2 * HG * SLICES])
        tokm, tok = sb("tokm", [P, 2, HG, SLICES]), sb("tok", [P, 2, SLICES])
        fold = sb("fold", [SLICES, C])
        tmp = sb("tmp", [P, PER, C])
        psM = ps("psM", L)
        psH, psL, psG, psQ, psS, psO = (ps(n) for n in ("psH", "psL", "psG", "psQ", "psS", "psO"))
        loaded, ones_set = sem("loaded"), sem("ones")
        pe_done, act_done, dve_done = sem("pe"), sem("act"), sem("dve")
        halves = [slice(0, HALF), slice(HALF, L)]
        at4 = at[0:HG * SLICES, :, :]
        ID = con[:, K_ID:K_ID + P]

        with nc.Block() as block:
            @block.sync
            def _(sp):
                sp.dma_start(w[:, :], weights).then_inc(loaded, 16)
                sp.dma_start(con[:, :], consts).then_inc(loaded, 16)

            @block.gpsimd
            def _(pool):
                nc.gpsimd.memset(hx[:, :, :], 1.0).then_inc(ones_set, 1)
                nc.gpsimd.memset(at[:, :, :], 0.0).then_inc(ones_set, 1)

            @block.tensor
            def _(pe):
                M = nc.tensor.matmul
                pe.wait_ge(loaded, 32)
                with pe.Fori(0, B) as img:
                    def act(name):
                        pe.wait_ge(act_done, act_s.after(name, img))

                    def dve(name):
                        pe.wait_ge(dve_done, dve_s.after(name, img))

                    def done(ins):
                        ins.then_inc(pe_done, 1)

                    act("copy")
                    for i in BLK:
                        last = M(psM[0:C, i * P:(i + 1) * P], tw[:, i, :], ID, start=True, stop=True)
                    done(last)
                    act("tnT")
                    for hs in halves:
                        last = M(psM[:, hs], w[0:C, SW_0:SW_0 + P], tnT[:, hs], start=True, stop=True)
                    done(last)
                    for i in BLK:
                        last = M(psH[:, i * C:(i + 1) * C], tnT[:, i * P:(i + 1) * P], w[0:C, SW_0:SW_0 + C],
                                 start=True, stop=True)
                    done(last)
                    act("hTc")
                    for i in BLK:
                        last = M(psL[:, i * SLICES:(i + 1) * SLICES], hT[:, i * P:(i + 1) * P], w[0:C, SW_S:SW_S + SLICES],
                                 start=True, stop=True)
                    done(last)
                    dve("sw")
                    for i in BLK:
                        last = M(psM[0:SLICES, i * P:(i + 1) * P], sw[:, i, :], ID, start=True, stop=True)
                    done(last)
                    for i in BLK:
                        last = M(psG[0:SLICES, 0:C + 1], sw[:, i, :], hx[:, i, :], start=i == 0, stop=i == PER - 1)
                    done(last)
                    dve("pooled")
                    done(M(psS[0:C + 1, 0:SLICES], pooled[:, :], con[0:SLICES, K_ID:K_ID + SLICES], start=True, stop=True))
                    act("poolTc")
                    for j in range(4):
                        last = M(psQ[:, j * SLICES:(j + 1) * SLICES], w[0:C + 1, SW_QKV + j * P:SW_QKV + (j + 1) * P], poolT[:, :],
                                 start=True, stop=True)
                    done(last)
                    done(M(psG[0:SLICES, 0:HD3], poolT[:, :], w[0:C + 1, SW_QKV + 2 * HD3:SW_QKV + 3 * HD3],
                           start=True, stop=True))
                    dve("qdiag")
                    for g in range(2):
                        last = M(psS[0:HG * SLICES, g * SLICES:(g + 1) * SLICES], qd[:, g, :, :].rearrange("p h s -> p (h s)"),
                                 qk[:, 2 + g, :], start=True, stop=True)
                    done(last)
                    dve("attn")
                    for g in range(2):
                        last = M(psL[0:SLICES, g * HG * SLICES:(g + 1) * HG * SLICES], at[:, g, :],
                                 con[:, K_ID:K_ID + HG * SLICES], start=True, stop=True)
                    done(last)
                    act("attnTc")
                    for g in range(2):
                        last = M(psQ[:, g * HG * SLICES:(g + 1) * HG * SLICES], v[:, g * P:(g + 1) * P],
                                 atT[:, g * HG * SLICES:(g + 1) * HG * SLICES], start=True, stop=True)
                    done(last)
                    dve("tok")
                    for g in range(2):
                        last = M(psG[0:SLICES, 0:C], tok[:, g, :], w[:, SW_OUT + g * C:SW_OUT + (g + 1) * C],
                                 start=g == 0, stop=g == 1)
                    done(last)
                    act("foldc")
                    for i in BLK:
                        last = M(psO[:, i * C:(i + 1) * C], swT[:, i * P:(i + 1) * P], fold[:, :], start=True, stop=True)
                    done(last)

            @block.scalar
            def _(act):
                A = nc.scalar.activation
                act.wait_ge(loaded, 32)
                A(rs[:, 0, 0:1], con[0:HG * SLICES, 0:1], ACT.Copy).then_inc(act_done, 1)
                with act.Fori(0, B) as img:
                    def pe(name):
                        act.wait_ge(pe_done, pe_s.after(name, img) - 1)

                    def dve(name):
                        act.wait_ge(dve_done, dve_s.after(name, img))

                    act.wait_ge(dve_done, dve_s.all(img))
                    A(tw[:, :, :], tn_sb[:, bass.ds(img * PER, PER), :], ACT.Copy).then_inc(act_done, 1)
                    pe("turn")
                    A(tnT[:, :], psM[0:C, :], ACT.Copy).then_inc(act_done, 1)
                    pe("hT")
                    A(hT[:, :], psM[0:C, :], ACT.Identity, bias=w[0:C, SV_B0:SV_B0 + 1]).then_inc(act_done, 1)
                    dve("sub")
                    A(sw[:, :, :], sw[:, :, :], ACT.Exp).then_inc(act_done, 1)
                    pe("swT")
                    A(swT[:, :], psM[0:SLICES, :], ACT.Copy).then_inc(act_done, 1)
                    pe("poolT")
                    A(poolT[:, :], psS[0:C + 1, 0:SLICES], ACT.Copy).then_inc(act_done, 1)
                    pe("qk")
                    A(qk[:, :, :], psQ[:, 0:4 * SLICES].rearrange("p (j s) -> p j s", j=4), ACT.Copy).then_inc(act_done, 1)
                    dve("ssub")
                    A(at4, at4, ACT.Exp, scale=HDIM3 ** -0.5).then_inc(act_done, 1)
                    pe("attnT")
                    A(atT[:, :], psL[0:SLICES, 0:2 * HG * SLICES], ACT.Copy).then_inc(act_done, 1)
                    pe("fold")
                    A(fold[:, :], psG[0:SLICES, 0:C], ACT.Copy).then_inc(act_done, 1)

            @block.vector
            def _(dve):
                V = nc.vector
                dve.wait_ge(loaded, 32)
                dve.wait_ge(ones_set, 2)
                V.memset(tmp[:, 0, 0:1], 0.0).then_inc(dve_done, 1)
                with dve.Fori(0, B) as img:
                    def pe(name):
                        dve.wait_ge(pe_done, pe_s.after(name, img) - 1)

                    def act(name):
                        dve.wait_ge(act_done, act_s.after(name, img))

                    def own(name):
                        dve.wait_ge(dve_done, dve_s.after(name, img))

                    def done(ins):
                        ins.then_inc(dve_done, 1)

                    def row(v_, shape):
                        return v_.unsqueeze(1).broadcast_to(shape)

                    pe("h")
                    done(V.tensor_tensor(hx[:, :, 0:C], psH[:, :].rearrange("p (i c) -> p i c", i=PER),
                                         row(w[:, SR_B0:SR_B0 + C], [P, PER, C]), ALU.add))
                    pe("logits")
                    done(V.tensor_tensor(sw[:, :, :], psL[:, 0:PER * SLICES].rearrange("p (i s) -> p i s", i=PER),
                                         row(w[:, SR_BS:SR_BS + SLICES], [P, PER, SLICES]), ALU.add))
                    own("lg")
                    done(V.reduce_max(r8[:, 0, :], sw[:, :, :], AX))
                    own("max")
                    wide = [P, PER, SLICES]
                    done(V.tensor_tensor(sw[:, :, :], sw[:, :, :], r8[:, 0, :].unsqueeze(2).broadcast_to(wide), ALU.subtract))
                    act("esw")
                    done(V.reduce_sum(r8[:, 1, :], sw[:, :, :], AX))
                    own("sum")
                    done(V.reciprocal(r8[:, 1, :], r8[:, 1, :]))
                    own("rsum")
                    done(V.tensor_tensor(sw[:, :, :], sw[:, :, :], r8[:, 1, :].unsqueeze(2).broadcast_to(wide), ALU.mult))
                    pe("pool")
                    done(V.tensor_scalar_add(dn[:, :], psG[0:SLICES, C:C + 1], 1e-9))
                    own("dn")
                    done(V.reciprocal(dn[:, :], dn[:, :]))
                    own("rdn")
                    done(V.tensor_scalar(pooled[:, :], psG[0:SLICES, 0:C + 1], dn[:, :], None, ALU.mult))
                    pe("v")
                    done(V.tensor_copy(v[:, :], psG[0:SLICES, 0:HD3]))
                    act("qkc")
                    done(V.tensor_tensor(qd[:, :, :, :], qk[:, 0:2, :].unsqueeze(2).broadcast_to([P, 2, HG, SLICES]),
                                         con[:, K_MASK:K_MASK + 64].rearrange("p (h s) -> p h s", h=HG).unsqueeze(1).broadcast_to(
                                             [P, 2, HG, SLICES]), ALU.mult))
                    pe("scores")
                    sc = psS[0:HG * SLICES, 0:2 * SLICES].rearrange("p (g s) -> p g s", g=2)
                    done(V.reduce_max(rs[:, 0, :], sc, AX))
                    own("smax")
                    wide2 = [HG * SLICES, 2, SLICES]
                    done(V.tensor_tensor(at4, sc, rs[:, 0, :].unsqueeze(2).broadcast_to(wide2), ALU.subtract))
                    act("eat")
                    done(V.reduce_sum(rs[:, 1, :], at4, AX))
                    own("ssum")
                    done(V.reciprocal(rs[:, 1, :], rs[:, 1, :]))
                    own("srec")
                    done(V.tensor_tensor(at4, at4, rs[:, 1, :].unsqueeze(2).broadcast_to(wide2), ALU.mult))
                    pe("tokT")
                    done(V.tensor_tensor(tokm[:, :, :, :], psQ[:, 0:2 * HG * SLICES].rearrange("p (g h s) -> p g h s", g=2, h=HG),
                                         con[:, K_MASK:K_MASK + 64].rearrange("p (h s) -> p h s", h=HG).unsqueeze(1).broadcast_to(
                                             [P, 2, HG, SLICES]), ALU.mult))
                    own("tokm")
                    done(V.tensor_reduce(tok[:, :, :], tokm[:, :, :, :].rearrange("p g h s -> p g s h"), AX, ALU.add))
                    pe("out")
                    done(V.tensor_tensor(tmp[:, :, :], psO[:, :].rearrange("p (i c) -> p i c", i=PER),
                                         row(w[:, SR_BO:SR_BO + C], [P, PER, C]), ALU.add))
                    own("outb")
                    t_now = t_sb[:, bass.ds(img * PER, PER), :]
                    done(V.tensor_tensor(t_now, t_now, tmp[:, :, :], ALU.add))
EDGES = 262144
ECOLS = EDGES // P
COL_BITS, PART_BITS = 11, 7
NODES = TOK
SRC_BITS = 13
KEY_BASE = 0x20000000
OUTSIDE = 1 << 20
BIG = 1e30


def sort_stage(nc, edges, consts, src_d, keep_d, pen_d, first_d, ends_d, place_d, target0_d):
    import concourse.bass as bass
    from concourse import mybir
    from contextlib import ExitStack

    fp32, i32 = mybir.dt.float32, mybir.dt.int32
    ALU, ACT = mybir.AluOpType, mybir.ActivationFunctionType

    with ExitStack() as ctx:
        def sb(name, shape, dt=fp32):
            return ctx.enter_context(nc.sbuf_tensor("o_" + name, shape, dt))

        def sem(name):
            return ctx.enter_context(nc.semaphore("o_" + name))

        con = sb("con", [P, K_COLS])
        es, ed = sb("es", [P, ECOLS], i32), sb("ed", [P, ECOLS], i32)
        f1, f2 = sb("f1", [P, ECOLS]), sb("f2", [P, ECOLS])
        key = [sb("key0", [P, ECOLS]), sb("key1", [P, ECOLS])]
        edge_col = sb("edge_col", [P, 2], i32)
        es2 = sb("es2", [P, ECOLS], i32)
        place = sb("place", [P, ECOLS], i32)
        ps = ctx.enter_context(nc.psum_tensor("o_ps", [P, ECOLS], fp32))
        loaded, link, turned, copied, shifted, placed, stored = (
            sem(n) for n in ("loaded", "link", "turned", "copied", "shifted", "placed", "stored"))
        apart = sem("apart")
        BLOCKS = ECOLS // P

        steps = []
        for k in range(1, COL_BITS + PART_BITS + 1):
            steps.append(("flip", k))
            if k > COL_BITS:
                steps.append(("turn", None))
                steps += [("across", j - COL_BITS) for j in range(k - 1, COL_BITS - 1, -1)]
                steps.append(("turn", None))
            steps += [("along", j) for j in range(min(k, COL_BITS) - 1, -1, -1)]
        link_at, buf_at, made, buf = {}, {}, 9, 0
        for n, (kind, at) in enumerate(steps):
            link_at[n], buf_at[n] = made, buf
            if kind == "flip":
                made += 2 if at == COL_BITS else 1
            elif kind != "turn":
                made, buf = made + 2, 1 - buf
        TURNS = [n for n, (kind, _) in enumerate(steps) if kind == "turn"]

        with nc.Block() as block:
            @block.sync
            def _(sp):
                sp.dma_start(con[:, :], consts).then_inc(loaded, 16)
                sp.dma_start(es[:, :], edges[0, :, :]).then_inc(loaded, 16)
                sp.dma_start(ed[:, :], edges[1, :, :]).then_inc(loaded, 16)
                sp.wait_ge(shifted, 2)
                sp.wait_ge(apart, 1)
                sp.dma_start(edge_col[1:P, 0:1], ed[0:P - 1, ECOLS - 1:ECOLS]).then_inc(placed, 16)
                sp.dma_start(edge_col[0:P - 1, 1:2], ed[1:P, 0:1]).then_inc(placed, 16)
                sp.dma_start(src_d, es[:, :]).then_inc(stored, 16)
                sp.dma_start(target0_d, ed[:, 0:1]).then_inc(stored, 16)
                sp.wait_ge(copied, len(TURNS) + 1)
                sp.dma_start(keep_d, f1[:, :]).then_inc(stored, 16)
                sp.dma_start(pen_d, f2[:, :]).then_inc(stored, 16)
                sp.wait_ge(copied, len(TURNS) + 2)
                sp.dma_start(first_d, key[0][:, :]).then_inc(stored, 16)
                sp.wait_ge(copied, len(TURNS) + 3)
                sp.dma_start(ends_d, key[1][:, :].bitcast(i32)).then_inc(stored, 16)
                sp.dma_start(place_d, place[:, :]).then_inc(stored, 16)
                sp.wait_ge(stored, 16 * 7)

            @block.gpsimd
            def _(pool):
                nc.gpsimd.iota(place[:, :], pattern=[[2, ECOLS]], base=0, channel_multiplier=2 * ECOLS).then_inc(shifted, 1)
                nc.gpsimd.memset(edge_col[:, :], -1).then_inc(shifted, 1)

            @block.tensor
            def _(pe):
                pe.wait_ge(loaded, 48)
                for turn, n in enumerate(TURNS):
                    pe.wait_ge(link, link_at[n])
                    for r in range(BLOCKS):
                        last = nc.tensor.transpose(ps[:, r * P:(r + 1) * P], key[buf_at[n]][:, r * P:(r + 1) * P],
                                                   con[:, K_ID:K_ID + P])
                    last.then_inc(turned, 1)

            @block.scalar
            def _(act):
                for turn, n in enumerate(TURNS):
                    act.wait_ge(turned, turn + 1)
                    nc.scalar.activation(key[buf_at[n]][:, :], ps[:, :], ACT.Copy).then_inc(copied, 1)

            @block.vector
            def _(dve):
                V = nc.vector
                count = [0]

                def after(ins):
                    ins.then_inc(link, 1)
                    count[0] += 1

                def ready():
                    dve.wait_ge(link, count[0])

                dve.wait_ge(loaded, 48)
                after(V.tensor_scalar(f1[:, :], es[:, :], 0.0, float(NODES), ALU.is_lt, ALU.mult)); ready()
                after(V.tensor_tensor(f1[:, :], f1[:, :], es[:, :], ALU.add)); ready()
                after(V.tensor_scalar(es[:, :], f1[:, :], 0.0, float(NODES - 1), ALU.max, ALU.min)); ready()
                after(V.tensor_scalar(f1[:, :], ed[:, :], 0.0, float(NODES), ALU.is_lt, ALU.mult)); ready()
                after(V.tensor_scalar(f2[:, :], ed[:, :], 0.0, float(NODES), ALU.max, ALU.min)); ready()
                after(V.tensor_tensor(f1[:, :], f1[:, :], f2[:, :], ALU.add)); ready()
                after(V.tensor_scalar(ed[:, :], f1[:, :], float(NODES), None, ALU.min)); ready()
                after(V.tensor_scalar(ed[:, :], ed[:, :], SRC_BITS, KEY_BASE, ALU.logical_shift_left, ALU.bitwise_or)); ready()
                after(V.tensor_tensor(key[0][:, :].bitcast(i32), ed[:, :], es[:, :], ALU.bitwise_or)); ready()

                cur, turns = 0, 0
                for n, (kind, at) in enumerate(steps):
                    K = key[cur]
                    if kind == "flip" and at < COL_BITS:
                        w = 1 << (at - 1)
                        four = K[:, :].rearrange("p (b w) -> p b w", w=4 * w)
                        part = four[:, :, w:3 * w] if at > 1 else four[:, :, 2:4]
                        after(V.tensor_scalar(part, part, -1.0, None, ALU.mult)); ready()
                    elif kind == "flip" and at == COL_BITS:
                        half = ECOLS // 2
                        for h in range(2):
                            part = K[:, h * half:(h + 1) * half]
                            after(V.tensor_scalar(part, part, con[:, K_SIGN + h:K_SIGN + h + 1], None, ALU.mult))
                        ready()
                    elif kind == "flip":
                        c = K_SIGN + 1 + at - COL_BITS
                        after(V.tensor_scalar(K[:, :], K[:, :], con[:, c:c + 1], None, ALU.mult)); ready()
                    elif kind == "turn":
                        assert (link_at[n], buf_at[n]) == (count[0], cur)
                        turns += 1
                        dve.wait_ge(copied, turns)
                    else:
                        w = 1 << at
                        a = K[:, :].rearrange("p (b two w) -> p b two w", two=2, w=w)
                        o = key[1 - cur][:, :].rearrange("p (b two w) -> p b two w", two=2, w=w)
                        after(V.tensor_tensor(o[:, :, 0, :], a[:, :, 0, :], a[:, :, 1, :], ALU.min))
                        after(V.tensor_tensor(o[:, :, 1, :], a[:, :, 0, :], a[:, :, 1, :], ALU.max))
                        ready()
                        cur = 1 - cur

                S = key[cur][:, :].bitcast(i32)
                after(V.tensor_scalar(es[:, :], S, NODES - 1, None, ALU.bitwise_and)); ready()
                V.tensor_scalar(ed[:, :], S, SRC_BITS, 2 * NODES - 1, ALU.logical_shift_right, ALU.bitwise_and).then_inc(apart, 1)
                dve.wait_ge(apart, 1)
                dve.wait_ge(placed, 32)
                after(V.tensor_tensor(f1[:, 1:ECOLS], ed[:, 1:ECOLS], ed[:, 0:ECOLS - 1], ALU.is_equal))
                after(V.tensor_tensor(f1[:, 0:1], ed[:, 0:1], edge_col[:, 0:1], ALU.is_equal)); ready()
                V.tensor_scalar(f2[:, :], f1[:, :], 1.0, BIG, ALU.subtract, ALU.mult).then_inc(copied, 1)
                dve.wait_ge(copied, len(TURNS) + 1)
                V.tensor_tensor_scan(key[0][:, :], f1[:, :], f1[:, :], 1.0, ALU.mult, ALU.mult).then_inc(copied, 1)
                dve.wait_ge(copied, len(TURNS) + 2)
                after(V.tensor_copy(es2[:, :], key[0][:, :])); ready()
                after(V.tensor_tensor(place[:, :], place[:, :], es2[:, :], ALU.bitwise_or)); ready()
                E1 = key[1][:, :].bitcast(i32)
                after(V.tensor_tensor(E1[:, 0:ECOLS - 1], ed[:, 0:ECOLS - 1], ed[:, 1:ECOLS], ALU.is_equal))
                after(V.tensor_tensor(E1[:, ECOLS - 1:ECOLS], ed[:, ECOLS - 1:ECOLS], edge_col[:, 1:2], ALU.is_equal)); ready()
                after(V.tensor_scalar(E1, E1, float(OUTSIDE), None, ALU.mult)); ready()
                V.tensor_tensor(E1, E1, ed[:, :], ALU.bitwise_or).then_inc(copied, 1)
                dve.wait_ge(copied, len(TURNS) + 3)


def graph_tables(nc):
    from concourse import mybir
    fp32, i32 = mybir.dt.float32, mybir.dt.int32

    def dram(name, shape, dt):
        return nc.dram_tensor("scratch_" + name, shape, dt, kind="Internal").ap()

    return {
        "src": dram("src", (P, ECOLS), i32), "keep": dram("keep", (P, ECOLS), fp32), "pen": dram("pen", (P, ECOLS), fp32),
        "first": dram("first", (P, ECOLS), fp32), "ends_i": dram("ends_i", (P, ECOLS), i32),
        "place_i": dram("place_i", (P, ECOLS), i32), "target0": dram("target0", (P, 1), i32),
        "ends": dram("ends", (NODES, 1), i32), "start": dram("start", (NODES, 1), i32),
        "node": dram("node", (NODES, 20), fp32), "target": dram("target", (NODES, 4), fp32),
        "place": dram("place", (EDGES, 4), fp32), "edge": dram("edge", (EDGES, 24), fp32),
        "carry": dram("carry", (P, 24), fp32),
    }
GATES = 4
HEADS_G = 4
HE = HEADS_G * GATES
ROW_T = HE + HEADS_G
ROW_O = 2 * HEADS_G + HE
CHUNK = 32
CHUNKS = ECOLS // CHUNK


class EndsNotes:

    def __init__(self, nc, ctx, ends_d, place_d, ends_tbl):
        from concourse import mybir
        i32 = mybir.dt.int32
        self.nc, self.ends_d, self.place_d, self.ends_tbl = nc, ends_d, place_d, ends_tbl
        self.ends, self.place = (ctx.enter_context(nc.sbuf_tensor("e_" + n, [P, ECOLS], i32)) for n in ("ends", "place"))
        self.ends_w, self.place_w = (ctx.enter_context(nc.sbuf_tensor("e_" + n, [P, CHUNK], i32)) for n in ("ends_w", "place_w"))
        self.none, self.gate = (ctx.enter_context(nc.sbuf_tensor("e_" + n, [P, TILES], i32)) for n in ("none", "gate"))
        self.loaded, self.copied, self.scattered, self.set_ = (
            ctx.enter_context(nc.semaphore("e_" + n)) for n in ("loaded", "copied", "scattered", "set"))

    def scatter(self, pool, first, last):
        import concourse.bass as bass
        from concourse import mybir
        nc = self.nc
        if first == 0:
            self.begin(pool)
        with pool.Fori(first, last) as c:
            pool.wait_ge(self.scattered, c * (16 * CHUNK) + 16)
            nc.gpsimd.tensor_copy(self.ends_w[:, :], self.ends[:, bass.ds(c * CHUNK, CHUNK)]).then_inc(self.copied, 1)
            nc.gpsimd.tensor_copy(self.place_w[:, :], self.place[:, bass.ds(c * CHUNK, CHUNK)]).then_inc(self.copied, 1)
            pool.wait_ge(self.copied, c * 2 + 2)
            nc.gpsimd.tensor_tensor(self.gate[:, 0:1], self.gate[:, 1:2], self.gate[:, 2:3], mybir.AluOpType.add)
            for j in range(CHUNK):
                nc.gpsimd.indirect_dma_start(
                    out=self.ends_tbl, out_offset=bass.IndirectOffsetOnAxis(ap=self.ends_w[:, j:j + 1], axis=0),
                    in_=self.place_w[:, j:j + 1], in_offset=None, bounds_check=NODES - 1, oob_is_err=False,
                ).then_inc(self.scattered, 16)
        pool.wait_ge(self.scattered, 16 * CHUNK * last + 16)

    def begin(self, pool):
        nc = self.nc
        pool.dma_start(self.ends[:, :], self.ends_d).then_inc(self.loaded, 16)
        pool.dma_start(self.place[:, :], self.place_d).then_inc(self.loaded, 16)
        nc.gpsimd.memset(self.none[:, :], -1).then_inc(self.set_, 1)
        nc.gpsimd.memset(self.gate[:, :], 0).then_inc(self.set_, 1)
        pool.wait_ge(self.set_, 2)
        pool.dma_start(self.ends_tbl.rearrange("(p i) o -> p (i o)", p=P), self.none[:, :]).then_inc(self.scattered, 16)
        pool.wait_ge(self.loaded, 32)


def graph_stage(nc, att_rows, feat, tables, x):
    import concourse.bass as bass
    from concourse import mybir
    from contextlib import ExitStack

    fp32, i32 = mybir.dt.float32, mybir.dt.int32
    ALU, ACT, AX = mybir.AluOpType, mybir.ActivationFunctionType, mybir.AxisListType.X
    Off = bass.IndirectOffsetOnAxis
    node_tbl, target_tbl, place_tbl, edge_tbl, carry_tbl, start_tbl, ends_tbl = (
        tables[n] for n in ("node", "target", "place", "edge", "carry", "start", "ends"))
    scores = x["scores"]

    def whole(t):
        return t[tuple([slice(None)] * len(t.shape))]

    with ExitStack() as outer:
        def keep_sb(name, shape, dt=fp32):
            return outer.enter_context(nc.sbuf_tensor("r_" + name, shape, dt))

        row = keep_sb("row", [P, TILES, ROW_T])
        adst = keep_sb("adst", [P, TILES, HEADS_G])
        att = keep_sb("att", [P, 5 * HE])
        end_i, end_f = keep_sb("end_i", [P, TILES], i32), keep_sb("end_f", [P, TILES])
        end_idx, start_idx, carry_idx = (keep_sb(n, [P, TILES], i32) for n in ("end_idx", "start_idx", "carry_idx"))
        state = keep_sb("state", [P, ROW_O])
        ad0 = keep_sb("ad0", [P, HEADS_G])

        with ExitStack() as ctx:
            def sb(name, shape, dt=fp32):
                return ctx.enter_context(nc.sbuf_tensor("n_" + name, shape, dt))

            def sem(name):
                return ctx.enter_context(nc.semaphore("n_" + name))

            prod = sb("prod", [P, TILES, HE])
            zero = sb("zero", [P, ECOLS])
            line = sb("line", [1, NODES], i32)
            top = sb("top", [1, NODES + 1])
            t0 = sb("t0", [P, 1], i32)
            part = sb("part", [P, TILES], i32)
            lf, lg = sb("lf", [P, TILES]), sb("lg", [P, TILES])
            loaded, zeroed, link, rows_out, starts_out, starts_in, filled, spread = (
                sem(n) for n in ("loaded", "zeroed", "link", "rows_out", "starts_out", "starts_in", "filled", "spread"))

            with nc.Block() as block:
                NODE_ROWS, START_ROW = 5, 11

                @block.sync
                def _(sp):
                    sp.dma_start(whole(att), att_rows).then_inc(loaded, 16)
                    sp.dma_start(line[:, :], ends_tbl.rearrange("n o -> o n")).then_inc(loaded, 16)
                    sp.dma_start(end_i[:, :], ends_tbl.rearrange("(i p) o -> p (i o)", p=P),
                                 allow_slow_non_contiguous=True).then_inc(loaded, 16)
                    sp.dma_start(t0[:, :], x["target0"]).then_inc(loaded, 16)
                    sp.wait_ge(zeroed, 1)
                    place_v = place_tbl.rearrange("(q p c) h -> q p (c h)", q=4, p=P)
                    for q in range(4):
                        sp.dma_start(place_v[q, :, :], zero[:, :]).then_inc(filled, 16)
                    sp.wait_ge(link, NODE_ROWS)
                    sp.dma_start(node_tbl.rearrange("(i p) f -> p i f", p=P), whole(row)).then_inc(rows_out, 16)
                    sp.dma_start(target_tbl.rearrange("(i p) f -> p i f", p=P), whole(adst)).then_inc(rows_out, 16)
                    sp.wait_ge(link, START_ROW)
                    sp.dma_start(start_tbl.rearrange("n o -> o n"), line[:, :]).then_inc(starts_out, 16)
                    sp.wait_ge(starts_out, 16)
                    sp.dma_start(start_idx[:, :], start_tbl.rearrange("(i p) o -> p (i o)", p=P),
                                 allow_slow_non_contiguous=True).then_inc(starts_in, 16)
                    sp.wait_ge(starts_in, 16)

                @block.gpsimd
                def _(pool):
                    nc.gpsimd.memset(zero[:, :], 0.0).then_inc(zeroed, 1)
                    nc.gpsimd.memset(ad0[:, :], 0.0).then_inc(zeroed, 1)
                    pool.wait_ge(zeroed, 2)
                    pool.wait_ge(loaded, 64)
                    pool.wait_ge(rows_out, 32)
                    nc.gpsimd.indirect_dma_start(out=ad0[:, :], out_offset=None, in_=target_tbl,
                                                 in_offset=Off(ap=t0[:, 0:1], axis=0),
                                                 bounds_check=NODES - 1, oob_is_err=False).then_inc(spread, 16)
                    pool.wait_ge(filled, 64)
                    pool.wait_ge(starts_in, 16)
                    for i in range(TILES):
                        nc.gpsimd.indirect_dma_start(out=place_tbl, out_offset=Off(ap=start_idx[:, i:i + 1], axis=0),
                                                     in_=adst[:, i, :], in_offset=None,
                                                     bounds_check=EDGES - 1, oob_is_err=False).then_inc(spread, 16)
                    pool.wait_ge(spread, 16 * (TILES + 1))

                @block.vector
                def _(dve):
                    V = nc.vector
                    count = [0]

                    def link_(ins):
                        ins.then_inc(link, 1)
                        count[0] += 1
                        dve.wait_ge(link, count[0])

                    dve.wait_ge(loaded, 64)

                    def att_sum(out, at):
                        link_(V.tensor_tensor(whole(prod), whole(feat), att[:, at * HE:(at + 1) * HE].unsqueeze(1).broadcast_to([P, TILES, HE]), ALU.mult))
                        link_(V.tensor_reduce(out, prod[:, :, :].rearrange("p i (h e) -> p i h e", h=HEADS_G), AX, ALU.add))

                    att_sum(adst[:, :, :], 1)
                    att_sum(row[:, :, HE:ROW_T], 0)
                    link_(V.tensor_copy(row[:, :, 0:HE], whole(feat)))
                    assert count[0] == NODE_ROWS
                    link_(V.tensor_scalar(line[:, :], line[:, :], 1, None, ALU.arith_shift_right))
                    link_(V.memset(top[:, 0:1], -1.0))
                    link_(V.tensor_tensor_scan(top[:, 1:NODES + 1], line[:, :], line[:, :], -1.0, ALU.max, ALU.max))
                    link_(V.tensor_scalar(line[:, :], line[:, :], 0.0, float(OUTSIDE), ALU.is_lt, ALU.mult))
                    link_(V.scalar_tensor_tensor(line[:, :], top[:, 0:NODES], 1.0, line[:, :], ALU.add, ALU.add))
                    link_(V.tensor_copy(part[:, :], end_i[:, :]))
                    assert count[0] == START_ROW
                    link_(V.tensor_scalar(end_idx[:, :], end_i[:, :], 1, None, ALU.arith_shift_right))
                    link_(V.tensor_copy(end_f[:, :], end_idx[:, :]))
                    link_(V.tensor_scalar(lg[:, :], end_f[:, :], 0.0, 2.0 * OUTSIDE, ALU.is_lt, ALU.mult))
                    link_(V.tensor_tensor(end_f[:, :], end_f[:, :], lg[:, :], ALU.add))
                    link_(V.tensor_scalar(part[:, :], part[:, :], 1, None, ALU.bitwise_and))
                    link_(V.tensor_copy(lf[:, :], part[:, :]))
                    link_(V.tensor_scalar(lf[:, :], lf[:, :], -float(OUTSIDE), float(OUTSIDE), ALU.mult, ALU.add))
                    link_(V.tensor_tensor(lf[:, :], lf[:, :], lg[:, :], ALU.add))
                    link_(V.tensor_scalar(part[:, :], end_idx[:, :], COL_BITS, None, ALU.arith_shift_right))
                    link_(V.tensor_copy(lg[:, :], part[:, :]))
                    link_(V.tensor_tensor(carry_idx[:, :], lf[:, :], lg[:, :], ALU.add))
                    link_(V.tensor_copy(end_idx[:, :], end_f[:, :]))

        with ExitStack() as ctx:
            def sb(name, shape, dt=fp32):
                return ctx.enter_context(nc.sbuf_tensor("g2_" + name, shape, dt))

            def sem(name):
                return ctx.enter_context(nc.semaphore("g2_" + name))

            src = sb("src", [P, ECOLS], i32)
            keep, pen = sb("keep", [P, ECOLS]), sb("pen", [P, ECOLS])
            tgt = sb("tgt", [P, ECOLS, HEADS_G])
            gate, spare, done = sb("gate", [P, 4]), sb("spare", [P, 4]), sb("done", [P, 1])
            idx = [sb(f"idx{k}", [P, CHUNK], i32) for k in range(2)]
            got = [sb(f"got{k}", [P, CHUNK, ROW_T]) for k in range(2)]
            out = [sb(f"out{k}", [P, CHUNK, ROW_O]) for k in range(2)]
            ad, e, w, r = (sb(n, [P, HEADS_G, CHUNK]) for n in ("ad", "e", "w", "r"))
            m = sb("m", [P, HEADS_G, CHUNK + 1])
            msg = sb("msg", [P, HE, CHUNK])
            loaded, copied, set_, link = sem("loaded"), sem("copied"), sem("set"), sem("link")
            gathered = [sem("gathered0"), sem("gathered1")]
            consumed, exps, written = sem("consumed"), sem("exps"), [sem("written0"), sem("written1")]
            DVE_STEPS = Steps("t1 t2 t3 t4 adkeep e leaky m1 m2 m3 m4 w0 r0 r1 s1 s2 s3 s4 msg "
                              + " ".join(f"f{k}" for k in range(HE)) + " mcopy mkeep skeep")
            edge_v = edge_tbl.rearrange("(p c) f -> p (c f)", p=P)

            with nc.Block() as block:
                @block.sync
                def _(sp):
                    sp.dma_start(src[:, :], x["src"]).then_inc(loaded, 16)
                    sp.dma_start(keep[:, :], x["keep"]).then_inc(loaded, 16)
                    sp.dma_start(pen[:, :], x["pen"]).then_inc(loaded, 16)
                    sp.dma_start(whole(tgt), place_tbl.rearrange("(p c) h -> p c h", p=P)).then_inc(loaded, 16)
                    for k in range(2):
                        sp.dma_start(spare[:, 2 * k:2 * k + 2], x["first"][:, 0:2]).then_inc(written[k], 16)
                    with sp.Fori(0, CHUNKS // 2) as pair:
                        for k in range(2):
                            c = pair * 2 + k
                            sp.wait_ge(link, DVE_STEPS.after("skeep", c))
                            sp.dma_start(edge_v[:, bass.ds(c * (CHUNK * ROW_O), CHUNK * ROW_O)],
                                         out[k][:, :, :].rearrange("p c f -> p (c f)")).then_inc(written[k], 16)
                    for k in range(2):
                        sp.wait_ge(written[k], 16 * (CHUNKS // 2) + 16)

                @block.gpsimd
                def _(pool):
                    nc.gpsimd.memset(gate[:, :], 0.0).then_inc(set_, 1)
                    pool.wait_ge(loaded, 64)
                    pool.wait_ge(set_, 1)
                    with pool.Fori(0, CHUNKS // 2) as pair:
                        for k in range(2):
                            c = pair * 2 + k
                            pool.wait_ge(consumed, c + 1)
                            nc.gpsimd.tensor_copy(idx[k][:, :], src[:, bass.ds(c * CHUNK, CHUNK)]).then_inc(copied, 1)
                            pool.wait_ge(copied, c + 1)
                            nc.gpsimd.tensor_tensor(gate[:, 0:1], gate[:, 1:2], gate[:, 2:3], ALU.add)
                            for j in range(CHUNK):
                                nc.gpsimd.indirect_dma_start(out=got[k][:, j, :], out_offset=None, in_=node_tbl,
                                                             in_offset=Off(ap=idx[k][:, j:j + 1], axis=0),
                                                             bounds_check=NODES - 1, oob_is_err=False).then_inc(gathered[k], 16)

                @block.scalar
                def _(act):
                    nc.scalar.preload_act_table_set("natural_log_exp_and_others")
                    with act.Fori(0, CHUNKS) as c:
                        act.wait_ge(link, DVE_STEPS.after("w0", c))
                        nc.scalar.activation(w[:, :, :], w[:, :, :], ACT.Exp).then_inc(exps, 1)
                        act.wait_ge(link, DVE_STEPS.after("r1", c))
                        nc.scalar.activation(r[:, :, :], r[:, :, :], ACT.Exp).then_inc(exps, 1)

                @block.vector
                def _(dve):
                    V = nc.vector
                    dve.wait_ge(loaded, 64)
                    V.memset(m[:, :, 0:1], -BIG).then_inc(link, 1)
                    V.memset(state[:, :], 0.0).then_inc(consumed, 2)
                    dve.wait_ge(link, 1)
                    dve.wait_ge(consumed, 2)
                    with dve.Fori(0, CHUNKS // 2) as pair:
                        for k in range(2):
                            c = pair * 2 + k
                            cols = bass.ds(c * CHUNK, CHUNK)

                            def own(name):
                                dve.wait_ge(link, DVE_STEPS.after(name, c))

                            for h in range(HEADS_G):
                                V.tensor_tensor_scan(ad[:, h, :], keep[:, cols], tgt[:, cols, h:h + 1].rearrange("p c o -> p (c o)"),
                                                     ad0[:, h:h + 1], ALU.mult, ALU.add).then_inc(link, 1)
                            own("t4")
                            V.tensor_copy(ad0[:, :], ad[:, :, CHUNK - 1]).then_inc(link, 1)
                            dve.wait_ge(gathered[k], pair * (16 * CHUNK) + 16 * CHUNK)
                            V.tensor_tensor(e[:, :, :], ad[:, :, :], got[k][:, :, HE:ROW_T].rearrange("p c h -> p h c"),
                                            ALU.add).then_inc(link, 1)
                            own("e")
                            V.scalar_tensor_tensor(e[:, :, :], e[:, :, :], 0.2, e[:, :, :], ALU.mult, ALU.max).then_inc(link, 1)
                            own("leaky")
                            for h in range(HEADS_G):
                                V.tensor_tensor_scan(m[:, h, 1:CHUNK + 1], pen[:, cols], e[:, h, :],
                                                     m[:, h, 0:1], ALU.add, ALU.max).then_inc(link, 1)
                            own("m4")
                            V.tensor_tensor(w[:, :, :], e[:, :, :], m[:, :, 1:CHUNK + 1], ALU.subtract).then_inc(link, 1)
                            V.tensor_tensor(r[:, :, :], m[:, :, 0:CHUNK],
                                            pen[:, cols].unsqueeze(1).broadcast_to([P, HEADS_G, CHUNK]), ALU.add).then_inc(link, 1)
                            own("r0")
                            V.tensor_tensor(r[:, :, :], r[:, :, :], m[:, :, 1:CHUNK + 1], ALU.subtract).then_inc(link, 1)
                            dve.wait_ge(exps, c * 2 + 2)
                            dve.wait_ge(written[k], pair * 16 + 16)
                            for h in range(HEADS_G):
                                V.tensor_tensor_scan(out[k][:, :, HEADS_G + h], r[:, h, :], w[:, h, :],
                                                     state[:, HEADS_G + h:HEADS_G + h + 1], ALU.mult, ALU.add).then_inc(link, 1)
                            V.tensor_tensor(msg[:, :, :].rearrange("p (h e) c -> p h e c", h=HEADS_G),
                                            got[k][:, :, 0:HE].rearrange("p c (h e) -> p h e c", h=HEADS_G),
                                            w[:, :, :].unsqueeze(2).broadcast_to([P, HEADS_G, GATES, CHUNK]), ALU.mult).then_inc(link, 1)
                            own("msg")
                            for f in range(HE):
                                V.tensor_tensor_scan(out[k][:, :, 2 * HEADS_G + f], r[:, f // GATES, :], msg[:, f, :],
                                                     state[:, 2 * HEADS_G + f:2 * HEADS_G + f + 1],
                                                     ALU.mult, ALU.add).then_inc(link, 1)
                            V.tensor_copy(out[k][:, :, 0:HEADS_G].rearrange("p c h -> p h c"), m[:, :, 1:CHUNK + 1]).then_inc(link, 1)
                            own("mcopy")
                            V.tensor_copy(m[:, :, 0:1], m[:, :, CHUNK:CHUNK + 1]).then_inc(link, 1)
                            V.tensor_copy(state[:, :], out[k][:, CHUNK - 1, :]).then_inc(link, 1)
                            own("skeep")
                            V.tensor_copy(done[:, 0:1], state[:, 0:1]).then_inc(consumed, 1)
                            dve.wait_ge(consumed, c + 3)

        with ExitStack() as ctx:
            def sb(name, shape, dt=fp32):
                return ctx.enter_context(nc.sbuf_tensor("k_" + name, shape, dt))

            def sem(name):
                return ctx.enter_context(nc.semaphore("k_" + name))

            con = sb("con", [P, K_COLS])
            whole_run = sb("whole_run", [P, 2])
            wide = sb("wide", [P, 4, HE])
            line, prev = sb("line", [HE, 4, P]), sb("prev", [HE, P])
            grow, wt = sb("grow", [HE, P]), sb("wt", [HE, P])
            shifted = sb("shifted", [HE, 3, P])
            back = sb("back", [P, ROW_O])
            ps = ctx.enter_context(nc.psum_tensor("k_ps", [P, HALF], fp32))
            ps2 = ctx.enter_context(nc.psum_tensor("k_ps2", [P, HALF], fp32))
            loaded, link, pe_done, exp_done, out_done = sem("loaded"), sem("link"), sem("pe"), sem("exp"), sem("out")
            exp_in = sem("exp_in")

            with nc.Block() as block:
                WIDE, EXPS, SHIFTED, LAST = 4, 11, 18, 21

                @block.sync
                def _(sp):
                    sp.dma_start(con[:, :], x["consts"]).then_inc(loaded, 16)
                    sp.dma_start(whole_run[:, :], x["first"][:, ECOLS - 2:ECOLS]).then_inc(loaded, 16)
                    sp.wait_ge(link, LAST)
                    sp.dma_start(carry_tbl, back[:, :]).then_inc(out_done, 16)
                    sp.wait_ge(out_done, 16)

                @block.tensor
                def _(pe):
                    pe.wait_ge(loaded, 32)
                    pe.wait_ge(link, WIDE)
                    for q in range(4):
                        last = nc.tensor.transpose(ps[0:HE, q * P:(q + 1) * P], wide[:, q, :], con[:, K_ID:K_ID + P])
                    last.then_inc(pe_done, 1)
                    pe.wait_ge(link, SHIFTED)
                    for q in range(3):
                        last = nc.tensor.transpose(ps2[:, q * HE:(q + 1) * HE], shifted[:, q, :], con[0:HE, K_ID:K_ID + HE])
                    last.then_inc(pe_done, 1)

                @block.scalar
                def _(act):
                    act.wait_ge(link, EXPS)
                    nc.scalar.activation(grow[:, :], grow[:, :], ACT.Exp).then_inc(exp_done, 1)
                    nc.scalar.activation(wt[:, :], wt[:, :], ACT.Exp).then_inc(exp_done, 1)

                @block.vector
                def _(dve):
                    V = nc.vector
                    count = [0]

                    def link_(ins):
                        ins.then_inc(link, 1)
                        count[0] += 1
                        dve.wait_ge(link, count[0])

                    def spread(a):
                        return a.unsqueeze(2).broadcast_to([P, HEADS_G, GATES])

                    def q4(q):
                        return wide[:, q, :].rearrange("p (h e) -> p h e", h=HEADS_G)

                    dve.wait_ge(loaded, 32)
                    link_(V.tensor_copy(wide[:, 0, :], whole_run[:, 1:2].broadcast_to([P, HE])))
                    link_(V.tensor_copy(q4(1), spread(state[:, 0:HEADS_G])))
                    link_(V.tensor_copy(q4(2), spread(state[:, HEADS_G:2 * HEADS_G])))
                    link_(V.tensor_copy(wide[:, 3, :], state[:, 2 * HEADS_G:ROW_O]))
                    assert count[0] == WIDE
                    dve.wait_ge(pe_done, 1)
                    link_(V.tensor_copy(line[:, :, :], ps[0:HE, :].rearrange("p (q c) -> p q c", q=4)))
                    link_(V.tensor_scalar(line[:, 0, :], line[:, 0, :], 1.0, BIG, ALU.subtract, ALU.mult))
                    link_(V.tensor_tensor_scan(shifted[:, 0, :], line[:, 0, :], line[:, 1, :], -BIG, ALU.add, ALU.max))
                    link_(V.memset(prev[:, 0:1], -BIG))
                    link_(V.tensor_copy(prev[:, 1:P], shifted[:, 0, 0:P - 1]))
                    link_(V.tensor_tensor(grow[:, :], prev[:, :], line[:, 0, :], ALU.add))
                    V.tensor_tensor(wt[:, :], line[:, 1, :], shifted[:, 0, :], ALU.subtract).then_inc(exp_in, 1)
                    dve.wait_ge(exp_in, 1)
                    link_(V.tensor_tensor(grow[:, :], grow[:, :], shifted[:, 0, :], ALU.subtract))
                    assert count[0] == EXPS
                    dve.wait_ge(exp_done, 2)
                    link_(V.tensor_tensor(line[:, 2, :], line[:, 2, :], wt[:, :], ALU.mult))
                    link_(V.tensor_tensor(line[:, 3, :], line[:, 3, :], wt[:, :], ALU.mult))
                    link_(V.memset(shifted[:, 1:3, 0:1], 0.0))
                    link_(V.tensor_tensor_scan(shifted[:, 1, 1:P], grow[:, 0:P - 1], line[:, 2, 0:P - 1], 0.0, ALU.mult, ALU.add))
                    link_(V.tensor_tensor_scan(shifted[:, 2, 1:P], grow[:, 0:P - 1], line[:, 3, 0:P - 1], 0.0, ALU.mult, ALU.add))
                    link_(V.tensor_copy(shifted[:, 0, :], prev[:, :]))
                    link_(V.memset(line[:, 0, 0:1], 0.0))
                    assert count[0] == SHIFTED
                    dve.wait_ge(pe_done, 2)

                    def head(q):
                        return ps2[:, q * HE:(q + 1) * HE].rearrange("p (h e) -> p h e", h=HEADS_G)[:, :, 0]

                    link_(V.tensor_copy(back[:, 0:HEADS_G], head(0)))
                    link_(V.tensor_copy(back[:, HEADS_G:2 * HEADS_G], head(1)))
                    link_(V.tensor_copy(back[:, 2 * HEADS_G:ROW_O], ps2[:, 2 * HE:3 * HE]))
                    assert count[0] == LAST

        with ExitStack() as ctx:
            def sb(name, shape, dt=fp32):
                return ctx.enter_context(nc.sbuf_tensor("j_" + name, shape, dt))

            def sem(name):
                return ctx.enter_context(nc.semaphore("j_" + name))

            near, far = sb("near", [P, TILES, ROW_O]), sb("far", [P, TILES, ROW_O])
            H4, H16 = [P, TILES, HEADS_G], [P, TILES, HE]
            es, top = sb("es", H4), sb("top", H4)
            wts = sb("wts", [P, 3, TILES, HEADS_G])
            den, tmp4 = sb("den", H4), sb("tmp4", H4)
            agg, tmp = sb("agg", H16), sb("tmp", H16)
            mean, rstd = sb("mean", [P, TILES]), sb("rstd", [P, TILES])
            eps = sb("eps", [P, 1])
            set_, link, taken, exps = sem("set"), sem("link"), sem("taken"), sem("exps")

            with nc.Block() as block:
                VAR = 25

                @block.gpsimd
                def _(pool):
                    G = nc.gpsimd
                    for t in (near, far):
                        G.memset(t[:, :, 0:HEADS_G], -BIG).then_inc(set_, 1)
                        G.memset(t[:, :, HEADS_G:ROW_O], 0.0).then_inc(set_, 1)
                    G.memset(eps[:, :], 1e-5).then_inc(set_, 1)
                    pool.wait_ge(set_, 5)
                    for i in range(TILES):
                        G.indirect_dma_start(out=near[:, i, :], out_offset=None, in_=edge_tbl,
                                             in_offset=Off(ap=end_idx[:, i:i + 1], axis=0),
                                             bounds_check=EDGES - 1, oob_is_err=False).then_inc(taken, 16)
                        G.indirect_dma_start(out=far[:, i, :], out_offset=None, in_=carry_tbl,
                                             in_offset=Off(ap=carry_idx[:, i:i + 1], axis=0),
                                             bounds_check=P - 1, oob_is_err=False).then_inc(taken, 16)

                @block.scalar
                def _(act):
                    nc.scalar.preload_act_table_set("natural_log_exp_and_others")
                    act.wait_ge(link, 7)
                    nc.scalar.activation(whole(wts), whole(wts), ACT.Exp).then_inc(exps, 1)
                    act.wait_ge(link, VAR)
                    nc.scalar.activation(rstd[:, :], rstd[:, :], ACT.Ln, bias=eps[:, :], scale=1.0 / HE).then_inc(exps, 1)
                    act.wait_ge(exps, 2)
                    nc.scalar.activation(rstd[:, :], rstd[:, :], ACT.Exp, scale=-0.5).then_inc(exps, 1)

                @block.vector
                def _(dve):
                    V = nc.vector
                    TT = V.tensor_tensor
                    count = [0]

                    def link_(ins):
                        ins.then_inc(link, 1)
                        count[0] += 1
                        dve.wait_ge(link, count[0])

                    def spread(a):
                        return a.unsqueeze(3).broadcast_to([P, TILES, HEADS_G, GATES])

                    def heads(a):
                        return a.rearrange("p i (h e) -> p i h e", h=HEADS_G)

                    def vec(at):
                        return att[:, at * HE:(at + 1) * HE].unsqueeze(1).broadcast_to(H16)

                    NM, NS, NF = slice(0, HEADS_G), slice(HEADS_G, 2 * HEADS_G), slice(2 * HEADS_G, ROW_O)
                    dve.wait_ge(set_, 5)
                    link_(TT(whole(es), row[:, :, HE:ROW_T], whole(adst), ALU.add))
                    link_(V.scalar_tensor_tensor(whole(es), whole(es), 0.2, whole(es), ALU.mult, ALU.max))
                    dve.wait_ge(taken, 16 * 2 * TILES)
                    link_(TT(whole(top), near[:, :, NM], far[:, :, NM], ALU.max))
                    link_(TT(whole(top), whole(top), whole(es), ALU.max))
                    link_(TT(wts[:, 0, :, :], near[:, :, NM], whole(top), ALU.subtract))
                    link_(TT(wts[:, 1, :, :], far[:, :, NM], whole(top), ALU.subtract))
                    link_(TT(wts[:, 2, :, :], whole(es), whole(top), ALU.subtract))
                    dve.wait_ge(exps, 1)
                    link_(TT(whole(den), near[:, :, NS], wts[:, 0, :, :], ALU.mult))
                    link_(TT(whole(tmp4), far[:, :, NS], wts[:, 1, :, :], ALU.mult))
                    link_(TT(whole(den), whole(den), whole(tmp4), ALU.add))
                    link_(TT(whole(den), whole(den), wts[:, 2, :, :], ALU.add))
                    link_(V.tensor_scalar_add(whole(den), whole(den), 1e-16))
                    link_(V.reciprocal(whole(den), whole(den)))
                    link_(TT(heads(whole(agg)), heads(near[:, :, NF]), spread(wts[:, 0, :, :]), ALU.mult))
                    link_(TT(heads(whole(tmp)), heads(far[:, :, NF]), spread(wts[:, 1, :, :]), ALU.mult))
                    link_(TT(whole(agg), whole(agg), whole(tmp), ALU.add))
                    link_(TT(heads(whole(tmp)), heads(row[:, :, 0:HE]), spread(wts[:, 2, :, :]), ALU.mult))
                    link_(TT(whole(agg), whole(agg), whole(tmp), ALU.add))
                    link_(TT(heads(whole(agg)), heads(whole(agg)), spread(whole(den)), ALU.mult))
                    link_(TT(whole(agg), whole(agg), vec(2), ALU.add))
                    link_(V.reduce_sum(mean[:, :], whole(agg), AX))
                    link_(V.tensor_scalar(mean[:, :], mean[:, :], 1.0 / HE, None, ALU.mult))
                    link_(TT(whole(agg), whole(agg), mean[:, :].unsqueeze(2).broadcast_to(H16), ALU.subtract))
                    link_(TT(whole(tmp), whole(agg), whole(agg), ALU.mult))
                    link_(V.reduce_sum(rstd[:, :], whole(tmp), AX))
                    assert count[0] == VAR
                    dve.wait_ge(exps, 3)
                    link_(TT(whole(agg), whole(agg), rstd[:, :].unsqueeze(2).broadcast_to(H16), ALU.mult))
                    link_(TT(whole(agg), whole(agg), vec(3), ALU.mult))
                    link_(TT(whole(agg), whole(agg), vec(4), ALU.add))
                    link_(V.tensor_reduce(whole(scores), agg[:, :, :].rearrange("p i (h e) -> p i e h", h=HEADS_G), AX, ALU.add))
                    link_(V.tensor_scalar(whole(scores), whole(scores), 1.0 / HEADS_G, None, ALU.mult))
def _blocks(w):
    import numpy as np
    out = np.zeros(w.shape[:-2] + (2 * w.shape[-2], 2 * w.shape[-1]), w.dtype)
    out[..., :w.shape[-2], :w.shape[-1]] = w
    out[..., w.shape[-2]:, w.shape[-1]:] = w
    return out


def _ssm_parameters(inp):
    import numpy as np
    T = lambda a: np.swapaxes(a, -1, -2)
    out = np.zeros((LAYERS, P, W_COLS), np.float32)
    out[:, :, W_PROJ:W_PROJ + P] = _blocks(T(inp["L0_conv_proj_w"]))
    out[:, :, W_CF:W_CF + P] = _blocks(T(inp["L0_conv_convf_w"]))
    out[:, :, W_CB:W_CB + P] = _blocks(T(inp["L0_conv_convb_w"]))
    dbc = inp["L0_conv_dbc_w"]
    out[:, :2 * RANK, W_DL:W_DL + P] = _blocks(dbc[:, :RANK])
    for part in range(3):
        out[:, :, W_B + 32 * part:W_B + 32 * part + 32] = _blocks(T(dbc[:, RANK:RANK + NST]))
        out[:, :, W_C + 32 * part:W_C + 32 * part + 32] = _blocks(T(dbc[:, RANK + NST:]))
    out[:, :2 * RANK, W_DT:W_DT + P] = _blocks(T(inp["L0_conv_dtp_w"]))
    for col, name in ((V_G, "ln_g"), (V_LB, "ln_b"), (V_PB, "proj_b"), (V_CFB, "convf_b"), (V_CBB, "convb_b"), (V_DTB, "dtp_b"), (V_D, "D_param")):
        out[:, :, col] = np.concatenate([inp["L0_conv_" + name]] * 2, 1)
    out[:, :, V_ALOG:V_ALOG + NST] = np.concatenate([inp["L0_conv_A_log"]] * 2, 1)
    return out


def _constants():
    import numpy as np
    k = np.zeros((P, K_COLS), np.float32)
    row = np.arange(P)
    k[:, K_MEAN:K_MEAN + P] = (row[:, None] // C == row[None, :] // C) / np.float32(C)
    k[:, K_ID:K_ID + P] = np.eye(P)
    k[:, K_CEN:K_CEN + P] = k[:, K_ID:K_ID + P] - k[:, K_MEAN:K_MEAN + P]
    k[:, K_PAIR:K_PAIR + P] = (row[:, None] // 2 == row[None, :] // 2) / np.float32(2)
    k[:, K_ONE:K_ONE + P] = 1
    k[:, K_SPLIT] = np.where(row >= 32, -1, 0)
    k[:, K_SPLIT + 1] = np.where(row >= 64, -1, 0)
    k[:, K_SPLIT + 2] = 1e-5
    sign = lambda bit: 1 - 2 * ((row >> bit) & 1)
    k[:, K_SIGN], k[:, K_SIGN + 1] = sign(0), -sign(0)
    for b in range(1, 7):
        k[:, K_SIGN + 1 + b] = sign(b) * sign(b - 1)
    k[:, K_SIGN + 8] = sign(6)
    k[:, K_MASK:K_MASK + 64] = row[:, None] // 32 == np.arange(64)[None, :] // 16
    return k


def _selectors():
    import numpy as np
    k = np.arange(96)[:, None, None] % 32
    n = np.arange(NST)[None, :, None]
    m = np.arange(P)[None, None, :]
    return (k == (m // C) * NST + n).astype(np.float32).reshape(96, NST * P)


def _conv_weights(inp):
    import numpy as np
    out = np.zeros((P, CW_COLS), np.float32)
    tap = lambda w: w.transpose(2, 3, 1, 0).reshape(9, C, w.shape[0])
    for col, w in ((CW_Q, inp["L1_conv_wq"]), (CW_K, inp["L1_conv_wk"])):
        padded = np.zeros((9, C, 32), np.float32)
        padded[:, :, :C // 4] = tap(w)
        out[:, col:col + 9 * Q_COLS] = _blocks(padded).transpose(1, 0, 2).reshape(P, -1)
    out[:, CW_V:CW_V + 9 * P] = _blocks(tap(inp["L1_conv_wv"])).transpose(1, 0, 2).reshape(P, -1)
    out[:, CW_FC1:CW_FC1 + 8] = _blocks(inp["L1_conv_fc1_w"].T)
    out[:8, CW_FC2:CW_FC2 + P] = _blocks(inp["L1_conv_fc2_w"].T)
    fuse = inp["L1_conv_fuse_w"][:, :, 0, 0].T
    out[:C, CW_FL:CW_FL + C] = fuse[:C]
    out[:C, CW_FG:CW_FG + C] = out[C:, CW_FG:CW_FG + C] = fuse[C:]
    for b in range(2):
        out[32 * b:32 * b + 16, CV_BQ] = inp["L1_conv_bq"]
        out[32 * b:32 * b + 16, CV_BK] = inp["L1_conv_bk"]
        out[4 * b:4 * b + 4, CV_B1] = inp["L1_conv_fc1_b"]
        out[C * b:C * (b + 1), CV_B2] = inp["L1_conv_fc2_b"]
    out[:, CV_BV] = np.concatenate([inp["L1_conv_bv"]] * 2)
    out[:, CR_FB:CR_FB + C] = inp["L1_conv_fuse_b"][None]
    return out


def _padded_heads(w):
    import numpy as np
    out = np.zeros((C, HEADS2, 32), np.float32)
    out[:, :, :HDIM2] = w.reshape(C, HEADS2, HDIM2)
    return out.reshape(C, P)


def _slice_weights(inp):
    import numpy as np
    out = np.zeros((P, SW_COLS), np.float32)
    out[:C, SW_0:SW_0 + C] = inp["L3_attn_W0"]
    out[:C, SW_S:SW_S + SLICES] = inp["L3_attn_Ws"]
    out[:C, SW_QKV:SW_QKV + 3 * HD3] = inp["L3_attn_Wqkv"]
    out[C, SW_QKV:SW_QKV + 3 * HD3] = inp["L3_attn_bqkv"]
    out[:, SW_OUT:SW_OUT + 2 * C] = inp["L3_attn_Wout"].reshape(2, P, C).transpose(1, 0, 2).reshape(P, 2 * C)
    out[:C, SV_B0] = inp["L3_attn_b0"]
    out[:, SR_B0:SR_B0 + C] = inp["L3_attn_b0"][None]
    out[:, SR_BS:SR_BS + SLICES] = inp["L3_attn_bs"][None]
    out[:, SR_BO:SR_BO + C] = inp["L3_attn_bout"][None]
    return out


def _graph_vectors(inp):
    import numpy as np
    row = np.concatenate([inp["L2_ffn_" + n].reshape(-1) for n in ("att_src", "att_dst", "b_gat", "ln_gamma", "ln_beta")])
    return np.ascontiguousarray(np.broadcast_to(row[None], (P, row.size)))
def build(nc, a, out):
    from concourse import mybir
    from contextlib import ExitStack
    fp32 = mybir.dt.float32
    con = a["consts"]
    tables = graph_tables(nc)
    sort_stage(nc, a["edges"], con, *[tables[n] for n in ("src", "keep", "pen", "first", "ends_i", "place_i", "target0")])
    with nc.sbuf_tensor("t_sb", [P, TILES, C], fp32) as t_sb:
        with ExitStack() as notes_ctx:
            notes = EndsNotes(nc, notes_ctx, tables["ends_i"], tables["place_i"], tables["ends"])
            with nc.sbuf_tensor("x_sb", [P, PAIRS, L], fp32) as x_sb:
                ssm_stage(nc, a["x"], a["ssm"], con, a["selectors"], x_sb)
                conv_stage(nc, a["conv"], con, x_sb, t_sb, notes)
            with nc.sbuf_tensor("tn_a", [P, TILES, C], fp32) as tn_sb:
                norm_stage(nc, con, t_sb, tn_sb, "n1")
                graph_attn_stage(nc, a["attn_padded"], a["attn"], con, tn_sb, t_sb, notes)
        with nc.sbuf_tensor("tn_b", [P, TILES, C], fp32) as tn_sb:
            norm_stage(nc, con, t_sb, tn_sb, "n2")
            with (nc.sbuf_tensor("tnT_a", [C, TOK], fp32) as tnT_sb,
                  nc.sbuf_tensor("gates_a", [P, TILES, GATES], fp32) as gates,
                  nc.sbuf_tensor("feat", [P, TILES, HE], fp32) as feat):
                project_stage(nc, a["gat"], a["gat_bias"], con, tn_sb, tnT_sb, feat, "pa")
                graph_stage(nc, a["gat_vectors"], feat, tables, dict(tables, scores=gates, consts=con))
                top2_stage(nc, gates, "ta")
                expert_stage(nc, a["moe2_in"], None, a["moe2_out"], a["moe2_b1"], a["moe2_b2"], gates, tnT_sb, t_sb, "ea")
            norm_stage(nc, con, t_sb, tn_sb, "n3")
            slice_attn_stage(nc, a["slice"], con, tn_sb, t_sb)
            norm_stage(nc, con, t_sb, tn_sb, "n4")
            with (nc.sbuf_tensor("tnT_b", [C, TOK], fp32) as tnT_sb,
                  nc.sbuf_tensor("gates_b", [P, TILES, EXPERTS], fp32) as gates):
                project_stage(nc, a["gate_w"], a["gate_b"], con, tn_sb, tnT_sb, gates, "pb")
                top2_stage(nc, gates, "tb")
                expert_stage(nc, a["moe3_in"], a["moe3_gate"], a["moe3_out"], None, None, gates, tnT_sb, t_sb, "eb")
        with nc.semaphore("written_out") as written_out, nc.Block() as block:
            @block.sync
            def _(sp):
                sp.dma_start(out, t_sb[:, :, :]).then_inc(written_out, 16)
                sp.wait_ge(written_out, 16)


def kernel(**inputs):
    import numpy as np
    import concourse.bacc as bacc
    from concourse import mybir
    from concourse.bass_utils import run_bass_kernel_spmd

    inp = {k: np.asarray(v) for k, v in inputs.items()}
    flat = np.ascontiguousarray

    def rows(v):
        return flat(np.broadcast_to(v[None], (P,) + v.shape))

    arrays = {
        "x": flat(inp["x"].reshape(PAIRS, P, L).transpose(1, 0, 2)),
        "edges": flat(inp["L2_ffn_edge_index"].reshape(2, P, ECOLS)),
        "consts": _constants(), "selectors": _selectors(),
        "ssm": _ssm_parameters(inp), "conv": _conv_weights(inp),
        "attn_padded": _padded_heads(inp["L2_attn_W"]), "attn": flat(inp["L2_attn_W"]),
        "gat": flat(inp["L2_ffn_W_gat"]), "gat_bias": np.zeros((P, HE), np.float32), "gat_vectors": _graph_vectors(inp),
        "moe2_in": flat(inp["L2_ffn_W1"].transpose(1, 0, 2)), "moe2_out": flat(inp["L2_ffn_W2"].transpose(1, 0, 2)),
        "moe2_b1": flat(inp["L2_ffn_b1"].T), "moe2_b2": rows(inp["L2_ffn_b2"]),
        "slice": _slice_weights(inp),
        "gate_w": flat(inp["L3_ffn_gate_w"]), "gate_b": rows(inp["L3_ffn_gate_b"]),
        "moe3_in": flat(inp["L3_ffn_w1"].transpose(1, 0, 2)), "moe3_gate": flat(inp["L3_ffn_w2"].transpose(1, 0, 2)),
        "moe3_out": flat(inp["L3_ffn_w3"].transpose(1, 0, 2)),
    }
    nc = bacc.Bacc("TRN2", target_bir_lowering=False, num_devices=1)
    aps = {n: nc.dram_tensor("in_" + n, a.shape, mybir.dt.from_np(a.dtype), kind="ExternalInput").ap()
           for n, a in arrays.items()}
    out = nc.dram_tensor("out", (P, TILES, C), mybir.dt.float32, kind="ExternalOutput").ap()
    build(nc, aps, out)
    result = run_bass_kernel_spmd(nc, [{"in_" + n: a for n, a in arrays.items()}], core_ids=[0])
    tokens = result.results[0]["out"].transpose(1, 0, 2).reshape(B, L, C)
    return flat(tokens.transpose(0, 2, 1)).reshape(B, C, H, W)
```

```python
P = 128
B, C, H, W = 8, 64, 32, 32
L = H * W
PAIRS = B // 2
LAYERS = 12
NST = 16
RANK = 32
HALF = 512
TOK = B * L
TILES = TOK // P
PER = L // P

W_PROJ, W_CF, W_CB = 0, 128, 256
W_B = 384
W_C = W_B + 96
W_DL = W_C + 96
W_DT = W_DL + P
V_G, V_LB, V_PB, V_CFB, V_CBB, V_DTB, V_D = range(W_DT + P, W_DT + P + 7)
V_ALOG = V_D + 1
W_COLS = V_ALOG + NST

K_MEAN, K_ID, K_PAIR, K_ONE = 0, 128, 256, 384
K_SPLIT = 512
K_MASK = 520
K_SIGN = K_MASK + 64
K_TWO = K_SIGN + 9
K_COLS = K_TWO + 1


class Steps:

    def __init__(self, names):
        self.names = names.split()
        assert len(set(self.names)) == len(self.names)

    def after(self, name, turn=0):
        return turn * len(self.names) + (self.names.index(name) + 2)

    def all(self, turn):
        return turn * len(self.names) + 1


def ssm_stage(nc, x_in, params, consts, selectors, x_sb):
    import concourse.bass as bass
    from concourse import mybir
    from contextlib import ExitStack

    fp32, bf16 = mybir.dt.float32, mybir.dt.bfloat16
    ALU, ACT = mybir.AluOpType, mybir.ActivationFunctionType
    TURNS = LAYERS * PAIRS
    STEPS = 2 * NST

    pe_s = Steps("mean fold var xp cf cb dt0 B0 C0 dt1 B1 C1")
    act_s = Steps("mean fold A_exp sq A_neg lnv rstd xn xp z_abs z_neg z_pos cf_abs cf_relu cf_exp cf_ln cb_abs cb_relu cb_exp cb_ln "
                  "dt_abs0 dt_relu0 dt_exp0 dt_ln0 B_copy0 B_hi0 C_copy0 C_hi0 B_mid0 C_mid0 z_exp z_ln z_rec z_den "
                  "z_fix dt_abs1 dt_relu1 dt_exp1 dt_ln1 B_copy1 B_hi1 D_us B_mid1 C_copy1 C_hi1 C_mid1")
    pool_s = Steps("xc xhat xf xb delta0 dx0 B_r0 C_r0 B_split0 C_split0 z_prod z_low "
                   "z_r z_num z us delta1 dx1 B_r1 dz B_split1 C_r1 C_split1 xd")

    with ExitStack() as ctx:
        def sb(name, shape, dt=fp32):
            return ctx.enter_context(nc.sbuf_tensor(name, shape, dt))

        def sem(name):
            return ctx.enter_context(nc.semaphore(name))

        def two(name, shape, dt=fp32):
            return [sb(name + "_0", shape, dt), sb(name + "_1", shape, dt)]

        par = sb("par", [P, W_COLS])
        con = sb("con", [P, K_COLS])
        sel = sb("sel", [96, NST, P], bf16)
        negA, next_negA = sb("negA", [P, NST]), sb("next_negA", [P, NST])
        w_dt = sb("w_dt", [P, P])
        mean, xc, sq, rstd, xn, xp, sig, neg, z, us, gz = (sb(n, [P, L]) for n in
                                                     ("mean", "xc", "sq", "rstd", "xn", "xp", "sig", "neg", "z", "us", "gz"))
        ez, den, pos = mean, xc, sq
        relu, soft = two("relu", [P, L]), two("soft", [P, L])
        start = sb("start", [P, 12])
        u, delta, dx = two("u", [P, L]), two("delta", [P, L]), two("dx", [P, L])
        B3, C3 = two("B3", [96, L], bf16), two("C3", [96, L], bf16)
        raw, hi, rest = (dict(zip("BC", two(n, [96, L], dt))) for n, dt in (("raw", fp32), ("hi", bf16), ("rest", fp32)))
        dA, dBu, hst, hC = (two(n, [P, L]) for n in ("dA", "dBu", "h", "hC"))
        pp = ctx.enter_context(nc.psum_tensor("pp", [P, L], fp32))
        y_ps = ctx.enter_context(nc.psum_tensor("y_ps", [P, L], fp32))
        B_ps = ctx.enter_context(nc.psum_tensor("B_ps", [P, L], fp32))
        C_ps = ctx.enter_context(nc.psum_tensor("C_ps", [P, L], fp32))

        loaded, par_loaded, sel_ready, started, a_ready = (
            sem(n) for n in ("loaded", "par_loaded", "sel_ready", "started", "a_ready"))
        pe_done, act_done, pool_done = sem("pe_done"), sem("act_done"), sem("pool_done")
        b_ready, c_ready, decay_ready, dbu_ready, scanned, prod_ready, y_added = (
            sem(n) for n in ("b_ready", "c_ready", "decay_ready", "dbu_ready", "scanned", "prod_ready", "y_added"))
        gated, updated, carried = sem("gated"), sem("updated"), sem("carried")

        halves = [slice(0, HALF), slice(HALF, L)]

        def vec(col):
            return par[:, col:col + 1]

        def x_of(turn):
            if isinstance(turn, int):
                return x_sb[:, turn % PAIRS, :]
            return x_sb[:, bass.ds(turn % PAIRS, 1), :].rearrange("p o t -> p (o t)")

        def par_of(turn):
            return (turn // PAIRS) * 16 + 16

        def dir_of(k):
            return (k % STEPS) // NST, k % NST

        with nc.Block() as block:
            @block.sync
            def _(sp):
                sp.dma_start(x_sb[:, :, :], x_in).then_inc(loaded, 16)
                sp.dma_start(con[:, :], consts).then_inc(loaded, 16)
                for half in range(2):
                    sp.dma_start(soft[half][0:96, :], selectors[:, half * L:(half + 1) * L]).then_inc(loaded, 16)
                sp.dma_start(par[:, :], params[0, :, :]).then_inc(par_loaded, 16)
                with sp.Fori(1, LAYERS) as layer:
                    sp.wait_ge(pe_done, pe_s.after("C1", layer * PAIRS - 1) - 1)
                    sp.wait_ge(act_done, act_s.after("D_us", layer * PAIRS - 1))
                    sp.dma_start(par[:, :], params[bass.ds(layer, 1), :, :].rearrange("o p w -> (o p) w")
                                 ).then_inc(par_loaded, 16)

            @block.tensor
            def _(pe):
                def product(lhsT, rhs):
                    for hs in halves:
                        last = nc.tensor.matmul(pp[0:lhsT.shape[1], hs], lhsT, rhs[:, hs], start=True, stop=True)
                    last.then_inc(pe_done, 1)

                def after_act(name, turn):
                    pe.wait_ge(act_done, act_s.after(name, turn))

                def after_pool(name, turn):
                    pe.wait_ge(pool_done, pool_s.after(name, turn))

                def prepare_backward(t, k):
                    if k == 1:
                        after_act("C_hi0", t)
                        after_pool("xb", t)
                        product(w_dt[:, :], u[1])
                    elif k == 3:
                        after_act("dt_relu1", t)
                        product(par[:, W_B:W_B + 96], u[1])
                    elif k == 5:
                        after_act("B_hi1", t)
                        product(par[:, W_C:W_C + 96], u[1])
                    elif k == 7:
                        after_act("C_hi1", t)

                def prepare_next(t, k):
                    if k == 7:
                        product_x(t)
                    elif k == 9:
                        after_act("mean", t)
                        pe.wait_ge(par_loaded, par_of(t))
                        nc.tensor.matmul(pp[:, 0:P], par[0:2 * RANK, W_DL:W_DL + P], par[0:2 * RANK, W_DT:W_DT + P],
                                         start=True, stop=True).then_inc(pe_done, 1)
                    elif k == 11:
                        after_act("sq", t)
                        product(con[:, K_MEAN:K_MEAN + P], sq)
                    elif k == 15:
                        after_act("xn", t)
                        product(par[:, W_PROJ:W_PROJ + P], xn)
                    elif k == 17:
                        after_act("xp", t)
                        product(par[:, W_CF:W_CF + P], xp)
                    elif k == 19:
                        after_act("cf_relu", t)
                        product(par[:, W_CB:W_CB + P], xp)
                    elif k == 21:
                        after_act("cb_relu", t)
                        after_pool("xf", t)
                        product(w_dt[:, :], u[0])
                    elif k == 23:
                        after_act("dt_relu0", t)
                        product(par[:, W_B:W_B + 96], u[0])
                    elif k == 25:
                        after_act("B_hi0", t)
                        product(par[:, W_C:W_C + 96], u[0])

                def product_x(t):
                    for hs in halves:
                        xs = x_sb[:, t % PAIRS, hs] if isinstance(t, int) else \
                            x_sb[:, bass.ds(t % PAIRS, 1), hs].rearrange("p o t -> p (o t)")
                        last = nc.tensor.matmul(pp[:, hs], con[:, K_MEAN:K_MEAN + P], xs, start=True, stop=True)
                    last.then_inc(pe_done, 1)

                def copies(out, parts, k, ready):
                    d, n = dir_of(k)
                    for hs in halves:
                        last = nc.tensor.matmul(out[:, hs], sel[:, n, :], parts[d][:, hs], start=True, stop=True)
                    last.then_inc(ready, 1)

                def add_y(k):
                    for hs in halves:
                        last = nc.tensor.matmul(y_ps[:, hs], con[:, K_ID:K_ID + P], hC[k % 2][:, hs],
                                                start=(k == 0), stop=(k == STEPS - 1))
                    last.then_inc(y_added, 1)
                    return last

                def turn(it, last_turn):
                    for k in range(1, STEPS + 1):
                        s = it * STEPS + k
                        if last_turn and k == STEPS:
                            break
                        if not (last_turn and k == STEPS - 1):
                            if k == NST - 1:
                                after_pool("B_split1", it)
                            elif k == STEPS - 1:
                                after_pool("B_split0", it + 1)
                            pe.wait_ge(dbu_ready, s + 1)
                            copies(B_ps, B3, k + 1, b_ready)
                        if k == NST:
                            after_pool("C_split1", it)
                        elif k == STEPS:
                            after_pool("C_split0", it + 1)
                        pe.wait_ge(prod_ready, s)
                        copies(C_ps, C3, k, c_ready)
                        if k == 1:
                            pe.wait_ge(gated, it + 1)
                        add_y(k - 1)
                        prepare_backward(it, k)
                        if not last_turn:
                            prepare_next(it + 1, k)
                    if last_turn:
                        pe.wait_ge(prod_ready, TURNS * STEPS)
                        add_y(STEPS - 1)

                pe.wait_ge(loaded, 64)
                pe.wait_ge(sel_ready, 2)
                for k in range(1, STEPS):
                    prepare_next(0, k)
                after_pool("B_split0", 0)
                copies(B_ps, B3, 0, b_ready)
                pe.wait_ge(dbu_ready, 1)
                copies(B_ps, B3, 1, b_ready)
                after_pool("C_split0", 0)
                copies(C_ps, C3, 0, c_ready)
                with pe.Fori(0, TURNS - 1) as it:
                    turn(it, False)
                turn(TURNS - 1, True)

            @block.scalar
            def _(act):
                A = nc.scalar.activation

                def own(name, turn):
                    act.wait_ge(act_done, act_s.after(name, turn))

                def after_pe(name, turn):
                    act.wait_ge(pe_done, pe_s.after(name, turn) - 1)

                def after_pool(name, turn):
                    act.wait_ge(pool_done, pool_s.after(name, turn))

                def argument(t, pe_step, k, bias):
                    after_pe(pe_step, t)
                    A(soft[k][:, :], pp[:, :], ACT.Abs, bias=vec(bias)).then_inc(act_done, 1)
                    A(relu[k][:, :], pp[:, :], ACT.Relu, bias=vec(bias)).then_inc(act_done, 1)

                def logarithm(t, name, k):
                    own(name.format("abs"), t)
                    A(soft[k][:, :], soft[k][:, :], ACT.Exp, scale=-1.0).then_inc(act_done, 1)
                    own(name.format("exp"), t)
                    A(soft[k][:, :], soft[k][:, :], ACT.Ln, bias=con[:, K_ONE:K_ONE + 1]).then_inc(act_done, 1)

                def first_part(t, name, d):
                    after_pe(f"{name}{d}", t)
                    A(raw[name][:, :], pp[0:96, :], ACT.Copy).then_inc(act_done, 1)
                    A(hi[name][:, :], pp[0:96, :], ACT.Identity, scale=con[0:96, K_SPLIT:K_SPLIT + 1]).then_inc(act_done, 1)

                def second_part(t, name, d):
                    after_pool(f"{name}_r{d}", t)
                    A(hi[name][:, :], rest[name][:, :], ACT.Identity, scale=con[0:96, K_SPLIT + 1:K_SPLIT + 2]).then_inc(act_done, 1)

                def prepare_backward(t, k):
                    if k == 1:
                        after_pool("z_prod", t)
                        A(den[:, :], den[:, :], ACT.Identity, bias=con[:, K_TWO:K_TWO + 1], scale=-1.0).then_inc(act_done, 1)
                    elif k == 2:
                        argument(t, "dt1", 1, V_DTB)
                    elif k == 3:
                        logarithm(t, "dt_{}1", 1)
                    elif k == 4:
                        first_part(t, "B", 1)
                        after_pool("us", t)
                        A(us[:, :], us[:, :], ACT.Identity, scale=vec(V_D)).then_inc(act_done, 1)
                    elif k == 6:
                        second_part(t, "B", 1)
                        first_part(t, "C", 1)
                    elif k == 8:
                        second_part(t, "C", 1)

                def prepare_next(t, k):
                    if k == 8:
                        after_pe("mean", t)
                        A(mean[:, :], pp[:, :], ACT.Copy).then_inc(act_done, 1)
                    elif k == 10:
                        after_pe("fold", t)
                        A(w_dt[:, :], pp[:, 0:P], ACT.Copy).then_inc(act_done, 1)
                        A(next_negA[:, :], par[:, V_ALOG:V_ALOG + NST], ACT.Exp).then_inc(act_done, 1)
                        after_pool("xc", t)
                        A(sq[:, :], xc[:, :], ACT.Square).then_inc(act_done, 1)
                    elif k == 12:
                        own("A_exp", t)
                        A(next_negA[:, :], next_negA[:, :], ACT.Copy, scale=-1.0).then_inc(act_done, 1)
                        after_pe("var", t)
                        A(rstd[:, :], pp[:, :], ACT.Ln, bias=con[:, K_SPLIT + 2:K_SPLIT + 3]).then_inc(act_done, 1)
                        own("lnv", t)
                        A(rstd[:, :], rstd[:, :], ACT.Exp, scale=-0.5).then_inc(act_done, 1)
                    elif k == 14:
                        after_pool("xhat", t)
                        A(xn[:, :], xn[:, :], ACT.Identity, bias=vec(V_LB), scale=vec(V_G)).then_inc(act_done, 1)
                    elif k == 16:
                        after_pe("xp", t)
                        A(xp[:, :], pp[:, :], ACT.Identity, bias=vec(V_PB)).then_inc(act_done, 1)
                        own("xp", t)
                        A(sig[:, :], xp[:, :], ACT.Abs).then_inc(act_done, 1)
                        A(neg[:, :], xp[:, :], ACT.Relu, scale=-1.0).then_inc(act_done, 1)
                        A(pos[:, :], xp[:, :], ACT.Relu).then_inc(act_done, 1)
                    elif k == 18:
                        argument(t, "cf", 0, V_CFB)
                    elif k == 19:
                        logarithm(t, "cf_{}", 0)
                    elif k == 20:
                        argument(t, "cb", 1, V_CBB)
                    elif k == 21:
                        logarithm(t, "cb_{}", 1)
                    elif k == 22:
                        after_pool("xf", t)
                        argument(t, "dt0", 0, V_DTB)
                    elif k == 23:
                        logarithm(t, "dt_{}0", 0)
                    elif k == 24:
                        first_part(t, "B", 0)
                    elif k == 26:
                        first_part(t, "C", 0)
                    elif k == 27:
                        second_part(t, "B", 0)
                    elif k == 28:
                        second_part(t, "C", 0)
                    elif k == 29:
                        A(ez[:, :], sig[:, :], ACT.Exp, scale=-1.0).then_inc(act_done, 1)
                        own("z_exp", t)
                        A(sig[:, :], ez[:, :], ACT.Ln, bias=con[:, K_ONE:K_ONE + 1]).then_inc(act_done, 1)
                    elif k == 30:
                        own("z_ln", t)
                        A(sig[:, :], sig[:, :], ACT.Exp, scale=-1.0).then_inc(act_done, 1)
                        A(den[:, :], ez[:, :], ACT.Identity, bias=con[:, K_ONE:K_ONE + 1]).then_inc(act_done, 1)

                def decay(k):
                    d, n = dir_of(k)
                    A(dA[k % 2][:, :], delta[d][:, :], ACT.Exp, scale=negA[:, n:n + 1]).then_inc(decay_ready, 1)

                def turn(it, last_turn):
                    for k in range(1, STEPS + 1):
                        s = it * STEPS + k
                        if last_turn and k >= STEPS - 1:
                            break
                        if k == NST - 1:
                            after_pool("delta1", it)
                        elif k == STEPS - 1:
                            act.wait_ge(decay_ready, s + 1)
                            A(negA[:, :], next_negA[:, :], ACT.Copy).then_inc(a_ready, 1)
                            act.wait_ge(a_ready, it + 2)
                            after_pool("delta0", it + 1)
                        act.wait_ge(scanned, s)
                        decay(k + 1)
                        prepare_backward(it, k)
                        if not last_turn:
                            prepare_next(it + 1, k)

                nc.scalar.preload_act_table_set("natural_log_exp_and_others")
                act.wait_ge(loaded, 64)
                for half in range(2):
                    A(sel[:, half * (NST // 2):(half + 1) * (NST // 2), :],
                      soft[half][0:96, :].rearrange("k (n m) -> k n m", n=NST // 2), ACT.Copy).then_inc(sel_ready, 1)
                act.wait_ge(sel_ready, 2)
                A(start[:, 0:1], con[:, 0:1], ACT.Copy).then_inc(act_done, 1)
                for k in range(1, STEPS):
                    prepare_next(0, k)
                own("A_neg", 0)
                A(negA[:, :], next_negA[:, :], ACT.Copy).then_inc(a_ready, 1)
                act.wait_ge(a_ready, 1)
                after_pool("delta0", 0)
                decay(0)
                decay(1)
                with act.Fori(0, TURNS - 1) as it:
                    turn(it, False)
                turn(TURNS - 1, True)

            @block.gpsimd
            def _(pool):
                G = nc.gpsimd

                def after_act(name, turn):
                    pool.wait_ge(act_done, act_s.after(name, turn))

                def own(name, turn):
                    pool.wait_ge(pool_done, pool_s.after(name, turn))

                def done(ins):
                    ins.then_inc(pool_done, 1)

                def carry_waits(col):
                    G.tensor_tensor(start[:, col:col + 1], start[:, 8:9], start[:, 9:10], ALU.add)

                def softplus(out, t, act_step, k):
                    after_act(act_step, t)
                    done(G.tensor_tensor(out[:, :], relu[k][:, :], soft[k][:, :], ALU.add))

                def remainder(t, name, d):
                    after_act(f"{name}_hi{d}", t)
                    done(G.tensor_tensor(rest[name][:, :], raw[name][:, :], hi[name][:, :], ALU.add))

                def split(t, name, d):
                    after_act(f"{name}_mid{d}", t)
                    done(G.tensor_tensor({"B": B3, "C": C3}[name][d][:, :], rest[name][:, :], hi[name][:, :], ALU.add))

                def prepare_backward(t, k):
                    if k == 2:
                        after_act("z_fix", t)
                        done(G.tensor_tensor(sig[:, :], sig[:, :], den[:, :], ALU.mult))
                        own("z_low", t)
                        done(G.tensor_tensor(neg[:, :], pos[:, :], neg[:, :], ALU.subtract))
                        own("z_num", t)
                        pool.wait_ge(gated, t + 1)
                        done(G.tensor_tensor(z[:, :], neg[:, :], sig[:, :], ALU.mult))
                    elif k == 3:
                        done(G.tensor_tensor(us[:, :], u[0][:, :], u[1][:, :], ALU.add))
                    elif k == 4:
                        pool.wait_ge(decay_ready, t * STEPS + 1)
                        softplus(delta[1], t, "dt_ln1", 1)
                    elif k == 5:
                        own("delta1", t)
                        pool.wait_ge(dbu_ready, t * STEPS + 1)
                        done(G.tensor_tensor(dx[1][:, :], delta[1][:, :], u[1][:, :], ALU.mult))
                        remainder(t, "B", 1)
                        after_act("D_us", t)
                        done(G.tensor_tensor(us[:, :], us[:, :], z[:, :], ALU.mult))
                    elif k == 7:
                        pool.wait_ge(b_ready, t * STEPS + 1)
                        split(t, "B", 1)
                        remainder(t, "C", 1)
                    elif k == 9:
                        pool.wait_ge(c_ready, t * STEPS + 1)
                        split(t, "C", 1)
                    elif k == 10:
                        own("dz", t)
                        carry_waits(5)
                        done(G.tensor_tensor(x_of(t), x_of(t), us[:, :], ALU.add))

                def prepare_next(t, k, running=True):
                    def read_by_forward(sem_):
                        if running:
                            pool.wait_ge(sem_, (t - 1) * STEPS + NST)

                    if k == 9:
                        after_act("mean", t)
                        carry_waits(6)
                        done(G.tensor_tensor(xc[:, :], x_of(t), mean[:, :], ALU.subtract))
                    elif k == 13:
                        own("xc", t)
                        after_act("rstd", t)
                        done(G.tensor_tensor(xn[:, :], xc[:, :], rstd[:, :], ALU.mult))
                    elif k == 20:
                        softplus(u[0], t, "cf_ln", 0)
                    elif k == 22:
                        softplus(u[1], t, "cb_ln", 1)
                    elif k == 24:
                        read_by_forward(decay_ready)
                        softplus(delta[0], t, "dt_ln0", 0)
                    elif k == 25:
                        own("delta0", t)
                        read_by_forward(dbu_ready)
                        done(G.tensor_tensor(dx[0][:, :], delta[0][:, :], u[0][:, :], ALU.mult))
                    elif k == 26:
                        remainder(t, "B", 0)
                    elif k == 27:
                        remainder(t, "C", 0)
                    elif k == 28:
                        read_by_forward(b_ready)
                        split(t, "B", 0)
                    elif k == 29:
                        read_by_forward(c_ready)
                        split(t, "C", 0)
                    elif k == 30:
                        after_act("z_den", t)
                        done(G.tensor_tensor(den[:, :], den[:, :], sig[:, :], ALU.mult))
                        done(G.tensor_tensor(neg[:, :], neg[:, :], ez[:, :], ALU.mult))

                def update(it):
                    pool.wait_ge(gated, it + 2)
                    carry_waits(7)
                    G.tensor_tensor(x_of(it), x_of(it), gz[:, :], ALU.add).then_inc(updated, 1)

                def turn(it, last_turn):
                    for k in range(1, STEPS):
                        prepare_backward(it, k)
                        if not last_turn:
                            prepare_next(it + 1, k)
                    own("xd", it)
                    update(it)

                pool.wait_ge(loaded, 64)
                G.memset(start[:, 1:2], 0.0).then_inc(pool_done, 1)
                G.memset(start[:, 2:3], 0.0).then_inc(updated, 1)
                G.memset(start[:, 5:10], 0.0).then_inc(carried, 1)
                pool.wait_ge(carried, 1)
                for k in range(1, STEPS):
                    prepare_next(0, k, running=False)
                with pool.Fori(0, TURNS - 1) as it:
                    turn(it, False)
                turn(TURNS - 1, True)

            @block.vector
            def _(dve):
                V = nc.vector

                def input_part(k, s):
                    dve.wait_ge(b_ready, s + 1)
                    V.tensor_tensor(dBu[k % 2][:, :], dx[dir_of(k)[0]][:, :], B_ps[:, :], ALU.mult).then_inc(dbu_ready, 1)

                def scan(k, s):
                    step = (1, -1)[dir_of(k)[0]]
                    dve.wait_ge(dbu_ready, s + 1)
                    dve.wait_ge(decay_ready, s + 1)
                    V.tensor_tensor_scan(hst[k % 2][:, ::step], dA[k % 2][:, ::step], dBu[k % 2][:, ::step],
                                         0.0, ALU.mult, ALU.add).then_inc(scanned, 1)

                def output_part(k, s):
                    dve.wait_ge(scanned, s + 1)
                    dve.wait_ge(c_ready, s + 1)
                    dve.wait_ge(y_added, s + 1)
                    V.tensor_tensor(hC[k % 2][:, :], hst[k % 2][:, :], C_ps[:, :], ALU.mult).then_inc(prod_ready, 1)

                def gate(it):
                    dve.wait_ge(y_added, (it + 1) * STEPS + 2)
                    dve.wait_ge(updated, it + 1)
                    V.tensor_tensor(gz[:, :], z[:, :], y_ps[:, :], ALU.mult).then_inc(gated, 1)

                def turn(it, last_turn):
                    for k in range(1, STEPS + 1):
                        s = it * STEPS + k
                        if last_turn and k == STEPS:
                            break
                        scan(k, s)
                        if not (last_turn and k == STEPS - 1):
                            if k == NST - 1:
                                dve.wait_ge(pool_done, pool_s.after("dx1", it))
                            elif k == STEPS - 1:
                                dve.wait_ge(pool_done, pool_s.after("dx0", it + 1))
                            dve.wait_ge(scanned, s)
                            input_part(k + 1, s + 1)
                        if k == STEPS:
                            gate(it)
                        output_part(k, s)
                    if last_turn:
                        gate(it)

                dve.wait_ge(loaded, 64)
                V.memset(start[:, 3:4], 0.0).then_inc(gated, 1)
                V.memset(start[:, 4:5], 0.0).then_inc(y_added, 2)
                dve.wait_ge(pool_done, pool_s.after("dx0", 0))
                input_part(0, 0)
                scan(0, 0)
                input_part(1, 1)
                output_part(0, 0)
                with dve.Fori(0, TURNS - 1) as it:
                    turn(it, False)
                turn(TURNS - 1, True)


Q_COLS = 64
CW_QK, CW_V = 0, 9 * P
CW_FC1 = CW_V + 9 * P
CW_FC2 = CW_FC1 + 8
CW_FL = CW_FC2 + P
CW_FG = CW_FL + C
CV_BQ, CV_BK, CV_B1, CV_B2, CV_BV = range(CW_FG + C, CW_FG + C + 5)
CR_FB = CV_BV + 1
CW_COLS = CR_FB + C


def conv_stage(nc, weights, consts, x_sb, t_sb, notes):
    import concourse.bass as bass
    from concourse import mybir
    from contextlib import ExitStack

    fp32 = mybir.dt.float32
    ALU, ACT, AX = mybir.AluOpType, mybir.ActivationFunctionType, mybir.AxisListType.X
    IMAGES = range(2)
    BLK = range(PER)
    SCALE = (C // 4) ** -0.5
    PW = W + 2
    ROWS = HALF // W

    pe_s = Steps("gm gv fc1 fc2 qk v vt " + " ".join(
        " ".join(f"S{b}_{i}" for i in BLK) + f" mrep{b} " + " ".join(f"T{b}_{i}" for i in BLK)
        + f" loc{b} den{b} out{b} res{b}" for b in IMAGES))
    act_s = Steps("sq lnv rstd relu esig qs ks vb " + " ".join(
        f"mrepc{b} " + " ".join(f"E{b}_{i}" for i in BLK) + f" locc{b}" for b in IMAGES))
    dve_s = Steps("s1 gmean xc s2 v2 xhat ysum h1 h2 y xg vs " + " ".join(
        " ".join(f"max{b}_{i}" for i in BLK) + f" diag{b} " + " ".join(f"sub{b}_{i}" for i in BLK)
        + f" rden{b} scaled{b} summed{b} t{b}" for b in IMAGES))

    with ExitStack() as ctx:
        def sb(name, shape, dt=fp32):
            return ctx.enter_context(nc.sbuf_tensor(name, shape, dt))

        def ps(name, cols):
            return ctx.enter_context(nc.psum_tensor(name, [P, cols], fp32))

        def sem(name):
            return ctx.enter_context(nc.semaphore(name))

        cw = sb("cw", [P, CW_COLS])
        con = sb("con_c", [P, K_COLS])
        xc, sq, xg = (sb(n, [P, L]) for n in ("cxc", "csq", "cxg"))
        xw = sb("xw", [P, L])
        xpad = sb("xpad", [P, PW, PW])
        st = sb("st", [P, 16])
        S1, GM, S2, GV, YS, HID, Y = (st[:, i:i + 1] for i in range(7))
        q_sb, k_sb = sb("q_sb", [Q_COLS, L]), sb("k_sb", [Q_COLS, L])
        v_sb = sb("v_sb", [P, L])
        vT = sb("vT", [P, PER, 2, C + 1])
        mrow = sb("mrow", [P, 2, PER])
        diag = sb("diag", [P, PER, P])
        mrep = sb("mrep", [P, L])
        E = [sb("E0", [P, PER, L]), sb("E1", [P, PER, L])]
        loc = sb("loc", [C + 1, L])
        rden = sb("rden", [P, 2, PER])
        tmp = sb("tmp", [P, PER, C])
        psA, psB, psM = ps("psA", L), ps("psB", L), ps("psM", L)
        psO, psT = ps("psO", HALF), ps("psT", HALF)
        psS = [psA, psB]

        loaded, zeroed = sem("c_loaded"), sem("c_zeroed")
        xw_ready = sem("xw_ready")
        pe_done, act_done, dve_done = sem("c_pe"), sem("c_act"), sem("c_dve")
        halves = [slice(0, HALF), slice(HALF, L)]
        inner = xpad[:, 1:H + 1, 1:W + 1]
        EPS = con[:, K_SPLIT + 2:K_SPLIT + 3]

        def window(tap, row, rows):
            dy, dx = divmod(tap, 3)
            return xpad[:, row + dy:row + dy + rows, dx:dx + W]

        with nc.Block() as block:
            @block.sync
            def _(sp):
                sp.dma_start(cw[:, :], weights).then_inc(loaded, 16)
                sp.dma_start(con[:, :], consts).then_inc(loaded, 16)

            @block.gpsimd
            def _(pool):
                nc.gpsimd.memset(xpad[:, :, :], 0.0).then_inc(zeroed, 1)
                nc.gpsimd.memset(vT[:, :, :, :], 1.0).then_inc(zeroed, 1)
                notes.scatter(pool, 0, NOTED_FIRST)

            @block.tensor
            def _(pe):
                M = nc.tensor.matmul
                pe.wait_ge(loaded, 32)
                with pe.Fori(0, PAIRS) as pair:
                    def act(name):
                        pe.wait_ge(act_done, act_s.after(name, pair))

                    def dve(name):
                        pe.wait_ge(dve_done, dve_s.after(name, pair))

                    dve("s1")
                    M(psT[:, 0:1], con[:, K_PAIR:K_PAIR + P], S1, start=True, stop=True).then_inc(pe_done, 1)
                    dve("s2")
                    M(psT[:, 1:2], con[:, K_PAIR:K_PAIR + P], S2, start=True, stop=True).then_inc(pe_done, 1)
                    dve("ysum")
                    M(psT[0:8, 2:3], cw[:, CW_FC1:CW_FC1 + 8], YS, start=True, stop=True).then_inc(pe_done, 1)
                    act("relu")
                    M(psT[:, 3:4], cw[0:8, CW_FC2:CW_FC2 + P], HID[0:8, :], start=True, stop=True).then_inc(pe_done, 1)
                    for cols, before in ((CW_QK, None), (CW_V, "ks")):
                        if before:
                            act(before)
                        for h, hs in enumerate(halves):
                            for tap in range(9):
                                last = M(psM[:, hs], cw[:, cols + tap * P:cols + (tap + 1) * P],
                                         window(tap, h * ROWS, ROWS), start=tap == 0, stop=tap == 8)
                        last.then_inc(pe_done, 1)
                    act("vb")
                    for i in BLK:
                        last = M(psM[:, i * P:(i + 1) * P], v_sb[:, i * P:(i + 1) * P], con[:, K_ID:K_ID + P],
                                 start=True, stop=True)
                    last.then_inc(pe_done, 1)
                    for b in IMAGES:
                        qb, kb = q_sb[32 * b:32 * b + 32, :], k_sb[32 * b:32 * b + 32, :]
                        for i in BLK:
                            if i >= 2:
                                dve(f"max{b}_{i - 2}")
                            elif b:
                                dve(f"sub0_{PER - 2 + i}")
                            for hs in halves:
                                last = M(psS[i % 2][:, hs], qb[:, i * P:(i + 1) * P], kb[:, hs], start=True, stop=True)
                            last.then_inc(pe_done, 1)
                        dve(f"diag{b}")
                        if b:
                            act("locc0")
                        else:
                            dve("vs")
                        for i in BLK:
                            last = M(psM[:, i * P:(i + 1) * P], con[:, K_ONE:K_ONE + P], diag[:, i, :], start=True, stop=True)
                        last.then_inc(pe_done, 1)
                        for i in BLK:
                            dve(f"sub{b}_{i - 2}" if i >= 2 else f"max{b}_{PER - 2 + i}")
                            for hs in halves:
                                last = M(psS[i % 2][:, hs], kb[:, i * P:(i + 1) * P], qb[:, hs], start=True, stop=True)
                            last.then_inc(pe_done, 1)
                        act(f"E{b}_{PER - 1}")
                        for hs in halves:
                            for i in BLK:
                                last = M(psM[0:C + 1, hs], vT[:, i, b, :], E[b][:, i, hs],
                                         start=i == 0, stop=i == PER - 1)
                        last.then_inc(pe_done, 1)
                        if b:
                            dve("summed0")
                        act(f"locc{b}")
                        for i in BLK:
                            last = M(psT[:, 8 + i:9 + i], loc[:, i * P:(i + 1) * P], con[0:C + 1, K_ID + C:K_ID + C + 1],
                                     start=True, stop=True)
                        last.then_inc(pe_done, 1)
                        for i in BLK:
                            last = M(psO[:, i * C:(i + 1) * C], loc[0:C, i * P:(i + 1) * P], cw[0:C, CW_FL:CW_FL + C],
                                     start=True, stop=True)
                        last.then_inc(pe_done, 1)
                        dve(f"rden{b}")
                        rows = slice(b * C, (b + 1) * C)
                        for i in BLK:
                            M(psT[:, i * C:(i + 1) * C], xw[rows, i * P:(i + 1) * P], con[rows, K_ID + b * C:K_ID + (b + 1) * C],
                              start=True, stop=False)
                            last = M(psT[:, i * C:(i + 1) * C], xg[rows, i * P:(i + 1) * P], cw[rows, CW_FG:CW_FG + C],
                                     start=False, stop=True)
                        last.then_inc(pe_done, 1)

            @block.scalar
            def _(act):
                A = nc.scalar.activation
                nc.scalar.preload_act_table_set("natural_log_exp_and_others")
                act.wait_ge(loaded, 32)
                A(st[:, 8:9], con[:, 0:1], ACT.Copy).then_inc(act_done, 1)
                with act.Fori(0, PAIRS) as pair:
                    def pe(name):
                        act.wait_ge(pe_done, pe_s.after(name, pair) - 1)

                    def dve(name):
                        act.wait_ge(dve_done, dve_s.after(name, pair))

                    def own(name):
                        act.wait_ge(act_done, act_s.after(name, pair))

                    dve("xc")
                    A(sq[:, :], xc[:, :], ACT.Square).then_inc(act_done, 1)
                    dve("v2")
                    A(GV, GV, ACT.Ln, bias=EPS).then_inc(act_done, 1)
                    own("lnv")
                    A(GV, GV, ACT.Exp, scale=-0.5).then_inc(act_done, 1)
                    pe("fc1")
                    A(HID[0:8, :], psT[0:8, 2:3], ACT.Relu, bias=cw[0:8, CV_B1:CV_B1 + 1],
                      scale=1.0 / L).then_inc(act_done, 1)
                    dve("h1")
                    A(Y, Y, ACT.Exp, scale=-1.0).then_inc(act_done, 1)
                    pe("qk")
                    A(q_sb[:, :], psM[0:Q_COLS, :], ACT.Identity, bias=cw[0:Q_COLS, CV_BQ:CV_BQ + 1]).then_inc(act_done, 1)
                    A(k_sb[:, :], psM[Q_COLS:P, :], ACT.Identity, bias=cw[Q_COLS:P, CV_BK:CV_BK + 1]).then_inc(act_done, 1)
                    pe("v")
                    A(v_sb[:, :], psM[:, :], ACT.Identity, bias=cw[:, CV_BV:CV_BV + 1]).then_inc(act_done, 1)
                    for b in IMAGES:
                        pe(f"mrep{b}")
                        if b:
                            dve(f"sub0_{PER - 1}")
                        A(mrep[:, :], psM[:, :], ACT.Copy).then_inc(act_done, 1)
                        for i in BLK:
                            dve(f"sub{b}_{i}")
                            A(E[b][:, i, :], E[b][:, i, :], ACT.Exp, scale=SCALE).then_inc(act_done, 1)
                        pe(f"loc{b}")
                        if b:
                            pe("out0")
                        A(loc[:, :], psM[0:C + 1, :], ACT.Copy).then_inc(act_done, 1)

            @block.vector
            def _(dve):
                V = nc.vector
                dve.wait_ge(loaded, 32)
                dve.wait_ge(zeroed, 2)
                V.memset(st[:, 9:10], 0.0).then_inc(dve_done, 1)
                with dve.Fori(0, PAIRS) as pair:
                    def pe(name):
                        dve.wait_ge(pe_done, pe_s.after(name, pair) - 1)

                    def act(name):
                        dve.wait_ge(act_done, act_s.after(name, pair))

                    def own(name):
                        dve.wait_ge(dve_done, dve_s.after(name, pair))

                    def done(ins):
                        ins.then_inc(dve_done, 1)

                    x_pair = x_sb[:, bass.ds(pair, 1), :].rearrange("p o t -> p (o t)")
                    dve.wait_ge(dve_done, dve_s.all(pair))
                    V.tensor_copy(xw[:, :], x_pair).then_inc(xw_ready, 1)
                    dve.wait_ge(xw_ready, pair + 1)
                    V.reduce_sum(S1, xw[:, :], AX).then_inc(dve_done, 1)
                    pe("gm")
                    V.tensor_scalar(GM, psT[:, 0:1], 1.0 / L, None, ALU.mult).then_inc(dve_done, 1)
                    own("gmean")
                    V.tensor_scalar(xc[:, :], xw[:, :], GM, None, ALU.subtract).then_inc(dve_done, 1)
                    act("sq")
                    V.reduce_sum(S2, sq[:, :], AX).then_inc(dve_done, 1)
                    pe("gv")
                    V.tensor_scalar(GV, psT[:, 1:2], 1.0 / L, None, ALU.mult).then_inc(dve_done, 1)
                    act("rstd")
                    V.tensor_scalar(inner, xc[:, :].rearrange("p (h w) -> p h w", h=H), GV, None,
                                    ALU.mult).then_inc(dve_done, 1)
                    own("xhat")
                    V.tensor_reduce(YS, inner, mybir.AxisListType.XY, ALU.add).then_inc(dve_done, 1)
                    pe("fc2")
                    V.tensor_scalar(Y, psT[:, 3:4], cw[:, CV_B2:CV_B2 + 1], None, ALU.add).then_inc(dve_done, 1)
                    act("esig")
                    V.tensor_scalar_add(Y, Y, 1.0).then_inc(dve_done, 1)
                    own("h2")
                    V.reciprocal(Y, Y).then_inc(dve_done, 1)
                    own("y")
                    V.tensor_scalar(xg[:, :].rearrange("p (h w) -> p h w", h=H), inner, Y, None,
                                    ALU.mult).then_inc(dve_done, 1)
                    pe("vt")
                    V.tensor_copy(vT[:, :, :, 0:C], psM[:, :].rearrange("p (i b c) -> p i b c", i=PER, b=2)).then_inc(dve_done, 1)
                    for b in IMAGES:
                        for i in BLK:
                            pe(f"S{b}_{i}")
                            V.reduce_max(mrow[:, b, i:i + 1], psS[i % 2][:, :], AX).then_inc(dve_done, 1)
                        own(f"max{b}_{PER - 1}")
                        V.tensor_tensor(diag[:, :, :], con[:, K_ID:K_ID + P].unsqueeze(1).broadcast_to([P, PER, P]),
                                        mrow[:, b, :].unsqueeze(2).broadcast_to([P, PER, P]),
                                        ALU.mult).then_inc(dve_done, 1)
                        act(f"mrepc{b}")
                        for i in BLK:
                            pe(f"T{b}_{i}")
                            V.tensor_tensor(E[b][:, i, :], psS[i % 2][:, :], mrep[:, :], ALU.subtract).then_inc(dve_done, 1)
                        pe(f"den{b}")
                        V.reciprocal(rden[:, b, :], psT[:, 8:8 + PER]).then_inc(dve_done, 1)
                        pe(f"out{b}")
                        own(f"rden{b}")
                        V.tensor_tensor(tmp[:, :, :], psO[:, :].rearrange("p (i c) -> p i c", i=PER),
                                        rden[:, b, :].unsqueeze(2).broadcast_to([P, PER, C]), ALU.mult).then_inc(dve_done, 1)
                        pe(f"res{b}")
                        own(f"scaled{b}")
                        V.tensor_tensor(tmp[:, :, :], tmp[:, :, :], psT[:, :].rearrange("p (i c) -> p i c", i=PER),
                                        ALU.add).then_inc(dve_done, 1)
                        own(f"summed{b}")
                        V.tensor_tensor(t_sb[:, bass.ds(pair * 2 * PER + b * PER, PER), :], tmp[:, :, :],
                                        cw[:, CR_FB:CR_FB + C].unsqueeze(1).broadcast_to([P, PER, C]),
                                        ALU.add).then_inc(dve_done, 1)
def norm_stage(nc, consts, t_sb, tn_sb, tag):
    from concourse import mybir
    from contextlib import ExitStack

    fp32 = mybir.dt.float32
    ALU, ACT, AX = mybir.AluOpType, mybir.ActivationFunctionType, mybir.AxisListType.X
    act_s = Steps("sq lnv rstd")
    dve_s = Steps("sum mean centred sum2 normed")
    with ExitStack() as ctx:
        sq = ctx.enter_context(nc.sbuf_tensor(tag + "_sq", [P, TILES, C], fp32))
        mean = ctx.enter_context(nc.sbuf_tensor(tag + "_mean", [P, TILES], fp32))
        rstd = ctx.enter_context(nc.sbuf_tensor(tag + "_rstd", [P, TILES], fp32))
        eps = ctx.enter_context(nc.sbuf_tensor(tag + "_eps", [P, 1], fp32))
        act_done, dve_done, eps_set = (ctx.enter_context(nc.semaphore(tag + n)) for n in ("_act", "_dve", "_eps_set"))

        with nc.Block() as block:
            @block.gpsimd
            def _(pool):
                nc.gpsimd.memset(eps[:, :], 1e-5).then_inc(eps_set, 1)

            @block.scalar
            def _(act):
                nc.scalar.preload_act_table_set("natural_log_exp_and_others")
                act.wait_ge(dve_done, dve_s.after("centred") - 1)
                nc.scalar.activation(sq[:, :, :], tn_sb[:, :, :], ACT.Square).then_inc(act_done, 1)
                act.wait_ge(dve_done, dve_s.after("sum2") - 1)
                act.wait_ge(eps_set, 1)
                nc.scalar.activation(rstd[:, :], rstd[:, :], ACT.Ln, bias=eps[:, :], scale=1.0 / C).then_inc(act_done, 1)
                act.wait_ge(act_done, act_s.after("lnv") - 1)
                nc.scalar.activation(rstd[:, :], rstd[:, :], ACT.Exp, scale=-0.5).then_inc(act_done, 1)

            @block.vector
            def _(dve):
                V = nc.vector
                V.reduce_sum(mean[:, :], t_sb[:, :, :], AX).then_inc(dve_done, 1)
                dve.wait_ge(dve_done, dve_s.after("sum") - 1)
                V.tensor_scalar(mean[:, :], mean[:, :], 1.0 / C, None, ALU.mult).then_inc(dve_done, 1)
                dve.wait_ge(dve_done, dve_s.after("mean") - 1)
                V.tensor_tensor(tn_sb[:, :, :], t_sb[:, :, :], mean[:, :].unsqueeze(2).broadcast_to([P, TILES, C]),
                                ALU.subtract).then_inc(dve_done, 1)
                dve.wait_ge(act_done, act_s.after("sq") - 1)
                V.reduce_sum(rstd[:, :], sq[:, :, :], AX).then_inc(dve_done, 1)
                dve.wait_ge(act_done, act_s.after("rstd") - 1)
                V.tensor_tensor(tn_sb[:, :, :], tn_sb[:, :, :], rstd[:, :].unsqueeze(2).broadcast_to([P, TILES, C]),
                                ALU.mult).then_inc(dve_done, 1)


HEADS2, HDIM2 = 4, 16


def graph_attn_stage(nc, w_padded, w_plain, consts, tn_sb, t_sb, notes):
    import concourse.bass as bass
    from concourse import mybir
    from contextlib import ExitStack

    fp32 = mybir.dt.float32
    ALU, ACT, AX = mybir.AluOpType, mybir.ActivationFunctionType, mybir.AxisListType.X
    BLK, HEADS = range(PER), range(HEADS2)
    SCALE, SLOPE = HDIM2 ** -0.5, 0.2
    HW2 = 32

    def scores(h, *kinds):
        return " ".join(f"{k}{h}_{i}" for i in BLK for k in kinds)

    pe_s = Steps("turn WhT Wh " + " ".join(scores(h, "S") + f" mrep{h}" for h in HEADS))
    act_s = Steps("copy tnT WhTc Whc " + " ".join(scores(h, "scaled") + " " + scores(h, "E") for h in HEADS))
    dve_s = Steps(" ".join(f"leaky{h}_0 " + " ".join(f"leaky{h}_{i} max{h}_{i - 1}" for i in BLK if i)
                           + f" max{h}_{PER - 1} diag{h} " + scores(h, "sub") + (" V" if h == 0 else "")
                           for h in HEADS))
    fin_s = Steps("rden scaled t")

    with ExitStack() as ctx:
        def sb(name, shape, dt=fp32):
            return ctx.enter_context(nc.sbuf_tensor(name, shape, dt))

        def ps(name, cols):
            return ctx.enter_context(nc.psum_tensor(name, [P, cols], fp32))

        def sem(name):
            return ctx.enter_context(nc.semaphore(name))

        wp, wq = sb("g_wp", [C, P]), sb("g_w", [C, C])
        con = sb("g_con", [P, K_COLS])
        tw = sb("g_tw", [P, PER, C])
        tnT, whT = sb("g_tnT", [C, L]), sb("g_whT", [P, L])
        val, wh = sb("g_val", [P, PER, HEADS2, HW2]), sb("g_wh", [P, HALF])
        oT = sb("g_oT", [P, L])
        S = [sb("g_S0", [P, PER, L]), sb("g_S1", [P, PER, L])]
        mrow = sb("g_mrow", [P, HEADS2, PER])
        diag = sb("g_diag", [P, PER, P])
        rden = sb("g_rden", [P, PER, HEADS2])
        tmp = sb("g_tmp", [P, PER, HEADS2, HDIM2])
        psS = [ps("g_psA", L), ps("g_psB", L)]
        psM, psO = ps("g_psM", L), ps("g_psO", L)
        loaded, ones_set = sem("g_loaded"), sem("g_ones")
        pe_done, act_done, dve_done = sem("g_pe"), sem("g_act"), sem("g_dve")
        out_done, out_copied, turned, fin_done = sem("g_out"), sem("g_outc"), sem("g_turned"), sem("g_fin")
        halves = [slice(0, HALF), slice(HALF, L)]

        with nc.Block() as block:
            @block.sync
            def _(sp):
                sp.dma_start(wp[:, :], w_padded).then_inc(loaded, 16)
                sp.dma_start(wq[:, :], w_plain).then_inc(loaded, 16)
                sp.dma_start(con[:, :], consts).then_inc(loaded, 16)

            @block.gpsimd
            def _(pool):
                nc.gpsimd.memset(val[:, :, :, :], 1.0).then_inc(ones_set, 1)
                notes.scatter(pool, NOTED_FIRST, CHUNKS)

            @block.tensor
            def _(pe):
                M = nc.tensor.matmul
                pe.wait_ge(loaded, 48)

                def act(name, img):
                    pe.wait_ge(act_done, act_s.after(name, img))

                def dve(name, img):
                    pe.wait_ge(dve_done, dve_s.after(name, img))

                def score_tiles(img, h):
                    rows = slice(32 * h, 32 * h + 32)
                    for i in BLK:
                        if i >= 2:
                            act(f"scaled{h}_{i - 2}", img)
                        elif h:
                            act(f"scaled{h - 1}_{PER - 2 + i}", img)
                        for hs in halves:
                            last = M(psS[i % 2][:, hs], whT[rows, i * P:(i + 1) * P], whT[rows, hs], start=True, stop=True)
                        last.then_inc(pe_done, 1)
                    dve(f"diag{h}", img)
                    if h == 1:
                        pe.wait_ge(fin_done, fin_s.all(img))
                    if h:
                        dve(f"sub{h - 1}_{PER - 1}", img)
                    else:
                        act("Whc", img)
                    for i in BLK:
                        last = M(psM[:, i * P:(i + 1) * P], con[:, K_ONE:K_ONE + P], diag[:, i, :], start=True, stop=True)
                    last.then_inc(pe_done, 1)

                def begin(img):
                    act("copy", img)
                    for i in BLK:
                        last = M(psM[0:C, i * P:(i + 1) * P], tw[:, i, :], con[:, K_ID:K_ID + P], start=True, stop=True)
                    last.then_inc(pe_done, 1)
                    act("tnT", img)
                    for hs in halves:
                        last = M(psM[:, hs], wp[:, :], tnT[:, hs], start=True, stop=True)
                    last.then_inc(pe_done, 1)
                    act("WhTc", img)
                    for i in BLK:
                        last = M(psM[:, i * C:(i + 1) * C], tnT[:, i * P:(i + 1) * P], wq[:, :], start=True, stop=True)
                    last.then_inc(pe_done, 1)
                    score_tiles(img, 0)

                def image(img, last_image):
                    for h in HEADS:
                        if h + 1 < HEADS2:
                            score_tiles(img, h + 1)
                        elif not last_image:
                            dve(f"sub{h}_{PER - 1}", img)
                            begin(img + 1)
                        act(f"E{h}_{PER - 1}", img)
                        if h == 0:
                            dve("V", img)
                        for hs in halves:
                            for j in BLK:
                                last = M(psO[h * HW2:(h + 1) * HW2, hs], val[:, j, h, :], S[h % 2][:, j, hs],
                                         start=j == 0, stop=j == PER - 1)
                        last.then_inc(out_done, 1)
                    pe.wait_ge(out_copied, img + 1)
                    dve(f"sub{HEADS2 - 1}_{PER - 1}", img)
                    if not last_image:
                        dve(f"sub0_{PER - 1}", img + 1)
                    for i in BLK:
                        last = nc.tensor.transpose(psM[:, i * P:(i + 1) * P], oT[:, i * P:(i + 1) * P], con[:, K_ID:K_ID + P])
                    last.then_inc(turned, 1)

                begin(0)
                with pe.Fori(0, B - 1) as img:
                    image(img, False)
                image(B - 1, True)

            @block.scalar
            def _(act):
                A = nc.scalar.activation

                def pe(name, img):
                    act.wait_ge(pe_done, pe_s.after(name, img) - 1)

                def image(img):
                    if not isinstance(img, int):
                        pe(f"mrep{HEADS2 - 1}", img - 1)
                    A(tw[:, :, :], tn_sb[:, bass.ds(img * PER, PER), :], ACT.Copy).then_inc(act_done, 1)
                    pe("turn", img)
                    A(tnT[:, :], psM[0:C, :], ACT.Copy).then_inc(act_done, 1)
                    pe("WhT", img)
                    A(whT[:, :], psM[:, :], ACT.Copy).then_inc(act_done, 1)
                    pe("Wh", img)
                    A(wh[:, :], psM[:, 0:HALF], ACT.Copy).then_inc(act_done, 1)
                    head(img, 0)
                    if not isinstance(img, int):
                        copy_out(img - 1)
                    for h in range(1, HEADS2):
                        head(img, h)

                def copy_out(img):
                    act.wait_ge(out_done, img * HEADS2 + HEADS2)
                    A(oT[:, :], psO[:, :], ACT.Copy).then_inc(out_copied, 1)

                def head(img, h):
                    for i in BLK:
                        pe(f"S{h}_{i}", img)
                        if i == 0 and (h >= 2 or not isinstance(img, int)):
                            act.wait_ge(out_done, img * HEADS2 + h - 1)
                        A(S[h % 2][:, i, :], psS[i % 2][:, :], ACT.Copy, scale=SCALE).then_inc(act_done, 1)
                    for i in BLK:
                        act.wait_ge(dve_done, dve_s.after(f"sub{h}_{i}", img))
                        A(S[h % 2][:, i, :], S[h % 2][:, i, :], ACT.Exp).then_inc(act_done, 1)

                nc.scalar.preload_act_table_set("natural_log_exp_and_others")
                act.wait_ge(loaded, 48)
                A(mrow[:, 0, 0:1], con[:, 0:1], ACT.Copy).then_inc(act_done, 1)
                image(0)
                with act.Fori(1, B) as img:
                    image(img)
                copy_out(B - 1)

            @block.vector
            def _(dve):
                V = nc.vector

                def pe(name, img):
                    dve.wait_ge(pe_done, pe_s.after(name, img) - 1)

                def own(name, img):
                    dve.wait_ge(dve_done, dve_s.after(name, img))

                def weights(img, h):
                    def row_max(i):
                        own(f"leaky{h}_{i}", img)
                        V.reduce_max(mrow[:, h, i:i + 1], S[h % 2][:, i, :], AX).then_inc(dve_done, 1)

                    for i in BLK:
                        dve.wait_ge(act_done, act_s.after(f"scaled{h}_{i}", img))
                        V.scalar_tensor_tensor(S[h % 2][:, i, :], S[h % 2][:, i, :], SLOPE, S[h % 2][:, i, :],
                                               ALU.mult, ALU.max).then_inc(dve_done, 1)
                        if i:
                            row_max(i - 1)
                    row_max(PER - 1)
                    own(f"max{h}_{PER - 1}", img)
                    V.tensor_tensor(diag[:, :, :], con[:, K_ID:K_ID + P].unsqueeze(1).broadcast_to([P, PER, P]),
                                    mrow[:, h, :].unsqueeze(2).broadcast_to([P, PER, P]), ALU.mult).then_inc(dve_done, 1)
                    pe(f"mrep{h}", img)
                    for i in BLK:
                        V.tensor_tensor(S[h % 2][:, i, :], S[h % 2][:, i, :], psM[:, :], ALU.subtract).then_inc(dve_done, 1)

                def values(img):
                    dve.wait_ge(act_done, act_s.after("Whc", img))
                    V.tensor_copy(val[:, :, :, 0:HDIM2],
                                  wh[:, :].rearrange("p (i h d) -> p i h d", i=PER, h=HEADS2)).then_inc(dve_done, 1)

                def finish(img):
                    dve.wait_ge(turned, img + 1)
                    out = psM[:, :].rearrange("p (i h d) -> p i h d", i=PER, h=HEADS2)
                    V.reciprocal(rden[:, :, :], out[:, :, :, HDIM2]).then_inc(fin_done, 1)
                    dve.wait_ge(fin_done, fin_s.after("rden", img))
                    V.tensor_tensor(tmp[:, :, :, :], out[:, :, :, 0:HDIM2],
                                    rden[:, :, :].unsqueeze(3).broadcast_to([P, PER, HEADS2, HDIM2]), ALU.mult).then_inc(fin_done, 1)
                    dve.wait_ge(fin_done, fin_s.after("scaled", img))
                    t_img = t_sb[:, bass.ds(img * PER, PER), :]
                    V.tensor_tensor(t_img, t_img, tmp[:, :, :, :].rearrange("p i h d -> p i (h d)"), ALU.add).then_inc(fin_done, 1)

                def image(img, last_image):
                    for h in HEADS:
                        if h + 1 < HEADS2:
                            weights(img, h + 1)
                        elif not last_image:
                            weights(img + 1, 0)
                    if not last_image:
                        dve.wait_ge(out_done, img * HEADS2 + HEADS2)
                        values(img + 1)
                    finish(img)

                dve.wait_ge(loaded, 48)
                dve.wait_ge(ones_set, 1)
                V.memset(rden[:, 0, 0:1], 0.0).then_inc(dve_done, 1)
                V.memset(rden[:, 0, 1:2], 0.0).then_inc(fin_done, 1)
                weights(0, 0)
                values(0)
                with dve.Fori(0, B - 1) as img:
                    image(img, False)
                image(B - 1, True)
GROUP = 4
EXPERTS = 16


def project_stage(nc, weight, bias_rows, consts, tn_sb, tnT_sb, out_sb, tag):
    import concourse.bass as bass
    from concourse import mybir
    from contextlib import ExitStack

    fp32 = mybir.dt.float32
    ALU, ACT = mybir.AluOpType, mybir.ActivationFunctionType
    E = out_sb.shape[2]
    with ExitStack() as ctx:
        w = ctx.enter_context(nc.sbuf_tensor(tag + "_w", [C, E], fp32))
        brow = ctx.enter_context(nc.sbuf_tensor(tag + "_b", [P, E], fp32))
        con = ctx.enter_context(nc.sbuf_tensor(tag + "_con", [P, K_COLS], fp32))
        tw = [ctx.enter_context(nc.sbuf_tensor(f"{tag}_tw{k}", [P, GROUP, C], fp32)) for k in range(2)]
        wT = [ctx.enter_context(nc.sbuf_tensor(f"{tag}_wT{k}", [C, HALF], fp32)) for k in range(2)]
        psT = [ctx.enter_context(nc.psum_tensor(f"{tag}_psT{k}", [P, HALF], fp32)) for k in range(2)]
        psL = [ctx.enter_context(nc.psum_tensor(f"{tag}_psL{k}", [P, HALF], fp32)) for k in range(2)]
        loaded, copied, turned, kept, kept_all, projected, stored = (
            ctx.enter_context(nc.semaphore(tag + n)) for n in
            ("_loaded", "_copied", "_turned", "_kept", "_kept_all", "_projected", "_stored"))
        TURNS = TILES // GROUP

        with nc.Block() as block:
            @block.sync
            def _(sp):
                sp.dma_start(w[:, :], weight).then_inc(loaded, 16)
                sp.dma_start(brow[:, :], bias_rows).then_inc(loaded, 16)
                sp.dma_start(con[:, :], consts).then_inc(loaded, 16)

            @block.tensor
            def _(pe):
                pe.wait_ge(loaded, 48)
                with pe.Fori(0, TURNS // 2) as pair:
                    for k in range(2):
                        turn = pair * 2 + k
                        pe.wait_ge(copied, turn + 1)
                        for g in range(GROUP):
                            last = nc.tensor.matmul(psT[k][0:C, g * P:(g + 1) * P], tw[k][:, g, :], con[:, K_ID:K_ID + P],
                                                    start=True, stop=True)
                        last.then_inc(turned, 1)
                        pe.wait_ge(kept, turn + 1)
                        for g in range(GROUP):
                            last = nc.tensor.matmul(psL[k][:, g * E:(g + 1) * E], wT[k][:, g * P:(g + 1) * P], w[:, :],
                                                    start=True, stop=True)
                        last.then_inc(projected, 1)

            @block.scalar
            def _(act):
                act.wait_ge(loaded, 48)
                with act.Fori(0, TURNS // 2) as pair:
                    for k in range(2):
                        turn = pair * 2 + k
                        act.wait_ge(turned, turn + 1)
                        nc.scalar.activation(wT[k][:, :], psT[k][0:C, :], ACT.Copy).then_inc(kept, 1)
                        act.wait_ge(kept, turn + 1)
                        nc.scalar.activation(tnT_sb[:, bass.ds(turn * HALF, HALF)], wT[k][:, :], ACT.Copy).then_inc(kept_all, 1)

            @block.vector
            def _(dve):
                V = nc.vector
                dve.wait_ge(loaded, 48)
                V.memset(tw[0][:, 0, 0:1], 0.0).then_inc(stored, 2)
                with dve.Fori(0, TURNS // 2) as pair:
                    for k in range(2):
                        turn = pair * 2 + k
                        dve.wait_ge(stored, turn + 1)
                        V.tensor_copy(tw[k][:, :, :], tn_sb[:, bass.ds(turn * GROUP, GROUP), :]).then_inc(copied, 1)
                    for k in range(2):
                        turn = pair * 2 + k
                        dve.wait_ge(projected, turn + 1)
                        dve.wait_ge(kept_all, turn + 1)
                        V.tensor_tensor(out_sb[:, bass.ds(turn * GROUP, GROUP), :],
                                        psL[k][:, 0:GROUP * E].rearrange("p (g e) -> p g e", g=GROUP),
                                        brow[:, :].unsqueeze(1).broadcast_to([P, GROUP, E]), ALU.add).then_inc(stored, 1)


def top2_stage(nc, logits, tag):
    from concourse import mybir
    from contextlib import ExitStack

    fp32 = mybir.dt.float32
    ALU, ACT, AX = mybir.AluOpType, mybir.ActivationFunctionType, mybir.AxisListType.X
    E = logits.shape[2]
    FAR = 1e30
    with ExitStack() as ctx:
        rank, hit, first = (ctx.enter_context(nc.sbuf_tensor(tag + n, [P, TILES, E], fp32)) for n in ("_rank", "_hit", "_first"))
        top, pos, g1, g2 = (ctx.enter_context(nc.sbuf_tensor(tag + n, [P, 2, TILES], fp32)) for n in ("_top", "_pos", "_g1", "_g2"))
        ranked, exp_done, link = (ctx.enter_context(nc.semaphore(tag + n)) for n in ("_ranked", "_exp_done", "_link"))

        def wide(a):
            return a.unsqueeze(2).broadcast_to([P, TILES, E])

        with nc.Block() as block:
            @block.gpsimd
            def _(pool):
                for e in range(E):
                    nc.gpsimd.memset(rank[:, :, e:e + 1], float(E - e)).then_inc(ranked, 1)

            @block.scalar
            def _(act):
                act.wait_ge(link, 8)
                nc.scalar.activation(g2[:, 0, :], g2[:, 0, :], ACT.Exp).then_inc(exp_done, 1)

            @block.vector
            def _(dve):
                V = nc.vector
                dve.wait_ge(ranked, E)
                V.reduce_max(top[:, 0, :], logits[:, :, :], AX).then_inc(link, 1)
                dve.wait_ge(link, 1)
                V.tensor_tensor(hit[:, :, :], logits[:, :, :], wide(top[:, 0, :]), ALU.is_equal).then_inc(link, 1)
                dve.wait_ge(link, 2)
                V.tensor_tensor(hit[:, :, :], hit[:, :, :], rank[:, :, :], ALU.mult).then_inc(link, 1)
                dve.wait_ge(link, 3)
                V.reduce_max(pos[:, 0, :], hit[:, :, :], AX).then_inc(link, 1)
                dve.wait_ge(link, 4)
                V.tensor_tensor(first[:, :, :], rank[:, :, :], wide(pos[:, 0, :]), ALU.is_equal).then_inc(link, 1)
                dve.wait_ge(link, 5)
                V.scalar_tensor_tensor(logits[:, :, :], first[:, :, :], -FAR, logits[:, :, :], ALU.mult, ALU.add).then_inc(link, 1)
                dve.wait_ge(link, 6)
                V.reduce_max(top[:, 1, :], logits[:, :, :], AX).then_inc(link, 1)
                dve.wait_ge(link, 7)
                V.tensor_tensor(g2[:, 0, :], top[:, 1, :], top[:, 0, :], ALU.subtract).then_inc(link, 1)
                V.tensor_tensor(hit[:, :, :], logits[:, :, :], wide(top[:, 1, :]), ALU.is_equal).then_inc(link, 1)
                dve.wait_ge(link, 9)
                V.tensor_tensor(hit[:, :, :], hit[:, :, :], rank[:, :, :], ALU.mult).then_inc(link, 1)
                dve.wait_ge(link, 10)
                V.reduce_max(pos[:, 1, :], hit[:, :, :], AX).then_inc(link, 1)
                dve.wait_ge(link, 11)
                V.tensor_tensor(hit[:, :, :], rank[:, :, :], wide(pos[:, 1, :]), ALU.is_equal).then_inc(link, 1)
                dve.wait_ge(exp_done, 1)
                V.tensor_scalar_add(g1[:, 0, :], g2[:, 0, :], 1.0).then_inc(link, 1)
                dve.wait_ge(link, 13)
                V.reciprocal(g1[:, 0, :], g1[:, 0, :]).then_inc(link, 1)
                dve.wait_ge(link, 14)
                V.tensor_tensor(g2[:, 0, :], g2[:, 0, :], g1[:, 0, :], ALU.mult).then_inc(link, 1)
                V.tensor_tensor(first[:, :, :], first[:, :, :], wide(g1[:, 0, :]), ALU.mult).then_inc(link, 1)
                dve.wait_ge(link, 16)
                V.tensor_tensor(hit[:, :, :], hit[:, :, :], wide(g2[:, 0, :]), ALU.mult).then_inc(link, 1)
                dve.wait_ge(link, 17)
                V.tensor_tensor(logits[:, :, :], first[:, :, :], hit[:, :, :], ALU.add).then_inc(link, 1)
                dve.wait_ge(link, 18)


def expert_stage(nc, w_in, w_gate, w_out, gates, tnT_sb, t_sb, tag):
    import concourse.bass as bass
    from concourse import mybir
    from contextlib import ExitStack

    fp32 = mybir.dt.float32
    ALU, ACT = mybir.AluOpType, mybir.ActivationFunctionType
    E = gates.shape[2]
    FOUR = 4
    QUADS = E // FOUR
    TURNS = TILES // GROUP
    with ExitStack() as ctx:
        def sb(name, shape):
            return ctx.enter_context(nc.sbuf_tensor(tag + name, shape, fp32))

        def sem(name):
            return ctx.enter_context(nc.semaphore(tag + name))

        win, wout = sb("_win", [C, E, P]), sb("_wout", [P, E, C])
        wg = sb("_wg", [C, E, P])
        hid = [sb(f"_hid{k}", [P, HALF]) for k in range(2)]
        act_out = [sb(f"_act{k}", [P, HALF]) for k in range(2)]
        tmp = sb("_tmp", [P, GROUP, FOUR, C])
        red = sb("_red", [P, GROUP, C])
        ps1 = [ctx.enter_context(nc.psum_tensor(f"{tag}_ps1{k}", [P, HALF], fp32)) for k in range(2)]
        ps2 = [ctx.enter_context(nc.psum_tensor(f"{tag}_ps2{k}", [P, HALF], fp32)) for k in range(2)]
        psY = [ctx.enter_context(nc.psum_tensor(f"{tag}_psY{k}", [P, GROUP * FOUR * C], fp32)) for k in range(2)]
        loaded, h_ready, activated, hid_ready, y_ready, gated = (
            sem(n) for n in ("_loaded", "_h_ready", "_activated", "_hid_ready", "_y_ready", "_gated"))
        reduced, added, fetched = sem("_reduced"), sem("_added"), sem("_fetched")
        turns_done = sem("_turns_done")
        tokens = [sb(f"_tok{k}", [C, HALF]) for k in range(2)]
        loads = [(win, w_in), (wout, w_out), (wg, w_gate)]
        LOADED = 16 * len(loads)

        with nc.Block() as block:
            @block.sync
            def _(sp):
                for dst, src in loads:
                    sp.dma_start(dst[tuple([slice(None)] * len(dst.shape))], src).then_inc(loaded, 16)

            @block.tensor
            def _(pe):
                M = nc.tensor.matmul
                pe.wait_ge(loaded, LOADED)
                with pe.Fori(0, TURNS // 2) as pair:
                    def into(turn, e):
                        s = turn * E + e
                        rhs = tokens[k][:, :]
                        if e == 0:
                            pe.wait_ge(fetched, turn + 1)
                        pe.wait_ge(hid_ready, s + 1)
                        M(ps1[e % 2][:, :], win[:, e, :], rhs, start=True, stop=True).then_inc(h_ready, 1)
                        M(ps2[e % 2][:, :], wg[:, e, :], rhs, start=True, stop=True).then_inc(h_ready, 1)

                    def out_of(turn, e):
                        s = turn * E + e
                        quad, q = divmod(e, FOUR)
                        if q == 0:
                            pe.wait_ge(gated, turn * QUADS + quad + 1)
                        pe.wait_ge(hid_ready, s + 3)
                        for g in range(GROUP):
                            last = M(psY[quad % 2][:, (g * FOUR + q) * C:(g * FOUR + q + 1) * C],
                                     hid[e % 2][:, g * P:(g + 1) * P], wout[:, e, :], start=True, stop=True)
                            if e == E - 1 and g == 0:
                                last.then_inc(turns_done, 1)
                        last.then_inc(y_ready, 1)

                    for k in range(2):
                        turn = pair * 2 + k
                        into(turn, 0)
                        for e in range(E):
                            if e + 1 < E:
                                into(turn, e + 1)
                            out_of(turn, e)

            @block.gpsimd
            def _(pool):
                with pool.Fori(0, TURNS // 2) as pair:
                    for k in range(2):
                        turn = pair * 2 + k
                        pool.wait_ge(turns_done, turn + 1)
                        nc.gpsimd.tensor_copy(tokens[k][:, :], tnT_sb[:, bass.ds(turn * HALF, HALF)]).then_inc(fetched, 1)

            @block.scalar
            def _(act):
                act.wait_ge(loaded, LOADED)
                with act.Fori(0, TURNS // 2) as pair:
                    for k, e in [(k, e) for k in range(2) for e in range(E)]:
                        s = (pair * 2 + k) * E + e
                        act.wait_ge(h_ready, s * 2 + 1)
                        act.wait_ge(hid_ready, s + 1)
                        nc.scalar.activation(act_out[e % 2][:, :], ps1[e % 2][:, :], ACT.Silu).then_inc(activated, 1)

            @block.vector
            def _(dve):
                V = nc.vector
                dve.wait_ge(loaded, LOADED)
                V.memset(red[:, 0, 0:1], 0.0).then_inc(y_ready, 2)
                V.memset(red[:, 0, 1:2], 0.0).then_inc(gated, 2)
                V.memset(red[:, 0, 2:3], 0.0).then_inc(hid_ready, 2)
                V.memset(red[:, 0, 3:4], 0.0).then_inc(turns_done, 2)
                with dve.Fori(0, TURNS // 2) as pair:
                    def gate(turn, quad):
                        s = turn * QUADS + quad
                        y = psY[quad % 2][:, :].rearrange("p (g e c) -> p g e c", g=GROUP, e=FOUR)
                        dve.wait_ge(y_ready, s * FOUR + FOUR + 2)
                        g4 = gates[:, bass.ds(turn * GROUP, GROUP), quad * FOUR:(quad + 1) * FOUR]
                        V.tensor_tensor(tmp[:, :, :, :], y, g4.unsqueeze(3).broadcast_to([P, GROUP, FOUR, C]),
                                        ALU.mult).then_inc(gated, 1)
                        dve.wait_ge(gated, s + 3)
                        V.tensor_reduce(red[:, :, :], tmp[:, :, :, :].rearrange("p g e c -> p g c e"),
                                        mybir.AxisListType.X, ALU.add).then_inc(reduced, 1)
                        dve.wait_ge(reduced, s + 1)
                        t_now = t_sb[:, bass.ds(turn * GROUP, GROUP), :]
                        V.tensor_tensor(t_now, t_now, red[:, :, :], ALU.add).then_inc(added, 1)
                        dve.wait_ge(added, s + 1)

                    for k2, e in [(k2, e) for k2 in range(2) for e in range(E)]:
                        turn = pair * 2 + k2
                        s = turn * E + e
                        dve.wait_ge(activated, s + 1)
                        dve.wait_ge(h_ready, s * 2 + 2)
                        dve.wait_ge(y_ready, s + 1)
                        V.tensor_tensor(hid[e % 2][:, :], act_out[e % 2][:, :], ps2[e % 2][:, :], ALU.mult).then_inc(hid_ready, 1)
                        if e % FOUR == 1 and e > FOUR:
                            gate(turn, e // FOUR - 1)
                        if e == E - 1:
                            gate(turn, QUADS - 1)
SLICES, HEADS3, HDIM3 = 16, 8, 32
HD3 = HEADS3 * HDIM3
SW_0 = 0
SW_S = SW_0 + P
SW_QKV = SW_S + SLICES
SW_OUT = SW_QKV + 3 * HD3
SV_B0 = SW_OUT + 2 * C
SR_B0 = SV_B0 + 1
SR_BS = SR_B0 + C
SR_BO = SR_BS + SLICES
SW_COLS = SR_BO + C


def slice_attn_stage(nc, weights, consts, tn_sb, t_sb):
    import concourse.bass as bass
    from concourse import mybir
    from contextlib import ExitStack

    fp32 = mybir.dt.float32
    ALU, ACT, AX = mybir.AluOpType, mybir.ActivationFunctionType, mybir.AxisListType.X
    BLK = range(PER)
    HG = 4
    pe_s = Steps("turn hT h logits swT pool poolT qk v scores attnT tokT fold out")
    act_s = Steps("copy tnT hTc esw swTc poolTc qkc eat attnTc foldc")
    dve_s = Steps("hx lg max sub sum rsum sw dn rdn pooled vc qdiag smax ssub ssum srec attn tokm tok outb t")

    with ExitStack() as ctx:
        def sb(name, shape):
            return ctx.enter_context(nc.sbuf_tensor("s_" + name, shape, fp32))

        def ps(name, cols=HALF):
            return ctx.enter_context(nc.psum_tensor("s_" + name, [P, cols], fp32))

        def sem(name):
            return ctx.enter_context(nc.semaphore("s_" + name))

        w, con = sb("w", [P, SW_COLS]), sb("con", [P, K_COLS])
        tw = sb("tw", [P, PER, C])
        tnT, hT = sb("tnT", [C, L]), sb("hT", [C, L])
        hx = sb("hx", [P, PER, C + 1])
        sw = sb("sw", [P, PER, SLICES])
        r8 = sb("r8", [P, 2, PER])
        swT = sb("swT", [SLICES, L])
        pooled, dn = sb("pooled", [SLICES, C + 1]), sb("dn", [SLICES, 1])
        poolT = sb("poolT", [C + 1, SLICES])
        qk = sb("qk", [P, 4, SLICES])
        v = sb("v", [SLICES, HD3])
        qd = sb("qd", [P, 2, HG, SLICES])
        at = sb("at", [P, 2, SLICES])
        rs = sb("rs", [HG * SLICES, 2, 2])
        atT = sb("atT", [SLICES, 2 * HG * SLICES])
        tokm, tok = sb("tokm", [P, 2, HG, SLICES]), sb("tok", [P, 2, SLICES])
        fold = sb("fold", [SLICES, C])
        tmp = sb("tmp", [P, PER, C])
        psM = ps("psM", L)
        psH, psL, psG, psQ, psS, psO = (ps(n) for n in ("psH", "psL", "psG", "psQ", "psS", "psO"))
        loaded, ones_set = sem("loaded"), sem("ones")
        pe_done, act_done, dve_done = sem("pe"), sem("act"), sem("dve")
        halves = [slice(0, HALF), slice(HALF, L)]
        at4 = at[0:HG * SLICES, :, :]
        ID = con[:, K_ID:K_ID + P]

        with nc.Block() as block:
            @block.sync
            def _(sp):
                sp.dma_start(w[:, :], weights).then_inc(loaded, 16)
                sp.dma_start(con[:, :], consts).then_inc(loaded, 16)

            @block.gpsimd
            def _(pool):
                nc.gpsimd.memset(hx[:, :, :], 1.0).then_inc(ones_set, 1)
                nc.gpsimd.memset(at[:, :, :], 0.0).then_inc(ones_set, 1)

            @block.tensor
            def _(pe):
                M = nc.tensor.matmul
                pe.wait_ge(loaded, 32)
                with pe.Fori(0, B) as img:
                    def act(name):
                        pe.wait_ge(act_done, act_s.after(name, img))

                    def dve(name):
                        pe.wait_ge(dve_done, dve_s.after(name, img))

                    def done(ins):
                        ins.then_inc(pe_done, 1)

                    act("copy")
                    for i in BLK:
                        last = M(psM[0:C, i * P:(i + 1) * P], tw[:, i, :], ID, start=True, stop=True)
                    done(last)
                    act("tnT")
                    for hs in halves:
                        last = M(psM[:, hs], w[0:C, SW_0:SW_0 + P], tnT[:, hs], start=True, stop=True)
                    done(last)
                    for i in BLK:
                        last = M(psH[:, i * C:(i + 1) * C], tnT[:, i * P:(i + 1) * P], w[0:C, SW_0:SW_0 + C],
                                 start=True, stop=True)
                    done(last)
                    act("hTc")
                    for i in BLK:
                        last = M(psL[:, i * SLICES:(i + 1) * SLICES], hT[:, i * P:(i + 1) * P], w[0:C, SW_S:SW_S + SLICES],
                                 start=True, stop=True)
                    done(last)
                    dve("sw")
                    for i in BLK:
                        last = M(psM[0:SLICES, i * P:(i + 1) * P], sw[:, i, :], ID, start=True, stop=True)
                    done(last)
                    for i in BLK:
                        last = M(psG[0:SLICES, 0:C + 1], sw[:, i, :], hx[:, i, :], start=i == 0, stop=i == PER - 1)
                    done(last)
                    dve("pooled")
                    done(M(psS[0:C + 1, 0:SLICES], pooled[:, :], con[0:SLICES, K_ID:K_ID + SLICES], start=True, stop=True))
                    act("poolTc")
                    for j in range(4):
                        last = M(psQ[:, j * SLICES:(j + 1) * SLICES], w[0:C + 1, SW_QKV + j * P:SW_QKV + (j + 1) * P], poolT[:, :],
                                 start=True, stop=True)
                    done(last)
                    done(M(psG[0:SLICES, 0:HD3], poolT[:, :], w[0:C + 1, SW_QKV + 2 * HD3:SW_QKV + 3 * HD3],
                           start=True, stop=True))
                    dve("qdiag")
                    for g in range(2):
                        last = M(psS[0:HG * SLICES, g * SLICES:(g + 1) * SLICES], qd[:, g, :, :].rearrange("p h s -> p (h s)"),
                                 qk[:, 2 + g, :], start=True, stop=True)
                    done(last)
                    dve("attn")
                    for g in range(2):
                        last = M(psL[0:SLICES, g * HG * SLICES:(g + 1) * HG * SLICES], at[:, g, :],
                                 con[:, K_ID:K_ID + HG * SLICES], start=True, stop=True)
                    done(last)
                    act("attnTc")
                    for g in range(2):
                        last = M(psQ[:, g * HG * SLICES:(g + 1) * HG * SLICES], v[:, g * P:(g + 1) * P],
                                 atT[:, g * HG * SLICES:(g + 1) * HG * SLICES], start=True, stop=True)
                    done(last)
                    dve("tok")
                    for g in range(2):
                        last = M(psG[0:SLICES, 0:C], tok[:, g, :], w[:, SW_OUT + g * C:SW_OUT + (g + 1) * C],
                                 start=g == 0, stop=g == 1)
                    done(last)
                    act("foldc")
                    for i in BLK:
                        last = M(psO[:, i * C:(i + 1) * C], swT[:, i * P:(i + 1) * P], fold[:, :], start=True, stop=True)
                    done(last)

            @block.scalar
            def _(act):
                A = nc.scalar.activation
                act.wait_ge(loaded, 32)
                A(rs[:, 0, 0:1], con[0:HG * SLICES, 0:1], ACT.Copy).then_inc(act_done, 1)
                with act.Fori(0, B) as img:
                    def pe(name):
                        act.wait_ge(pe_done, pe_s.after(name, img) - 1)

                    def dve(name):
                        act.wait_ge(dve_done, dve_s.after(name, img))

                    act.wait_ge(dve_done, dve_s.all(img))
                    A(tw[:, :, :], tn_sb[:, bass.ds(img * PER, PER), :], ACT.Copy).then_inc(act_done, 1)
                    pe("turn")
                    A(tnT[:, :], psM[0:C, :], ACT.Copy).then_inc(act_done, 1)
                    pe("hT")
                    A(hT[:, :], psM[0:C, :], ACT.Identity, bias=w[0:C, SV_B0:SV_B0 + 1]).then_inc(act_done, 1)
                    dve("sub")
                    A(sw[:, :, :], sw[:, :, :], ACT.Exp).then_inc(act_done, 1)
                    pe("swT")
                    A(swT[:, :], psM[0:SLICES, :], ACT.Copy).then_inc(act_done, 1)
                    pe("poolT")
                    A(poolT[:, :], psS[0:C + 1, 0:SLICES], ACT.Copy).then_inc(act_done, 1)
                    pe("qk")
                    A(qk[:, :, :], psQ[:, 0:4 * SLICES].rearrange("p (j s) -> p j s", j=4), ACT.Copy).then_inc(act_done, 1)
                    dve("ssub")
                    A(at4, at4, ACT.Exp, scale=HDIM3 ** -0.5).then_inc(act_done, 1)
                    pe("attnT")
                    A(atT[:, :], psL[0:SLICES, 0:2 * HG * SLICES], ACT.Copy).then_inc(act_done, 1)
                    pe("fold")
                    A(fold[:, :], psG[0:SLICES, 0:C], ACT.Copy).then_inc(act_done, 1)

            @block.vector
            def _(dve):
                V = nc.vector
                dve.wait_ge(loaded, 32)
                dve.wait_ge(ones_set, 2)
                V.memset(tmp[:, 0, 0:1], 0.0).then_inc(dve_done, 1)
                with dve.Fori(0, B) as img:
                    def pe(name):
                        dve.wait_ge(pe_done, pe_s.after(name, img) - 1)

                    def act(name):
                        dve.wait_ge(act_done, act_s.after(name, img))

                    def own(name):
                        dve.wait_ge(dve_done, dve_s.after(name, img))

                    def done(ins):
                        ins.then_inc(dve_done, 1)

                    def row(v_, shape):
                        return v_.unsqueeze(1).broadcast_to(shape)

                    pe("h")
                    done(V.tensor_tensor(hx[:, :, 0:C], psH[:, :].rearrange("p (i c) -> p i c", i=PER),
                                         row(w[:, SR_B0:SR_B0 + C], [P, PER, C]), ALU.add))
                    pe("logits")
                    done(V.tensor_tensor(sw[:, :, :], psL[:, 0:PER * SLICES].rearrange("p (i s) -> p i s", i=PER),
                                         row(w[:, SR_BS:SR_BS + SLICES], [P, PER, SLICES]), ALU.add))
                    own("lg")
                    done(V.reduce_max(r8[:, 0, :], sw[:, :, :], AX))
                    own("max")
                    wide = [P, PER, SLICES]
                    done(V.tensor_tensor(sw[:, :, :], sw[:, :, :], r8[:, 0, :].unsqueeze(2).broadcast_to(wide), ALU.subtract))
                    act("esw")
                    done(V.reduce_sum(r8[:, 1, :], sw[:, :, :], AX))
                    own("sum")
                    done(V.reciprocal(r8[:, 1, :], r8[:, 1, :]))
                    own("rsum")
                    done(V.tensor_tensor(sw[:, :, :], sw[:, :, :], r8[:, 1, :].unsqueeze(2).broadcast_to(wide), ALU.mult))
                    pe("pool")
                    done(V.tensor_scalar_add(dn[:, :], psG[0:SLICES, C:C + 1], 1e-9))
                    own("dn")
                    done(V.reciprocal(dn[:, :], dn[:, :]))
                    own("rdn")
                    done(V.tensor_scalar(pooled[:, :], psG[0:SLICES, 0:C + 1], dn[:, :], None, ALU.mult))
                    pe("v")
                    done(V.tensor_copy(v[:, :], psG[0:SLICES, 0:HD3]))
                    act("qkc")
                    done(V.tensor_tensor(qd[:, :, :, :], qk[:, 0:2, :].unsqueeze(2).broadcast_to([P, 2, HG, SLICES]),
                                         con[:, K_MASK:K_MASK + 64].rearrange("p (h s) -> p h s", h=HG).unsqueeze(1).broadcast_to(
                                             [P, 2, HG, SLICES]), ALU.mult))
                    pe("scores")
                    sc = psS[0:HG * SLICES, 0:2 * SLICES].rearrange("p (g s) -> p g s", g=2)
                    done(V.reduce_max(rs[:, 0, :], sc, AX))
                    own("smax")
                    wide2 = [HG * SLICES, 2, SLICES]
                    done(V.tensor_tensor(at4, sc, rs[:, 0, :].unsqueeze(2).broadcast_to(wide2), ALU.subtract))
                    act("eat")
                    done(V.reduce_sum(rs[:, 1, :], at4, AX))
                    own("ssum")
                    done(V.reciprocal(rs[:, 1, :], rs[:, 1, :]))
                    own("srec")
                    done(V.tensor_tensor(at4, at4, rs[:, 1, :].unsqueeze(2).broadcast_to(wide2), ALU.mult))
                    pe("tokT")
                    done(V.tensor_tensor(tokm[:, :, :, :], psQ[:, 0:2 * HG * SLICES].rearrange("p (g h s) -> p g h s", g=2, h=HG),
                                         con[:, K_MASK:K_MASK + 64].rearrange("p (h s) -> p h s", h=HG).unsqueeze(1).broadcast_to(
                                             [P, 2, HG, SLICES]), ALU.mult))
                    own("tokm")
                    done(V.tensor_reduce(tok[:, :, :], tokm[:, :, :, :].rearrange("p g h s -> p g s h"), AX, ALU.add))
                    pe("out")
                    done(V.tensor_tensor(tmp[:, :, :], psO[:, :].rearrange("p (i c) -> p i c", i=PER),
                                         row(w[:, SR_BO:SR_BO + C], [P, PER, C]), ALU.add))
                    own("outb")
                    t_now = t_sb[:, bass.ds(img * PER, PER), :]
                    done(V.tensor_tensor(t_now, t_now, tmp[:, :, :], ALU.add))
EDGES = 262144
ECOLS = EDGES // P
COL_BITS, PART_BITS = 11, 7
NODES = TOK
SRC_BITS = 13
KEY_BASE = 0x20000000
OUTSIDE = 1 << 20
BIG = 1e30


def sort_stage(nc, edges, consts, src_d, keep_d, pen_d, first_d, ends_d, place_d, target0_d):
    import concourse.bass as bass
    from concourse import mybir
    from contextlib import ExitStack

    fp32, i32 = mybir.dt.float32, mybir.dt.int32
    ALU, ACT = mybir.AluOpType, mybir.ActivationFunctionType

    with ExitStack() as ctx:
        def sb(name, shape, dt=fp32):
            return ctx.enter_context(nc.sbuf_tensor("o_" + name, shape, dt))

        def sem(name):
            return ctx.enter_context(nc.semaphore("o_" + name))

        con = sb("con", [P, K_COLS])
        es, ed = sb("es", [P, ECOLS], i32), sb("ed", [P, ECOLS], i32)
        f1, f2 = sb("f1", [P, ECOLS]), sb("f2", [P, ECOLS])
        key = [sb("key0", [P, ECOLS]), sb("key1", [P, ECOLS])]
        edge_col = sb("edge_col", [P, 2], i32)
        es2 = sb("es2", [P, ECOLS], i32)
        place = sb("place", [P, ECOLS], i32)
        ps = ctx.enter_context(nc.psum_tensor("o_ps", [P, ECOLS], fp32))
        loaded, link, turned, copied, shifted, placed, stored = (
            sem(n) for n in ("loaded", "link", "turned", "copied", "shifted", "placed", "stored"))
        apart = sem("apart")
        BLOCKS = ECOLS // P

        steps = []
        for k in range(1, COL_BITS + PART_BITS + 1):
            steps.append(("flip", k))
            if k > COL_BITS:
                steps.append(("turn", None))
                steps += [("across", j - COL_BITS) for j in range(k - 1, COL_BITS - 1, -1)]
                steps.append(("turn", None))
            steps += [("along", j) for j in range(min(k, COL_BITS) - 1, -1, -1)]
        link_at, buf_at, made, buf = {}, {}, 9, 0
        for n, (kind, at) in enumerate(steps):
            link_at[n], buf_at[n] = made, buf
            if kind == "flip":
                made += 2 if at == COL_BITS else 1
            elif kind != "turn":
                made, buf = made + 2, 1 - buf
        TURNS = [n for n, (kind, _) in enumerate(steps) if kind == "turn"]

        with nc.Block() as block:
            @block.sync
            def _(sp):
                sp.dma_start(con[:, :], consts).then_inc(loaded, 16)
                sp.dma_start(es[:, :], edges[0, :, :]).then_inc(loaded, 16)
                sp.dma_start(ed[:, :], edges[1, :, :]).then_inc(loaded, 16)
                sp.wait_ge(shifted, 2)
                sp.wait_ge(apart, 1)
                sp.dma_start(edge_col[1:P, 0:1], ed[0:P - 1, ECOLS - 1:ECOLS]).then_inc(placed, 16)
                sp.dma_start(edge_col[0:P - 1, 1:2], ed[1:P, 0:1]).then_inc(placed, 16)
                sp.dma_start(src_d, es[:, :]).then_inc(stored, 16)
                sp.dma_start(target0_d, ed[:, 0:1]).then_inc(stored, 16)
                sp.wait_ge(copied, len(TURNS) + 1)
                sp.dma_start(keep_d, f1[:, :]).then_inc(stored, 16)
                sp.dma_start(pen_d, f2[:, :]).then_inc(stored, 16)
                sp.wait_ge(copied, len(TURNS) + 2)
                sp.dma_start(first_d, key[0][:, :]).then_inc(stored, 16)
                sp.wait_ge(copied, len(TURNS) + 3)
                sp.dma_start(ends_d, key[1][:, :].bitcast(i32)).then_inc(stored, 16)
                sp.dma_start(place_d, place[:, :]).then_inc(stored, 16)
                sp.wait_ge(stored, 16 * 7)

            @block.gpsimd
            def _(pool):
                nc.gpsimd.iota(place[:, :], pattern=[[2, ECOLS]], base=0, channel_multiplier=2 * ECOLS).then_inc(shifted, 1)
                nc.gpsimd.memset(edge_col[:, :], -1).then_inc(shifted, 1)

            @block.tensor
            def _(pe):
                pe.wait_ge(loaded, 48)
                for turn, n in enumerate(TURNS):
                    pe.wait_ge(link, link_at[n])
                    for r in range(BLOCKS):
                        last = nc.tensor.transpose(ps[:, r * P:(r + 1) * P], key[buf_at[n]][:, r * P:(r + 1) * P],
                                                   con[:, K_ID:K_ID + P])
                    last.then_inc(turned, 1)

            @block.scalar
            def _(act):
                for turn, n in enumerate(TURNS):
                    act.wait_ge(turned, turn + 1)
                    nc.scalar.activation(key[buf_at[n]][:, :], ps[:, :], ACT.Copy).then_inc(copied, 1)

            @block.vector
            def _(dve):
                V = nc.vector
                count = [0]

                def after(ins):
                    ins.then_inc(link, 1)
                    count[0] += 1

                def ready():
                    dve.wait_ge(link, count[0])

                dve.wait_ge(loaded, 48)
                after(V.tensor_scalar(f1[:, :], es[:, :], 0.0, float(NODES), ALU.is_lt, ALU.mult)); ready()
                after(V.tensor_tensor(f1[:, :], f1[:, :], es[:, :], ALU.add)); ready()
                after(V.tensor_scalar(es[:, :], f1[:, :], 0.0, float(NODES - 1), ALU.max, ALU.min)); ready()
                after(V.tensor_scalar(f1[:, :], ed[:, :], 0.0, float(NODES), ALU.is_lt, ALU.mult)); ready()
                after(V.tensor_scalar(f2[:, :], ed[:, :], 0.0, float(NODES), ALU.max, ALU.min)); ready()
                after(V.tensor_tensor(f1[:, :], f1[:, :], f2[:, :], ALU.add)); ready()
                after(V.tensor_scalar(ed[:, :], f1[:, :], float(NODES), None, ALU.min)); ready()
                after(V.tensor_scalar(ed[:, :], ed[:, :], SRC_BITS, KEY_BASE, ALU.logical_shift_left, ALU.bitwise_or)); ready()
                after(V.tensor_tensor(key[0][:, :].bitcast(i32), ed[:, :], es[:, :], ALU.bitwise_or)); ready()

                cur, turns = 0, 0
                for n, (kind, at) in enumerate(steps):
                    K = key[cur]
                    if kind == "flip" and at < COL_BITS:
                        w = 1 << (at - 1)
                        four = K[:, :].rearrange("p (b w) -> p b w", w=4 * w)
                        part = four[:, :, w:3 * w] if at > 1 else four[:, :, 2:4]
                        after(V.tensor_scalar(part, part, -1.0, None, ALU.mult)); ready()
                    elif kind == "flip" and at == COL_BITS:
                        half = ECOLS // 2
                        for h in range(2):
                            part = K[:, h * half:(h + 1) * half]
                            after(V.tensor_scalar(part, part, con[:, K_SIGN + h:K_SIGN + h + 1], None, ALU.mult))
                        ready()
                    elif kind == "flip":
                        c = K_SIGN + 1 + at - COL_BITS
                        after(V.tensor_scalar(K[:, :], K[:, :], con[:, c:c + 1], None, ALU.mult)); ready()
                    elif kind == "turn":
                        assert (link_at[n], buf_at[n]) == (count[0], cur)
                        turns += 1
                        dve.wait_ge(copied, turns)
                    else:
                        w = 1 << at
                        a = K[:, :].rearrange("p (b two w) -> p b two w", two=2, w=w)
                        o = key[1 - cur][:, :].rearrange("p (b two w) -> p b two w", two=2, w=w)
                        after(V.tensor_tensor(o[:, :, 0, :], a[:, :, 0, :], a[:, :, 1, :], ALU.min))
                        after(V.tensor_tensor(o[:, :, 1, :], a[:, :, 0, :], a[:, :, 1, :], ALU.max))
                        ready()
                        cur = 1 - cur

                S = key[cur][:, :].bitcast(i32)
                after(V.tensor_scalar(es[:, :], S, NODES - 1, None, ALU.bitwise_and)); ready()
                V.tensor_scalar(ed[:, :], S, SRC_BITS, 2 * NODES - 1, ALU.logical_shift_right, ALU.bitwise_and).then_inc(apart, 1)
                dve.wait_ge(apart, 1)
                dve.wait_ge(placed, 32)
                after(V.tensor_tensor(f1[:, 1:ECOLS], ed[:, 1:ECOLS], ed[:, 0:ECOLS - 1], ALU.is_equal))
                after(V.tensor_tensor(f1[:, 0:1], ed[:, 0:1], edge_col[:, 0:1], ALU.is_equal)); ready()
                V.tensor_scalar(f2[:, :], f1[:, :], 1.0, BIG, ALU.subtract, ALU.mult).then_inc(copied, 1)
                dve.wait_ge(copied, len(TURNS) + 1)
                V.tensor_tensor_scan(key[0][:, :], f1[:, :], f1[:, :], 1.0, ALU.mult, ALU.mult).then_inc(copied, 1)
                dve.wait_ge(copied, len(TURNS) + 2)
                after(V.tensor_copy(es2[:, :], key[0][:, :])); ready()
                after(V.tensor_tensor(place[:, :], place[:, :], es2[:, :], ALU.bitwise_or)); ready()
                E1 = key[1][:, :].bitcast(i32)
                after(V.tensor_tensor(E1[:, 0:ECOLS - 1], ed[:, 0:ECOLS - 1], ed[:, 1:ECOLS], ALU.is_equal))
                after(V.tensor_tensor(E1[:, ECOLS - 1:ECOLS], ed[:, ECOLS - 1:ECOLS], edge_col[:, 1:2], ALU.is_equal)); ready()
                after(V.tensor_scalar(E1, E1, float(OUTSIDE), None, ALU.mult)); ready()
                V.tensor_tensor(E1, E1, ed[:, :], ALU.bitwise_or).then_inc(copied, 1)
                dve.wait_ge(copied, len(TURNS) + 3)


def graph_tables(nc):
    from concourse import mybir
    fp32, i32 = mybir.dt.float32, mybir.dt.int32

    def dram(name, shape, dt):
        return nc.dram_tensor("scratch_" + name, shape, dt, kind="Internal").ap()

    return {
        "src": dram("src", (P, ECOLS), i32), "keep": dram("keep", (P, ECOLS), fp32), "pen": dram("pen", (P, ECOLS), fp32),
        "first": dram("first", (P, ECOLS), fp32), "ends_i": dram("ends_i", (P, ECOLS), i32),
        "place_i": dram("place_i", (P, ECOLS), i32), "target0": dram("target0", (P, 1), i32),
        "ends": dram("ends", (NODES, 1), i32), "start": dram("start", (NODES, 1), i32),
        "node": dram("node", (NODES, 20), fp32), "target": dram("target", (NODES, 4), fp32),
        "place": dram("place", (EDGES, 4), fp32), "edge": dram("edge", (EDGES, 24), fp32),
        "carry": dram("carry", (P, 24), fp32),
    }
GATES = 4
HEADS_G = 4
HE = HEADS_G * GATES
ROW_T = HE + HEADS_G
ROW_O = 2 * HEADS_G + HE
CHUNK = 32
CHUNKS = ECOLS // CHUNK
NOTED_FIRST = 3 * CHUNKS // 8


class EndsNotes:

    def __init__(self, nc, ctx, ends_d, place_d, ends_tbl):
        from concourse import mybir
        i32 = mybir.dt.int32
        self.nc, self.ends_d, self.place_d, self.ends_tbl = nc, ends_d, place_d, ends_tbl
        self.ends, self.place = (ctx.enter_context(nc.sbuf_tensor("e_" + n, [P, ECOLS], i32)) for n in ("ends", "place"))
        self.ends_w, self.place_w = (ctx.enter_context(nc.sbuf_tensor("e_" + n, [P, CHUNK], i32)) for n in ("ends_w", "place_w"))
        self.none, self.gate = (ctx.enter_context(nc.sbuf_tensor("e_" + n, [P, TILES], i32)) for n in ("none", "gate"))
        self.loaded, self.copied, self.set_, *self.scattered = (
            ctx.enter_context(nc.semaphore("e_" + n)) for n in ("loaded", "copied", "set", "scattered_0", "scattered_1"))

    def scatter(self, pool, first, last):
        import concourse.bass as bass
        from concourse import mybir
        nc = self.nc
        if first == 0:
            scattered = self.scattered[0]
            self.begin(pool)
        else:
            scattered = self.scattered[1]
            pool.dma_start(self.place_w[:, :], self.place_d[:, 0:CHUNK]).then_inc(scattered, 16)
        with pool.Fori(first, last) as c:
            pool.wait_ge(scattered, (c - first) * (16 * CHUNK) + 16)
            nc.gpsimd.tensor_copy(self.ends_w[:, :], self.ends[:, bass.ds(c * CHUNK, CHUNK)]).then_inc(self.copied, 1)
            nc.gpsimd.tensor_copy(self.place_w[:, :], self.place[:, bass.ds(c * CHUNK, CHUNK)]).then_inc(self.copied, 1)
            pool.wait_ge(self.copied, c * 2 + 2)
            nc.gpsimd.tensor_tensor(self.gate[:, 0:1], self.gate[:, 1:2], self.gate[:, 2:3], mybir.AluOpType.add)
            for j in range(CHUNK):
                nc.gpsimd.indirect_dma_start(
                    out=self.ends_tbl, out_offset=bass.IndirectOffsetOnAxis(ap=self.ends_w[:, j:j + 1], axis=0),
                    in_=self.place_w[:, j:j + 1], in_offset=None, bounds_check=NODES - 1, oob_is_err=False,
                ).then_inc(scattered, 16)
        pool.wait_ge(scattered, 16 * CHUNK * (last - first) + 16)

    def begin(self, pool):
        nc = self.nc
        pool.dma_start(self.ends[:, :], self.ends_d).then_inc(self.loaded, 16)
        pool.dma_start(self.place[:, :], self.place_d).then_inc(self.loaded, 16)
        nc.gpsimd.memset(self.none[:, :], -1).then_inc(self.set_, 1)
        nc.gpsimd.memset(self.gate[:, :], 0).then_inc(self.set_, 1)
        pool.wait_ge(self.set_, 2)
        pool.dma_start(self.ends_tbl.rearrange("(p i) o -> p (i o)", p=P), self.none[:, :]).then_inc(self.scattered[0], 16)
        pool.wait_ge(self.loaded, 32)


def graph_stage(nc, att_rows, feat, tables, experts, tnT_sb, y_all, x):
    import concourse.bass as bass
    from concourse import mybir
    from contextlib import ExitStack

    fp32, i32 = mybir.dt.float32, mybir.dt.int32
    ALU, ACT, AX = mybir.AluOpType, mybir.ActivationFunctionType, mybir.AxisListType.X
    Off = bass.IndirectOffsetOnAxis
    node_tbl, target_tbl, place_tbl, edge_tbl, carry_tbl, start_tbl, ends_tbl = (
        tables[n] for n in ("node", "target", "place", "edge", "carry", "start", "ends"))
    scores = x["scores"]

    def whole(t):
        return t[tuple([slice(None)] * len(t.shape))]

    with ExitStack() as outer:
        def keep_sb(name, shape, dt=fp32):
            return outer.enter_context(nc.sbuf_tensor("r_" + name, shape, dt))

        row = keep_sb("row", [P, TILES, ROW_T])
        adst = keep_sb("adst", [P, TILES, HEADS_G])
        att = keep_sb("att", [P, 5 * HE])
        end_i, end_f = keep_sb("end_i", [P, TILES], i32), keep_sb("end_f", [P, TILES])
        end_idx, start_idx, carry_idx = (keep_sb(n, [P, TILES], i32) for n in ("end_idx", "start_idx", "carry_idx"))
        state = keep_sb("state", [P, ROW_O])
        ad0 = keep_sb("ad0", [P, HEADS_G])

        with ExitStack() as ctx:
            def sb(name, shape, dt=fp32):
                return ctx.enter_context(nc.sbuf_tensor("n_" + name, shape, dt))

            def sem(name):
                return ctx.enter_context(nc.semaphore("n_" + name))

            prod = sb("prod", [P, TILES, HE])
            zero = sb("zero", [P, ECOLS])
            line = sb("line", [1, NODES], i32)
            top = sb("top", [1, NODES + 1])
            t0 = sb("t0", [P, 1], i32)
            part = sb("part", [P, TILES], i32)
            lf, lg = sb("lf", [P, TILES]), sb("lg", [P, TILES])
            loaded, zeroed, link, rows_out, starts_out, starts_in, filled, spread = (
                sem(n) for n in ("loaded", "zeroed", "link", "rows_out", "starts_out", "starts_in", "filled", "spread"))

            with nc.Block() as block:
                NODE_ROWS, START_ROW = 5, 11

                @block.sync
                def _(sp):
                    sp.dma_start(whole(att), att_rows).then_inc(loaded, 16)
                    sp.dma_start(line[:, :], ends_tbl.rearrange("n o -> o n")).then_inc(loaded, 16)
                    sp.dma_start(end_i[:, :], ends_tbl.rearrange("(i p) o -> p (i o)", p=P),
                                 allow_slow_non_contiguous=True).then_inc(loaded, 16)
                    sp.dma_start(t0[:, :], x["target0"]).then_inc(loaded, 16)
                    sp.wait_ge(zeroed, 1)
                    place_v = place_tbl.rearrange("(q p c) h -> q p (c h)", q=4, p=P)
                    for q in range(4):
                        sp.dma_start(place_v[q, :, :], zero[:, :]).then_inc(filled, 16)
                    sp.wait_ge(link, NODE_ROWS)
                    sp.dma_start(node_tbl.rearrange("(i p) f -> p i f", p=P), whole(row)).then_inc(rows_out, 16)
                    sp.dma_start(target_tbl.rearrange("(i p) f -> p i f", p=P), whole(adst)).then_inc(rows_out, 16)
                    sp.wait_ge(link, START_ROW)
                    sp.dma_start(start_tbl.rearrange("n o -> o n"), line[:, :]).then_inc(starts_out, 16)
                    sp.wait_ge(starts_out, 16)
                    sp.dma_start(start_idx[:, :], start_tbl.rearrange("(i p) o -> p (i o)", p=P),
                                 allow_slow_non_contiguous=True).then_inc(starts_in, 16)
                    sp.wait_ge(starts_in, 16)

                @block.gpsimd
                def _(pool):
                    nc.gpsimd.memset(zero[:, :], 0.0).then_inc(zeroed, 1)
                    nc.gpsimd.memset(ad0[:, :], 0.0).then_inc(zeroed, 1)
                    pool.wait_ge(zeroed, 2)
                    pool.wait_ge(loaded, 64)
                    pool.wait_ge(rows_out, 32)
                    nc.gpsimd.indirect_dma_start(out=ad0[:, :], out_offset=None, in_=target_tbl,
                                                 in_offset=Off(ap=t0[:, 0:1], axis=0),
                                                 bounds_check=NODES - 1, oob_is_err=False).then_inc(spread, 16)
                    pool.wait_ge(filled, 64)
                    pool.wait_ge(starts_in, 16)
                    for i in range(TILES):
                        nc.gpsimd.indirect_dma_start(out=place_tbl, out_offset=Off(ap=start_idx[:, i:i + 1], axis=0),
                                                     in_=adst[:, i, :], in_offset=None,
                                                     bounds_check=EDGES - 1, oob_is_err=False).then_inc(spread, 16)
                    pool.wait_ge(spread, 16 * (TILES + 1))

                @block.vector
                def _(dve):
                    V = nc.vector
                    count = [0]

                    def link_(ins):
                        ins.then_inc(link, 1)
                        count[0] += 1
                        dve.wait_ge(link, count[0])

                    dve.wait_ge(loaded, 64)

                    def att_sum(out, at):
                        link_(V.tensor_tensor(whole(prod), whole(feat), att[:, at * HE:(at + 1) * HE].unsqueeze(1).broadcast_to([P, TILES, HE]), ALU.mult))
                        link_(V.tensor_reduce(out, prod[:, :, :].rearrange("p i (h e) -> p i h e", h=HEADS_G), AX, ALU.add))

                    att_sum(adst[:, :, :], 1)
                    att_sum(row[:, :, HE:ROW_T], 0)
                    link_(V.tensor_copy(row[:, :, 0:HE], whole(feat)))
                    assert count[0] == NODE_ROWS
                    link_(V.tensor_scalar(line[:, :], line[:, :], 1, None, ALU.arith_shift_right))
                    link_(V.memset(top[:, 0:1], -1.0))
                    link_(V.tensor_tensor_scan(top[:, 1:NODES + 1], line[:, :], line[:, :], -1.0, ALU.max, ALU.max))
                    link_(V.tensor_scalar(line[:, :], line[:, :], 0.0, float(OUTSIDE), ALU.is_lt, ALU.mult))
                    link_(V.scalar_tensor_tensor(line[:, :], top[:, 0:NODES], 1.0, line[:, :], ALU.add, ALU.add))
                    link_(V.tensor_copy(part[:, :], end_i[:, :]))
                    assert count[0] == START_ROW
                    link_(V.tensor_scalar(end_idx[:, :], end_i[:, :], 1, None, ALU.arith_shift_right))
                    link_(V.tensor_copy(end_f[:, :], end_idx[:, :]))
                    link_(V.tensor_scalar(lg[:, :], end_f[:, :], 0.0, 2.0 * OUTSIDE, ALU.is_lt, ALU.mult))
                    link_(V.tensor_tensor(end_f[:, :], end_f[:, :], lg[:, :], ALU.add))
                    link_(V.tensor_scalar(part[:, :], part[:, :], 1, None, ALU.bitwise_and))
                    link_(V.tensor_copy(lf[:, :], part[:, :]))
                    link_(V.tensor_scalar(lf[:, :], lf[:, :], -float(OUTSIDE), float(OUTSIDE), ALU.mult, ALU.add))
                    link_(V.tensor_tensor(lf[:, :], lf[:, :], lg[:, :], ALU.add))
                    link_(V.tensor_scalar(part[:, :], end_idx[:, :], COL_BITS, None, ALU.arith_shift_right))
                    link_(V.tensor_copy(lg[:, :], part[:, :]))
                    link_(V.tensor_tensor(carry_idx[:, :], lf[:, :], lg[:, :], ALU.add))
                    link_(V.tensor_copy(end_idx[:, :], end_f[:, :]))

        with ExitStack() as ctx:
            def sb(name, shape, dt=fp32):
                return ctx.enter_context(nc.sbuf_tensor("g2_" + name, shape, dt))

            def sem(name):
                return ctx.enter_context(nc.semaphore("g2_" + name))

            src = sb("src", [P, ECOLS], i32)
            keep, pen = sb("keep", [P, ECOLS]), sb("pen", [P, ECOLS])
            tgt = sb("tgt", [P, ECOLS, HEADS_G])
            gate, spare, done = sb("gate", [P, 4]), sb("spare", [P, 4]), sb("done", [P, 1])
            idx = [sb(f"idx{k}", [P, CHUNK], i32) for k in range(2)]
            got = [sb(f"got{k}", [P, CHUNK, ROW_T]) for k in range(2)]
            out = [sb(f"out{k}", [P, CHUNK, ROW_O]) for k in range(2)]
            ad, e, w, r = (sb(n, [P, HEADS_G, CHUNK]) for n in ("ad", "e", "w", "r"))
            m = sb("m", [P, HEADS_G, CHUNK + 1])
            msg = sb("msg", [P, HE, CHUNK])
            loaded, copied, set_, link = sem("loaded"), sem("copied"), sem("set"), sem("link")
            gathered = [sem("gathered0"), sem("gathered1")]
            consumed, exps, written = sem("consumed"), sem("exps"), [sem("written0"), sem("written1")]
            DVE_STEPS = Steps("t1 t2 t3 t4 adkeep e leaky m1 m2 m3 m4 w0 r0 r1 s1 s2 s3 s4 msg "
                              + " ".join(f"f{k}" for k in range(HE)) + " mcopy mkeep skeep")
            edge_v = edge_tbl.rearrange("(p c) f -> p (c f)", p=P)
            assert CHUNKS == GATES * (TILES // GROUP)
            win, wout = sb("win", [C, GATES, P]), sb("wout", [P, GATES, C])
            b1, b2 = sb("b1", [P, GATES]), sb("b2", [P, GATES, C])
            tokens, hid = sb("tokens", [C, HALF]), sb("hid", [P, HALF])
            ps_h = ctx.enter_context(nc.psum_tensor("g2_ps_h", [P, HALF], fp32))
            ps_y = ctx.enter_context(nc.psum_tensor("g2_ps_y", [P, GROUP * C], fp32))
            w_loaded, tok_ready, h_ready, hid_ready, y_ready, y_kept = (
                sem(n) for n in ("w_loaded", "tok_ready", "h_ready", "hid_ready", "y_ready", "y_kept"))

            with nc.Block() as block:
                @block.sync
                def _(sp):
                    for dst, given in zip((win, wout, b1, b2), experts):
                        sp.dma_start(whole(dst), given).then_inc(w_loaded, 16)
                    sp.dma_start(src[:, :], x["src"]).then_inc(loaded, 16)
                    sp.dma_start(keep[:, :], x["keep"]).then_inc(loaded, 16)
                    sp.dma_start(pen[:, :], x["pen"]).then_inc(loaded, 16)
                    sp.dma_start(whole(tgt), place_tbl.rearrange("(p c) h -> p c h", p=P)).then_inc(loaded, 16)
                    for k in range(2):
                        sp.dma_start(spare[:, 2 * k:2 * k + 2], x["first"][:, 0:2]).then_inc(written[k], 16)
                    with sp.Fori(0, CHUNKS // 2) as pair:
                        for k in range(2):
                            c = pair * 2 + k
                            sp.wait_ge(link, DVE_STEPS.after("skeep", c))
                            sp.dma_start(edge_v[:, bass.ds(c * (CHUNK * ROW_O), CHUNK * ROW_O)],
                                         out[k][:, :, :].rearrange("p c f -> p (c f)")).then_inc(written[k], 16)
                    for k in range(2):
                        sp.wait_ge(written[k], 16 * (CHUNKS // 2) + 16)

                @block.gpsimd
                def _(pool):
                    nc.gpsimd.memset(gate[:, :], 0.0).then_inc(set_, 1)
                    pool.wait_ge(loaded, 64)
                    pool.wait_ge(set_, 1)
                    with pool.Fori(0, CHUNKS // 2) as pair:
                        for k in range(2):
                            c = pair * 2 + k
                            pool.wait_ge(consumed, c + 1)
                            nc.gpsimd.tensor_copy(idx[k][:, :], src[:, bass.ds(c * CHUNK, CHUNK)]).then_inc(copied, 1)
                            pool.wait_ge(copied, c + 1)
                            nc.gpsimd.tensor_tensor(gate[:, 0:1], gate[:, 1:2], gate[:, 2:3], ALU.add)
                            for j in range(CHUNK):
                                nc.gpsimd.indirect_dma_start(out=got[k][:, j, :], out_offset=None, in_=node_tbl,
                                                             in_offset=Off(ap=idx[k][:, j:j + 1], axis=0),
                                                             bounds_check=NODES - 1, oob_is_err=False).then_inc(gathered[k], 16)

                @block.tensor
                def _(pe):
                    pe.wait_ge(w_loaded, 64)
                    with pe.Fori(0, CHUNKS // GATES) as turn:
                        for ex in range(GATES):
                            c = turn * GATES + ex
                            if ex == 0:
                                pe.wait_ge(tok_ready, turn + 1)
                            pe.wait_ge(hid_ready, c + 1)
                            nc.tensor.matmul(ps_h[:, :], win[:, ex, :], tokens[:, :], start=True, stop=True).then_inc(h_ready, 1)
                            pe.wait_ge(hid_ready, c + 2)
                            pe.wait_ge(y_kept, c + 1)
                            for g in range(GROUP):
                                last = nc.tensor.matmul(ps_y[:, g * C:(g + 1) * C], hid[:, g * P:(g + 1) * P], wout[:, ex, :],
                                                        start=True, stop=True)
                            last.then_inc(y_ready, 1)

                @block.scalar
                def _(act):
                    act.wait_ge(w_loaded, 64)
                    nc.scalar.activation(hid[:, 0:1], b1[:, 0:1], ACT.Copy).then_inc(hid_ready, 1)
                    act.wait_ge(y_kept, 1)
                    with act.Fori(0, CHUNKS // GATES) as turn:
                        for ex in range(GATES):
                            c = turn * GATES + ex
                            if ex == 0:
                                act.wait_ge(y_kept, c + 1)
                                nc.scalar.activation(tokens[:, :], tnT_sb[:, bass.ds(turn * HALF, HALF)], ACT.Copy).then_inc(tok_ready, 1)
                            act.wait_ge(link, DVE_STEPS.after("w0", c))
                            nc.scalar.activation(w[:, :, :], w[:, :, :], ACT.Exp).then_inc(exps, 1)
                            act.wait_ge(link, DVE_STEPS.after("r1", c))
                            nc.scalar.activation(r[:, :, :], r[:, :, :], ACT.Exp).then_inc(exps, 1)
                            act.wait_ge(y_kept, c + 1)
                            act.wait_ge(h_ready, c + 1)
                            nc.scalar.activation(hid[:, :], ps_h[:, :], ACT.Gelu, bias=b1[:, ex:ex + 1]).then_inc(hid_ready, 1)

                @block.vector
                def _(dve):
                    V = nc.vector
                    dve.wait_ge(loaded, 64)
                    V.memset(m[:, :, 0:1], -BIG).then_inc(link, 1)
                    V.memset(state[:, :], 0.0).then_inc(consumed, 2)
                    dve.wait_ge(link, 1)
                    dve.wait_ge(consumed, 2)
                    dve.wait_ge(w_loaded, 64)
                    V.memset(done[:, 0:1], 0.0).then_inc(y_kept, 1)
                    dve.wait_ge(y_kept, 1)
                    with dve.Fori(0, CHUNKS // GATES) as turn:
                        for ex in range(GATES):
                            c, k, pair = turn * GATES + ex, ex % 2, turn * (GATES // 2) + ex // 2
                            cols = bass.ds(c * CHUNK, CHUNK)

                            def own(name):
                                dve.wait_ge(link, DVE_STEPS.after(name, c))

                            for h in range(HEADS_G):
                                V.tensor_tensor_scan(ad[:, h, :], keep[:, cols], tgt[:, cols, h:h + 1].rearrange("p c o -> p (c o)"),
                                                     ad0[:, h:h + 1], ALU.mult, ALU.add).then_inc(link, 1)
                            own("t4")
                            V.tensor_copy(ad0[:, :], ad[:, :, CHUNK - 1]).then_inc(link, 1)
                            dve.wait_ge(gathered[k], pair * (16 * CHUNK) + 16 * CHUNK)
                            V.tensor_tensor(e[:, :, :], ad[:, :, :], got[k][:, :, HE:ROW_T].rearrange("p c h -> p h c"),
                                            ALU.add).then_inc(link, 1)
                            own("e")
                            V.scalar_tensor_tensor(e[:, :, :], e[:, :, :], 0.2, e[:, :, :], ALU.mult, ALU.max).then_inc(link, 1)
                            own("leaky")
                            for h in range(HEADS_G):
                                V.tensor_tensor_scan(m[:, h, 1:CHUNK + 1], pen[:, cols], e[:, h, :],
                                                     m[:, h, 0:1], ALU.add, ALU.max).then_inc(link, 1)
                            own("m4")
                            V.tensor_tensor(w[:, :, :], e[:, :, :], m[:, :, 1:CHUNK + 1], ALU.subtract).then_inc(link, 1)
                            V.tensor_tensor(r[:, :, :], m[:, :, 0:CHUNK],
                                            pen[:, cols].unsqueeze(1).broadcast_to([P, HEADS_G, CHUNK]), ALU.add).then_inc(link, 1)
                            own("r0")
                            V.tensor_tensor(r[:, :, :], r[:, :, :], m[:, :, 1:CHUNK + 1], ALU.subtract).then_inc(link, 1)
                            dve.wait_ge(exps, c * 2 + 2)
                            dve.wait_ge(written[k], pair * 16 + 16)
                            for h in range(HEADS_G):
                                V.tensor_tensor_scan(out[k][:, :, HEADS_G + h], r[:, h, :], w[:, h, :],
                                                     state[:, HEADS_G + h:HEADS_G + h + 1], ALU.mult, ALU.add).then_inc(link, 1)
                            V.tensor_tensor(msg[:, :, :].rearrange("p (h e) c -> p h e c", h=HEADS_G),
                                            got[k][:, :, 0:HE].rearrange("p c (h e) -> p h e c", h=HEADS_G),
                                            w[:, :, :].unsqueeze(2).broadcast_to([P, HEADS_G, GATES, CHUNK]), ALU.mult).then_inc(link, 1)
                            own("msg")
                            for f in range(HE):
                                V.tensor_tensor_scan(out[k][:, :, 2 * HEADS_G + f], r[:, f // GATES, :], msg[:, f, :],
                                                     state[:, 2 * HEADS_G + f:2 * HEADS_G + f + 1],
                                                     ALU.mult, ALU.add).then_inc(link, 1)
                            V.tensor_copy(out[k][:, :, 0:HEADS_G].rearrange("p c h -> p h c"), m[:, :, 1:CHUNK + 1]).then_inc(link, 1)
                            own("mcopy")
                            V.tensor_copy(m[:, :, 0:1], m[:, :, CHUNK:CHUNK + 1]).then_inc(link, 1)
                            V.tensor_copy(state[:, :], out[k][:, CHUNK - 1, :]).then_inc(link, 1)
                            own("skeep")
                            V.tensor_copy(done[:, 0:1], state[:, 0:1]).then_inc(consumed, 1)
                            dve.wait_ge(consumed, c + 3)
                            dve.wait_ge(y_ready, c + 1)
                            V.tensor_tensor(y_all[:, bass.ds(turn * GROUP, GROUP), ex * C:(ex + 1) * C],
                                            ps_y[:, :].rearrange("p (g c) -> p g c", g=GROUP),
                                            b2[:, ex, :].unsqueeze(1).broadcast_to([P, GROUP, C]), ALU.add).then_inc(y_kept, 1)

        with ExitStack() as ctx:
            def sb(name, shape, dt=fp32):
                return ctx.enter_context(nc.sbuf_tensor("k_" + name, shape, dt))

            def sem(name):
                return ctx.enter_context(nc.semaphore("k_" + name))

            con = sb("con", [P, K_COLS])
            whole_run = sb("whole_run", [P, 2])
            wide = sb("wide", [P, 4, HE])
            line, prev = sb("line", [HE, 4, P]), sb("prev", [HE, P])
            grow, wt = sb("grow", [HE, P]), sb("wt", [HE, P])
            shifted = sb("shifted", [HE, 3, P])
            back = sb("back", [P, ROW_O])
            ps = ctx.enter_context(nc.psum_tensor("k_ps", [P, HALF], fp32))
            ps2 = ctx.enter_context(nc.psum_tensor("k_ps2", [P, HALF], fp32))
            loaded, link, pe_done, exp_done, out_done = sem("loaded"), sem("link"), sem("pe"), sem("exp"), sem("out")
            exp_in = sem("exp_in")

            with nc.Block() as block:
                WIDE, EXPS, SHIFTED, LAST = 4, 11, 18, 21

                @block.sync
                def _(sp):
                    sp.dma_start(con[:, :], x["consts"]).then_inc(loaded, 16)
                    sp.dma_start(whole_run[:, :], x["first"][:, ECOLS - 2:ECOLS]).then_inc(loaded, 16)
                    sp.wait_ge(link, LAST)
                    sp.dma_start(carry_tbl, back[:, :]).then_inc(out_done, 16)
                    sp.wait_ge(out_done, 16)

                @block.tensor
                def _(pe):
                    pe.wait_ge(loaded, 32)
                    pe.wait_ge(link, WIDE)
                    for q in range(4):
                        last = nc.tensor.transpose(ps[0:HE, q * P:(q + 1) * P], wide[:, q, :], con[:, K_ID:K_ID + P])
                    last.then_inc(pe_done, 1)
                    pe.wait_ge(link, SHIFTED)
                    for q in range(3):
                        last = nc.tensor.transpose(ps2[:, q * HE:(q + 1) * HE], shifted[:, q, :], con[0:HE, K_ID:K_ID + HE])
                    last.then_inc(pe_done, 1)

                @block.scalar
                def _(act):
                    act.wait_ge(link, EXPS)
                    nc.scalar.activation(grow[:, :], grow[:, :], ACT.Exp).then_inc(exp_done, 1)
                    nc.scalar.activation(wt[:, :], wt[:, :], ACT.Exp).then_inc(exp_done, 1)

                @block.vector
                def _(dve):
                    V = nc.vector
                    count = [0]

                    def link_(ins):
                        ins.then_inc(link, 1)
                        count[0] += 1
                        dve.wait_ge(link, count[0])

                    def spread(a):
                        return a.unsqueeze(2).broadcast_to([P, HEADS_G, GATES])

                    def q4(q):
                        return wide[:, q, :].rearrange("p (h e) -> p h e", h=HEADS_G)

                    dve.wait_ge(loaded, 32)
                    link_(V.tensor_copy(wide[:, 0, :], whole_run[:, 1:2].broadcast_to([P, HE])))
                    link_(V.tensor_copy(q4(1), spread(state[:, 0:HEADS_G])))
                    link_(V.tensor_copy(q4(2), spread(state[:, HEADS_G:2 * HEADS_G])))
                    link_(V.tensor_copy(wide[:, 3, :], state[:, 2 * HEADS_G:ROW_O]))
                    assert count[0] == WIDE
                    dve.wait_ge(pe_done, 1)
                    link_(V.tensor_copy(line[:, :, :], ps[0:HE, :].rearrange("p (q c) -> p q c", q=4)))
                    link_(V.tensor_scalar(line[:, 0, :], line[:, 0, :], 1.0, BIG, ALU.subtract, ALU.mult))
                    link_(V.tensor_tensor_scan(shifted[:, 0, :], line[:, 0, :], line[:, 1, :], -BIG, ALU.add, ALU.max))
                    link_(V.memset(prev[:, 0:1], -BIG))
                    link_(V.tensor_copy(prev[:, 1:P], shifted[:, 0, 0:P - 1]))
                    link_(V.tensor_tensor(grow[:, :], prev[:, :], line[:, 0, :], ALU.add))
                    V.tensor_tensor(wt[:, :], line[:, 1, :], shifted[:, 0, :], ALU.subtract).then_inc(exp_in, 1)
                    dve.wait_ge(exp_in, 1)
                    link_(V.tensor_tensor(grow[:, :], grow[:, :], shifted[:, 0, :], ALU.subtract))
                    assert count[0] == EXPS
                    dve.wait_ge(exp_done, 2)
                    link_(V.tensor_tensor(line[:, 2, :], line[:, 2, :], wt[:, :], ALU.mult))
                    link_(V.tensor_tensor(line[:, 3, :], line[:, 3, :], wt[:, :], ALU.mult))
                    link_(V.memset(shifted[:, 1:3, 0:1], 0.0))
                    link_(V.tensor_tensor_scan(shifted[:, 1, 1:P], grow[:, 0:P - 1], line[:, 2, 0:P - 1], 0.0, ALU.mult, ALU.add))
                    link_(V.tensor_tensor_scan(shifted[:, 2, 1:P], grow[:, 0:P - 1], line[:, 3, 0:P - 1], 0.0, ALU.mult, ALU.add))
                    link_(V.tensor_copy(shifted[:, 0, :], prev[:, :]))
                    link_(V.memset(line[:, 0, 0:1], 0.0))
                    assert count[0] == SHIFTED
                    dve.wait_ge(pe_done, 2)

                    def head(q):
                        return ps2[:, q * HE:(q + 1) * HE].rearrange("p (h e) -> p h e", h=HEADS_G)[:, :, 0]

                    link_(V.tensor_copy(back[:, 0:HEADS_G], head(0)))
                    link_(V.tensor_copy(back[:, HEADS_G:2 * HEADS_G], head(1)))
                    link_(V.tensor_copy(back[:, 2 * HEADS_G:ROW_O], ps2[:, 2 * HE:3 * HE]))
                    assert count[0] == LAST

        with ExitStack() as ctx:
            def sb(name, shape, dt=fp32):
                return ctx.enter_context(nc.sbuf_tensor("j_" + name, shape, dt))

            def sem(name):
                return ctx.enter_context(nc.semaphore("j_" + name))

            near, far = sb("near", [P, TILES, ROW_O]), sb("far", [P, TILES, ROW_O])
            H4, H16 = [P, TILES, HEADS_G], [P, TILES, HE]
            es, top = sb("es", H4), sb("top", H4)
            wts = sb("wts", [P, 3, TILES, HEADS_G])
            den, tmp4 = sb("den", H4), sb("tmp4", H4)
            agg, tmp = sb("agg", H16), sb("tmp", H16)
            mean, rstd = sb("mean", [P, TILES]), sb("rstd", [P, TILES])
            eps = sb("eps", [P, 1])
            set_, link, taken, exps = sem("set"), sem("link"), sem("taken"), sem("exps")

            with nc.Block() as block:
                VAR = 25

                @block.gpsimd
                def _(pool):
                    G = nc.gpsimd
                    for t in (near, far):
                        G.memset(t[:, :, 0:HEADS_G], -BIG).then_inc(set_, 1)
                        G.memset(t[:, :, HEADS_G:ROW_O], 0.0).then_inc(set_, 1)
                    G.memset(eps[:, :], 1e-5).then_inc(set_, 1)
                    pool.wait_ge(set_, 5)
                    for i in range(TILES):
                        G.indirect_dma_start(out=near[:, i, :], out_offset=None, in_=edge_tbl,
                                             in_offset=Off(ap=end_idx[:, i:i + 1], axis=0),
                                             bounds_check=EDGES - 1, oob_is_err=False).then_inc(taken, 16)
                        G.indirect_dma_start(out=far[:, i, :], out_offset=None, in_=carry_tbl,
                                             in_offset=Off(ap=carry_idx[:, i:i + 1], axis=0),
                                             bounds_check=P - 1, oob_is_err=False).then_inc(taken, 16)

                @block.scalar
                def _(act):
                    nc.scalar.preload_act_table_set("natural_log_exp_and_others")
                    act.wait_ge(link, 7)
                    nc.scalar.activation(whole(wts), whole(wts), ACT.Exp).then_inc(exps, 1)
                    act.wait_ge(link, VAR)
                    nc.scalar.activation(rstd[:, :], rstd[:, :], ACT.Ln, bias=eps[:, :], scale=1.0 / HE).then_inc(exps, 1)
                    act.wait_ge(exps, 2)
                    nc.scalar.activation(rstd[:, :], rstd[:, :], ACT.Exp, scale=-0.5).then_inc(exps, 1)

                @block.vector
                def _(dve):
                    V = nc.vector
                    TT = V.tensor_tensor
                    count = [0]

                    def link_(ins):
                        ins.then_inc(link, 1)
                        count[0] += 1
                        dve.wait_ge(link, count[0])

                    def spread(a):
                        return a.unsqueeze(3).broadcast_to([P, TILES, HEADS_G, GATES])

                    def heads(a):
                        return a.rearrange("p i (h e) -> p i h e", h=HEADS_G)

                    def vec(at):
                        return att[:, at * HE:(at + 1) * HE].unsqueeze(1).broadcast_to(H16)

                    NM, NS, NF = slice(0, HEADS_G), slice(HEADS_G, 2 * HEADS_G), slice(2 * HEADS_G, ROW_O)
                    dve.wait_ge(set_, 5)
                    link_(TT(whole(es), row[:, :, HE:ROW_T], whole(adst), ALU.add))
                    link_(V.scalar_tensor_tensor(whole(es), whole(es), 0.2, whole(es), ALU.mult, ALU.max))
                    dve.wait_ge(taken, 16 * 2 * TILES)
                    link_(TT(whole(top), near[:, :, NM], far[:, :, NM], ALU.max))
                    link_(TT(whole(top), whole(top), whole(es), ALU.max))
                    link_(TT(wts[:, 0, :, :], near[:, :, NM], whole(top), ALU.subtract))
                    link_(TT(wts[:, 1, :, :], far[:, :, NM], whole(top), ALU.subtract))
                    link_(TT(wts[:, 2, :, :], whole(es), whole(top), ALU.subtract))
                    dve.wait_ge(exps, 1)
                    link_(TT(whole(den), near[:, :, NS], wts[:, 0, :, :], ALU.mult))
                    link_(TT(whole(tmp4), far[:, :, NS], wts[:, 1, :, :], ALU.mult))
                    link_(TT(whole(den), whole(den), whole(tmp4), ALU.add))
                    link_(TT(whole(den), whole(den), wts[:, 2, :, :], ALU.add))
                    link_(V.tensor_scalar_add(whole(den), whole(den), 1e-16))
                    link_(V.reciprocal(whole(den), whole(den)))
                    link_(TT(heads(whole(agg)), heads(near[:, :, NF]), spread(wts[:, 0, :, :]), ALU.mult))
                    link_(TT(heads(whole(tmp)), heads(far[:, :, NF]), spread(wts[:, 1, :, :]), ALU.mult))
                    link_(TT(whole(agg), whole(agg), whole(tmp), ALU.add))
                    link_(TT(heads(whole(tmp)), heads(row[:, :, 0:HE]), spread(wts[:, 2, :, :]), ALU.mult))
                    link_(TT(whole(agg), whole(agg), whole(tmp), ALU.add))
                    link_(TT(heads(whole(agg)), heads(whole(agg)), spread(whole(den)), ALU.mult))
                    link_(TT(whole(agg), whole(agg), vec(2), ALU.add))
                    link_(V.reduce_sum(mean[:, :], whole(agg), AX))
                    link_(V.tensor_scalar(mean[:, :], mean[:, :], 1.0 / HE, None, ALU.mult))
                    link_(TT(whole(agg), whole(agg), mean[:, :].unsqueeze(2).broadcast_to(H16), ALU.subtract))
                    link_(TT(whole(tmp), whole(agg), whole(agg), ALU.mult))
                    link_(V.reduce_sum(rstd[:, :], whole(tmp), AX))
                    assert count[0] == VAR
                    dve.wait_ge(exps, 3)
                    link_(TT(whole(agg), whole(agg), rstd[:, :].unsqueeze(2).broadcast_to(H16), ALU.mult))
                    link_(TT(whole(agg), whole(agg), vec(3), ALU.mult))
                    link_(TT(whole(agg), whole(agg), vec(4), ALU.add))
                    link_(V.tensor_reduce(whole(scores), agg[:, :, :].rearrange("p i (h e) -> p i e h", h=HEADS_G), AX, ALU.add))
                    link_(V.tensor_scalar(whole(scores), whole(scores), 1.0 / HEADS_G, None, ALU.mult))


def gated_sum_stage(nc, gates, y_all, t_sb):
    from concourse import mybir
    fp32, ALU = mybir.dt.float32, mybir.AluOpType
    with nc.sbuf_tensor("gs_sum", [P, TILES, C], fp32) as total, nc.semaphore("gs_link") as link, nc.Block() as block:
        @block.vector
        def _(dve):
            V = nc.vector
            y = y_all[:, :, :].rearrange("p i (e c) -> p i e c", e=GATES)
            V.tensor_tensor(y, y, gates[:, :, :].unsqueeze(3).broadcast_to([P, TILES, GATES, C]), ALU.mult).then_inc(link, 1)
            dve.wait_ge(link, 1)
            V.tensor_reduce(total[:, :, :], y_all[:, :, :].rearrange("p i (e c) -> p i c e", e=GATES),
                            mybir.AxisListType.X, ALU.add).then_inc(link, 1)
            dve.wait_ge(link, 2)
            V.tensor_tensor(t_sb[:, :, :], t_sb[:, :, :], total[:, :, :], ALU.add).then_inc(link, 1)
            dve.wait_ge(link, 3)


def _blocks(w):
    import numpy as np
    out = np.zeros(w.shape[:-2] + (2 * w.shape[-2], 2 * w.shape[-1]), w.dtype)
    out[..., :w.shape[-2], :w.shape[-1]] = w
    out[..., w.shape[-2]:, w.shape[-1]:] = w
    return out


def _ssm_parameters(inp):
    import numpy as np
    T = lambda a: np.swapaxes(a, -1, -2)
    out = np.zeros((LAYERS, P, W_COLS), np.float32)
    out[:, :, W_PROJ:W_PROJ + P] = _blocks(T(inp["L0_conv_proj_w"]))
    out[:, :, W_CF:W_CF + P] = _blocks(T(inp["L0_conv_convf_w"]))
    out[:, :, W_CB:W_CB + P] = _blocks(T(inp["L0_conv_convb_w"]))
    dbc = inp["L0_conv_dbc_w"]
    out[:, :2 * RANK, W_DL:W_DL + P] = _blocks(dbc[:, :RANK])
    for part in range(3):
        out[:, :, W_B + 32 * part:W_B + 32 * part + 32] = _blocks(T(dbc[:, RANK:RANK + NST]))
        out[:, :, W_C + 32 * part:W_C + 32 * part + 32] = _blocks(T(dbc[:, RANK + NST:]))
    out[:, :2 * RANK, W_DT:W_DT + P] = _blocks(T(inp["L0_conv_dtp_w"]))
    for col, name in ((V_G, "ln_g"), (V_LB, "ln_b"), (V_PB, "proj_b"), (V_CFB, "convf_b"), (V_CBB, "convb_b"), (V_DTB, "dtp_b"), (V_D, "D_param")):
        out[:, :, col] = np.concatenate([inp["L0_conv_" + name]] * 2, 1)
    out[:, :, V_ALOG:V_ALOG + NST] = np.concatenate([inp["L0_conv_A_log"]] * 2, 1)
    return out


def _constants():
    import numpy as np
    k = np.zeros((P, K_COLS), np.float32)
    row = np.arange(P)
    k[:, K_MEAN:K_MEAN + P] = (row[:, None] // C == row[None, :] // C) / np.float32(C)
    k[:, K_ID:K_ID + P] = np.eye(P)
    k[:, K_PAIR:K_PAIR + P] = (row[:, None] // 2 == row[None, :] // 2) / np.float32(2)
    k[:, K_ONE:K_ONE + P] = 1
    k[:, K_TWO] = 2
    k[:, K_SPLIT] = np.where(row >= 32, -1, 0)
    k[:, K_SPLIT + 1] = np.where(row >= 64, -1, 0)
    k[:, K_SPLIT + 2] = 1e-5
    sign = lambda bit: 1 - 2 * ((row >> bit) & 1)
    k[:, K_SIGN], k[:, K_SIGN + 1] = sign(0), -sign(0)
    for b in range(1, 7):
        k[:, K_SIGN + 1 + b] = sign(b) * sign(b - 1)
    k[:, K_SIGN + 8] = sign(6)
    k[:, K_MASK:K_MASK + 64] = row[:, None] // 32 == np.arange(64)[None, :] // 16
    return k


def _selectors():
    import numpy as np
    k = np.arange(96)[:, None, None] % 32
    n = np.arange(NST)[None, :, None]
    m = np.arange(P)[None, None, :]
    return (k == (m // C) * NST + n).astype(np.float32).reshape(96, NST * P)


def _conv_weights(inp):
    import numpy as np
    out = np.zeros((P, CW_COLS), np.float32)
    tap = lambda w: w.transpose(2, 3, 1, 0).reshape(9, C, w.shape[0])
    qk = np.zeros((P, 9, P), np.float32)
    for col, w in ((0, inp["L1_conv_wq"]), (Q_COLS, inp["L1_conv_wk"])):
        padded = np.zeros((9, C, 32), np.float32)
        padded[:, :, :C // 4] = tap(w)
        qk[:, :, col:col + Q_COLS] = _blocks(padded).transpose(1, 0, 2)
    out[:, CW_QK:CW_QK + 9 * P] = qk.reshape(P, -1)
    out[:, CW_V:CW_V + 9 * P] = _blocks(tap(inp["L1_conv_wv"])).transpose(1, 0, 2).reshape(P, -1)
    out[:, CW_FC1:CW_FC1 + 8] = _blocks(inp["L1_conv_fc1_w"].T)
    out[:8, CW_FC2:CW_FC2 + P] = _blocks(inp["L1_conv_fc2_w"].T)
    fuse = inp["L1_conv_fuse_w"][:, :, 0, 0].T
    out[:C, CW_FL:CW_FL + C] = fuse[:C]
    out[:C, CW_FG:CW_FG + C] = out[C:, CW_FG:CW_FG + C] = fuse[C:]
    for b in range(2):
        out[32 * b:32 * b + 16, CV_BQ] = inp["L1_conv_bq"]
        out[Q_COLS + 32 * b:Q_COLS + 32 * b + 16, CV_BK] = inp["L1_conv_bk"]
        out[4 * b:4 * b + 4, CV_B1] = inp["L1_conv_fc1_b"]
        out[C * b:C * (b + 1), CV_B2] = inp["L1_conv_fc2_b"]
    out[:, CV_BV] = np.concatenate([inp["L1_conv_bv"]] * 2)
    out[:, CR_FB:CR_FB + C] = inp["L1_conv_fuse_b"][None]
    return out


def _padded_heads(w):
    import numpy as np
    out = np.zeros((C, HEADS2, 32), np.float32)
    out[:, :, :HDIM2] = w.reshape(C, HEADS2, HDIM2)
    return out.reshape(C, P)


def _slice_weights(inp):
    import numpy as np
    out = np.zeros((P, SW_COLS), np.float32)
    out[:C, SW_0:SW_0 + C] = inp["L3_attn_W0"]
    out[:C, SW_S:SW_S + SLICES] = inp["L3_attn_Ws"]
    out[:C, SW_QKV:SW_QKV + 3 * HD3] = inp["L3_attn_Wqkv"]
    out[C, SW_QKV:SW_QKV + 3 * HD3] = inp["L3_attn_bqkv"]
    out[:, SW_OUT:SW_OUT + 2 * C] = inp["L3_attn_Wout"].reshape(2, P, C).transpose(1, 0, 2).reshape(P, 2 * C)
    out[:C, SV_B0] = inp["L3_attn_b0"]
    out[:, SR_B0:SR_B0 + C] = inp["L3_attn_b0"][None]
    out[:, SR_BS:SR_BS + SLICES] = inp["L3_attn_bs"][None]
    out[:, SR_BO:SR_BO + C] = inp["L3_attn_bout"][None]
    return out


def _graph_vectors(inp):
    import numpy as np
    row = np.concatenate([inp["L2_ffn_" + n].reshape(-1) for n in ("att_src", "att_dst", "b_gat", "ln_gamma", "ln_beta")])
    return np.ascontiguousarray(np.broadcast_to(row[None], (P, row.size)))
def build(nc, a, out):
    from concourse import mybir
    from contextlib import ExitStack
    fp32 = mybir.dt.float32
    con = a["consts"]
    tables = graph_tables(nc)
    sort_stage(nc, a["edges"], con, *[tables[n] for n in ("src", "keep", "pen", "first", "ends_i", "place_i", "target0")])
    with nc.sbuf_tensor("t_sb", [P, TILES, C], fp32) as t_sb:
        with ExitStack() as notes_ctx:
            notes = EndsNotes(nc, notes_ctx, tables["ends_i"], tables["place_i"], tables["ends"])
            with nc.sbuf_tensor("x_sb", [P, PAIRS, L], fp32) as x_sb:
                ssm_stage(nc, a["x"], a["ssm"], con, a["selectors"], x_sb)
                conv_stage(nc, a["conv"], con, x_sb, t_sb, notes)
            with nc.sbuf_tensor("tn_a", [P, TILES, C], fp32) as tn_sb:
                norm_stage(nc, con, t_sb, tn_sb, "n1")
                graph_attn_stage(nc, a["attn_padded"], a["attn"], con, tn_sb, t_sb, notes)
        with (nc.sbuf_tensor("tnT_a", [C, TOK], fp32) as tnT_sb,
              nc.sbuf_tensor("gates_a", [P, TILES, GATES], fp32) as gates,
              nc.sbuf_tensor("feat", [P, TILES, HE], fp32) as feat):
            with nc.sbuf_tensor("tn_b", [P, TILES, C], fp32) as tn_sb:
                norm_stage(nc, con, t_sb, tn_sb, "n2")
                project_stage(nc, a["gat"], a["gat_bias"], con, tn_sb, tnT_sb, feat, "pa")
            with nc.sbuf_tensor("y_all", [P, TILES, GATES * C], fp32) as y_all:
                graph_stage(nc, a["gat_vectors"], feat, tables, [a["moe2_" + n] for n in ("in", "out", "b1", "b2")],
                            tnT_sb, y_all, dict(tables, scores=gates, consts=con))
                top2_stage(nc, gates, "ta")
                gated_sum_stage(nc, gates, y_all, t_sb)
        with nc.sbuf_tensor("tn_c", [P, TILES, C], fp32) as tn_sb:
            norm_stage(nc, con, t_sb, tn_sb, "n3")
            slice_attn_stage(nc, a["slice"], con, tn_sb, t_sb)
            norm_stage(nc, con, t_sb, tn_sb, "n4")
            with (nc.sbuf_tensor("tnT_b", [C, TOK], fp32) as tnT_sb,
                  nc.sbuf_tensor("gates_b", [P, TILES, EXPERTS], fp32) as gates):
                project_stage(nc, a["gate_w"], a["gate_b"], con, tn_sb, tnT_sb, gates, "pb")
                top2_stage(nc, gates, "tb")
                expert_stage(nc, a["moe3_in"], a["moe3_gate"], a["moe3_out"], gates, tnT_sb, t_sb, "eb")
        with nc.semaphore("written_out") as written_out, nc.Block() as block:
            @block.sync
            def _(sp):
                sp.dma_start(out, t_sb[:, :, :]).then_inc(written_out, 16)
                sp.wait_ge(written_out, 16)


def kernel(**inputs):
    import numpy as np
    import concourse.bacc as bacc
    from concourse import mybir
    from concourse.bass_utils import run_bass_kernel_spmd

    inp = {k: np.asarray(v) for k, v in inputs.items()}
    flat = np.ascontiguousarray

    def rows(v):
        return flat(np.broadcast_to(v[None], (P,) + v.shape))

    arrays = {
        "x": flat(inp["x"].reshape(PAIRS, P, L).transpose(1, 0, 2)),
        "edges": flat(inp["L2_ffn_edge_index"].reshape(2, P, ECOLS)),
        "consts": _constants(), "selectors": _selectors(),
        "ssm": _ssm_parameters(inp), "conv": _conv_weights(inp),
        "attn_padded": _padded_heads(inp["L2_attn_W"]), "attn": flat(inp["L2_attn_W"]),
        "gat": flat(inp["L2_ffn_W_gat"]), "gat_bias": np.zeros((P, HE), np.float32), "gat_vectors": _graph_vectors(inp),
        "moe2_in": flat(inp["L2_ffn_W1"].transpose(1, 0, 2)), "moe2_out": flat(inp["L2_ffn_W2"].transpose(1, 0, 2)),
        "moe2_b1": flat(inp["L2_ffn_b1"].T), "moe2_b2": rows(inp["L2_ffn_b2"]),
        "slice": _slice_weights(inp),
        "gate_w": flat(inp["L3_ffn_gate_w"]), "gate_b": rows(inp["L3_ffn_gate_b"]),
        "moe3_in": flat(inp["L3_ffn_w1"].transpose(1, 0, 2)), "moe3_gate": flat(inp["L3_ffn_w2"].transpose(1, 0, 2)),
        "moe3_out": flat(inp["L3_ffn_w3"].transpose(1, 0, 2)),
    }
    nc = bacc.Bacc("TRN2", target_bir_lowering=False, num_devices=1)
    aps = {n: nc.dram_tensor("in_" + n, a.shape, mybir.dt.from_np(a.dtype), kind="ExternalInput").ap()
           for n, a in arrays.items()}
    out = nc.dram_tensor("out", (P, TILES, C), mybir.dt.float32, kind="ExternalOutput").ap()
    build(nc, aps, out)
    result = run_bass_kernel_spmd(nc, [{"in_" + n: a for n, a in arrays.items()}], core_ids=[0])
    tokens = result.results[0]["out"].transpose(1, 0, 2).reshape(B, L, C)
    return flat(tokens.transpose(0, 2, 1)).reshape(B, C, H, W)
```
